# Optimizing a Trainium2 kernel written in Bass

```python
import numpy as np
import jax
import jax.numpy as jnp

def _softmax(x, axis=-1):
    return jax.nn.softmax(x, axis=axis)

def _gelu(x):
    return jax.nn.gelu(x, approximate=True)

def _silu(x):
    return jax.nn.silu(x)

def _sigmoid(x):
    return jax.nn.sigmoid(x)

def _layernorm(x, axis=-1, eps=1e-05):
    m = jnp.mean(x, axis=axis, keepdims=True)
    v = jnp.var(x, axis=axis, keepdims=True)
    return (x - m) / jnp.sqrt(v + eps)

def _scatter_add(tgt, idx, src, axis=0):
    return tgt.at[idx].add(src)

def _segment_sum(src, seg, n):
    return jax.ops.segment_sum(src, seg, n)
kernel_name = 'mk_recurrent_d4_jaxref_r8_a92b42'

def setup_inputs(seed: int=0):
    np.random.seed(seed)
    _w = jnp.asarray

    def _L0_attn_setup():
        import jax, jax.numpy as jnp
        import numpy as np
        N_LAYER, N_HEAD, D_MODEL, D_FF = (6, 16, 128, 512)
        D_HEAD = D_MODEL // N_HEAD
        M_FEAT = 2 * D_MODEL // N_HEAD
        CHUNK = 128
        LN_EPS = 1e-05
        ATT_EPS = 1e-06
        B, S = (4, 256)

        def _layer_norm(x, g, b):
            mu = x.mean(-1, keepdims=True)
            var = ((x - mu) ** 2).mean(-1, keepdims=True)
            return (x - mu) * jax.lax.rsqrt(var + LN_EPS) * g + b

        def _favor_phi(x, omega):
            x = x * D_HEAD ** (-0.25)
            u = jnp.einsum('bhsd,dm->bhsm', x, omega)
            nrm = 0.5 * jnp.sum(x * x, axis=-1, keepdims=True)
            phi = jnp.concatenate([jnp.exp(u - nrm), jnp.exp(-u - nrm)], axis=-1)
            return phi * M_FEAT ** (-0.5)

        def _causal_linear_attention(Qp, Kp, V):
            b, h, s, m = Qp.shape
            d = V.shape[-1]
            c = s // CHUNK
            Qc = Qp.reshape(b, h, c, CHUNK, m)
            Kc = Kp.reshape(b, h, c, CHUNK, m)
            Vc = V.reshape(b, h, c, CHUNK, d)
            kv = jnp.einsum('bhclm,bhcld->bhcmd', Kc, Vc)
            ksum = Kc.sum(axis=3)
            kv_pre = jnp.cumsum(kv, axis=2) - kv
            ks_pre = jnp.cumsum(ksum, axis=2) - ksum
            scores = jnp.einsum('bhcim,bhcjm->bhcij', Qc, Kc)
            mask = jnp.tril(jnp.ones((CHUNK, CHUNK), bool))
            scores = jnp.where(mask, scores, 0.0)
            num = jnp.einsum('bhcij,bhcjd->bhcid', scores, Vc) + jnp.einsum('bhcim,bhcmd->bhcid', Qc, kv_pre)
            den = scores.sum(-1) + jnp.einsum('bhcim,bhcm->bhci', Qc, ks_pre)
            out = num / (den[..., None] + ATT_EPS)
            return out.reshape(b, h, s, d)

        def _forward(x, Wq, bq, Wk, bk, Wv, bv, Wo, bo, omega, g1, be1, W1, bf1, W2, bf2, g2, be2):
            bsz, slen, _ = x.shape
            out = x
            for l in range(N_LAYER):

                def proj(W, bvec):
                    y = jnp.einsum('bsd,de->bse', out, W) + bvec
                    return y.reshape(bsz, slen, N_HEAD, D_HEAD).transpose(0, 2, 1, 3)
                q = proj(Wq[l], bq[l])
                k = proj(Wk[l], bk[l])
                v = proj(Wv[l], bv[l])
                Qp = _favor_phi(q, omega[l])
                Kp = _favor_phi(k, omega[l])
                a = _causal_linear_attention(Qp, Kp, v)
                a = a.transpose(0, 2, 1, 3).reshape(bsz, slen, D_MODEL)
                a = jnp.einsum('bsd,de->bse', a, Wo[l]) + bo[l]
                h1 = _layer_norm(out + a, g1[l], be1[l])
                y = jax.nn.relu(jnp.einsum('bsd,df->bsf', h1, W1[l]) + bf1[l])
                y = jnp.einsum('bsf,fd->bsd', y, W2[l]) + bf2[l]
                out = _layer_norm(h1 + y, g2[l], be2[l])
            return out
        key = jax.random.key(seed)
        ks = jax.random.split(key, 12)
        s = D_MODEL ** (-0.5)
        f32 = jnp.float32
        return {'x': jax.random.normal(ks[0], (B, S, D_MODEL), f32), 'Wq': jax.random.normal(ks[1], (N_LAYER, D_MODEL, D_MODEL), f32) * s, 'bq': jnp.zeros((N_LAYER, D_MODEL), f32), 'Wk': jax.random.normal(ks[2], (N_LAYER, D_MODEL, D_MODEL), f32) * s, 'bk': jnp.zeros((N_LAYER, D_MODEL), f32), 'Wv': jax.random.normal(ks[3], (N_LAYER, D_MODEL, D_MODEL), f32) * s, 'bv': jnp.zeros((N_LAYER, D_MODEL), f32), 'Wo': jax.random.normal(ks[4], (N_LAYER, D_MODEL, D_MODEL), f32) * s, 'bo': jnp.zeros((N_LAYER, D_MODEL), f32), 'omega': jax.random.normal(ks[5], (N_LAYER, D_HEAD, M_FEAT // 2), f32), 'g1': jnp.ones((N_LAYER, D_MODEL), f32), 'be1': jnp.zeros((N_LAYER, D_MODEL), f32), 'W1': jax.random.normal(ks[6], (N_LAYER, D_MODEL, D_FF), f32) * s, 'bf1': jnp.zeros((N_LAYER, D_FF), f32), 'W2': jax.random.normal(ks[7], (N_LAYER, D_FF, D_MODEL), f32) * D_FF ** (-0.5), 'bf2': jnp.zeros((N_LAYER, D_MODEL), f32), 'g2': jnp.ones((N_LAYER, D_MODEL), f32), 'be2': jnp.zeros((N_LAYER, D_MODEL), f32)}
    _L0_attn_in = _L0_attn_setup()

    def _L0_ffn_setup():
        import jax, jax.numpy as jnp
        import numpy as np
        DIM = 128
        DEPTH = 2
        HEADS = 8
        DIM_HEAD = 64
        WINDOW = 64
        INNER = HEADS * DIM_HEAD
        HID = int(DIM * 4 * 2 / 3)
        B, N = (2, 1024)
        QK_SCALE = 8.0

        def shift_token(t):
            t1, t2 = jnp.split(t, 2, axis=-1)
            t2 = jnp.pad(t2, ((0, 0), (1, 0), (0, 0)))[:, :-1]
            return jnp.concatenate([t1, t2], axis=-1)

        def l2norm(t):
            return t / jnp.clip(jnp.linalg.norm(t, axis=-1, keepdims=True), 1e-12)

        def rotate_half(x):
            x1, x2 = jnp.split(x, 2, axis=-1)
            return jnp.concatenate([-x2, x1], axis=-1)

        def rotary_xpos(q, k):
            n = q.shape[-2]
            half_idx = jnp.arange(0, DIM_HEAD, 2, dtype=jnp.float32)
            inv_freq = 1.0 / 10000.0 ** (half_idx / DIM_HEAD)
            t = jnp.arange(n, dtype=jnp.float32)
            freqs = t[:, None] * inv_freq[None, :]
            freqs = jnp.concatenate([freqs, freqs], axis=-1)
            base = (half_idx + 0.4 * DIM_HEAD) / (1.4 * DIM_HEAD)
            power = (t - n // 2) / float(WINDOW // 2)
            scale = base[None, :] ** power[:, None]
            scale = jnp.concatenate([scale, scale], axis=-1)
            cos, sin = (jnp.cos(freqs), jnp.sin(freqs))
            q = q * cos * scale + rotate_half(q) * sin * scale
            k = k * cos / scale + rotate_half(k) * sin / scale
            return (q, k)

        def local_attention(q, k, v):
            b, h, n, d = q.shape
            w = n // WINDOW
            bq = q.reshape(b, h, w, WINDOW, d) * QK_SCALE
            bk = k.reshape(b, h, w, WINDOW, d)
            bv = v.reshape(b, h, w, WINDOW, d)

            def look_around(t):
                p = jnp.pad(t, ((0, 0), (0, 0), (1, 0), (0, 0), (0, 0)))
                return jnp.concatenate([p[:, :, :w], p[:, :, 1:]], axis=3)
            bk, bv = (look_around(bk), look_around(bv))
            bt = jnp.arange(n).reshape(w, WINDOW)
            btp = jnp.pad(bt, ((1, 0), (0, 0)), constant_values=-1)
            btk = jnp.concatenate([btp[:w], btp[1:]], axis=1)
            sim = jnp.einsum('bhwid,bhwjd->bhwij', bq, bk)
            i = bt[:, :, None]
            j = btk[:, None, :]
            mask = (i < j) | (i > j + WINDOW) | (j == -1)
            sim = jnp.where(mask, -jnp.finfo(sim.dtype).max, sim)
            attn = jax.nn.softmax(sim, axis=-1)
            out = jnp.einsum('bhwij,bhwjd->bhwid', attn, bv)
            return out.reshape(b, h, n, d)

        def _layer(x, wqkv, qs, ksc, wo, lg, lb, w1, b1, w2, b2):
            b, n, _ = x.shape
            h = shift_token(x)
            qkv = h @ wqkv
            q, k, v = jnp.split(qkv, 3, axis=-1)
            to_heads = lambda t: t.reshape(b, n, HEADS, DIM_HEAD).transpose(0, 2, 1, 3)
            q, k, v = (to_heads(q), to_heads(k), to_heads(v))
            q = l2norm(q) * qs
            k = l2norm(k) * ksc
            q, k = rotary_xpos(q, k)
            o = local_attention(q, k, v)
            o = o.transpose(0, 2, 1, 3).reshape(b, n, INNER)
            x = x + o @ wo
            h = shift_token(x)
            mu = h.mean(-1, keepdims=True)
            var = h.var(-1, keepdims=True)
            h = (h - mu) / jnp.sqrt(var + 1e-05) * lg + lb
            h = h @ w1 + b1
            a, g = jnp.split(h, 2, axis=-1)
            h = a * jax.nn.gelu(g, approximate=False)
            x = x + h @ w2 + b2
            return x
        key = jax.random.key(seed)
        ks = jax.random.split(key, 6)
        return {'x': jax.random.normal(ks[0], (B, N, DIM), jnp.float32), 'wqkv': jax.random.normal(ks[1], (DEPTH, DIM, 3 * INNER), jnp.float32) * 0.02, 'q_scale': jnp.ones((DEPTH, DIM_HEAD), jnp.float32), 'k_scale': jnp.ones((DEPTH, DIM_HEAD), jnp.float32), 'wo': jax.random.normal(ks[2], (DEPTH, INNER, DIM), jnp.float32) * 0.02, 'ln_g': jnp.ones((DEPTH, DIM), jnp.float32), 'ln_b': jnp.zeros((DEPTH, DIM), jnp.float32), 'w1': jax.random.normal(ks[3], (DEPTH, DIM, 2 * HID), jnp.float32) * 0.02, 'b1': jnp.zeros((DEPTH, 2 * HID), jnp.float32), 'w2': jax.random.normal(ks[4], (DEPTH, HID, DIM), jnp.float32) * 0.02, 'b2': jnp.zeros((DEPTH, DIM), jnp.float32)}
    _L0_ffn_in = _L0_ffn_setup()

    def _L1_attn_setup():
        import jax, jax.numpy as jnp
        import numpy as np
        B, T, D = (2, 512, 128)
        H, DK, DV = (8, 128, 128)
        INTER = 512
        CHUNK = 128
        EPS = 1e-05

        def rmsnorm(x, w, eps=EPS):
            return x * jax.lax.rsqrt(jnp.mean(x * x, axis=-1, keepdims=True) + eps) * w

        def linear_attention(x, Wq, Wk, Wv, Wo, out_norm_w):
            b, t, d = x.shape
            n = t // CHUNK
            q = (x @ Wq).reshape(b, t, H, DK).transpose(0, 2, 1, 3)
            k = (x @ Wk).reshape(b, t, H, DK).transpose(0, 2, 1, 3)
            v = (x @ Wv).reshape(b, t, H, DV).transpose(0, 2, 1, 3)
            qc = q.reshape(b, H, n, CHUNK, DK).transpose(2, 0, 1, 3, 4)
            kc = k.reshape(b, H, n, CHUNK, DK).transpose(2, 0, 1, 3, 4)
            vc = v.reshape(b, H, n, CHUNK, DV).transpose(2, 0, 1, 3, 4)
            causal = jnp.tril(jnp.ones((CHUNK, CHUNK), dtype=bool))

            def step(S, qkv):
                qb, kb, vb = qkv
                attn = jnp.einsum('bhid,bhjd->bhij', qb, kb)
                attn = jnp.where(causal, attn, 0.0)
                o = jnp.einsum('bhij,bhjv->bhiv', attn, vb) + jnp.einsum('bhid,bhdv->bhiv', qb, S)
                S = S + jnp.einsum('bhid,bhiv->bhdv', kb, vb)
                return (S, o)
            S0 = jnp.zeros((b, H, DK, DV), x.dtype)
            _, o = jax.lax.scan(step, S0, (qc, kc, vc))
            o = o.transpose(1, 2, 0, 3, 4).reshape(b, H, t, DV)
            o = rmsnorm(o, out_norm_w)
            o = o.transpose(0, 2, 1, 3).reshape(b, t, H * DV)
            return o @ Wo
        key = jax.random.key(seed)
        ks = jax.random.split(key, 9)
        s = 0.02
        return {'hidden_states': jax.random.normal(ks[0], (B, T, D), jnp.float32), 'attn_norm_w': jnp.ones((D,), jnp.float32), 'Wq': jax.random.normal(ks[1], (D, H * DK), jnp.float32) * s, 'Wk': jax.random.normal(ks[2], (D, H * DK), jnp.float32) * s, 'Wv': jax.random.normal(ks[3], (D, H * DV), jnp.float32) * s, 'Wo': jax.random.normal(ks[4], (H * DV, D), jnp.float32) * s, 'attn_out_norm_w': jnp.ones((DV,), jnp.float32), 'mlp_norm_w': jnp.ones((D,), jnp.float32), 'Wgate': jax.random.normal(ks[5], (D, INTER), jnp.float32) * s, 'Wup': jax.random.normal(ks[6], (D, INTER), jnp.float32) * s, 'Wdown': jax.random.normal(ks[7], (INTER, D), jnp.float32) * s}
    _L1_attn_in = _L1_attn_setup()

    def _L1_ffn_setup():
        import jax, jax.numpy as jnp
        import numpy as np
        T, Z, D_DIM = (8, 256, 128)
        N_EXP, P_SLOT, H = (64, 32, 128)
        LN_EPS = 1e-05
        key = jax.random.key(seed)
        k = jax.random.split(key, 5)
        s = 0.02
        return {'x': jax.random.normal(k[0], (T, Z, D_DIM), dtype=jnp.float32), 'phi_w': jax.random.normal(k[1], (N_EXP * P_SLOT, D_DIM), dtype=jnp.float32) * s, 'phi_b': jax.random.normal(k[2], (N_EXP * P_SLOT,), dtype=jnp.float32) * s, 'expert_w': jax.random.normal(k[3], (N_EXP, D_DIM, H), dtype=jnp.float32) * s, 'expert_b': jax.random.normal(k[4], (N_EXP, H), dtype=jnp.float32) * s}
    _L1_ffn_in = _L1_ffn_setup()

    def _L2_attn_setup():
        import jax, jax.numpy as jnp
        import numpy as np
        DIM, SSM, RNN = (128, 64, 128)
        key = jax.random.key(seed)
        ks = jax.random.split(key, 16)
        s = 0.02
        B, N = (8, 256)
        return {'x': jax.random.normal(ks[0], (B, N, DIM), jnp.float32), 'A': jax.random.normal(ks[1], (SSM, SSM), jnp.float32) * s, 'Bw': jax.random.normal(ks[2], (SSM, DIM), jnp.float32) * s, 'Bb': jnp.zeros((SSM,), jnp.float32), 'Cw': jax.random.normal(ks[3], (DIM, SSM), jnp.float32) * s, 'Cb': jnp.zeros((DIM,), jnp.float32), 'Dw': jax.random.normal(ks[4], (DIM, DIM), jnp.float32) * s, 'Db': jnp.zeros((DIM,), jnp.float32), 'W_ih': jax.random.normal(ks[5], (3 * RNN, DIM), jnp.float32) * s, 'b_ih': jnp.zeros((3 * RNN,), jnp.float32), 'W_hh': jax.random.normal(ks[6], (3 * RNN, RNN), jnp.float32) * s, 'b_hh': jnp.zeros((3 * RNN,), jnp.float32), 'proj_w': jax.random.normal(ks[7], (DIM, RNN), jnp.float32) * s, 'proj_b': jnp.zeros((DIM,), jnp.float32), 'gate_w': jax.random.normal(ks[8], (2, DIM), jnp.float32) * s, 'gate_b': jnp.zeros((2,), jnp.float32)}
    _L2_attn_in = _L2_attn_setup()

    def _L2_ffn_setup():
        import jax, jax.numpy as jnp
        import numpy as np
        K = 2
        key = jax.random.key(seed)
        ks = jax.random.split(key, 9)
        B, S, D, O, E = (4, 128, 128, 128, 8)
        sc = 0.02
        return {'x': jax.random.normal(ks[0], (B, S, D), dtype=jnp.float32), 'gate_w': jax.random.normal(ks[1], (D, E), dtype=jnp.float32) * sc, 'gate_b': jax.random.normal(ks[2], (E,), dtype=jnp.float32) * sc, 'w1': jax.random.normal(ks[3], (E, D, O), dtype=jnp.float32) * sc, 'b1': jax.random.normal(ks[4], (E, O), dtype=jnp.float32) * sc, 'w2': jax.random.normal(ks[5], (E, O, O), dtype=jnp.float32) * sc, 'b2': jax.random.normal(ks[6], (E, O), dtype=jnp.float32) * sc, 'w3': jax.random.normal(ks[7], (E, O, O), dtype=jnp.float32) * sc, 'b3': jax.random.normal(ks[8], (E, O), dtype=jnp.float32) * sc}
    _L2_ffn_in = _L2_ffn_setup()

    def _L3_attn_setup():
        import jax, jax.numpy as jnp
        import numpy as np
        EMBED_DIM = 128
        HEADS = 16
        HEAD_DIM = EMBED_DIM // HEADS
        key = jax.random.key(seed)
        ks = jax.random.split(key, 9)
        D = EMBED_DIM
        s = 1.0 / np.sqrt(D)
        x = jax.random.normal(ks[0], (4, 256, D), dtype=jnp.float32)
        Wq = jax.random.uniform(ks[1], (D, D), jnp.float32, -s, s)
        bq = jnp.zeros((D,), jnp.float32)
        Wk = jax.random.uniform(ks[2], (D, D), jnp.float32, -s, s)
        bk = jnp.zeros((D,), jnp.float32)
        Wv = jax.random.uniform(ks[3], (D, D), jnp.float32, -s, s)
        bv = jnp.zeros((D,), jnp.float32)
        Wo = jax.random.uniform(ks[4], (D, D), jnp.float32, -s, s)
        bo = jnp.zeros((D,), jnp.float32)
        gamma = jnp.ones((D,), jnp.float32)
        beta = jnp.zeros((D,), jnp.float32)
        return {'x': x, 'Wq': Wq, 'bq': bq, 'Wk': Wk, 'bk': bk, 'Wv': Wv, 'bv': bv, 'Wo': Wo, 'bo': bo, 'gamma': gamma, 'beta': beta}
    _L3_attn_in = _L3_attn_setup()

    def _L3_ffn_setup():
        import jax, jax.numpy as jnp
        import numpy as np
        key = jax.random.key(seed)
        ks = jax.random.split(key, 5)
        B, S, D_in, D_out, E, R = (4, 128, 128, 128, 8, 16)
        x = jax.random.normal(ks[0], (B, S, D_in), dtype=jnp.float32)
        weight = jax.random.normal(ks[1], (D_out, D_in), dtype=jnp.float32) / np.sqrt(D_in)
        gate_w = jax.random.normal(ks[2], (E, D_in), dtype=jnp.float32) / np.sqrt(D_in)
        lora_U = jax.random.normal(ks[3], (E, R, D_in), dtype=jnp.float32) / np.sqrt(D_in)
        lora_V = jax.random.normal(ks[4], (E, D_out, R), dtype=jnp.float32) / np.sqrt(R)
        return {'x': x, 'weight': weight, 'gate_w': gate_w, 'lora_U': lora_U, 'lora_V': lora_V}
    _L3_ffn_in = _L3_ffn_setup()
    _d = {'L0_attn_x': _L0_attn_in['x'], 'L0_attn_Wq': _L0_attn_in['Wq'], 'L0_attn_bq': _L0_attn_in['bq'], 'L0_attn_Wk': _L0_attn_in['Wk'], 'L0_attn_bk': _L0_attn_in['bk'], 'L0_attn_Wv': _L0_attn_in['Wv'], 'L0_attn_bv': _L0_attn_in['bv'], 'L0_attn_Wo': _L0_attn_in['Wo'], 'L0_attn_bo': _L0_attn_in['bo'], 'L0_attn_omega': _L0_attn_in['omega'], 'L0_attn_g1': _L0_attn_in['g1'], 'L0_attn_be1': _L0_attn_in['be1'], 'L0_attn_W1': _L0_attn_in['W1'], 'L0_attn_bf1': _L0_attn_in['bf1'], 'L0_attn_W2': _L0_attn_in['W2'], 'L0_attn_bf2': _L0_attn_in['bf2'], 'L0_attn_g2': _L0_attn_in['g2'], 'L0_attn_be2': _L0_attn_in['be2'], 'L0_ffn_wqkv': _L0_ffn_in['wqkv'], 'L0_ffn_q_scale': _L0_ffn_in['q_scale'], 'L0_ffn_k_scale': _L0_ffn_in['k_scale'], 'L0_ffn_wo': _L0_ffn_in['wo'], 'L0_ffn_ln_g': _L0_ffn_in['ln_g'], 'L0_ffn_ln_b': _L0_ffn_in['ln_b'], 'L0_ffn_w1': _L0_ffn_in['w1'], 'L0_ffn_b1': _L0_ffn_in['b1'], 'L0_ffn_w2': _L0_ffn_in['w2'], 'L0_ffn_b2': _L0_ffn_in['b2'], 'L1_attn_attn_norm_w': _L1_attn_in['attn_norm_w'], 'L1_attn_Wq': _L1_attn_in['Wq'], 'L1_attn_Wk': _L1_attn_in['Wk'], 'L1_attn_Wv': _L1_attn_in['Wv'], 'L1_attn_Wo': _L1_attn_in['Wo'], 'L1_attn_attn_out_norm_w': _L1_attn_in['attn_out_norm_w'], 'L1_attn_mlp_norm_w': _L1_attn_in['mlp_norm_w'], 'L1_attn_Wgate': _L1_attn_in['Wgate'], 'L1_attn_Wup': _L1_attn_in['Wup'], 'L1_attn_Wdown': _L1_attn_in['Wdown'], 'L1_ffn_phi_w': _L1_ffn_in['phi_w'], 'L1_ffn_phi_b': _L1_ffn_in['phi_b'], 'L1_ffn_expert_w': _L1_ffn_in['expert_w'], 'L1_ffn_expert_b': _L1_ffn_in['expert_b'], 'L2_attn_A': _L2_attn_in['A'], 'L2_attn_Bw': _L2_attn_in['Bw'], 'L2_attn_Bb': _L2_attn_in['Bb'], 'L2_attn_Cw': _L2_attn_in['Cw'], 'L2_attn_Cb': _L2_attn_in['Cb'], 'L2_attn_Dw': _L2_attn_in['Dw'], 'L2_attn_Db': _L2_attn_in['Db'], 'L2_attn_W_ih': _L2_attn_in['W_ih'], 'L2_attn_b_ih': _L2_attn_in['b_ih'], 'L2_attn_W_hh': _L2_attn_in['W_hh'], 'L2_attn_b_hh': _L2_attn_in['b_hh'], 'L2_attn_proj_w': _L2_attn_in['proj_w'], 'L2_attn_proj_b': _L2_attn_in['proj_b'], 'L2_attn_gate_w': _L2_attn_in['gate_w'], 'L2_attn_gate_b': _L2_attn_in['gate_b'], 'L2_ffn_gate_w': _L2_ffn_in['gate_w'], 'L2_ffn_gate_b': _L2_ffn_in['gate_b'], 'L2_ffn_w1': _L2_ffn_in['w1'], 'L2_ffn_b1': _L2_ffn_in['b1'], 'L2_ffn_w2': _L2_ffn_in['w2'], 'L2_ffn_b2': _L2_ffn_in['b2'], 'L2_ffn_w3': _L2_ffn_in['w3'], 'L2_ffn_b3': _L2_ffn_in['b3'], 'L3_attn_Wq': _L3_attn_in['Wq'], 'L3_attn_bq': _L3_attn_in['bq'], 'L3_attn_Wk': _L3_attn_in['Wk'], 'L3_attn_bk': _L3_attn_in['bk'], 'L3_attn_Wv': _L3_attn_in['Wv'], 'L3_attn_bv': _L3_attn_in['bv'], 'L3_attn_Wo': _L3_attn_in['Wo'], 'L3_attn_bo': _L3_attn_in['bo'], 'L3_attn_gamma': _L3_attn_in['gamma'], 'L3_attn_beta': _L3_attn_in['beta'], 'L3_ffn_weight': _L3_ffn_in['weight'], 'L3_ffn_gate_w': _L3_ffn_in['gate_w'], 'L3_ffn_lora_U': _L3_ffn_in['lora_U'], 'L3_ffn_lora_V': _L3_ffn_in['lora_V']}
    _x0 = _d['L0_attn_x']
    _d['L0_attn_x'] = jax.random.normal(jax.random.fold_in(jax.random.key(seed), 1), (4, 512, 128), dtype=_x0.dtype)
    del _x0
    return _d

def reference(L0_attn_x, L0_attn_Wq, L0_attn_bq, L0_attn_Wk, L0_attn_bk, L0_attn_Wv, L0_attn_bv, L0_attn_Wo, L0_attn_bo, L0_attn_omega, L0_attn_g1, L0_attn_be1, L0_attn_W1, L0_attn_bf1, L0_attn_W2, L0_attn_bf2, L0_attn_g2, L0_attn_be2, L0_ffn_wqkv, L0_ffn_q_scale, L0_ffn_k_scale, L0_ffn_wo, L0_ffn_ln_g, L0_ffn_ln_b, L0_ffn_w1, L0_ffn_b1, L0_ffn_w2, L0_ffn_b2, L1_attn_attn_norm_w, L1_attn_Wq, L1_attn_Wk, L1_attn_Wv, L1_attn_Wo, L1_attn_attn_out_norm_w, L1_attn_mlp_norm_w, L1_attn_Wgate, L1_attn_Wup, L1_attn_Wdown, L1_ffn_phi_w, L1_ffn_phi_b, L1_ffn_expert_w, L1_ffn_expert_b, L2_attn_A, L2_attn_Bw, L2_attn_Bb, L2_attn_Cw, L2_attn_Cb, L2_attn_Dw, L2_attn_Db, L2_attn_W_ih, L2_attn_b_ih, L2_attn_W_hh, L2_attn_b_hh, L2_attn_proj_w, L2_attn_proj_b, L2_attn_gate_w, L2_attn_gate_b, L2_ffn_gate_w, L2_ffn_gate_b, L2_ffn_w1, L2_ffn_b1, L2_ffn_w2, L2_ffn_b2, L2_ffn_w3, L2_ffn_b3, L3_attn_Wq, L3_attn_bq, L3_attn_Wk, L3_attn_bk, L3_attn_Wv, L3_attn_bv, L3_attn_Wo, L3_attn_bo, L3_attn_gamma, L3_attn_beta, L3_ffn_weight, L3_ffn_gate_w, L3_ffn_lora_U, L3_ffn_lora_V):

    def _L0_attn_ref(x, Wq, bq, Wk, bk, Wv, bv, Wo, bo, omega, g1, be1, W1, bf1, W2, bf2, g2, be2):
        import jax, jax.numpy as jnp
        import numpy as np
        N_LAYER, N_HEAD, D_MODEL, D_FF = (6, 16, 128, 512)
        D_HEAD = D_MODEL // N_HEAD
        M_FEAT = 2 * D_MODEL // N_HEAD
        CHUNK = 128
        LN_EPS = 1e-05
        ATT_EPS = 1e-06
        B, S = (4, 256)

        def _layer_norm(x, g, b):
            mu = x.mean(-1, keepdims=True)
            var = ((x - mu) ** 2).mean(-1, keepdims=True)
            return (x - mu) * jax.lax.rsqrt(var + LN_EPS) * g + b

        def _favor_phi(x, omega):
            x = x * D_HEAD ** (-0.25)
            u = jnp.einsum('bhsd,dm->bhsm', x, omega)
            nrm = 0.5 * jnp.sum(x * x, axis=-1, keepdims=True)
            phi = jnp.concatenate([jnp.exp(u - nrm), jnp.exp(-u - nrm)], axis=-1)
            return phi * M_FEAT ** (-0.5)

        def _causal_linear_attention(Qp, Kp, V):
            b, h, s, m = Qp.shape
            d = V.shape[-1]
            c = s // CHUNK
            Qc = Qp.reshape(b, h, c, CHUNK, m)
            Kc = Kp.reshape(b, h, c, CHUNK, m)
            Vc = V.reshape(b, h, c, CHUNK, d)
            kv = jnp.einsum('bhclm,bhcld->bhcmd', Kc, Vc)
            ksum = Kc.sum(axis=3)
            kv_pre = jnp.cumsum(kv, axis=2) - kv
            ks_pre = jnp.cumsum(ksum, axis=2) - ksum
            scores = jnp.einsum('bhcim,bhcjm->bhcij', Qc, Kc)
            mask = jnp.tril(jnp.ones((CHUNK, CHUNK), bool))
            scores = jnp.where(mask, scores, 0.0)
            num = jnp.einsum('bhcij,bhcjd->bhcid', scores, Vc) + jnp.einsum('bhcim,bhcmd->bhcid', Qc, kv_pre)
            den = scores.sum(-1) + jnp.einsum('bhcim,bhcm->bhci', Qc, ks_pre)
            out = num / (den[..., None] + ATT_EPS)
            return out.reshape(b, h, s, d)

        def _forward(x, Wq, bq, Wk, bk, Wv, bv, Wo, bo, omega, g1, be1, W1, bf1, W2, bf2, g2, be2):
            bsz, slen, _ = x.shape
            out = x
            for l in range(N_LAYER):

                def proj(W, bvec):
                    y = jnp.einsum('bsd,de->bse', out, W) + bvec
                    return y.reshape(bsz, slen, N_HEAD, D_HEAD).transpose(0, 2, 1, 3)
                q = proj(Wq[l], bq[l])
                k = proj(Wk[l], bk[l])
                v = proj(Wv[l], bv[l])
                Qp = _favor_phi(q, omega[l])
                Kp = _favor_phi(k, omega[l])
                a = _causal_linear_attention(Qp, Kp, v)
                a = a.transpose(0, 2, 1, 3).reshape(bsz, slen, D_MODEL)
                a = jnp.einsum('bsd,de->bse', a, Wo[l]) + bo[l]
                h1 = _layer_norm(out + a, g1[l], be1[l])
                y = jax.nn.relu(jnp.einsum('bsd,df->bsf', h1, W1[l]) + bf1[l])
                y = jnp.einsum('bsf,fd->bsd', y, W2[l]) + bf2[l]
                out = _layer_norm(h1 + y, g2[l], be2[l])
            return out
        return _forward(x, Wq, bq, Wk, bk, Wv, bv, Wo, bo, omega, g1, be1, W1, bf1, W2, bf2, g2, be2)

    def _L0_ffn_ref(x, wqkv, q_scale, k_scale, wo, ln_g, ln_b, w1, b1, w2, b2):
        import jax, jax.numpy as jnp
        import numpy as np
        DIM = 128
        DEPTH = 2
        HEADS = 8
        DIM_HEAD = 64
        WINDOW = 64
        INNER = HEADS * DIM_HEAD
        HID = int(DIM * 4 * 2 / 3)
        B, N = (2, 1024)
        QK_SCALE = 8.0

        def shift_token(t):
            t1, t2 = jnp.split(t, 2, axis=-1)
            t2 = jnp.pad(t2, ((0, 0), (1, 0), (0, 0)))[:, :-1]
            return jnp.concatenate([t1, t2], axis=-1)

        def l2norm(t):
            return t / jnp.clip(jnp.linalg.norm(t, axis=-1, keepdims=True), 1e-12)

        def rotate_half(x):
            x1, x2 = jnp.split(x, 2, axis=-1)
            return jnp.concatenate([-x2, x1], axis=-1)

        def rotary_xpos(q, k):
            n = q.shape[-2]
            half_idx = jnp.arange(0, DIM_HEAD, 2, dtype=jnp.float32)
            inv_freq = 1.0 / 10000.0 ** (half_idx / DIM_HEAD)
            t = jnp.arange(n, dtype=jnp.float32)
            freqs = t[:, None] * inv_freq[None, :]
            freqs = jnp.concatenate([freqs, freqs], axis=-1)
            base = (half_idx + 0.4 * DIM_HEAD) / (1.4 * DIM_HEAD)
            power = (t - n // 2) / float(WINDOW // 2)
            scale = base[None, :] ** power[:, None]
            scale = jnp.concatenate([scale, scale], axis=-1)
            cos, sin = (jnp.cos(freqs), jnp.sin(freqs))
            q = q * cos * scale + rotate_half(q) * sin * scale
            k = k * cos / scale + rotate_half(k) * sin / scale
            return (q, k)

        def local_attention(q, k, v):
            b, h, n, d = q.shape
            w = n // WINDOW
            bq = q.reshape(b, h, w, WINDOW, d) * QK_SCALE
            bk = k.reshape(b, h, w, WINDOW, d)
            bv = v.reshape(b, h, w, WINDOW, d)

            def look_around(t):
                p = jnp.pad(t, ((0, 0), (0, 0), (1, 0), (0, 0), (0, 0)))
                return jnp.concatenate([p[:, :, :w], p[:, :, 1:]], axis=3)
            bk, bv = (look_around(bk), look_around(bv))
            bt = jnp.arange(n).reshape(w, WINDOW)
            btp = jnp.pad(bt, ((1, 0), (0, 0)), constant_values=-1)
            btk = jnp.concatenate([btp[:w], btp[1:]], axis=1)
            sim = jnp.einsum('bhwid,bhwjd->bhwij', bq, bk)
            i = bt[:, :, None]
            j = btk[:, None, :]
            mask = (i < j) | (i > j + WINDOW) | (j == -1)
            sim = jnp.where(mask, -jnp.finfo(sim.dtype).max, sim)
            attn = jax.nn.softmax(sim, axis=-1)
            out = jnp.einsum('bhwij,bhwjd->bhwid', attn, bv)
            return out.reshape(b, h, n, d)

        def _layer(x, wqkv, qs, ksc, wo, lg, lb, w1, b1, w2, b2):
            b, n, _ = x.shape
            h = shift_token(x)
            qkv = h @ wqkv
            q, k, v = jnp.split(qkv, 3, axis=-1)
            to_heads = lambda t: t.reshape(b, n, HEADS, DIM_HEAD).transpose(0, 2, 1, 3)
            q, k, v = (to_heads(q), to_heads(k), to_heads(v))
            q = l2norm(q) * qs
            k = l2norm(k) * ksc
            q, k = rotary_xpos(q, k)
            o = local_attention(q, k, v)
            o = o.transpose(0, 2, 1, 3).reshape(b, n, INNER)
            x = x + o @ wo
            h = shift_token(x)
            mu = h.mean(-1, keepdims=True)
            var = h.var(-1, keepdims=True)
            h = (h - mu) / jnp.sqrt(var + 1e-05) * lg + lb
            h = h @ w1 + b1
            a, g = jnp.split(h, 2, axis=-1)
            h = a * jax.nn.gelu(g, approximate=False)
            x = x + h @ w2 + b2
            return x
        for l in range(DEPTH):
            x = _layer(x, wqkv[l], q_scale[l], k_scale[l], wo[l], ln_g[l], ln_b[l], w1[l], b1[l], w2[l], b2[l])
        return x

    def _L1_attn_ref(hidden_states, attn_norm_w, Wq, Wk, Wv, Wo, attn_out_norm_w, mlp_norm_w, Wgate, Wup, Wdown):
        import jax, jax.numpy as jnp
        import numpy as np
        B, T, D = (2, 512, 128)
        H, DK, DV = (8, 128, 128)
        INTER = 512
        CHUNK = 128
        EPS = 1e-05

        def rmsnorm(x, w, eps=EPS):
            return x * jax.lax.rsqrt(jnp.mean(x * x, axis=-1, keepdims=True) + eps) * w

        def linear_attention(x, Wq, Wk, Wv, Wo, out_norm_w):
            b, t, d = x.shape
            n = t // CHUNK
            q = (x @ Wq).reshape(b, t, H, DK).transpose(0, 2, 1, 3)
            k = (x @ Wk).reshape(b, t, H, DK).transpose(0, 2, 1, 3)
            v = (x @ Wv).reshape(b, t, H, DV).transpose(0, 2, 1, 3)
            qc = q.reshape(b, H, n, CHUNK, DK).transpose(2, 0, 1, 3, 4)
            kc = k.reshape(b, H, n, CHUNK, DK).transpose(2, 0, 1, 3, 4)
            vc = v.reshape(b, H, n, CHUNK, DV).transpose(2, 0, 1, 3, 4)
            causal = jnp.tril(jnp.ones((CHUNK, CHUNK), dtype=bool))

            def step(S, qkv):
                qb, kb, vb = qkv
                attn = jnp.einsum('bhid,bhjd->bhij', qb, kb)
                attn = jnp.where(causal, attn, 0.0)
                o = jnp.einsum('bhij,bhjv->bhiv', attn, vb) + jnp.einsum('bhid,bhdv->bhiv', qb, S)
                S = S + jnp.einsum('bhid,bhiv->bhdv', kb, vb)
                return (S, o)
            S0 = jnp.zeros((b, H, DK, DV), x.dtype)
            _, o = jax.lax.scan(step, S0, (qc, kc, vc))
            o = o.transpose(1, 2, 0, 3, 4).reshape(b, H, t, DV)
            o = rmsnorm(o, out_norm_w)
            o = o.transpose(0, 2, 1, 3).reshape(b, t, H * DV)
            return o @ Wo
        x = hidden_states
        h = rmsnorm(x, attn_norm_w)
        x = x + linear_attention(h, Wq, Wk, Wv, Wo, attn_out_norm_w)
        h = rmsnorm(x, mlp_norm_w)
        x = x + jax.nn.silu(h @ Wgate) * (h @ Wup) @ Wdown
        return x

    def _L1_ffn_ref(x, phi_w, phi_b, expert_w, expert_b):
        import jax, jax.numpy as jnp
        import numpy as np
        T, Z, D_DIM = (8, 256, 128)
        N_EXP, P_SLOT, H = (64, 32, 128)
        LN_EPS = 1e-05
        t, z, d = x.shape
        n = expert_w.shape[0]
        p = phi_w.shape[0] // n
        logits = (jnp.einsum('tzd,ed->tze', x, phi_w) + phi_b).reshape(t, z, n, p)
        D = jax.nn.softmax(logits, axis=3)
        C = jax.nn.softmax(logits, axis=2)
        X_tilde = jnp.einsum('tznp,tzd->npd', D, x)
        X_tilde = jnp.clip(X_tilde, -33000.0, 65000.0)
        mu = jnp.mean(X_tilde, axis=-1, keepdims=True)
        var = jnp.mean(jnp.square(X_tilde - mu), axis=-1, keepdims=True)
        X_tilde = (X_tilde - mu) * jax.lax.rsqrt(var + LN_EPS)
        X_tilde = jnp.tanh(X_tilde)
        Y_tilde = jnp.einsum('npd,ndH->npH', X_tilde, expert_w) + expert_b[:, None, :]
        Y = jnp.einsum('tznp,npH->tzH', C, Y_tilde)
        return Y

    def _L2_attn_ref(x, A, Bw, Bb, Cw, Cb, Dw, Db, W_ih, b_ih, W_hh, b_hh, proj_w, proj_b, gate_w, gate_b):
        import jax, jax.numpy as jnp
        import numpy as np
        DIM, SSM, RNN = (128, 64, 128)
        B, N, D = x.shape
        R = W_hh.shape[1]
        bx = jnp.einsum('bnd,sd->bns', x, Bw) + Bb
        dx = jnp.einsum('bnd,ed->bne', x, Dw) + Db
        gx = jax.nn.sigmoid(jnp.einsum('bnd,gd->bng', x, gate_w) + gate_b)
        ih = jnp.einsum('bnd,rd->bnr', x, W_ih) + b_ih
        bx_t = jnp.swapaxes(bx, 0, 1)
        dx_t = jnp.swapaxes(dx, 0, 1)
        gx_t = jnp.swapaxes(gx, 0, 1)
        ih_t = jnp.swapaxes(ih, 0, 1)
        h_ssm0 = jnp.zeros((B, A.shape[0]), x.dtype)
        h_rnn0 = jnp.zeros((B, R), x.dtype)

        def step(carry, inp):
            h_ssm, h_rnn = carry
            bxt, dxt, gxt, iht = inp
            h_ssm = jax.nn.silu(h_ssm @ A.T + bxt)
            y_ssm = h_ssm @ Cw.T + Cb + dxt
            hh = h_rnn @ W_hh.T + b_hh
            i_r, i_z, i_n = jnp.split(iht, 3, axis=-1)
            h_r, h_z, h_n = jnp.split(hh, 3, axis=-1)
            r = jax.nn.sigmoid(i_r + h_r)
            z = jax.nn.sigmoid(i_z + h_z)
            n = jnp.tanh(i_n + r * h_n)
            h_rnn = (1.0 - z) * n + z * h_rnn
            y_rnn = h_rnn @ proj_w.T + proj_b
            fused = gxt[:, :1] * y_ssm + gxt[:, 1:2] * y_rnn
            return ((h_ssm, h_rnn), fused)
        _, out = jax.lax.scan(step, (h_ssm0, h_rnn0), (bx_t, dx_t, gx_t, ih_t))
        return jnp.swapaxes(out, 0, 1)

    def _L2_ffn_ref(x, gate_w, gate_b, w1, b1, w2, b2, w3, b3):
        import jax, jax.numpy as jnp
        import numpy as np
        K = 2
        E = gate_w.shape[-1]
        logits = jnp.einsum('bsd,de->bse', x, gate_w) + gate_b
        probs = jax.nn.softmax(logits, axis=1)
        vals, idx = jax.lax.top_k(probs, K)
        h = jax.nn.relu(jnp.einsum('bsd,edo->ebso', x, w1) + b1[:, None, None, :])
        h = jax.nn.relu(jnp.einsum('ebso,eop->ebsp', h, w2) + b2[:, None, None, :])
        y = jax.nn.relu(jnp.einsum('ebso,eop->ebsp', h, w3) + b3[:, None, None, :])
        onehot = jax.nn.one_hot(idx, E, dtype=x.dtype)
        w_tok = jnp.einsum('bske,bsk->bse', onehot, vals)
        ind = onehot.max(axis=2)
        v = jnp.einsum('ebso,bse->eo', y, w_tok)
        out = jnp.einsum('bse,eo->bso', ind, v)
        return out

    def _L3_attn_ref(x, Wq, bq, Wk, bk, Wv, bv, Wo, bo, gamma, beta):
        import jax, jax.numpy as jnp
        import numpy as np
        EMBED_DIM = 128
        HEADS = 16
        HEAD_DIM = EMBED_DIM // HEADS
        B, S, D = x.shape
        H, Dh = (HEADS, HEAD_DIM)
        q = (x @ Wq + bq).reshape(B, S, H, Dh).transpose(0, 2, 1, 3)
        k = (x @ Wk + bk).reshape(B, S, H, Dh).transpose(0, 2, 1, 3)
        v = (x @ Wv + bv).reshape(B, S, H, Dh).transpose(0, 2, 1, 3)
        scores = jnp.einsum('bhqd,bhkd->bhqk', q, k) / jnp.sqrt(jnp.float32(Dh))
        attn = jax.nn.softmax(scores, axis=-1)
        ctx = jnp.einsum('bhqk,bhkd->bhqd', attn, v)
        ctx = ctx.transpose(0, 2, 1, 3).reshape(B, S, D)
        out = ctx @ Wo + bo
        h = out + x
        mu = jnp.mean(h, axis=-1, keepdims=True)
        var = jnp.mean(jnp.square(h - mu), axis=-1, keepdims=True)
        return (h - mu) * jax.lax.rsqrt(var + 1e-05) * gamma + beta

    def _L3_ffn_ref(x, weight, gate_w, lora_U, lora_V):
        import jax, jax.numpy as jnp
        import numpy as np
        scaling = 1.0 / lora_U.shape[1]
        B, S, D_in = x.shape
        xt = x.reshape(-1, D_in)
        gate = jax.nn.softmax(xt @ gate_w.T, axis=-1)
        base = xt @ weight.T
        t = jnp.einsum('nh,erh->ner', xt, lora_U)
        lora = jnp.einsum('ne,eor,ner->no', gate, lora_V, t)
        out = base + scaling * lora
        return out.reshape(B, S, -1)
    x = L0_attn_x
    xn = _layernorm(x, axis=-1)
    s = _L0_attn_ref(xn, L0_attn_Wq, L0_attn_bq, L0_attn_Wk, L0_attn_bk, L0_attn_Wv, L0_attn_bv, L0_attn_Wo, L0_attn_bo, L0_attn_omega, L0_attn_g1, L0_attn_be1, L0_attn_W1, L0_attn_bf1, L0_attn_W2, L0_attn_bf2, L0_attn_g2, L0_attn_be2)
    g = _silu(_L0_ffn_ref(xn, L0_ffn_wqkv, L0_ffn_q_scale, L0_ffn_k_scale, L0_ffn_wo, L0_ffn_ln_g, L0_ffn_ln_b, L0_ffn_w1, L0_ffn_b1, L0_ffn_w2, L0_ffn_b2))
    x = x + s * g
    xn = _layernorm(x, axis=-1)
    s = _L1_attn_ref(xn, L1_attn_attn_norm_w, L1_attn_Wq, L1_attn_Wk, L1_attn_Wv, L1_attn_Wo, L1_attn_attn_out_norm_w, L1_attn_mlp_norm_w, L1_attn_Wgate, L1_attn_Wup, L1_attn_Wdown)
    g = _silu(_L1_ffn_ref(xn, L1_ffn_phi_w, L1_ffn_phi_b, L1_ffn_expert_w, L1_ffn_expert_b))
    x = x + s * g
    xn = _layernorm(x, axis=-1)
    s = _L2_attn_ref(xn, L2_attn_A, L2_attn_Bw, L2_attn_Bb, L2_attn_Cw, L2_attn_Cb, L2_attn_Dw, L2_attn_Db, L2_attn_W_ih, L2_attn_b_ih, L2_attn_W_hh, L2_attn_b_hh, L2_attn_proj_w, L2_attn_proj_b, L2_attn_gate_w, L2_attn_gate_b)
    g = _silu(_L2_ffn_ref(xn, L2_ffn_gate_w, L2_ffn_gate_b, L2_ffn_w1, L2_ffn_b1, L2_ffn_w2, L2_ffn_b2, L2_ffn_w3, L2_ffn_b3))
    x = x + s * g
    xn = _layernorm(x, axis=-1)
    s = _L3_attn_ref(xn, L3_attn_Wq, L3_attn_bq, L3_attn_Wk, L3_attn_bk, L3_attn_Wv, L3_attn_bv, L3_attn_Wo, L3_attn_bo, L3_attn_gamma, L3_attn_beta)
    g = _silu(_L3_ffn_ref(xn, L3_ffn_weight, L3_ffn_gate_w, L3_ffn_lora_U, L3_ffn_lora_V))
    x = x + s * g
    return x

_drawn_inputs = setup_inputs


def setup_inputs(seed=0):
    import zlib

    import numpy as np

    out = dict(_drawn_inputs(seed))
    spreads = {'L0_attn_bq': (0.0, 0.397),
     'L0_attn_bk': (0.0, 0.532),
     'L0_attn_bv': (0.0, 0.1),
     'L0_attn_bo': (0.0, 0.1),
     'L0_attn_g1': (1.0, 0.2),
     'L0_attn_be1': (0.0, 0.1),
     'L0_attn_bf1': (0.0, 0.1),
     'L0_attn_bf2': (0.0, 0.1),
     'L0_attn_g2': (1.0, 0.2),
     'L0_attn_be2': (0.0, 0.1),
     'L0_ffn_q_scale': (1.0, 0.6),
     'L0_ffn_k_scale': (1.0, 0.6),
     'L0_ffn_ln_g': (1.0, 0.6),
     'L0_ffn_ln_b': (0.0, 0.8),
     'L0_ffn_b1': (0.0, 0.8),
     'L0_ffn_b2': (0.0, 0.1),
     'L1_attn_attn_norm_w': (1.0, 0.2),
     'L1_attn_attn_out_norm_w': (1.0, 0.536),
     'L1_attn_mlp_norm_w': (1.0, 0.6),
     'L2_attn_Bb': (0.0, 0.8),
     'L2_attn_Cb': (0.0, 0.8),
     'L2_attn_Db': (0.0, 0.8),
     'L2_attn_b_ih': (0.0, 0.8),
     'L2_attn_b_hh': (0.0, 0.8),
     'L2_attn_proj_b': (0.0, 0.8),
     'L2_attn_gate_b': (0.0, 0.8),
     'L3_attn_bq': (0.0, 2.0),
     'L3_attn_bk': (0.0, 2.0),
     'L3_attn_bv': (0.0, 2.0),
     'L3_attn_bo': (0.0, 0.8),
     'L3_attn_gamma': (1.0, 0.6),
     'L3_attn_beta': (0.0, 0.8)}
    factors = {'L0_ffn_wqkv': 3.006,
     'L0_ffn_wo': 3.015,
     'L0_ffn_w1': 5.37,
     'L0_ffn_w2': 5.252,
     'L1_attn_Wgate': 8.0,
     'L1_attn_Wup': 8.0,
     'L1_attn_Wdown': 8.0,
     'L1_ffn_phi_w': 4.399,
     'L1_ffn_phi_b': 8.0,
     'L2_attn_A': 8.0,
     'L2_attn_Bw': 8.0,
     'L2_attn_Cw': 8.0,
     'L2_attn_Dw': 8.0,
     'L2_attn_W_ih': 8.0,
     'L2_attn_W_hh': 8.0,
     'L2_attn_proj_w': 8.0,
     'L2_attn_gate_w': 8.0,
     'L2_ffn_gate_w': 8.0,
     'L2_ffn_gate_b': 200.0,
     'L2_ffn_w1': 8.0,
     'L2_ffn_b1': 8.0,
     'L2_ffn_w2': 8.0,
     'L2_ffn_b2': 8.0,
     'L2_ffn_w3': 8.0,
     'L2_ffn_b3': 8.0,
     'L3_attn_Wq': 71.504,
     'L3_attn_Wk': 69.465,
     'L3_ffn_gate_w': 7.069,
     'L3_ffn_lora_U': 4.948,
     'L3_ffn_lora_V': 4.818,
     'L3_attn_Wv': 2.716}
    for name, (base, spread) in spreads.items():
        noise = np.random.default_rng([zlib.crc32(name.encode()), seed]).standard_normal(out[name].shape)
        drawn = base * np.exp(spread * noise) if base else spread * noise
        out[name] = jnp.asarray(drawn.astype(out[name].dtype))
    for name, factor in factors.items():
        out[name] = (out[name] * factor).astype(out[name].dtype)
    return out
```

```python
from contextlib import ExitStack

import concourse.bass as bass
from concourse import mybir

P = 128
B = 4
N = 512
T = B * N
CH = N // P

F32 = mybir.dt.float32
U32 = mybir.dt.uint32
ALU = mybir.AluOpType
ACT = mybir.ActivationFunctionType
AX = mybir.AxisListType
EXP_LN_SET = "natural_log_exp_and_others"
LN_EPS = 1e-5


class Fields:

    def __init__(self, *fields):
        self.at, self.width = {}, 0
        for name, width in fields:
            self.at[name] = (self.width, width)
            self.width += width

    def of(self, buf, name, part=0, width=None):
        start, whole = self.at[name]
        width = width or whole
        return buf[:, start + part * width:start + (part + 1) * width]


CONST = Fields(("ident", P), ("mean", P), ("causal", N), ("eps5", 1))
CONST_L0A = Fields(("kvmask", 16 * 9), ("causal4", N), ("sign", P), ("nhalf", P))
CONST_L0F = Fields(("ones64", P), ("swap64", P), ("window_first", 2 * P), ("window", 2 * P),
                   ("rope_qc", N), ("rope_qs", N), ("rope_kc", N), ("rope_ks", N), ("eps_l2", 1), ("l2_back", 1))
CONST_L2F = Fields(("sel8", 8 * P), ("index8", 8))


class Signal:

    def __init__(self, sem, per_round=1):
        self.sem = sem
        self.per_round = per_round

    def at(self, r, k=0):
        return r * self.per_round + k + 1


def apart(eng, passed):
    eng.sem_inc(passed.sem, 1)


class Core:

    def __init__(self, nc, ctx, dram):
        self.nc, self.dram = nc, dram
        sb = lambda name, cols: ctx.enter_context(nc.sbuf_tensor(name, [P, cols], F32))
        self.x = sb("x_res", T)
        self.xn = sb("x_norm", T)
        self.s = sb("s_branch", T)
        self.g = sb("g_branch", T)
        self.const = sb("const", CONST.width)
        self.psum = ctx.enter_context(nc.psum_tensor("psum", [P, 8, N], F32))

    def c(self, name):
        return CONST.of(self.const, name)


class Phase:

    def __init__(self, core, name):
        self.core, self.nc, self.name = core, core.nc, name

    def __enter__(self):
        self.ctx = ExitStack()
        self.sems = []
        return self

    def buf(self, name, *shape, dtype=F32):
        return self.ctx.enter_context(self.nc.sbuf_tensor(f"{self.name}_{name}", [P, *shape], dtype))

    def semaphore(self, name, per_round=1):
        sem = self.ctx.enter_context(self.nc.semaphore(f"{self.name}_{name}"))
        self.sems.append(sem)
        return Signal(sem, per_round)

    def __exit__(self, *failure):
        if failure[0] is None:
            with self.nc.Block() as block:
                @block.sync
                def _(sp):
                    for sem in self.sems:
                        sp.sem_clear(sem)
        self.ctx.close()


def cols(r, width=N):
    return bass.ds(r * width, width)


class ColumnNorm:

    def __init__(self, ph, name, mean_bank, var_bank, centre=True, per_round=1, eps="eps5"):
        self.core, self.centre, self.eps = ph.core, centre, eps
        self.mean_bank, self.var_bank = mean_bank, var_bank
        self.centred = ph.buf(name + "_centred", N)
        self.squared = ph.buf(name + "_squared", N)
        self.logvar = ph.buf(name + "_logvar", N)
        self.rstd = ph.buf(name + "_rstd", N)
        self.mean_ready = ph.semaphore(name + "_mean_ready", per_round)
        self.centred_ready = ph.semaphore(name + "_centred_ready", per_round)
        self.squared_ready = ph.semaphore(name + "_squared_ready", per_round)
        self.var_ready = ph.semaphore(name + "_var_ready", per_round)
        self.logvar_ready = ph.semaphore(name + "_logvar_ready", per_round)
        self.rstd_ready = ph.semaphore(name + "_rstd_ready", per_round)

    def tensor(self, pe, r, x, k=0):
        mean = self.core.c("mean")
        if self.centre:
            pe.matmul(self.core.psum[:, self.mean_bank, :], mean, x, start=True, stop=True)\
              .then_inc(self.mean_ready.sem, 1)
        pe.wait_ge(self.squared_ready.sem, self.squared_ready.at(r, k))
        pe.matmul(self.core.psum[:, self.var_bank, :], mean, self.squared[:, :], start=True, stop=True)\
          .then_inc(self.var_ready.sem, 1)

    def vector(self, dve, r, x, k=0):
        dve.wait_ge(self.mean_ready.sem, self.mean_ready.at(r, k))
        dve.tensor_tensor(self.centred[:, :], x, self.core.psum[:, self.mean_bank, :], ALU.subtract)\
           .then_inc(self.centred_ready.sem, 1)

    def scalar(self, act, r, x=None, k=0):
        if self.centre:
            act.wait_ge(self.centred_ready.sem, self.centred_ready.at(r, k))
            x = self.centred[:, :]
        act.activation(self.squared[:, :], x, ACT.Square).then_inc(self.squared_ready.sem, 1)
        act.wait_ge(self.var_ready.sem, self.var_ready.at(r, k))
        act.activation(self.logvar[:, :], self.core.psum[:, self.var_bank, :], ACT.Ln,
                       bias=self.core.c(self.eps)).then_inc(self.logvar_ready.sem, 1)
        act.wait_ge(self.logvar_ready.sem, self.logvar_ready.at(r, k))
        act.activation(self.rstd[:, :], self.logvar[:, :], ACT.Exp, scale=-0.5)\
           .then_inc(self.rstd_ready.sem, 1)


LAYOUTS = []


def pack(np, pieces):
    out = np.zeros((P, sum(a.shape[1] for a in pieces)), np.float32)
    at = 0
    for a in pieces:
        out[:a.shape[0], at:at + a.shape[1]] = a
        at += a.shape[1]
    return out


def blocks(np, w, size=P):
    k, n = w.shape[0] // size, w.shape[1]
    return w.reshape(k, size, n).transpose(1, 0, 2).reshape(size, k * n)


def column(v):
    return v.reshape(-1, 1)




def load_phase(core):
    nc = core.nc
    with Phase(core, "load") as ph:
        rows = ph.buf("rows", T // P, P)
        const_in = ph.semaphore("const_in")
        rows_in = ph.semaphore("rows_in")
        turned = ph.semaphore("turned")
        x_ready = ph.semaphore("x_ready")
        with nc.Block() as block:
            @block.sync
            def _(sp):
                sp.dma_start(core.const[:, :], core.dram["const"]).then_inc(const_in.sem, 16)
                sp.dma_start(rows[:, :, :], core.dram["x"].rearrange("b (c p) d -> p (b c) d", p=P))\
                  .then_inc(rows_in.sem, 16)

            @block.tensor
            def _(pe):
                pe.wait_ge(const_in.sem, 16)
                pe.wait_ge(rows_in.sem, 16)
                for b in range(B):
                    for c in range(CH):
                        turn = pe.transpose(core.psum[:, b, c * P:(c + 1) * P], rows[:, b * CH + c, :],
                                            core.c("ident"))
                    turn.then_inc(turned.sem, 1)

            @block.vector
            def _(dve):
                for b in range(B):
                    dve.wait_ge(turned.sem, b + 1)
                    dve.tensor_copy(core.x[:, b * N:(b + 1) * N], core.psum[:, b, :]).then_inc(x_ready.sem, 1)


def mix_phase(core, name, mix=True, norm=True):
    nc = core.nc
    with Phase(core, name) as ph:
        gate = ph.buf("gate", T)
        gated = ph.buf("gated", T)
        centred = ph.buf("centred", T)
        squared = ph.buf("squared", T)
        logvar = ph.buf("logvar", T)
        rstd = ph.buf("rstd", T)
        gate_ready = ph.semaphore("gate_ready")
        gated_ready = ph.semaphore("gated_ready")
        x_ready = ph.semaphore("x_ready")
        mean_ready = ph.semaphore("mean_ready")
        centred_ready = ph.semaphore("centred_ready")
        squared_ready = ph.semaphore("squared_ready")
        var_ready = ph.semaphore("var_ready")
        logvar_ready = ph.semaphore("logvar_ready")
        rstd_ready = ph.semaphore("rstd_ready")
        xn_ready = ph.semaphore("xn_ready")
        batch = [slice(b * N, (b + 1) * N) for b in range(B)]
        mean_bank = [core.psum[:, b, :] for b in range(B)]
        var_bank = [core.psum[:, B + b, :] for b in range(B)]
        with nc.Block() as block:
            @block.tensor
            def _(pe):
                if not norm:
                    return
                for b in range(B):
                    if mix:
                        pe.wait_ge(x_ready.sem, x_ready.at(b))
                    pe.matmul(mean_bank[b], core.c("mean"), core.x[:, batch[b]], start=True, stop=True)\
                      .then_inc(mean_ready.sem, 1)
                for b in range(B):
                    pe.wait_ge(squared_ready.sem, squared_ready.at(b))
                    pe.matmul(var_bank[b], core.c("mean"), squared[:, batch[b]], start=True, stop=True)\
                      .then_inc(var_ready.sem, 1)

            @block.vector
            def _(dve):
                if mix:
                    for b in range(B):
                        dve.wait_ge(gate_ready.sem, gate_ready.at(b))
                        dve.tensor_tensor(gated[:, batch[b]], core.s[:, batch[b]], gate[:, batch[b]], ALU.mult)\
                           .then_inc(gated_ready.sem, 1)
                        dve.wait_ge(gated_ready.sem, gated_ready.at(b))
                        dve.tensor_tensor(core.x[:, batch[b]], core.x[:, batch[b]], gated[:, batch[b]], ALU.add)\
                           .then_inc(x_ready.sem, 1)
                if norm:
                    for b in range(B):
                        dve.wait_ge(mean_ready.sem, mean_ready.at(b))
                        dve.tensor_tensor(centred[:, batch[b]], core.x[:, batch[b]], mean_bank[b], ALU.subtract)\
                           .then_inc(centred_ready.sem, 1)
                    for b in range(B):
                        dve.wait_ge(rstd_ready.sem, rstd_ready.at(b))
                        dve.tensor_tensor(core.xn[:, batch[b]], centred[:, batch[b]], rstd[:, batch[b]], ALU.mult)\
                           .then_inc(xn_ready.sem, 1)

            @block.scalar
            def _(act):
                if mix:
                    for b in range(B):
                        act.activation(gate[:, batch[b]], core.g[:, batch[b]], ACT.Silu).then_inc(gate_ready.sem, 1)
                if norm:
                    act.preload_act_table_set(EXP_LN_SET)
                    for b in range(B):
                        act.wait_ge(centred_ready.sem, centred_ready.at(b))
                        act.activation(squared[:, batch[b]], centred[:, batch[b]], ACT.Square)\
                           .then_inc(squared_ready.sem, 1)
                    for b in range(B):
                        act.wait_ge(var_ready.sem, var_ready.at(b))
                        act.activation(logvar[:, batch[b]], var_bank[b], ACT.Ln, bias=core.c("eps5"))\
                           .then_inc(logvar_ready.sem, 1)
                        act.wait_ge(logvar_ready.sem, logvar_ready.at(b))
                        act.activation(rstd[:, batch[b]], logvar[:, batch[b]], ACT.Exp, scale=-0.5)\
                           .then_inc(rstd_ready.sem, 1)


def store_phase(core):
    nc = core.nc
    with Phase(core, "store") as ph:
        rows = ph.buf("rows", T // P, P)
        turned = ph.semaphore("turned")
        rows_ready = ph.semaphore("rows_ready")
        stored = ph.semaphore("stored")
        out = core.dram["out"].rearrange("b (c p) d -> p (b c) d", p=P)
        with nc.Block() as block:
            @block.tensor
            def _(pe):
                for b in range(B):
                    for c in range(CH):
                        t = b * CH + c
                        turn = pe.transpose(core.psum[:, b, c * P:(c + 1) * P], core.x[:, t * P:(t + 1) * P],
                                            core.c("ident"))
                    turn.then_inc(turned.sem, 1)

            @block.vector
            def _(dve):
                for b in range(B):
                    dve.wait_ge(turned.sem, turned.at(b))
                    dve.tensor_copy(rows[:, b * CH:(b + 1) * CH, :],
                                    core.psum[:, b, :].rearrange("p (c d) -> p c d", c=CH))\
                       .then_inc(rows_ready.sem, 1)

            @block.sync
            def _(sp):
                for b in range(B):
                    sp.wait_ge(rows_ready.sem, rows_ready.at(b))
                    sp.dma_start(out[:, b * CH:(b + 1) * CH, :], rows[:, b * CH:(b + 1) * CH, :])\
                      .then_inc(stored.sem, 16)
                sp.wait_ge(stored.sem, 16 * B)


L0_LAYERS, L0_HEADS, L0_FF = 6, 16, 512
L0_DH = P // L0_HEADS
L0A = Fields(("wq", 2 * P), ("wk", 2 * P), ("wv", P), ("wo", P), ("omega", P), ("bv", P),
             ("w1", L0_FF), ("w2", L0_FF), ("bq", 2), ("bk", 2), ("bo", 1), ("g1", 1), ("be1", 1),
             ("bf1", L0_FF // P), ("bf2", 1), ("g2", 1), ("be2", 1))


def l0_attn_layout(np, i):
    g = lambda k: i["L0_attn_" + k]
    order = [np.concatenate([np.arange(32 * x, 32 * x + 32) for x in (2 * t, 2 * t, 2 * t + 1, 2 * t + 1)])
             for t in range(2)]
    out = []
    for n in range(L0_LAYERS):
        omega = np.zeros((P, 4, 32), np.float32)
        for top in (0, 64):
            for h in range(4):
                rows = slice(top + 8 * h, top + 8 * h + 8)
                omega[rows, h, 0:8] = g("omega")[n]
                omega[rows, h, 8:16] = g("omega")[n]
        out.append(pack(np, [
            g("Wq")[n][:, order[0]], g("Wq")[n][:, order[1]], g("Wk")[n][:, order[0]], g("Wk")[n][:, order[1]],
            g("Wv")[n], g("Wo")[n], omega.reshape(P, P), np.tile(g("bv")[n], (P, 1)),
            g("W1")[n], blocks(np, g("W2")[n]),
            g("bq")[n][order[0]][:, None], g("bq")[n][order[1]][:, None],
            g("bk")[n][order[0]][:, None], g("bk")[n][order[1]][:, None],
            column(g("bo")[n]), column(g("g1")[n]), column(g("be1")[n]), g("bf1")[n].reshape(-1, P).T,
            column(g("bf2")[n]), column(g("g2")[n]), column(g("be2")[n])]))
    return {"l0a": np.stack(out)}


LAYOUTS.append(l0_attn_layout)


def l0_attn_phase(core):
    nc, psum = core.nc, core.psum
    F, G, DH, DV = L0_FF // P, L0_HEADS // 4, L0_DH, L0_DH + 1
    SCALE = float(DH) ** -0.25
    ATT_EPS = 16 * 1e-6
    with Phase(core, "l0a") as ph:
        w = ph.buf("w", L0A.width)
        col = lambda name, k=0: L0A.of(w, name, k, 1)
        h_in = ph.buf("h_in", N)
        qk = ph.buf("qk", 4, N)
        omega = ph.buf("omega", P)
        omega_signed = ph.buf("omega_signed", P)
        feat = ph.buf("feat", 8, N)
        v = ph.buf("v", CH, L0_HEADS, DV)
        k_tok = ph.buf("k_tok", CH - 1, G * P)
        kv = ph.buf("kv", CH - 1, L0_HEADS * DV)
        state = ph.buf("state", CH - 1, L0_HEADS * DV)
        scores = ph.buf("scores", 2, 4, N)
        den = ph.buf("den", CH, L0_HEADS)
        rden = ph.buf("rden", CH, L0_HEADS)
        att = ph.buf("att", CH, P)
        att_t = ph.buf("att_t", N)
        res1, res2 = ph.buf("res1", N), ph.buf("res2", N)
        scaled1, scaled2 = ph.buf("scaled1", N), ph.buf("scaled2", N)
        h1 = ph.buf("h1", N)
        y = ph.buf("y", F, N)

        table = ph.buf("table", CONST_L0A.width)
        const = lambda name: CONST_L0A.of(table, name)
        table_in = ph.semaphore("table_in")
        passed = ph.semaphore("passed")
        w_in = ph.semaphore("w_in")
        copied = ph.semaphore("copied", B)
        ones_ready = ph.semaphore("ones_ready")
        round_done = ph.semaphore("round_done")
        omega_signed_ready, omega_ready = ph.semaphore("omega_signed_ready"), ph.semaphore("omega_ready")
        h_ready = ph.semaphore("h_ready")
        proj_ready = ph.semaphore("proj_ready", 4)
        qk_ready, qk_sq_ready = ph.semaphore("qk_ready", 4), ph.semaphore("qk_sq_ready", 4)
        v_ready, v_kept = ph.semaphore("v_ready"), ph.semaphore("v_kept", CH)
        arg_ready, feat_ready = ph.semaphore("arg_ready", 8), ph.semaphore("feat_ready", 8)
        k_tok_ready, k_tok_kept = ph.semaphore("k_tok_ready", CH - 1), ph.semaphore("k_tok_kept", CH - 1)
        kv_ready, kv_kept = ph.semaphore("kv_ready", CH - 1), ph.semaphore("kv_kept", CH - 1)
        state_ready = ph.semaphore("state_ready", CH - 1)
        scores_ready, scores_kept = ph.semaphore("scores_ready", CH * G), ph.semaphore("scores_kept", CH * G)
        num_ready = ph.semaphore("num_ready", CH)
        den_ready, rden_ready = ph.semaphore("den_ready", CH), ph.semaphore("rden_ready", CH)
        att_ready = ph.semaphore("att_ready", CH)
        att_t_ready, att_t_kept = ph.semaphore("att_t_ready"), ph.semaphore("att_t_kept")
        out_ready, res_ready = ph.semaphore("out_ready", 2), ph.semaphore("res_ready", 2)
        norm = ColumnNorm(ph, "norm", 4, 5, per_round=2)
        scaled_ready = ph.semaphore("scaled_ready", 2)
        h1_ready = ph.semaphore("h1_ready")
        up_ready, y_ready = ph.semaphore("up_ready", F), ph.semaphore("y_ready", F)

        with nc.Block() as block:
            @block.sync
            def _(sp):
                sp.dma_start(table[:, :], core.dram["const_l0a"]).then_inc(table_in.sem, 16)
                with sp.Fori(0, L0_LAYERS) as layer:
                    sp.wait_ge(round_done.sem, layer * B + 1)
                    sp.dma_start(w[:, :], core.dram["l0a"][bass.ds(layer, 1), :, :].rearrange("a p c -> (a p) c"))\
                      .then_inc(w_in.sem, 16)

            @block.gpsimd
            def _(pool):
                pool.wait_ge(table_in.sem, 16)
                for b in range(B):
                    pool.tensor_copy(core.s[:, b * N:(b + 1) * N], core.xn[:, b * N:(b + 1) * N])\
                        .then_inc(copied.sem, 1)
                pool.memset(v[:, :, :, DH:DV], 1.0).then_inc(ones_ready.sem, 1)
                with pool.Fori(0, L0_LAYERS) as layer:
                    pool.wait_ge(w_in.sem, layer * 16 + 16)
                    pool.tensor_tensor(omega_signed[:, :], L0A.of(w, "omega"), const("sign"), ALU.mult)\
                        .then_inc(omega_signed_ready.sem, 1)
                    pool.wait_ge(omega_signed_ready.sem, omega_signed_ready.at(layer))
                    pool.tensor_tensor(omega[:, :], omega_signed[:, :], const("nhalf"), ALU.add)\
                        .then_inc(omega_ready.sem, 1)
                    pool.wait_ge(round_done.sem, layer * B + B + 1)
                    apart(pool, passed)

            @block.tensor
            def _(pe):
                pe.wait_ge(table_in.sem, 16)
                pe.wait_ge(ones_ready.sem, 1)
                with pe.Fori(0, L0_LAYERS) as layer:
                    pe.wait_ge(w_in.sem, layer * 16 + 16)
                    pe.wait_ge(omega_ready.sem, omega_ready.at(layer))
                    apart(pe, passed)
                    with pe.Fori(0, B) as b:
                        r = layer * B + b
                        pe.wait_ge(h_ready.sem, h_ready.at(r))
                        for t in range(4):
                            pe.matmul(psum[:, t, :], L0A.of(w, "wq" if t < 2 else "wk", t % 2, P), h_in[:, :],
                                      start=True, stop=True).then_inc(proj_ready.sem, 1)
                        for c in range(CH):
                            mm = pe.matmul(psum[:, 4, c * P:(c + 1) * P], h_in[:, c * P:(c + 1) * P],
                                           L0A.of(w, "wv"), start=(c == 0), stop=(c == CH - 1),
                                           skip_group_check=True)
                        mm.then_inc(v_ready.sem, 1)
                        for n in (4, 5, 6, 7, 0, 1, 2, 3):
                            t, half = n // 2, 64 * (n % 2)
                            bank = (n + 4) % 8
                            pe.wait_ge(qk_sq_ready.sem, qk_sq_ready.at(r, t))
                            if n == 4 or n == 5:
                                pe.wait_ge(qk_ready.sem, qk_ready.at(r, 3))
                            if n == 0:
                                pe.wait_ge(v_kept.sem, v_kept.at(r, CH - 1))
                            pe.matmul(psum[:, bank, :], omega[half:half + 64, :], qk[half:half + 64, t, :],
                                      start=True, stop=True).then_inc(arg_ready.sem, 1)
                        for c in range(CH - 1):
                            pe.wait_ge(feat_ready.sem, feat_ready.at(r, 3 if c < CH - 2 else 7))
                            for g in range(G):
                                mm = pe.transpose(psum[:, c, g * P:(g + 1) * P], feat[:, 4 + g, c * P:(c + 1) * P],
                                                  core.c("ident"))
                            mm.then_inc(k_tok_ready.sem, 1)
                        pe.wait_ge(k_tok_kept.sem, k_tok_kept.at(r, CH - 2))

                        def score(c):
                            if c >= 1:
                                pe.wait_ge(scores_kept.sem, scores_kept.at(r, c * 4 - 1))
                            for g in range(G):
                                for h in range(4):
                                    rows = slice(32 * h, 32 * h + 16)
                                    mm = pe.matmul(psum[:, h, g * P:(g + 1) * P],
                                                   feat[rows, 4 + g, c * P:(c + 1) * P],
                                                   feat[rows, g, c * P:(c + 1) * P],
                                                   start=(g == 0), stop=(g == G - 1), skip_group_check=True)
                                    if g == G - 1:
                                        mm.then_inc(scores_ready.sem, 1)

                        def gather(c):
                            bank = 6 + c % 2
                            if c >= 2:
                                pe.wait_ge(att_ready.sem, att_ready.at(r, c - 2))
                            if c >= 1:
                                pe.wait_ge(state_ready.sem, state_ready.at(r, c - 1))
                            pe.wait_ge(scores_kept.sem, scores_kept.at(r, c * 4 + 3))
                            for g in range(G):
                                if c >= 1:
                                    pe.matmul(psum[:, bank, g * 4 * DV:(g + 1) * 4 * DV],
                                              feat[:, g, c * P:(c + 1) * P],
                                              state[:, c - 1, g * 4 * DV:(g + 1) * 4 * DV],
                                              start=(g == 0), stop=False, skip_group_check=True)
                                for h in range(4):
                                    mm = pe.matmul(psum[:, bank, (4 * g + h) * DV:(4 * g + h + 1) * DV],
                                                   scores[:, c % 2, h, g * P:(g + 1) * P], v[:, c, 4 * g + h, :],
                                                   start=(c == 0 and g == 0 and h == 0),
                                                   stop=(g == G - 1 and h == 3), skip_group_check=True)
                            mm.then_inc(num_ready.sem, 1)

                        def turn(c):
                            pe.wait_ge(att_ready.sem, att_ready.at(r, c))
                            mm = pe.transpose(psum[:, 4, c * P:(c + 1) * P], att[:, c, :], core.c("ident"))
                            if c == CH - 1:
                                mm.then_inc(att_t_ready.sem, 1)

                        score(0)
                        for c in range(CH - 1):
                            pe.wait_ge(k_tok_kept.sem, k_tok_kept.at(r, c))
                            if c >= 1:
                                pe.wait_ge(kv_kept.sem, kv_kept.at(r, c - 1))
                            for g in range(G):
                                mm = pe.matmul(psum[:, 5, g * 4 * DV:(g + 1) * 4 * DV], k_tok[:, c, g * P:(g + 1) * P],
                                               v[:, c, 4 * g:4 * g + 4, :],
                                               start=(g == 0), stop=(g == G - 1), skip_group_check=True)
                            mm.then_inc(kv_ready.sem, 1)
                        for c in range(1, CH + 1):
                            if c < CH:
                                score(c)
                            gather(c - 1)
                            if c >= 2:
                                turn(c - 2)
                        turn(CH - 1)
                        pe.wait_ge(att_t_kept.sem, att_t_kept.at(r))
                        pe.matmul(psum[:, 0, :], L0A.of(w, "wo"), att_t[:, :], start=True, stop=True)\
                          .then_inc(out_ready.sem, 1)
                        pe.wait_ge(res_ready.sem, res_ready.at(r, 0))
                        norm.tensor(pe, r, res1[:, :], 0)
                        pe.wait_ge(h1_ready.sem, h1_ready.at(r))
                        for f in range(F):
                            pe.matmul(psum[:, f, :], L0A.of(w, "w1", f, P), h1[:, :], start=True, stop=True)\
                              .then_inc(up_ready.sem, 1)
                        for f in range(F):
                            pe.wait_ge(y_ready.sem, y_ready.at(r, f))
                            mm = pe.matmul(psum[:, 6, :], L0A.of(w, "w2", f, P), y[:, f, :],
                                           start=(f == 0), stop=(f == F - 1))
                        mm.then_inc(out_ready.sem, 1)
                        pe.wait_ge(res_ready.sem, res_ready.at(r, 1))
                        norm.tensor(pe, r, res2[:, :], 1)

            @block.scalar
            def _(act):
                act.wait_ge(table_in.sem, 16)
                act.preload_act_table_set(EXP_LN_SET)
                with act.Fori(0, L0_LAYERS) as layer:
                    act.wait_ge(w_in.sem, layer * 16 + 16)
                    apart(act, passed)
                    with act.Fori(0, B) as b:
                        r = layer * B + b
                        for t in (2, 3, 0, 1):
                            act.wait_ge(qk_ready.sem, qk_ready.at(r, t))
                            for rows in (slice(32, 64), slice(96, 128)):
                                sq = act.activation(qk[rows, t, :], qk[rows, t, :], ACT.Square)
                            sq.then_inc(qk_sq_ready.sem, 1)
                        for k in range(8):
                            n = (4, 5, 6, 7, 0, 1, 2, 3)[k]
                            act.wait_ge(arg_ready.sem, arg_ready.at(r, k))
                            act.activation(feat[:, n, :], psum[:, (n + 4) % 8, :], ACT.Exp)\
                               .then_inc(feat_ready.sem, 1)
                        for c in range(CH - 1):
                            act.wait_ge(k_tok_ready.sem, k_tok_ready.at(r, c))
                            act.copy(k_tok[:, c, :], psum[:, c, :]).then_inc(k_tok_kept.sem, 1)
                        act.wait_ge(att_t_ready.sem, att_t_ready.at(r))
                        act.copy(att_t[:, :], psum[:, 4, :]).then_inc(att_t_kept.sem, 1)
                        norm.scalar(act, r, k=0)
                        for f in range(F):
                            act.wait_ge(up_ready.sem, up_ready.at(r, f))
                            act.activation(y[:, f, :], psum[:, f, :], ACT.Relu, bias=col("bf1", f))\
                               .then_inc(y_ready.sem, 1)
                        norm.scalar(act, r, k=1)

            @block.vector
            def _(dve):
                dve.wait_ge(table_in.sem, 16)
                dve.sem_inc(round_done.sem, 1)
                dve.wait_ge(copied.sem, B)
                dve.wait_ge(ones_ready.sem, 1)
                with dve.Fori(0, L0_LAYERS) as layer:
                    dve.wait_ge(w_in.sem, layer * 16 + 16)
                    apart(dve, passed)
                    with dve.Fori(0, B) as b:
                        r = layer * B + b
                        dve.wait_ge(round_done.sem, r + 1)
                        dve.tensor_copy(h_in[:, :], core.s[:, cols(b)]).then_inc(h_ready.sem, 1)
                        for t in range(4):
                            dve.wait_ge(proj_ready.sem, proj_ready.at(r, t))
                            dve.tensor_scalar(qk[:, t, :], psum[:, t, :], col("bq" if t < 2 else "bk", t % 2), SCALE,
                                              ALU.add, ALU.mult).then_inc(qk_ready.sem, 1)
                        dve.wait_ge(v_ready.sem, v_ready.at(r))
                        for c in range(CH):
                            dve.tensor_tensor(v[:, c, :, 0:DH],
                                              psum[:, 4, c * P:(c + 1) * P].rearrange("p (h d) -> p h d", d=DH),
                                              L0A.of(w, "bv").rearrange("p (h d) -> p h d", d=DH), ALU.add)\
                               .then_inc(v_kept.sem, 1)

                        def keep_state(c):
                            dve.wait_ge(kv_ready.sem, kv_ready.at(r, c))
                            dst = state if c == 0 else kv
                            keep = dve.tensor_tensor(dst[:, c, :], psum[:, 5, 0:L0_HEADS * DV], const("kvmask"),
                                                     ALU.mult)
                            keep.then_inc(kv_kept.sem, 1)
                            dve.wait_ge(kv_kept.sem, kv_kept.at(r, c))
                            if c == 0:
                                dve.sem_inc(state_ready.sem, 1)
                            else:
                                dve.wait_ge(state_ready.sem, state_ready.at(r, c - 1))
                                dve.tensor_tensor(state[:, c, :], state[:, c - 1, :], kv[:, c, :], ALU.add)\
                                   .then_inc(state_ready.sem, 1)

                        def mask(c):
                            for h in range(4):
                                dve.wait_ge(scores_ready.sem, scores_ready.at(r, c * 4 + h))
                                dve.tensor_tensor(scores[:, c % 2, h, :], psum[:, h, :], const("causal4"),
                                                  ALU.mult).then_inc(scores_kept.sem, 1)

                        def divide(c):
                            dve.wait_ge(num_ready.sem, num_ready.at(r, c))
                            num = psum[:, 6 + c % 2, 0:L0_HEADS * DV].rearrange("p (h d) -> p h d", d=DV)
                            dve.tensor_scalar(den[:, c, :], num[:, :, DH], ATT_EPS, None, ALU.add)\
                               .then_inc(den_ready.sem, 1)
                            dve.wait_ge(den_ready.sem, den_ready.at(r, c))
                            dve.reciprocal(rden[:, c, :], den[:, c, :]).then_inc(rden_ready.sem, 1)
                            dve.wait_ge(rden_ready.sem, rden_ready.at(r, c))
                            dve.tensor_tensor(att[:, c, :].rearrange("p (h d) -> p h d", d=DH), num[:, :, 0:DH],
                                              rden[:, c, :].unsqueeze(2).to_broadcast([P, L0_HEADS, DH]), ALU.mult)\
                               .then_inc(att_ready.sem, 1)

                        mask(0)
                        for c in range(CH - 1):
                            keep_state(c)
                        for c in range(1, CH):
                            mask(c)
                            divide(c - 1)
                        divide(CH - 1)
                        dve.wait_ge(out_ready.sem, out_ready.at(r, 0))
                        dve.scalar_tensor_tensor(out=res1[:, :], in0=psum[:, 0, :], scalar=col("bo"), in1=h_in[:, :],
                                                 op0=ALU.add, op1=ALU.add).then_inc(res_ready.sem, 1)
                        dve.wait_ge(res_ready.sem, res_ready.at(r, 0))
                        norm.vector(dve, r, res1[:, :], 0)
                        dve.wait_ge(norm.rstd_ready.sem, norm.rstd_ready.at(r, 0))
                        dve.scalar_tensor_tensor(out=scaled1[:, :], in0=norm.centred[:, :], scalar=col("g1"),
                                                 in1=norm.rstd[:, :], op0=ALU.mult, op1=ALU.mult)\
                           .then_inc(scaled_ready.sem, 1)
                        dve.wait_ge(scaled_ready.sem, scaled_ready.at(r, 0))
                        dve.tensor_scalar(h1[:, :], scaled1[:, :], col("be1"), None, ALU.add).then_inc(h1_ready.sem, 1)
                        dve.wait_ge(h1_ready.sem, h1_ready.at(r))
                        dve.wait_ge(out_ready.sem, out_ready.at(r, 1))
                        dve.scalar_tensor_tensor(out=res2[:, :], in0=psum[:, 6, :], scalar=col("bf2"), in1=h1[:, :],
                                                 op0=ALU.add, op1=ALU.add).then_inc(res_ready.sem, 1)
                        dve.wait_ge(res_ready.sem, res_ready.at(r, 1))
                        norm.vector(dve, r, res2[:, :], 1)
                        dve.wait_ge(norm.rstd_ready.sem, norm.rstd_ready.at(r, 1))
                        dve.scalar_tensor_tensor(out=scaled2[:, :], in0=norm.centred[:, :], scalar=col("g2"),
                                                 in1=norm.rstd[:, :], op0=ALU.mult, op1=ALU.mult)\
                           .then_inc(scaled_ready.sem, 1)
                        dve.wait_ge(scaled_ready.sem, scaled_ready.at(r, 1))
                        dve.tensor_scalar(core.s[:, cols(b)], scaled2[:, :], col("be2"), None, ALU.add)\
                           .then_inc(round_done.sem, 1)


L0F_LAYERS, L0F_HEADS, L0F_INNER, L0F_HID = 2, 8, 512, 341
L0F_TILES = L0F_INNER // P
L0F_HT = -(-L0F_HID // P)
L0F = Fields(("wq", L0F_INNER), ("wk", L0F_INNER), ("wv", L0F_INNER), ("wo", L0F_INNER),
             ("w1", 2 * L0F_HT * P), ("w2", L0F_HT * P), ("q_scale", 1), ("k_scale", 1), ("ln_g", 1), ("ln_b", 1),
             ("b1", 2 * L0F_HT), ("b2", 1))


def l0_ffn_layout(np, i):
    g = lambda k: i["L0_ffn_" + k]
    hid = L0F_HID

    def halves(a):
        out = np.zeros((a.shape[0], 2, L0F_HT * P), np.float32)
        for x in range(2):
            out[:, x, :hid] = a[:, x * hid:(x + 1) * hid]
        return out.reshape(a.shape[0], 2 * L0F_HT, P)

    out = []
    for n in range(L0F_LAYERS):
        w2 = np.zeros((L0F_HT * P, P), np.float32)
        w2[:hid] = g("w2")[n]
        out.append(pack(np, [
            g("wqkv")[n], blocks(np, g("wo")[n]), halves(g("w1")[n]).reshape(P, 2 * L0F_HT * P), blocks(np, w2),
            np.tile(g("q_scale")[n], 2)[:, None], np.tile(g("k_scale")[n], 2)[:, None],
            column(g("ln_g")[n]), column(g("ln_b")[n]), halves(g("b1")[n][None])[0].T, column(g("b2")[n])]))
    return {"l0f": np.stack(out)}


LAYOUTS.append(l0_ffn_layout)


def l0_ffn_phase(core):
    nc, psum = core.nc, core.psum
    H, TL, HT, W = L0F_HEADS, L0F_TILES, L0F_HT, 64
    with Phase(core, "l0f") as ph:
        w = ph.buf("w", L0F.width)
        col = lambda name, k=0: L0F.of(w, name, k, 1)
        swap = ph.buf("swap", 2, P)
        h_in = ph.buf("h_in", N)
        sq = ph.buf("sq", 2, N)
        log, rinv = ph.buf("log", 2, N), ph.buf("rinv", 2, N)
        unit = ph.buf("unit", 2, N)
        unit_s = ph.buf("unit_s", 2, N)
        by_cos, by_sin = ph.buf("by_cos", 2, N), ph.buf("by_sin", 2, N)
        qk = ph.buf("qk", 2 * TL, N)
        v = ph.buf("v", CH, L0F_INNER)
        sim = ph.buf("sim", H, 2 * P)
        nmax, total, rtotal = ph.buf("nmax", CH, H), ph.buf("total", CH, H), ph.buf("rtotal", CH, H)
        prob = ph.buf("prob", H, 2 * P)
        prob_n = ph.buf("prob_n", H, 2 * P)
        prob_t = ph.buf("prob_t", 2 * H, P)
        o = ph.buf("o", TL, N)
        x1, shifted = ph.buf("x1", N), ph.buf("shifted", N)
        scaled, hn = ph.buf("scaled", N), ph.buf("hn", N)
        gelu, hidden = ph.buf("gelu", HT, N), ph.buf("hidden", HT, N)
        head = [(s // 2) % 2 + 2 * (2 * (s // 4) + s % 2) for s in range(H)]

        table = ph.buf("table", CONST_L0F.width)
        const = lambda name: CONST_L0F.of(table, name)
        table_in = ph.semaphore("table_in")
        passed = ph.semaphore("passed")
        w_in, zeroed = ph.semaphore("w_in"), ph.semaphore("zeroed", 3)
        copied = ph.semaphore("copied", B)
        round_done = ph.semaphore("round_done")
        swap_ready = ph.semaphore("swap_ready", 2)
        h_ready = ph.semaphore("h_ready", 2)
        qk_raw, sq_ready = ph.semaphore("qk_raw", 8), ph.semaphore("sq_ready", 8)
        sum_ready = ph.semaphore("sum_ready", 8)
        log_ready, rinv_ready = ph.semaphore("log_ready", 8), ph.semaphore("rinv_ready", 8)
        scaled_unit = ph.semaphore("scaled_unit", 8)
        unit_ready, rot_ready = ph.semaphore("unit_ready", 8), ph.semaphore("rot_ready", 8)
        cos_ready, sin_ready = ph.semaphore("cos_ready", 8), ph.semaphore("sin_ready", 8)
        qk_ready = ph.semaphore("qk_ready", 8)
        v_ready, v_kept = ph.semaphore("v_ready", CH), ph.semaphore("v_kept", CH)
        sim_ready, sim_kept = ph.semaphore("sim_ready", CH), ph.semaphore("sim_kept", CH)
        nmax_ready, prob_ready = ph.semaphore("nmax_ready", CH), ph.semaphore("prob_ready", CH)
        rtotal_ready, prob_n_ready = ph.semaphore("rtotal_ready", CH), ph.semaphore("prob_n_ready", CH)
        turned, turned_kept = ph.semaphore("turned", 4 * CH), ph.semaphore("turned_kept", 4 * CH)
        o_ready, o_kept = ph.semaphore("o_ready", CH), ph.semaphore("o_kept", CH)
        y_ready = ph.semaphore("y_ready", 2)
        x1_ready, shifted_ready = ph.semaphore("x1_ready"), ph.semaphore("shifted_ready", 2)
        norm = ColumnNorm(ph, "norm", 1, 2)
        scaled_ready, hn_ready = ph.semaphore("scaled_ready"), ph.semaphore("hn_ready")
        up_ready, gelu_ready, hidden_ready = ph.semaphore("up_ready", 2 * HT), ph.semaphore("gelu_ready", HT), ph.semaphore("hidden_ready", HT)

        def keys(c):
            return slice(W if c else P, 2 * P)

        with nc.Block() as block:
            @block.sync
            def _(sp):
                sp.dma_start(table[:, :], core.dram["const_l0f"]).then_inc(table_in.sem, 16)
                with sp.Fori(0, L0F_LAYERS) as layer:
                    sp.wait_ge(round_done.sem, layer * B + 1)
                    sp.dma_start(w[:, :], core.dram["l0f"][bass.ds(layer, 1), :, :].rearrange("a p c -> (a p) c"))\
                      .then_inc(w_in.sem, 16)

            @block.gpsimd
            def _(pool):
                pool.wait_ge(table_in.sem, 16)
                for b in range(B):
                    pool.tensor_copy(core.g[:, b * N:(b + 1) * N], core.xn[:, b * N:(b + 1) * N])\
                        .then_inc(copied.sem, 1)
                with pool.Fori(0, L0F_LAYERS) as layer:
                    pool.wait_ge(w_in.sem, layer * 16 + 16)
                    apart(pool, passed)
                    with pool.Fori(0, B) as b:
                        r = layer * B + b
                        pool.wait_ge(round_done.sem, r + 1)
                        for t in range(8):
                            pool.wait_ge(unit_ready.sem, unit_ready.at(r, t))
                            if t >= 2:
                                pool.wait_ge(qk_ready.sem, qk_ready.at(r, t - 2))
                            apart(pool, passed)
                            pool.tensor_scalar(unit_s[:, t % 2, :], unit[:, t % 2, :],
                                               col("q_scale" if t < 4 else "k_scale"), None, ALU.mult)\
                                .then_inc(scaled_unit.sem, 1)
                            pool.wait_ge(scaled_unit.sem, scaled_unit.at(r, t))
                            pool.tensor_tensor(by_cos[:, t % 2, :], unit_s[:, t % 2, :],
                                               const("rope_qc" if t < 4 else "rope_kc"), ALU.mult)\
                                .then_inc(cos_ready.sem, 1)
                        for c in range(CH):
                            pool.wait_ge(rtotal_ready.sem, rtotal_ready.at(r, c))
                            pool.wait_ge(prob_ready.sem, prob_ready.at(r, c))
                            if c >= 1:
                                pool.wait_ge(turned.sem, turned.at(r, 4 * c - 1))
                            k = keys(c)
                            pool.tensor_tensor(prob_n[:, :, k], prob[:, :, k],
                                               rtotal[:, c, :].unsqueeze(2).to_broadcast([P, H, 2 * P - k.start]),
                                               ALU.mult).then_inc(prob_n_ready.sem, 1)

            @block.tensor
            def _(pe):
                pe.wait_ge(table_in.sem, 16)
                pe.wait_ge(zeroed.sem, 3)
                with pe.Fori(0, L0F_LAYERS) as layer:
                    pe.wait_ge(w_in.sem, layer * 16 + 16)
                    apart(pe, passed)
                    with pe.Fori(0, B) as b:
                        r = layer * B + b
                        pe.wait_ge(h_ready.sem, h_ready.at(r, 1))

                        def project(t):
                            if t >= 2:
                                pe.wait_ge(unit_ready.sem, unit_ready.at(r, t - 2))
                            pe.matmul(psum[:, t % 2, :], L0F.of(w, "wq" if t < 4 else "wk", t % 4, P), h_in[:, :],
                                      start=True, stop=True).then_inc(qk_raw.sem, 1)

                        def sum_squares(t):
                            pe.wait_ge(sq_ready.sem, sq_ready.at(r, t))
                            pe.matmul(psum[:, 2 + t % 2, :], const("ones64"), sq[:, t % 2, :],
                                      start=True, stop=True).then_inc(sum_ready.sem, 1)

                        def rotate(t):
                            pe.wait_ge(unit_ready.sem, unit_ready.at(r, t))
                            if t == 0:
                                pe.wait_ge(swap_ready.sem, swap_ready.at(layer, 1))
                            if t >= 2:
                                pe.wait_ge(sin_ready.sem, sin_ready.at(r, t - 2))
                            pe.matmul(psum[:, 4 + t % 2, :], swap[:, 0 if t < 4 else 1, :], unit[:, t % 2, :],
                                      start=True, stop=True).then_inc(rot_ready.sem, 1)

                        def value(c):
                            if c >= 2:
                                pe.wait_ge(v_kept.sem, v_kept.at(r, c - 2))
                            pe.matmul(psum[:, 6 + c % 2, :], h_in[:, c * P:(c + 1) * P], L0F.of(w, "wv"),
                                      start=True, stop=True).then_inc(v_ready.sem, 1)

                        project(0)
                        project(1)
                        value(0)
                        value(1)
                        for t in range(8):
                            sum_squares(t)
                            if t == 2 or t == 4:
                                value(t // 2 + 1)
                            rotate(t)
                            if t + 2 < 8:
                                project(t + 2)

                        def score(c):
                            if c == 0:
                                pe.wait_ge(qk_ready.sem, qk_ready.at(r, 7))
                                pe.wait_ge(v_kept.sem, v_kept.at(r, CH - 1))
                            else:
                                pe.wait_ge(sim_kept.sem, sim_kept.at(r, c - 1))
                            k = keys(c)
                            first = (c - 1) * P + k.start
                            for u in range(2):
                                for bank in range(4):
                                    h = head[2 * bank + u]
                                    rows = slice(64 * (h % 2), 64 * (h % 2) + 64)
                                    mm = pe.matmul(psum[:, bank, u * 2 * P + k.start:u * 2 * P + 2 * P],
                                                   qk[rows, h // 2, c * P:(c + 1) * P],
                                                   qk[rows, TL + h // 2, first:(c + 1) * P],
                                                   start=(u == 0), stop=(u == 1), skip_group_check=True)
                            mm.then_inc(sim_ready.sem, 1)

                        def turn(c):
                            pe.wait_ge(prob_n_ready.sem, prob_n_ready.at(r, c))
                            for j in range(4):
                                n = 4 * c + j
                                if n >= 3:
                                    pe.wait_ge(turned_kept.sem, turned_kept.at(r, n - 3))
                                for i in range(4):
                                    slot, own = 2 * j + i // 2, i % 2
                                    if c == 0 and not own:
                                        continue
                                    mm = pe.transpose(psum[:, 4 + n % 3, i * P:(i + 1) * P],
                                                      prob_n[:, slot, own * P:(own + 1) * P], core.c("ident"))
                                mm.then_inc(turned.sem, 1)

                        def draw(c):
                            if c >= 1:
                                pe.wait_ge(o_kept.sem, o_kept.at(r, c - 1))
                            pe.wait_ge(turned_kept.sem, turned_kept.at(r, 4 * c + 3))
                            for s in range(H):
                                h = head[s]
                                rows = slice(64 * (h % 2), 64 * (h % 2) + 64)
                                dst = psum[rows, 7, (h // 2) * P:(h // 2 + 1) * P]
                                for own in ((0, 1) if c else (1,)):
                                    mm = pe.matmul(dst, v[:, c - 1 + own, h * W:(h + 1) * W],
                                                   prob_t[:, 2 * s + own, :],
                                                   start=(own == 0 or c == 0) , stop=(own == 1),
                                                   skip_group_check=True)
                            mm.then_inc(o_ready.sem, 1)

                        score(0)
                        for c in range(CH):
                            if c + 1 < CH:
                                score(c + 1)
                            turn(c)
                            draw(c)
                        pe.wait_ge(o_kept.sem, o_kept.at(r, CH - 1))
                        for t in range(TL):
                            mm = pe.matmul(psum[:, 0, :], L0F.of(w, "wo", t, P), o[:, t, :],
                                           start=(t == 0), stop=(t == TL - 1))
                        mm.then_inc(y_ready.sem, 1)
                        pe.wait_ge(shifted_ready.sem, shifted_ready.at(r, 1))
                        norm.tensor(pe, r, shifted[:, :])
                        pe.wait_ge(hn_ready.sem, hn_ready.at(r))
                        for t in [HT + x for x in range(HT)] + list(range(HT)):
                            pe.matmul(psum[:, 2 + t, :], L0F.of(w, "w1", t, P), hn[:, :], start=True, stop=True)\
                              .then_inc(up_ready.sem, 1)
                        for t in range(HT):
                            pe.wait_ge(hidden_ready.sem, hidden_ready.at(r, t))
                            mm = pe.matmul(psum[:, 0, :], L0F.of(w, "w2", t, P), hidden[:, t, :],
                                           start=(t == 0), stop=(t == HT - 1))
                        mm.then_inc(y_ready.sem, 1)

            @block.scalar
            def _(act):
                act.wait_ge(table_in.sem, 16)
                with act.Fori(0, L0F_LAYERS) as layer:
                    act.wait_ge(w_in.sem, layer * 16 + 16)
                    apart(act, passed)
                    with act.Fori(0, B) as b:
                        r = layer * B + b
                        act.wait_ge(round_done.sem, r + 1)
                        apart(act, passed)
                        act.preload_act_table_set(EXP_LN_SET)

                        def square(t):
                            act.wait_ge(qk_raw.sem, qk_raw.at(r, t))
                            if t >= 2:
                                act.wait_ge(sum_ready.sem, sum_ready.at(r, t - 2))
                            act.activation(sq[:, t % 2, :], psum[:, t % 2, :], ACT.Square).then_inc(sq_ready.sem, 1)

                        def inverse(t):
                            act.wait_ge(sum_ready.sem, sum_ready.at(r, t))
                            act.activation(log[:, t % 2, :], psum[:, 2 + t % 2, :], ACT.Ln, scale=2.0 ** 30,
                                           bias=const("eps_l2")).then_inc(log_ready.sem, 1)
                            act.wait_ge(log_ready.sem, log_ready.at(r, t))
                            if t >= 2:
                                act.wait_ge(unit_ready.sem, unit_ready.at(r, t - 2))
                            act.activation(rinv[:, t % 2, :], log[:, t % 2, :], ACT.Exp, scale=-0.5,
                                           bias=const("l2_back")).then_inc(rinv_ready.sem, 1)

                        def keep_value(c):
                            act.wait_ge(v_ready.sem, v_ready.at(r, c))
                            act.copy(v[:, c, :], psum[:, 6 + c % 2, :]).then_inc(v_kept.sem, 1)

                        square(0)
                        square(1)
                        keep_value(0)
                        keep_value(1)
                        for t in range(8):
                            inverse(t)
                            if t == 2 or t == 4:
                                keep_value(t // 2 + 1)
                            if t + 2 < 8:
                                square(t + 2)
                        for c in range(CH):
                            act.wait_ge(nmax_ready.sem, nmax_ready.at(r, c))
                            if c >= 1:
                                act.wait_ge(prob_n_ready.sem, prob_n_ready.at(r, c - 1))
                            k = keys(c)
                            for s in range(H):
                                e = act.activation(prob[:, s, k], sim[:, s, k], ACT.Exp, bias=nmax[:, c, s:s + 1],
                                                   accum_out=total[:, c, s:s + 1])
                            e.then_inc(prob_ready.sem, 1)
                            for j in range(4):
                                n = 4 * c + j
                                act.wait_ge(turned.sem, turned.at(r, n))
                                if c >= 1:
                                    act.wait_ge(o_ready.sem, o_ready.at(r, c - 1))
                                dst = prob_t[:, 4 * j:4 * j + 4, :]
                                src = psum[:, 4 + n % 3, :].rearrange("p (i q) -> p i q", i=4)
                                if c == 0:
                                    dst, src = prob_t[:, 4 * j + 1:4 * j + 4:2, :], src[:, 1:4:2, :]
                                act.copy(dst, src).then_inc(turned_kept.sem, 1)
                            act.wait_ge(o_ready.sem, o_ready.at(r, c))
                            act.copy(o[:, :, c * P:(c + 1) * P], psum[:, 7, :].rearrange("p (t q) -> p t q", t=TL))\
                               .then_inc(o_kept.sem, 1)
                        norm.scalar(act, r)
                        for t in range(HT):
                            act.wait_ge(up_ready.sem, up_ready.at(r, t))
                            act.activation(gelu[:, t, :], psum[:, 2 + HT + t, :], ACT.Gelu, bias=col("b1", HT + t))\
                               .then_inc(gelu_ready.sem, 1)

            @block.vector
            def _(dve):
                dve.wait_ge(table_in.sem, 16)
                dve.sem_inc(round_done.sem, 1)
                dve.memset(h_in[64:P, 0:1], 0.0).then_inc(zeroed.sem, 1)
                dve.memset(shifted[64:P, 0:1], 0.0).then_inc(zeroed.sem, 1)
                dve.memset(prob_n[:, :, 0:W], 0.0).then_inc(zeroed.sem, 1)
                dve.wait_ge(copied.sem, B)
                with dve.Fori(0, L0F_LAYERS) as layer:
                    dve.wait_ge(w_in.sem, layer * 16 + 16)
                    dve.tensor_scalar(swap[:, 0, :], const("swap64"), col("q_scale"), None, ALU.mult)\
                       .then_inc(swap_ready.sem, 1)
                    dve.tensor_scalar(swap[:, 1, :], const("swap64"), col("k_scale"), None, ALU.mult)\
                       .then_inc(swap_ready.sem, 1)
                    apart(dve, passed)
                    with dve.Fori(0, B) as b:
                        r = layer * B + b
                        dve.wait_ge(round_done.sem, r + 1)
                        dve.tensor_copy(h_in[0:64, :], core.g[0:64, cols(b)]).then_inc(h_ready.sem, 1)
                        dve.tensor_copy(h_in[64:P, 1:N], core.g[64:P, bass.ds(b * N, N - 1)]).then_inc(h_ready.sem, 1)

                        def divide(t):
                            dve.wait_ge(rinv_ready.sem, rinv_ready.at(r, t))
                            if t >= 2:
                                dve.wait_ge(rot_ready.sem, rot_ready.at(r, t - 2))
                                dve.wait_ge(cos_ready.sem, cos_ready.at(r, t - 2))
                            dve.scalar_tensor_tensor(out=unit[:, t % 2, :], in0=rinv[:, t % 2, :], scalar=1e12,
                                                     in1=psum[:, t % 2, :], op0=ALU.min, op1=ALU.mult)\
                               .then_inc(unit_ready.sem, 1)

                        def rotate(t):
                            dve.wait_ge(rot_ready.sem, rot_ready.at(r, t))
                            dve.tensor_tensor(by_sin[:, t % 2, :], psum[:, 4 + t % 2, :],
                                              const("rope_qs" if t < 4 else "rope_ks"), ALU.mult)\
                               .then_inc(sin_ready.sem, 1)
                            dve.wait_ge(sin_ready.sem, sin_ready.at(r, t))
                            dve.wait_ge(cos_ready.sem, cos_ready.at(r, t))
                            dve.tensor_tensor(qk[:, t, :], by_cos[:, t % 2, :], by_sin[:, t % 2, :], ALU.add)\
                               .then_inc(qk_ready.sem, 1)

                        for t in range(9):
                            if t < 8:
                                divide(t)
                            if t >= 1:
                                rotate(t - 1)

                        def mask(c):
                            dve.wait_ge(sim_ready.sem, sim_ready.at(r, c))
                            if c >= 1:
                                dve.wait_ge(prob_ready.sem, prob_ready.at(r, c - 1))
                            k = keys(c)
                            bias = const("window" if c else "window_first")[:, k]
                            dve.tensor_tensor(sim[:, :, k],
                                              psum[:, 0:4, :].rearrange("p b (u k) -> p (b u) k", u=2)[:, :, k],
                                              bias.unsqueeze(1).to_broadcast([P, H, 2 * P - k.start]), ALU.add)\
                               .then_inc(sim_kept.sem, 1)
                            dve.wait_ge(sim_kept.sem, sim_kept.at(r, c))
                            dve.tensor_reduce(nmax[:, c, :], sim[:, :, k], AX.X, ALU.max, negate=True)\
                               .then_inc(nmax_ready.sem, 1)

                        for c in range(CH + 1):
                            if c < CH:
                                mask(c)
                            if c >= 1:
                                dve.wait_ge(prob_ready.sem, prob_ready.at(r, c - 1))
                                dve.reciprocal(rtotal[:, c - 1, :], total[:, c - 1, :]).then_inc(rtotal_ready.sem, 1)
                        dve.wait_ge(y_ready.sem, y_ready.at(r, 0))
                        dve.tensor_tensor(x1[:, :], core.g[:, cols(b)], psum[:, 0, :], ALU.add)\
                           .then_inc(x1_ready.sem, 1)
                        dve.wait_ge(x1_ready.sem, x1_ready.at(r))
                        dve.tensor_copy(shifted[0:64, :], x1[0:64, :]).then_inc(shifted_ready.sem, 1)
                        dve.tensor_copy(shifted[64:P, 1:N], x1[64:P, 0:N - 1]).then_inc(shifted_ready.sem, 1)
                        dve.wait_ge(shifted_ready.sem, shifted_ready.at(r, 1))
                        norm.vector(dve, r, shifted[:, :])
                        dve.wait_ge(norm.rstd_ready.sem, norm.rstd_ready.at(r))
                        dve.scalar_tensor_tensor(out=scaled[:, :], in0=norm.centred[:, :], scalar=col("ln_g"),
                                                 in1=norm.rstd[:, :], op0=ALU.mult, op1=ALU.mult)\
                           .then_inc(scaled_ready.sem, 1)
                        dve.wait_ge(scaled_ready.sem, scaled_ready.at(r))
                        dve.tensor_scalar(hn[:, :], scaled[:, :], col("ln_b"), None, ALU.add).then_inc(hn_ready.sem, 1)
                        for t in range(HT):
                            dve.wait_ge(up_ready.sem, up_ready.at(r, HT + t))
                            dve.wait_ge(gelu_ready.sem, gelu_ready.at(r, t))
                            dve.scalar_tensor_tensor(out=hidden[:, t, :], in0=psum[:, 2 + t, :], scalar=col("b1", t),
                                                     in1=gelu[:, t, :], op0=ALU.add, op1=ALU.mult)\
                               .then_inc(hidden_ready.sem, 1)
                        dve.wait_ge(y_ready.sem, y_ready.at(r, 1))
                        dve.scalar_tensor_tensor(out=core.g[:, cols(b)], in0=psum[:, 0, :], scalar=col("b2"),
                                                 in1=x1[:, :], op0=ALU.add, op1=ALU.add).then_inc(round_done.sem, 1)


L1_HEADS, L1_INTER = 8, 512
L1A = Fields(("wq", L1_HEADS * P), ("wk", L1_HEADS * P), ("wv", L1_HEADS * P), ("wo", L1_HEADS * P),
             ("gate", L1_INTER), ("up", L1_INTER), ("down", L1_INTER),
             ("attn_norm", 1), ("out_norm", 1), ("mlp_norm", 1))


def l1_attn_layout(np, i):
    g = lambda k: i["L1_attn_" + k]
    return {"l1a": pack(np, [
        g("Wq"), g("Wk"), g("Wv"), blocks(np, g("Wo")), g("Wgate"), g("Wup"), blocks(np, g("Wdown")),
        column(g("attn_norm_w")), column(g("attn_out_norm_w")), column(g("mlp_norm_w"))])}


LAYOUTS.append(l1_attn_layout)


def l1_attn_phase(core):
    nc, psum = core.nc, core.psum
    H, F = L1_HEADS, L1_INTER // P
    Q, K, S, O, Y, V = 0, 1, 2, 4, 6, 7
    with Phase(core, "l1a") as ph:
        w = ph.buf("w", L1A.width)
        col = lambda name: L1A.of(w, name)
        h_t = ph.buf("h", N)
        v = ph.buf("v", CH, H * P)
        q = ph.buf("q", 2, N)
        k = ph.buf("k", 2, N)
        scores = ph.buf("scores", 2, CH, N)
        normed = ph.buf("normed", 2, N)
        out_sq, out_log, out_rstd = ph.buf("out_sq", N), ph.buf("out_log", N), ph.buf("out_rstd", N)
        x1 = ph.buf("x1", N)
        silu = ph.buf("silu", F, N)
        hidden = ph.buf("hidden", F, N)

        passed = ph.semaphore("passed")
        w_in = ph.semaphore("w_in")
        round_done = ph.semaphore("round_done")
        norm = ColumnNorm(ph, "norm", V, V, centre=False, per_round=2)
        h_ready = ph.semaphore("h_ready", 2)
        v_ready = ph.semaphore("v_ready", 2 * CH)
        v_kept = ph.semaphore("v_kept", 2 * CH)
        q_ready, q_kept = ph.semaphore("q_ready", H), ph.semaphore("q_kept", H)
        k_ready, k_kept = ph.semaphore("k_ready", H), ph.semaphore("k_kept", H)
        scores_ready = ph.semaphore("scores_ready", H * CH)
        scores_kept = ph.semaphore("scores_kept", H * CH)
        out_ready = ph.semaphore("out_ready", H)
        out_sq_ready = ph.semaphore("out_sq_ready", H)
        out_var_ready = ph.semaphore("out_var_ready", H)
        out_log_ready = ph.semaphore("out_log_ready", H)
        out_rstd_ready = ph.semaphore("out_rstd_ready", H)
        normed_ready = ph.semaphore("normed_ready", H)
        y_ready = ph.semaphore("y_ready", 2)
        x1_ready = ph.semaphore("x1_ready")
        gate_ready, silu_ready = ph.semaphore("gate_ready", F), ph.semaphore("silu_ready", F)
        up_ready, hidden_ready = ph.semaphore("up_ready", F), ph.semaphore("hidden_ready", F)

        with nc.Block() as block:
            @block.sync
            def _(sp):
                sp.dma_start(w[:, :], core.dram["l1a"]).then_inc(w_in.sem, 16)

            @block.tensor
            def _(pe):
                pe.wait_ge(w_in.sem, 16)
                with pe.Fori(0, B) as b:
                    pe.wait_ge(round_done.sem, round_done.at(b))
                    norm.tensor(pe, b, None, 0)
                    pe.wait_ge(h_ready.sem, h_ready.at(b, 0))
                    for c in range(CH):
                        for half in range(2):
                            n = 2 * c + half
                            if n >= 4:
                                pe.wait_ge(v_kept.sem, v_kept.at(b, n - 4))
                            pe.matmul(psum[:, n % 4, :], h_t[:, c * P:(c + 1) * P],
                                      L1A.of(w, "wv", half, N), start=True, stop=True)\
                              .then_inc(v_ready.sem, 1)
                    pe.wait_ge(v_kept.sem, v_kept.at(b, 2 * CH - 1))

                    def query_key(h):
                        if h >= 1:
                            pe.wait_ge(q_kept.sem, q_kept.at(b, h - 1))
                            pe.wait_ge(k_kept.sem, k_kept.at(b, h - 1))
                        pe.matmul(psum[:, Q, :], L1A.of(w, "wq", h, P), h_t[:, :], start=True, stop=True)\
                          .then_inc(q_ready.sem, 1)
                        pe.matmul(psum[:, K, :], L1A.of(w, "wk", h, P), h_t[:, :], start=True, stop=True)\
                          .then_inc(k_ready.sem, 1)

                    def score(h, c):
                        n = h * CH + c
                        if n >= 2:
                            pe.wait_ge(scores_kept.sem, scores_kept.at(b, n - 2))
                        pe.matmul(psum[:, S + c % 2, 0:N - c * P], k[:, h % 2, c * P:(c + 1) * P],
                                  q[:, h % 2, c * P:N], start=True, stop=True).then_inc(scores_ready.sem, 1)

                    def output(h):
                        for c in range(CH):
                            pe.wait_ge(scores_kept.sem, scores_kept.at(b, h * CH + c))
                            mm = pe.matmul(psum[:, O + h % 2, c * P:N], v[:, c, h * P:(h + 1) * P],
                                           scores[:, h % 2, c, 0:N - c * P], start=(c == 0), stop=(c == CH - 1))
                        mm.then_inc(out_ready.sem, 1)

                    def out_var(h):
                        pe.wait_ge(out_sq_ready.sem, out_sq_ready.at(b, h))
                        pe.matmul(psum[:, V, :], core.c("mean"), out_sq[:, :], start=True, stop=True)\
                          .then_inc(out_var_ready.sem, 1)

                    def project(h):
                        pe.wait_ge(normed_ready.sem, normed_ready.at(b, h))
                        mm = pe.matmul(psum[:, Y, :], L1A.of(w, "wo", h, P), normed[:, h % 2, :],
                                       start=(h == 0), stop=(h == H - 1))
                        if h == H - 1:
                            mm.then_inc(y_ready.sem, 1)

                    query_key(0)
                    for h in range(H):
                        pe.wait_ge(q_kept.sem, q_kept.at(b, h))
                        pe.wait_ge(k_kept.sem, k_kept.at(b, h))
                        score(h, 0)
                        score(h, 1)
                        if h + 1 < H:
                            query_key(h + 1)
                        score(h, 2)
                        score(h, 3)
                        if h >= 1:
                            out_var(h - 1)
                        output(h)
                        if h >= 1:
                            project(h - 1)
                    out_var(H - 1)
                    project(H - 1)

                    norm.tensor(pe, b, None, 1)
                    pe.wait_ge(h_ready.sem, h_ready.at(b, 1))
                    for f in range(F):
                        if f >= 1:
                            pe.wait_ge(silu_ready.sem, silu_ready.at(b, f - 1))
                            pe.wait_ge(hidden_ready.sem, hidden_ready.at(b, f - 1))
                        pe.matmul(psum[:, Q, :], L1A.of(w, "gate", f, P), h_t[:, :], start=True, stop=True)\
                          .then_inc(gate_ready.sem, 1)
                        pe.matmul(psum[:, K, :], L1A.of(w, "up", f, P), h_t[:, :], start=True, stop=True)\
                          .then_inc(up_ready.sem, 1)
                    for f in range(F):
                        pe.wait_ge(hidden_ready.sem, hidden_ready.at(b, f))
                        mm = pe.matmul(psum[:, Y, :], L1A.of(w, "down", f, P), hidden[:, f, :],
                                       start=(f == 0), stop=(f == F - 1))
                    mm.then_inc(y_ready.sem, 1)

            @block.scalar
            def _(act):
                with act.Fori(0, B) as b:
                    act.wait_ge(round_done.sem, round_done.at(b))
                    apart(act, passed)
                    act.preload_act_table_set(EXP_LN_SET)
                    norm.scalar(act, b, core.xn[:, cols(b)], 0)
                    for n in range(2 * CH):
                        act.wait_ge(v_ready.sem, v_ready.at(b, n))
                        act.copy(v[:, n // 2, (n % 2) * N:(n % 2 + 1) * N], psum[:, n % 4, :])\
                           .then_inc(v_kept.sem, 1)

                    def keep(h):
                        act.wait_ge(q_ready.sem, q_ready.at(b, h))
                        act.copy(q[:, h % 2, :], psum[:, Q, :]).then_inc(q_kept.sem, 1)
                        act.wait_ge(k_ready.sem, k_ready.at(b, h))
                        act.copy(k[:, h % 2, :], psum[:, K, :]).then_inc(k_kept.sem, 1)

                    def out_norm(h):
                        act.wait_ge(out_ready.sem, out_ready.at(b, h))
                        if h >= 1:
                            act.wait_ge(normed_ready.sem, normed_ready.at(b, h - 1))
                        act.activation(out_sq[:, :], psum[:, O + h % 2, :], ACT.Square)\
                           .then_inc(out_sq_ready.sem, 1)
                        act.wait_ge(out_var_ready.sem, out_var_ready.at(b, h))
                        act.activation(out_log[:, :], psum[:, V, :], ACT.Ln, bias=core.c("eps5"))\
                           .then_inc(out_log_ready.sem, 1)
                        act.wait_ge(out_log_ready.sem, out_log_ready.at(b, h))
                        act.activation(out_rstd[:, :], out_log[:, :], ACT.Exp, scale=-0.5)\
                           .then_inc(out_rstd_ready.sem, 1)

                    keep(0)
                    for h in range(H):
                        if h + 1 < H:
                            keep(h + 1)
                        out_norm(h)
                    act.wait_ge(x1_ready.sem, x1_ready.at(b))
                    norm.scalar(act, b, x1[:, :], 1)
                    for f in range(F):
                        act.wait_ge(gate_ready.sem, gate_ready.at(b, f))
                        act.activation(silu[:, f, :], psum[:, Q, :], ACT.Silu).then_inc(silu_ready.sem, 1)

            @block.vector
            def _(dve):
                dve.sem_inc(round_done.sem, 1)
                dve.wait_ge(w_in.sem, 16)
                with dve.Fori(0, B) as b:
                    dve.wait_ge(norm.rstd_ready.sem, norm.rstd_ready.at(b, 0))
                    dve.scalar_tensor_tensor(out=h_t[:, :], in0=core.xn[:, cols(b)], scalar=col("attn_norm"),
                                             in1=norm.rstd[:, :], op0=ALU.mult, op1=ALU.mult)\
                       .then_inc(h_ready.sem, 1)

                    def mask(h):
                        for c in range(CH):
                            dve.wait_ge(scores_ready.sem, scores_ready.at(b, h * CH + c))
                            dve.tensor_tensor(scores[:, h % 2, c, 0:N - c * P], psum[:, S + c % 2, 0:N - c * P],
                                              core.c("causal")[:, 0:N - c * P], ALU.mult)\
                               .then_inc(scores_kept.sem, 1)

                    def apply_norm(h):
                        dve.wait_ge(out_rstd_ready.sem, out_rstd_ready.at(b, h))
                        dve.scalar_tensor_tensor(out=normed[:, h % 2, :], in0=psum[:, O + h % 2, :],
                                                 scalar=col("out_norm"), in1=out_rstd[:, :],
                                                 op0=ALU.mult, op1=ALU.mult).then_inc(normed_ready.sem, 1)

                    for h in range(H):
                        mask(h)
                        if h >= 1:
                            apply_norm(h - 1)
                    apply_norm(H - 1)
                    dve.wait_ge(y_ready.sem, y_ready.at(b, 0))
                    dve.tensor_tensor(x1[:, :], core.xn[:, cols(b)], psum[:, Y, :], ALU.add)\
                       .then_inc(x1_ready.sem, 1)
                    dve.wait_ge(norm.rstd_ready.sem, norm.rstd_ready.at(b, 1))
                    dve.scalar_tensor_tensor(out=h_t[:, :], in0=x1[:, :], scalar=col("mlp_norm"),
                                             in1=norm.rstd[:, :], op0=ALU.mult, op1=ALU.mult)\
                       .then_inc(h_ready.sem, 1)
                    for f in range(F):
                        dve.wait_ge(silu_ready.sem, silu_ready.at(b, f))
                        dve.wait_ge(up_ready.sem, up_ready.at(b, f))
                        dve.tensor_tensor(hidden[:, f, :], silu[:, f, :], psum[:, K, :], ALU.mult)\
                           .then_inc(hidden_ready.sem, 1)
                    dve.wait_ge(y_ready.sem, y_ready.at(b, 1))
                    dve.tensor_tensor(core.s[:, cols(b)], x1[:, :], psum[:, Y, :], ALU.add)\
                       .then_inc(round_done.sem, 1)


L1_EXPERTS, L1_SLOTS = 64, 32
L1_E = L1_EXPERTS * L1_SLOTS
ET = L1_E // P
PIECE = Fields(("w", 16 * P), ("bias", 4 * P))


def l1_ffn_layout(np, i):
    g = lambda k: i["L1_ffn_" + k]
    pieces = []
    for n in range(4):
        w = g("expert_w")[16 * n:16 * n + 16].transpose(1, 0, 2).reshape(P, 16 * P)
        bias = np.repeat(g("expert_b")[16 * n:16 * n + 16], L1_SLOTS, axis=0)
        pieces.append(pack(np, [w, blocks(np, bias)]))
    return {"l1f_phi": g("phi_w").T, "l1f_phi_b": np.tile(g("phi_b"), (P, 1)), "l1f_experts": np.stack(pieces)}


LAYOUTS.append(l1_ffn_layout)


def l1_ffn_phase(core):
    with ExitStack() as ctx:
        combine = ctx.enter_context(core.nc.sbuf_tensor("l1f_combine", [P, ET, T], F32))
        l1_route_phase(core, combine)
        l1_expert_phase(core, combine)


def l1_route_phase(core, combine):
    nc, psum = core.nc, core.psum
    NT = T // P
    LOGIT, TURN = 4, 6
    with Phase(core, "l1r") as ph:
        phi = ph.buf("phi", L1_E)
        phi_b = ph.buf("phi_b", L1_E)
        logit = ph.buf("logit", L1_E)
        dispatch = ph.buf("dispatch", L1_E)
        combine_tok = core.g
        x_t, x_tok = ph.buf("x_t", P), ph.buf("x_tok", P)
        nmax_e = ph.buf("max_e", L1_EXPERTS)
        nmax_s = ph.buf("max_s", L1_SLOTS)
        sum_e, rsum_e = ph.buf("sum_e", L1_EXPERTS), ph.buf("rsum_e", L1_EXPERTS)
        sum_s, rsum_s = ph.buf("sum_s", L1_SLOTS), ph.buf("rsum_s", P)
        rsum_t = ph.buf("rsum_t", P)

        w_in, zeroed = ph.semaphore("w_in"), ph.semaphore("zeroed")
        round_done = ph.semaphore("round_done")
        x_t_ready, x_turned, x_tok_ready = ph.semaphore("x_t_ready"), ph.semaphore("x_turned"), ph.semaphore("x_tok_ready")
        logit_ready, logit_kept = ph.semaphore("logit_ready", 4), ph.semaphore("logit_kept", 4)
        max_ready = ph.semaphore("max_ready", 2)
        shifted_ready, exp_ready = ph.semaphore("shifted_ready", 2), ph.semaphore("exp_ready", 2)
        sum_ready, rsum_ready = ph.semaphore("sum_ready", 2), ph.semaphore("rsum_ready", 2)
        dispatch_ready, summed = ph.semaphore("dispatch_ready"), ph.semaphore("summed")
        rsum_turned, rsum_t_ready = ph.semaphore("rsum_turned"), ph.semaphore("rsum_t_ready")
        turned, turned_kept = ph.semaphore("turned", 4), ph.semaphore("turned_kept", 4)

        by_expert = lambda a: a.rearrange("p (n s) -> p n s", s=L1_SLOTS)
        by_slot = lambda a: a.rearrange("p (n s) -> p s n", s=L1_SLOTS)

        with nc.Block() as block:
            @block.sync
            def _(sp):
                sp.dma_start(phi[:, :], core.dram["l1f_phi"]).then_inc(w_in.sem, 16)
                sp.dma_start(phi_b[:, :], core.dram["l1f_phi_b"]).then_inc(w_in.sem, 16)

            @block.tensor
            def _(pe):
                pe.wait_ge(w_in.sem, 32)
                pe.wait_ge(zeroed.sem, 1)
                for n in range(4):
                    pe.matmul(psum[:, n, :], x_tok[:, :], phi[:, n * N:(n + 1) * N],
                              start=True, stop=False, skip_group_check=True)
                with pe.Fori(0, NT) as t:
                    pe.wait_ge(round_done.sem, round_done.at(t))
                    pe.wait_ge(x_t_ready.sem, x_t_ready.at(t))
                    for n in range(4):
                        if n >= 2:
                            pe.wait_ge(logit_kept.sem, logit_kept.at(t, n - 2))
                        pe.matmul(psum[:, LOGIT + n % 2, :], x_t[:, :], phi[:, n * N:(n + 1) * N],
                                  start=True, stop=True).then_inc(logit_ready.sem, 1)
                    pe.transpose(psum[:, TURN, 0:P], x_t[:, :], core.c("ident")).then_inc(x_turned.sem, 1)
                    pe.wait_ge(x_tok_ready.sem, x_tok_ready.at(t))
                    pe.wait_ge(dispatch_ready.sem, dispatch_ready.at(t))
                    for n in range(4):
                        mm = pe.matmul(psum[:, n, :], x_tok[:, :], dispatch[:, n * N:(n + 1) * N],
                                       start=False, stop=False, skip_group_check=True)
                    mm.then_inc(summed.sem, 1)
                    pe.wait_ge(rsum_ready.sem, rsum_ready.at(t, 1))
                    pe.transpose(psum[:, TURN, 0:P], rsum_s[:, :], core.c("ident")).then_inc(rsum_turned.sem, 1)
                    pe.wait_ge(exp_ready.sem, exp_ready.at(t, 1))
                    for n in range(4):
                        if n == 1:
                            pe.wait_ge(rsum_t_ready.sem, rsum_t_ready.at(t))
                        if n >= 2:
                            pe.wait_ge(turned_kept.sem, turned_kept.at(t, n - 2))
                        for i in range(4):
                            e = 4 * n + i
                            mm = pe.transpose(psum[:, TURN + (n + 1) % 2, i * P:(i + 1) * P],
                                              combine_tok[:, e * P:(e + 1) * P], core.c("ident"))
                        mm.then_inc(turned.sem, 1)

            @block.gpsimd
            def _(pool):
                with pool.Fori(0, NT) as t:
                    pool.wait_ge(round_done.sem, round_done.at(t))
                    pool.wait_ge(max_ready.sem, max_ready.at(t, 0))
                    pool.tensor_tensor(by_expert(dispatch[:, :]), by_expert(logit[:, :]),
                                       nmax_e[:, :].unsqueeze(2).to_broadcast([P, L1_EXPERTS, L1_SLOTS]),
                                       ALU.subtract).then_inc(shifted_ready.sem, 1)
                    pool.wait_ge(max_ready.sem, max_ready.at(t, 1))
                    pool.tensor_tensor(by_expert(combine_tok[:, :]), by_expert(logit[:, :]),
                                       nmax_s[:, :].unsqueeze(1).to_broadcast([P, L1_EXPERTS, L1_SLOTS]),
                                       ALU.subtract).then_inc(shifted_ready.sem, 1)

            @block.scalar
            def _(act):
                with act.Fori(0, NT) as t:
                    act.wait_ge(round_done.sem, round_done.at(t))
                    act.copy(x_t[:, :], core.xn[:, cols(t, P)]).then_inc(x_t_ready.sem, 1)
                    act.wait_ge(x_turned.sem, x_turned.at(t))
                    act.copy(x_tok[:, :], psum[:, TURN, 0:P]).then_inc(x_tok_ready.sem, 1)
                    for k, buf in enumerate((dispatch, combine_tok)):
                        act.wait_ge(shifted_ready.sem, shifted_ready.at(t, k))
                        act.activation(buf[:, :], buf[:, :], ACT.Exp).then_inc(exp_ready.sem, 1)

            @block.vector
            def _(dve):
                dve.sem_inc(round_done.sem, 1)
                dve.memset(x_tok[:, :], 0.0).then_inc(zeroed.sem, 1)
                dve.wait_ge(w_in.sem, 32)
                with dve.Fori(0, NT) as t:
                    for n in range(4):
                        dve.wait_ge(logit_ready.sem, logit_ready.at(t, n))
                        dve.tensor_tensor(logit[:, n * N:(n + 1) * N], psum[:, LOGIT + n % 2, :],
                                          phi_b[:, n * N:(n + 1) * N], ALU.add).then_inc(logit_kept.sem, 1)
                    dve.wait_ge(logit_kept.sem, logit_kept.at(t, 3))
                    dve.tensor_reduce(nmax_e[:, :], by_expert(logit[:, :]), AX.X, ALU.max).then_inc(max_ready.sem, 1)
                    dve.tensor_reduce(nmax_s[:, :], by_slot(logit[:, :]), AX.X, ALU.max).then_inc(max_ready.sem, 1)
                    dve.wait_ge(exp_ready.sem, exp_ready.at(t, 0))
                    dve.tensor_reduce(sum_e[:, :], by_expert(dispatch[:, :]), AX.X, ALU.add).then_inc(sum_ready.sem, 1)
                    dve.wait_ge(sum_ready.sem, sum_ready.at(t, 0))
                    dve.reciprocal(rsum_e[:, :], sum_e[:, :]).then_inc(rsum_ready.sem, 1)
                    dve.wait_ge(rsum_ready.sem, rsum_ready.at(t, 0))
                    dve.tensor_tensor(by_expert(dispatch[:, :]), by_expert(dispatch[:, :]),
                                      rsum_e[:, :].unsqueeze(2).to_broadcast([P, L1_EXPERTS, L1_SLOTS]), ALU.mult)\
                       .then_inc(dispatch_ready.sem, 1)
                    dve.wait_ge(exp_ready.sem, exp_ready.at(t, 1))
                    dve.tensor_reduce(sum_s[:, :], by_slot(combine_tok[:, :]), AX.X, ALU.add)\
                       .then_inc(sum_ready.sem, 1)
                    dve.wait_ge(sum_ready.sem, sum_ready.at(t, 1))
                    dve.reciprocal(rsum_s[:, :].rearrange("p (j s) -> p j s", j=4),
                                   sum_s[:, :].unsqueeze(1).to_broadcast([P, 4, L1_SLOTS]))\
                       .then_inc(rsum_ready.sem, 1)
                    dve.wait_ge(rsum_turned.sem, rsum_turned.at(t))
                    dve.tensor_copy(rsum_t[:, :], psum[:, TURN, 0:P]).then_inc(rsum_t_ready.sem, 1)
                    dve.wait_ge(rsum_t_ready.sem, rsum_t_ready.at(t))
                    for n in range(4):
                        dve.wait_ge(turned.sem, turned.at(t, n))
                        keep = dve.tensor_tensor(combine[:, 4 * n:4 * n + 4, cols(t, P)],
                                                 psum[:, TURN + (n + 1) % 2, :].rearrange("p (i q) -> p i q", i=4),
                                                 rsum_t[:, :].unsqueeze(1).to_broadcast([P, 4, P]), ALU.mult)
                        keep.then_inc(turned_kept.sem, 1)
                    dve.wait_ge(turned_kept.sem, turned_kept.at(t, 3))
                    dve.wait_ge(summed.sem, summed.at(t))
                    dve.sem_inc(round_done.sem, 1)


def l1_expert_phase(core, combine):
    nc, psum = core.nc, core.psum
    with Phase(core, "l1e") as ph:
        piece = ph.buf("piece", 2, PIECE.width)
        slots = core.g
        out = ph.buf("slots_out", ET, P)
        pieces_in = [ph.semaphore("pieces_in_even"), ph.semaphore("pieces_in_odd")]
        clipped, normed, slots_ready = ph.semaphore("clipped"), ph.semaphore("normed"), ph.semaphore("slots_ready")
        out_ready, out_kept = ph.semaphore("out_ready"), ph.semaphore("out_kept")
        y_ready, y_kept = ph.semaphore("y_ready"), ph.semaphore("y_kept")
        norm = ColumnNorm(ph, "norm", 4, 5)
        quarter = [slice(n * N, (n + 1) * N) for n in range(4)]

        with nc.Block() as block:
            @block.sync
            def _(sp):
                for n in range(4):
                    if n >= 2:
                        sp.wait_ge(out_ready.sem, out_ready.at(n - 2))
                        sp.wait_ge(out_kept.sem, out_kept.at(n - 2))
                    sp.dma_start(piece[:, n % 2, :], core.dram["l1f_experts"][n]).then_inc(pieces_in[n % 2].sem, 16)

            @block.tensor
            def _(pe):
                for n in range(4):
                    pe.wait_ge(clipped.sem, clipped.at(n))
                    if n:
                        pe.wait_ge(norm.rstd_ready.sem, norm.rstd_ready.at(n - 1))
                    norm.tensor(pe, n, slots[:, quarter[n]])
                pe.wait_ge(slots_ready.sem, slots_ready.at(3))
                for n in range(4):
                    pe.wait_ge(pieces_in[n % 2].sem, 16 * (n // 2) + 16)
                    w = piece[:, n % 2, :]
                    for i in range(4):
                        for j in range(4):
                            expert = 4 * i + j
                            first = (16 * n + expert) * L1_SLOTS
                            mm = pe.matmul(psum[32 * j:32 * j + 32, n, i * P:(i + 1) * P],
                                           slots[:, first:first + L1_SLOTS], PIECE.of(w, "w", expert, P),
                                           start=(i == 0), stop=(i == 3), skip_group_check=True)
                    mm.then_inc(out_ready.sem, 1)
                for b in range(B):
                    pe.wait_ge(out_kept.sem, out_kept.at(3))
                    for e in range(ET):
                        mm = pe.matmul(psum[:, 4 + b, :], out[:, e, :], combine[:, e, b * N:(b + 1) * N],
                                       start=(e == 0), stop=(e == ET - 1))
                    mm.then_inc(y_ready.sem, 1)

            @block.scalar
            def _(act):
                act.preload_act_table_set(EXP_LN_SET)
                for n in range(4):
                    if n:
                        act.wait_ge(normed.sem, normed.at(n - 1))
                    norm.scalar(act, n)
                for n in range(4):
                    act.wait_ge(normed.sem, normed.at(n))
                    act.activation(slots[:, quarter[n]], slots[:, quarter[n]], ACT.Tanh).then_inc(slots_ready.sem, 1)

            @block.vector
            def _(dve):
                for n in range(4):
                    dve.tensor_scalar(slots[:, quarter[n]], psum[:, n, :], -33000.0, 65000.0, ALU.max, ALU.min)\
                       .then_inc(clipped.sem, 1)
                    dve.wait_ge(clipped.sem, clipped.at(n))
                    norm.vector(dve, n, slots[:, quarter[n]])
                    dve.wait_ge(norm.rstd_ready.sem, norm.rstd_ready.at(n))
                    dve.tensor_tensor(slots[:, quarter[n]], norm.centred[:, :], norm.rstd[:, :], ALU.mult)\
                       .then_inc(normed.sem, 1)
                for n in range(4):
                    dve.wait_ge(out_ready.sem, out_ready.at(n))
                    dve.tensor_tensor(out[:, 4 * n:4 * n + 4, :],
                                      psum[:, n, :].rearrange("p (i h) -> p i h", i=4),
                                      PIECE.of(piece[:, n % 2, :], "bias").rearrange("p (i h) -> p i h", i=4),
                                      ALU.add).then_inc(out_kept.sem, 1)
                for b in range(B):
                    dve.wait_ge(y_ready.sem, y_ready.at(b))
                    dve.tensor_copy(core.g[:, b * N:(b + 1) * N], psum[:, 4 + b, :]).then_inc(y_kept.sem, 1)


L2_SSM = 64
L2_GATES = 3
L2A = Fields(("wb", P), ("wih", 3 * P), ("wd", P), ("wa", P), ("wc", P), ("whh", 3 * P), ("proj", P),
             ("gate", 2 * P), ("bb", 1), ("cb", 1), ("db", 1), ("bih", 3), ("bhh", 3), ("pb", 1), ("gb", 2))


def l2_attn_layout(np, i):
    g = lambda k: i["L2_attn_" + k]
    bw = np.zeros((P, P), np.float32)
    bw[:, :L2_SSM] = g("Bw").T
    a = np.zeros((L2_SSM, P), np.float32)
    a[:, :L2_SSM] = g("A").T
    gate = np.repeat(g("gate_w")[:, :, None], P, axis=2)
    return {"l2a": pack(np, [
        bw, g("W_ih").T, g("Dw").T, a, g("Cw").T, g("W_hh").T, g("proj_w").T, gate[0], gate[1],
        column(g("Bb")), column(g("Cb")), column(g("Db")), g("b_ih").reshape(3, P).T, g("b_hh").reshape(3, P).T,
        column(g("proj_b")), np.tile(g("gate_b"), (P, 1))])}


LAYOUTS.append(l2_attn_layout)


def l2_attn_phase(core):
    with ExitStack() as ctx:
        sb = lambda name, *shape: ctx.enter_context(core.nc.sbuf_tensor("l2a_" + name, [P, *shape], F32))
        w = sb("w", L2A.width)
        drive = sb("drive", N + 32, 4, B)
        trail_h = sb("trail_h", N, B)
        trail_s = sb("trail_s", N, B)
        l2_drive_phase(core, w, drive)
        l2_scan_phase(core, w, drive, trail_h, trail_s)
        l2_output_phase(core, w, trail_h, trail_s)


def l2_drive_phase(core, w, drive):
    nc, psum = core.nc, core.psum
    with Phase(core, "l2d") as ph:
        w_in, made, kept = ph.semaphore("w_in"), ph.semaphore("made"), ph.semaphore("kept")
        col = lambda name, k=0: L2A.of(w, name, k, 1)
        with nc.Block() as block:
            @block.sync
            def _(sp):
                sp.dma_start(w[:, :], core.dram["l2a"]).then_inc(w_in.sem, 16)

            @block.tensor
            def _(pe):
                pe.wait_ge(w_in.sem, 16)
                for n in range(4 * B):
                    part, b = n // B, n % B
                    if n >= 8:
                        pe.wait_ge(kept.sem, kept.at(n - 8))
                    lhs = L2A.of(w, "wih", part, P) if part < 3 else L2A.of(w, "wb")
                    pe.matmul(psum[:, n % 8, :], lhs, core.xn[:, b * N:(b + 1) * N], start=True, stop=True)\
                      .then_inc(made.sem, 1)

            @block.vector
            def _(dve):
                dve.memset(drive[:, N:, :, :], 0.0)
                dve.wait_ge(w_in.sem, 16)
                for n in range(4 * B):
                    part, b = n // B, n % B
                    dve.wait_ge(made.sem, made.at(n))
                    if part < 2:
                        biases = (col("bih", part), col("bhh", part), ALU.add, ALU.add)
                    else:
                        biases = (col("bih", 2) if part == 2 else col("bb"), None, ALU.add)
                    dve.tensor_scalar(drive[:, 0:N, part, b], psum[:, n % 8, :], *biases).then_inc(kept.sem, 1)


def l2_scan_phase(core, w, drive, trail_h, trail_s):
    nc, psum = core.nc, core.psum
    U, S = 16, L2_SSM
    R, NB, Z, SB = 0, 1, 2, 3
    with Phase(core, "l2s") as ph:
        now = ph.buf("now", 2, U, 4, B)
        h = ph.buf("h", 2, U, B)
        s = ph.buf("s", 2, U, B)
        r_in, r = ph.buf("r_in", B), ph.buf("r", B)
        z_in, z, not_z = ph.buf("z_in", B), ph.buf("z", B), ph.buf("not_z", B)
        rn, n_in, n = ph.buf("rn", B), ph.buf("n_in", B), ph.buf("n", B)
        zh, zn = ph.buf("zh", B), ph.buf("zn", B)
        s_in, s_sig = ph.buf("s_in", B), ph.buf("s_sig", B)
        col = lambda name, k=0: L2A.of(w, name, k, 1)

        K = 2 * U
        zeroed = ph.semaphore("zeroed", 2)
        now_ready, moved = ph.semaphore("now_ready", 2), ph.semaphore("moved", 4)
        r_raw, n_raw, z_raw, s_raw = (ph.semaphore(x, K) for x in ("r_raw", "n_raw", "z_raw", "s_raw"))
        r_in_ready, r_ready = ph.semaphore("r_in_ready", K), ph.semaphore("r_ready", K)
        z_in_ready, z_ready, not_z_ready = ph.semaphore("z_in_ready", K), ph.semaphore("z_ready", K), ph.semaphore("not_z_ready", K)
        rn_ready, n_in_ready, n_ready = ph.semaphore("rn_ready", K), ph.semaphore("n_in_ready", K), ph.semaphore("n_ready", K)
        zh_ready, zn_ready = ph.semaphore("zh_ready", K), ph.semaphore("zn_ready", K)
        h_ready = ph.semaphore("h_ready", K)
        s_in_ready, s_sig_ready, s_ready = ph.semaphore("s_in_ready", K), ph.semaphore("s_sig_ready", K), ph.semaphore("s_ready", K)
        ROUNDS = N // K

        def before(buf, i):
            j = (i - 1) % K
            return buf[:, j // U, j % U, :]

        def at(buf, i):
            return buf[:, i // U, i % U, :]

        with nc.Block() as block:
            @block.gpsimd
            def _(pool):
                pool.sem_inc(moved.sem, 4)
                pool.memset(h[:, 1, U - 1, :], 0.0).then_inc(zeroed.sem, 1)
                pool.memset(s[:, 1, U - 1, :], 0.0).then_inc(zeroed.sem, 1)
                for half in range(2):
                    pool.tensor_copy(now[:, half, :, :, :], drive[:, half * U:(half + 1) * U, :, :])\
                        .then_inc(now_ready.sem, 1)
                with pool.Fori(0, ROUNDS) as k:
                    for half in range(2):
                        pool.wait_ge(h_ready.sem, h_ready.at(k, half * U + U))
                        pool.wait_ge(s_ready.sem, s_ready.at(k, half * U + U))
                        pool.tensor_copy(trail_h[:, bass.ds(k * K + half * U, U), :], h[:, half, :, :])\
                            .then_inc(moved.sem, 1)
                        pool.tensor_copy(trail_s[0:S, bass.ds(k * K + half * U, U), :], s[0:S, half, :, :])\
                            .then_inc(moved.sem, 1)
                        pool.tensor_copy(now[:, half, :, :, :], drive[:, bass.ds(k * K + K + half * U, U), :, :])\
                            .then_inc(now_ready.sem, 1)

            @block.tensor
            def _(pe):
                pe.wait_ge(zeroed.sem, 2)
                with pe.Fori(0, ROUNDS) as k:
                    for i in range(K):
                        pe.wait_ge(h_ready.sem, h_ready.at(k, i))
                        for bank, gate, raw in ((R, 0, r_raw), (NB, 2, n_raw), (Z, 1, z_raw)):
                            pe.matmul(psum[:, bank, 0:B], L2A.of(w, "whh", gate, P), before(h, i),
                                      start=True, stop=True).then_inc(raw.sem, 1)
                        pe.wait_ge(s_ready.sem, s_ready.at(k, i))
                        pe.matmul(psum[:, SB, 0:B], L2A.of(w, "wa")[0:S, :], before(s, i)[0:S, :],
                                  start=True, stop=True).then_inc(s_raw.sem, 1)

            @block.scalar
            def _(act):
                act.preload_act_table_set("sigmoid_and_others")
                with act.Fori(0, ROUNDS) as k:
                    for i in range(K):
                        act.wait_ge(r_in_ready.sem, r_in_ready.at(k, i))
                        act.activation(r[:, :], r_in[:, :], ACT.Sigmoid).then_inc(r_ready.sem, 1)
                        act.wait_ge(z_in_ready.sem, z_in_ready.at(k, i))
                        act.activation(z[:, :], z_in[:, :], ACT.Sigmoid).then_inc(z_ready.sem, 1)
                        act.wait_ge(n_in_ready.sem, n_in_ready.at(k, i))
                        act.activation(n[:, :], n_in[:, :], ACT.Tanh).then_inc(n_ready.sem, 1)
                        act.wait_ge(s_in_ready.sem, s_in_ready.at(k, i))
                        act.activation(s_sig[0:S, :], s_in[0:S, :], ACT.Sigmoid).then_inc(s_sig_ready.sem, 1)

            @block.vector
            def _(dve):
                dve.wait_ge(zeroed.sem, 2)
                dve.sem_inc(h_ready.sem, 1)
                dve.sem_inc(s_ready.sem, 1)
                with dve.Fori(0, ROUNDS) as k:
                    for i in range(K):
                        if i % U == 0:
                            dve.wait_ge(now_ready.sem, now_ready.at(k, i // U))
                            dve.wait_ge(moved.sem, k * 4 + (4 if i else 2))
                        drv = lambda part: now[:, i // U, i % U, part, :]
                        dve.wait_ge(r_raw.sem, r_raw.at(k, i))
                        dve.tensor_tensor(r_in[:, :], psum[:, R, 0:B], drv(0), ALU.add).then_inc(r_in_ready.sem, 1)
                        dve.wait_ge(r_ready.sem, r_ready.at(k, i))
                        dve.wait_ge(n_raw.sem, n_raw.at(k, i))
                        dve.scalar_tensor_tensor(out=rn[:, :], in0=psum[:, NB, 0:B], scalar=col("bhh", 2),
                                                 in1=r[:, :], op0=ALU.add, op1=ALU.mult).then_inc(rn_ready.sem, 1)
                        dve.wait_ge(rn_ready.sem, rn_ready.at(k, i))
                        dve.tensor_tensor(n_in[:, :], rn[:, :], drv(2), ALU.add).then_inc(n_in_ready.sem, 1)
                        dve.wait_ge(z_raw.sem, z_raw.at(k, i))
                        dve.tensor_tensor(z_in[:, :], psum[:, Z, 0:B], drv(1), ALU.add).then_inc(z_in_ready.sem, 1)
                        dve.wait_ge(s_raw.sem, s_raw.at(k, i))
                        dve.tensor_tensor(s_in[0:S, :], psum[0:S, SB, 0:B], drv(3)[0:S, :], ALU.add)\
                           .then_inc(s_in_ready.sem, 1)
                        dve.wait_ge(z_ready.sem, z_ready.at(k, i))
                        dve.tensor_scalar(not_z[:, :], z[:, :], -1.0, 1.0, ALU.mult, ALU.add)\
                           .then_inc(not_z_ready.sem, 1)
                        dve.tensor_tensor(zh[:, :], z[:, :], before(h, i), ALU.mult).then_inc(zh_ready.sem, 1)
                        dve.wait_ge(n_ready.sem, n_ready.at(k, i))
                        dve.wait_ge(not_z_ready.sem, not_z_ready.at(k, i))
                        dve.tensor_tensor(zn[:, :], not_z[:, :], n[:, :], ALU.mult).then_inc(zn_ready.sem, 1)
                        dve.wait_ge(zn_ready.sem, zn_ready.at(k, i))
                        dve.wait_ge(zh_ready.sem, zh_ready.at(k, i))
                        dve.tensor_tensor(at(h, i), zn[:, :], zh[:, :], ALU.add).then_inc(h_ready.sem, 1)
                        dve.wait_ge(s_sig_ready.sem, s_sig_ready.at(k, i))
                        dve.wait_ge(s_in_ready.sem, s_in_ready.at(k, i))
                        dve.tensor_tensor(at(s, i)[0:S, :], s_in[0:S, :], s_sig[0:S, :], ALU.mult)\
                           .then_inc(s_ready.sem, 1)


def l2_output_phase(core, w, trail_h, trail_s):
    nc, psum = core.nc, core.psum
    S = L2_SSM
    with Phase(core, "l2o") as ph:
        bias = ph.buf("bias", 1)
        gate, part = ph.buf("gate", 2, 2, N), ph.buf("part", 2, 2, N)
        bias_ready = ph.semaphore("bias_ready")
        gate_raw, gate_ready = ph.semaphore("gate_raw", 2), ph.semaphore("gate_ready", 2)
        y_ready, part_ready, out_ready = ph.semaphore("y_ready", 2), ph.semaphore("part_ready", 2), ph.semaphore("out_ready")
        col = lambda name, k=0: L2A.of(w, name, k, 1)
        with nc.Block() as block:
            @block.tensor
            def _(pe):
                for b in range(B):
                    x = core.xn[:, b * N:(b + 1) * N]
                    bank = 4 * (b % 2)
                    if b >= 2:
                        pe.wait_ge(part_ready.sem, part_ready.at(b - 2, 1))
                    for g in range(2):
                        pe.matmul(psum[:, bank + g, :], L2A.of(w, "gate", g, P), x, start=True, stop=True)\
                          .then_inc(gate_raw.sem, 1)
                    pe.matmul(psum[:, bank + 2, :], L2A.of(w, "wd"), x, start=True, stop=False)
                    pe.matmul(psum[:, bank + 2, :], L2A.of(w, "wc")[0:S, :], trail_s[0:S, :, b],
                              start=False, stop=True).then_inc(y_ready.sem, 1)
                    pe.matmul(psum[:, bank + 3, :], L2A.of(w, "proj"), trail_h[:, :, b], start=True, stop=True)\
                      .then_inc(y_ready.sem, 1)

            @block.scalar
            def _(act):
                for b in range(B):
                    if b >= 2:
                        act.wait_ge(part_ready.sem, part_ready.at(b - 2, 1))
                    for g in range(2):
                        act.wait_ge(gate_raw.sem, gate_raw.at(b, g))
                        act.activation(gate[:, b % 2, g, :], psum[:, 4 * (b % 2) + g, :], ACT.Sigmoid,
                                       bias=col("gb", g)).then_inc(gate_ready.sem, 1)

            @block.vector
            def _(dve):
                dve.tensor_tensor(bias[:, :], col("cb"), col("db"), ALU.add).then_inc(bias_ready.sem, 1)
                dve.wait_ge(bias_ready.sem, 1)
                for b in range(B):
                    if b >= 2:
                        dve.wait_ge(out_ready.sem, out_ready.at(b - 2))
                    for g in range(2):
                        dve.wait_ge(gate_ready.sem, gate_ready.at(b, g))
                        dve.wait_ge(y_ready.sem, y_ready.at(b, g))
                        dve.scalar_tensor_tensor(out=part[:, b % 2, g, :], in0=psum[:, 4 * (b % 2) + 2 + g, :],
                                                 scalar=col("pb") if g else bias[:, :], in1=gate[:, b % 2, g, :],
                                                 op0=ALU.add, op1=ALU.mult).then_inc(part_ready.sem, 1)
                    dve.wait_ge(part_ready.sem, part_ready.at(b, 1))
                    dve.tensor_tensor(core.s[:, b * N:(b + 1) * N], part[:, b % 2, 0, :], part[:, b % 2, 1, :],
                                      ALU.add).then_inc(out_ready.sem, 1)


L2_EXPERTS = 8
L2F = Fields(("gate", L2_EXPERTS), ("w1", L2_EXPERTS * P), ("w2", L2_EXPERTS * P), ("w3", L2_EXPERTS * P),
             ("b1", L2_EXPERTS), ("b2", L2_EXPERTS), ("b3", L2_EXPERTS), ("gb", 1))


def l2_ffn_layout(np, i):
    g = lambda k: i["L2_ffn_" + k]
    side = lambda w: w.transpose(1, 0, 2).reshape(P, L2_EXPERTS * P)
    return {"l2f": pack(np, [g("gate_w"), side(g("w1")), side(g("w2")), side(g("w3")),
                             g("b1").T, g("b2").T, g("b3").T, column(g("gate_b"))])}


LAYOUTS.append(l2_ffn_layout)


def l2_ffn_phase(core):
    with ExitStack() as ctx:
        sb = lambda name, *shape: ctx.enter_context(core.nc.sbuf_tensor("l2f_" + name, [P, *shape], F32))
        w = sb("w", L2F.width)
        table = sb("table", CONST_L2F.width)
        picked = sb("picked", T)
        weight = sb("weight", T)
        l2_pick_phase(core, w, table, picked, weight)
        l2_expert_phase(core, w, table, picked, weight)


def l2_pick_phase(core, w, table, picked, weight):
    nc, psum = core.nc, core.psum
    E, NT = L2_EXPERTS, T // P
    with Phase(core, "l2p") as ph:
        logit, prob = ph.buf("logit", T), ph.buf("prob", T)
        nmax, total, rtotal = ph.buf("nmax", B), ph.buf("total", B), ph.buf("rtotal", B)
        prob_tok, top = ph.buf("prob_tok", NT, E), ph.buf("top", NT, E)
        index = ph.buf("index", NT, E, dtype=U32)
        index_f = ph.buf("index_f", NT, 2)
        is_pick = ph.buf("is_pick", 2, NT, E)
        picked_tok = ph.buf("picked_tok", NT, E)
        w_in = ph.semaphore("w_in")
        logit_raw, logit_ready, nmax_ready = ph.semaphore("logit_raw"), ph.semaphore("logit_ready"), ph.semaphore("nmax_ready")
        exp_ready, rtotal_ready, prob_ready = ph.semaphore("exp_ready"), ph.semaphore("rtotal_ready"), ph.semaphore("prob_ready")
        turned, prob_tok_ready = ph.semaphore("turned"), ph.semaphore("prob_tok_ready")
        top_ready, index_ready, index_f_ready = ph.semaphore("top_ready"), ph.semaphore("index_ready"), ph.semaphore("index_f_ready")
        is_pick_ready, picked_tok_ready = ph.semaphore("is_pick_ready"), ph.semaphore("picked_tok_ready")
        back, picked_ready, weight_ready = ph.semaphore("back"), ph.semaphore("picked_ready"), ph.semaphore("weight_ready")
        batch = [slice(b * N, (b + 1) * N) for b in range(B)]
        with nc.Block() as block:
            @block.sync
            def _(sp):
                sp.dma_start(w[:, :], core.dram["l2f"]).then_inc(w_in.sem, 16)
                sp.dma_start(table[:, :], core.dram["const_l2f"]).then_inc(w_in.sem, 16)

            @block.tensor
            def _(pe):
                pe.wait_ge(w_in.sem, 32)
                for b in range(B):
                    pe.matmul(psum[0:E, b, :], L2F.of(w, "gate"), core.xn[:, batch[b]], start=True, stop=True)\
                      .then_inc(logit_raw.sem, 1)
                pe.wait_ge(prob_ready.sem, prob_ready.at(B - 1))
                for t in range(NT):
                    mm = pe.transpose(psum[:, 4, t * E:(t + 1) * E], prob[0:E, t * P:(t + 1) * P],
                                      core.c("ident")[0:E, 0:E])
                mm.then_inc(turned.sem, 1)
                pe.wait_ge(picked_tok_ready.sem, 1)
                for b in range(B):
                    for c in range(CH):
                        mm = pe.transpose(psum[0:E, b, c * P:(c + 1) * P], picked_tok[:, b * CH + c, :],
                                          core.c("ident"))
                    mm.then_inc(back.sem, 1)

            @block.scalar
            def _(act):
                for b in range(B):
                    act.wait_ge(nmax_ready.sem, nmax_ready.at(b))
                    act.activation(prob[0:E, batch[b]], logit[0:E, batch[b]], ACT.Exp, bias=nmax[0:E, b:b + 1],
                                   accum_out=total[0:E, b:b + 1]).then_inc(exp_ready.sem, 1)

            @block.vector
            def _(dve):
                dve.wait_ge(w_in.sem, 32)
                for b in range(B):
                    dve.wait_ge(logit_raw.sem, logit_raw.at(b))
                    dve.tensor_scalar(logit[0:E, batch[b]], psum[0:E, b, :], L2F.of(w, "gb")[0:E, :], None, ALU.add)\
                       .then_inc(logit_ready.sem, 1)
                    dve.wait_ge(logit_ready.sem, logit_ready.at(b))
                    dve.tensor_reduce(nmax[0:E, b:b + 1], logit[0:E, batch[b]], AX.X, ALU.max, negate=True)\
                       .then_inc(nmax_ready.sem, 1)
                for b in range(B):
                    dve.wait_ge(exp_ready.sem, exp_ready.at(b))
                    dve.reciprocal(rtotal[0:E, b:b + 1], total[0:E, b:b + 1]).then_inc(rtotal_ready.sem, 1)
                    dve.wait_ge(rtotal_ready.sem, rtotal_ready.at(b))
                    dve.tensor_scalar(prob[0:E, batch[b]], prob[0:E, batch[b]], rtotal[0:E, b:b + 1], None, ALU.mult)\
                       .then_inc(prob_ready.sem, 1)
                dve.wait_ge(turned.sem, 1)
                dve.tensor_copy(prob_tok[:, :, :], psum[:, 4, 0:NT * E].rearrange("p (t e) -> p t e", e=E))\
                   .then_inc(prob_tok_ready.sem, 1)
                dve.wait_ge(prob_tok_ready.sem, 1)
                for t in range(NT):
                    dve.max(top[:, t, :], prob_tok[:, t, :]).then_inc(top_ready.sem, 1)
                dve.wait_ge(top_ready.sem, top_ready.at(NT - 1))
                for t in range(NT):
                    dve.max_index(index[:, t, :], top[:, t, :], prob_tok[:, t, :]).then_inc(index_ready.sem, 1)
                dve.wait_ge(index_ready.sem, index_ready.at(NT - 1))
                dve.tensor_copy(index_f[:, :, :], index[:, :, 0:2]).then_inc(index_f_ready.sem, 1)
                dve.wait_ge(index_f_ready.sem, 1)
                for k in range(2):
                    dve.tensor_tensor(is_pick[:, k, :, :],
                                      CONST_L2F.of(table, "index8").unsqueeze(1).to_broadcast([P, NT, E]),
                                      index_f[:, :, k:k + 1].to_broadcast([P, NT, E]), ALU.is_equal)\
                       .then_inc(is_pick_ready.sem, 1)
                dve.wait_ge(is_pick_ready.sem, is_pick_ready.at(1))
                dve.tensor_tensor(picked_tok[:, :, :], is_pick[:, 0, :, :], is_pick[:, 1, :, :], ALU.add)\
                   .then_inc(picked_tok_ready.sem, 1)
                for b in range(B):
                    dve.wait_ge(back.sem, back.at(b))
                    dve.tensor_copy(picked[0:E, batch[b]], psum[0:E, b, :]).then_inc(picked_ready.sem, 1)
                    dve.wait_ge(picked_ready.sem, picked_ready.at(b))
                    dve.tensor_tensor(weight[0:E, batch[b]], prob[0:E, batch[b]], picked[0:E, batch[b]], ALU.mult)\
                       .then_inc(weight_ready.sem, 1)


def l2_expert_phase(core, w, table, picked, weight):
    nc, psum = core.nc, core.psum
    E = L2_EXPERTS
    with Phase(core, "l2e") as ph:
        h1, h2, y = ph.buf("h1", 2, N), ph.buf("h2", 2, N), ph.buf("y", 2, N)
        weighted = ph.buf("weighted", 2, N)
        part = ph.buf("part", E)
        total = ph.buf("total", E)
        total_t = ph.buf("total_t", P)
        passed = ph.semaphore("passed")
        round_done = ph.semaphore("round_done")
        up1, up2, up3 = ph.semaphore("up1", E), ph.semaphore("up2", E), ph.semaphore("up3", E)
        h1_ready, h2_ready, y_ready = ph.semaphore("h1_ready", E), ph.semaphore("h2_ready", E), ph.semaphore("y_ready", E)
        spread, part_ready = ph.semaphore("spread", E), ph.semaphore("part_ready", E)
        started, turned, total_ready = ph.semaphore("started"), ph.semaphore("turned"), ph.semaphore("total_ready")
        out_ready, out_kept = ph.semaphore("out_ready"), ph.semaphore("out_kept")
        col = lambda name, k: L2F.of(w, name, k, 1)
        with nc.Block() as block:
            @block.tensor
            def _(pe):
                with pe.Fori(0, B) as b:
                    pe.wait_ge(round_done.sem, round_done.at(b))
                    x, wt = core.xn[:, cols(b)], weight[0:E, cols(b)]
                    for i in range(E + 3):
                        if i < E:
                            if i >= 2:
                                pe.wait_ge(h1_ready.sem, h1_ready.at(b, i - 2))
                            pe.matmul(psum[:, i % 2, :], L2F.of(w, "w1", i, P), x, start=True, stop=True)\
                              .then_inc(up1.sem, 1)
                        if 0 <= i - 1 < E:
                            e = i - 1
                            pe.wait_ge(h1_ready.sem, h1_ready.at(b, e))
                            if e >= 2:
                                pe.wait_ge(h2_ready.sem, h2_ready.at(b, e - 2))
                            pe.matmul(psum[:, 2 + e % 2, :], L2F.of(w, "w2", e, P), h1[:, e % 2, :],
                                      start=True, stop=True).then_inc(up2.sem, 1)
                        if 0 <= i - 2 < E:
                            e = i - 2
                            pe.wait_ge(h2_ready.sem, h2_ready.at(b, e))
                            if e >= 2:
                                pe.wait_ge(y_ready.sem, y_ready.at(b, e - 2))
                            pe.matmul(psum[:, 4 + e % 2, :], L2F.of(w, "w3", e, P), h2[:, e % 2, :],
                                      start=True, stop=True).then_inc(up3.sem, 1)
                        if 0 <= i - 3 < E:
                            e = i - 3
                            if e >= 2:
                                pe.wait_ge(part_ready.sem, part_ready.at(b, e - 2))
                            apart(pe, passed)
                            pe.matmul(psum[:, 6 + e % 2, :], CONST_L2F.of(table, "sel8", e, P)[0:E, :], wt,
                                      start=True, stop=True).then_inc(spread.sem, 1)
                pe.wait_ge(round_done.sem, round_done.at(B))
                pe.transpose(psum[0:E, 0, 0:P], total[:, :], core.c("ident")).then_inc(turned.sem, 1)
                pe.wait_ge(total_ready.sem, 1)
                for b in range(B):
                    pe.matmul(psum[:, 1 + b, :], total_t[0:E, :], picked[0:E, b * N:(b + 1) * N],
                              start=True, stop=True).then_inc(out_ready.sem, 1)

            @block.scalar
            def _(act):
                with act.Fori(0, B) as b:
                    act.wait_ge(round_done.sem, round_done.at(b))
                    for i in range(E + 2):
                        if i < E:
                            act.wait_ge(up1.sem, up1.at(b, i))
                            if i >= 2:
                                act.wait_ge(up2.sem, up2.at(b, i - 2))
                            act.activation(h1[:, i % 2, :], psum[:, i % 2, :], ACT.Relu, bias=col("b1", i))\
                               .then_inc(h1_ready.sem, 1)
                        if i >= 2:
                            e = i - 2
                            act.wait_ge(up3.sem, up3.at(b, e))
                            if e >= 2:
                                act.wait_ge(part_ready.sem, part_ready.at(b, e - 2))
                            act.activation(y[:, e % 2, :], psum[:, 4 + e % 2, :], ACT.Relu, bias=col("b3", e))\
                               .then_inc(y_ready.sem, 1)

            @block.vector
            def _(dve):
                dve.sem_inc(round_done.sem, 1)
                dve.memset(total[:, :], 0.0).then_inc(started.sem, 1)
                dve.wait_ge(started.sem, 1)
                with dve.Fori(0, B) as b:
                    for i in range(E + 2):
                        if i < E:
                            dve.wait_ge(up2.sem, up2.at(b, i))
                            if i >= 2:
                                dve.wait_ge(up3.sem, up3.at(b, i - 2))
                            dve.tensor_scalar(h2[:, i % 2, :], psum[:, 2 + i % 2, :], col("b2", i), 0.0,
                                              ALU.add, ALU.max).then_inc(h2_ready.sem, 1)
                        if i >= 2:
                            e = i - 2
                            dve.wait_ge(y_ready.sem, y_ready.at(b, e))
                            dve.wait_ge(spread.sem, spread.at(b, e))
                            if e >= 2:
                                dve.wait_ge(part_ready.sem, part_ready.at(b, e - 2))
                            dve.tensor_tensor_reduce(out=weighted[:, e % 2, :], in0=y[:, e % 2, :],
                                                     in1=psum[:, 6 + e % 2, :], scale=1.0, scalar=0.0,
                                                     op0=ALU.mult, op1=ALU.add, accum_out=part[:, e:e + 1])\
                               .then_inc(part_ready.sem, 1)
                    dve.wait_ge(part_ready.sem, part_ready.at(b, E - 1))
                    dve.wait_ge(round_done.sem, b + 1)
                    dve.tensor_tensor(total[:, :], total[:, :], part[:, :], ALU.add).then_inc(round_done.sem, 1)
                dve.wait_ge(turned.sem, 1)
                dve.tensor_copy(total_t[0:E, :], psum[0:E, 0, 0:P]).then_inc(total_ready.sem, 1)
                for b in range(B):
                    dve.wait_ge(out_ready.sem, out_ready.at(b))
                    dve.tensor_copy(core.g[:, b * N:(b + 1) * N], psum[:, 1 + b, :]).then_inc(out_kept.sem, 1)


L3_HEADS = 16
L3A = Fields(("wq", 4 * P), ("wk", 4 * P), ("wv", P), ("wo", P), ("bv", P), ("bq", 4), ("bk", 4), ("bo", 1),
             ("gamma", 1), ("beta", 1))


def l3_attn_layout(np, i):
    g = lambda k: i["L3_attn_" + k]

    def spread(a):
        out = np.zeros((a.shape[0], L3_HEADS, 32), np.float32)
        out[:, :, :8] = a.reshape(-1, L3_HEADS, 8)
        return out.reshape(-1, 4 * P)

    return {"l3a": pack(np, [
        spread(g("Wq")), spread(g("Wk")), g("Wv"), g("Wo"), np.tile(g("bv"), (P, 1)),
        spread(g("bq")[None]).reshape(4, P).T, spread(g("bk")[None]).reshape(4, P).T,
        column(g("bo")), column(g("gamma")), column(g("beta"))])}


LAYOUTS.append(l3_attn_layout)


def l3_attn_phase(core):
    nc, psum = core.nc, core.psum
    H, DH, DV = L3_HEADS, 8, 9
    SCALE = float(DH) ** -0.5
    SIM, TURN, NUM, MISC = 0, 3, 5, 7
    STEPS = CH * H
    with Phase(core, "l3a") as ph:
        w = ph.buf("w", L3A.width)
        col = lambda name, k=0: L3A.of(w, name, k, 1)
        x = ph.buf("x", N)
        q, k = ph.buf("q", 4, N), ph.buf("k", 4, N)
        v = ph.buf("v", CH, H, DV)
        nmax = ph.buf("nmax", STEPS)
        prob = ph.buf("prob", 3, N)
        prob_t = ph.buf("prob_t", 3, N)
        rden = ph.buf("rden", CH, H)
        att, att_t = ph.buf("att", CH, P), ph.buf("att_t", N)
        res, scaled = ph.buf("res", N), ph.buf("scaled", N)

        w_in, ones_ready = ph.semaphore("w_in"), ph.semaphore("ones_ready")
        round_done = ph.semaphore("round_done")
        x_ready = ph.semaphore("x_ready")
        qk_raw, qk_ready = ph.semaphore("qk_raw", 8), ph.semaphore("qk_ready", 8)
        v_raw, v_ready = ph.semaphore("v_raw"), ph.semaphore("v_ready", CH)
        sim_ready, nmax_ready, prob_ready = (ph.semaphore(s, STEPS) for s in ("sim_ready", "nmax_ready", "prob_ready"))
        turned = ph.semaphore("turned", STEPS)
        even_kept, odd_kept = ph.semaphore("even_kept", STEPS // 2), ph.semaphore("odd_kept", STEPS // 2)
        drawn = ph.semaphore("drawn", STEPS)
        rden_ready, att_ready = ph.semaphore("rden_ready", CH), ph.semaphore("att_ready", CH)
        att_turned, att_t_ready = ph.semaphore("att_turned"), ph.semaphore("att_t_ready")
        out_ready, res_ready, scaled_ready = ph.semaphore("out_ready"), ph.semaphore("res_ready"), ph.semaphore("scaled_ready")
        norm = ColumnNorm(ph, "norm", 0, 1)

        def wait_turned_kept(eng, r, n):
            kept = odd_kept if n % 2 else even_kept
            eng.wait_ge(kept.sem, kept.at(r, n // 2))

        with nc.Block() as block:
            @block.sync
            def _(sp):
                sp.dma_start(w[:, :], core.dram["l3a"]).then_inc(w_in.sem, 16)

            @block.gpsimd
            def _(pool):
                pool.memset(v[:, :, :, DH:DV], 1.0).then_inc(ones_ready.sem, 1)
                with pool.Fori(0, B) as r:
                    pool.wait_ge(round_done.sem, round_done.at(r))
                    pool.tensor_copy(x[:, :], core.xn[:, cols(r)]).then_inc(x_ready.sem, 1)

            @block.tensor
            def _(pe):
                pe.wait_ge(w_in.sem, 16)
                pe.wait_ge(ones_ready.sem, 1)
                with pe.Fori(0, B) as r:
                    pe.wait_ge(x_ready.sem, x_ready.at(r))
                    for t in range(8):
                        if t >= 4:
                            pe.wait_ge(qk_ready.sem, qk_ready.at(r, t - 4))
                        pe.matmul(psum[:, t % 4, :], L3A.of(w, "wq" if t < 4 else "wk", t % 4, P), x[:, :],
                                  start=True, stop=True).then_inc(qk_raw.sem, 1)
                    for c in range(CH):
                        mm = pe.matmul(psum[:, MISC, c * P:(c + 1) * P], x[:, c * P:(c + 1) * P], L3A.of(w, "wv"),
                                       start=(c == 0), stop=(c == CH - 1), skip_group_check=True)
                    mm.then_inc(v_raw.sem, 1)
                    pe.wait_ge(qk_ready.sem, qk_ready.at(r, 7))
                    pe.wait_ge(v_ready.sem, v_ready.at(r, CH - 1))

                    def score(n):
                        c, h = n // H, n % H
                        if n >= 3:
                            pe.wait_ge(prob_ready.sem, prob_ready.at(r, n - 3))
                        rows = slice(32 * (h % 4), 32 * (h % 4) + DH)
                        pe.matmul(psum[:, SIM + n % 3, :], q[rows, h // 4, c * P:(c + 1) * P], k[rows, h // 4, :],
                                  start=True, stop=True).then_inc(sim_ready.sem, 1)

                    def turn(n):
                        pe.wait_ge(prob_ready.sem, prob_ready.at(r, n))
                        if n >= 2:
                            wait_turned_kept(pe, r, n - 2)
                        for j in range(CH):
                            mm = pe.transpose(psum[:, TURN + n % 2, j * P:(j + 1) * P],
                                              prob[:, n % 3, j * P:(j + 1) * P], core.c("ident"))
                        mm.then_inc(turned.sem, 1)

                    def draw(n):
                        c, h = n // H, n % H
                        if h == 0 and c >= 2:
                            pe.wait_ge(att_ready.sem, att_ready.at(r, c - 2))
                        wait_turned_kept(pe, r, n)
                        for j in range(CH):
                            mm = pe.matmul(psum[:, NUM + c % 2, h * DV:(h + 1) * DV],
                                           prob_t[:, n % 3, j * P:(j + 1) * P], v[:, j, h, :],
                                           start=(h == 0 and j == 0), stop=(h == H - 1 and j == CH - 1),
                                           skip_group_check=True)
                        mm.then_inc(drawn.sem, 1)

                    for i in range(STEPS + 4):
                        if i < STEPS:
                            score(i)
                        if 0 <= i - 2 < STEPS:
                            turn(i - 2)
                        if 0 <= i - 4 < STEPS:
                            draw(i - 4)
                    for c in range(CH):
                        pe.wait_ge(att_ready.sem, att_ready.at(r, c))
                        mm = pe.transpose(psum[:, MISC, c * P:(c + 1) * P], att[:, c, :], core.c("ident"))
                    mm.then_inc(att_turned.sem, 1)
                    pe.wait_ge(att_t_ready.sem, att_t_ready.at(r))
                    pe.matmul(psum[:, 2, :], L3A.of(w, "wo"), att_t[:, :], start=True, stop=True)\
                      .then_inc(out_ready.sem, 1)
                    pe.wait_ge(res_ready.sem, res_ready.at(r))
                    norm.tensor(pe, r, res[:, :])

            @block.scalar
            def _(act):
                act.preload_act_table_set(EXP_LN_SET)
                with act.Fori(0, B) as r:
                    def keep(n):
                        act.wait_ge(turned.sem, turned.at(r, n))
                        if n >= 3:
                            act.wait_ge(drawn.sem, drawn.at(r, n - 3))
                        act.copy(prob_t[:, n % 3, :], psum[:, TURN + n % 2, :]).then_inc(odd_kept.sem, 1)

                    for n in range(STEPS):
                        act.wait_ge(nmax_ready.sem, nmax_ready.at(r, n))
                        if n >= 3:
                            act.wait_ge(turned.sem, turned.at(r, n - 3))
                        act.activation(prob[:, n % 3, :], psum[:, SIM + n % 3, :], ACT.Exp, bias=nmax[:, n:n + 1])\
                           .then_inc(prob_ready.sem, 1)
                        if n >= 3 and n % 2:
                            keep(n - 2)
                    keep(STEPS - 1)
                    act.wait_ge(att_turned.sem, att_turned.at(r))
                    act.copy(att_t[:, :], psum[:, MISC, :]).then_inc(att_t_ready.sem, 1)
                    norm.scalar(act, r)

            @block.vector
            def _(dve):
                dve.sem_inc(round_done.sem, 1)
                dve.wait_ge(w_in.sem, 16)
                dve.wait_ge(ones_ready.sem, 1)
                with dve.Fori(0, B) as r:
                    for t in range(8):
                        dve.wait_ge(qk_raw.sem, qk_raw.at(r, t))
                        dst = (q if t < 4 else k)[:, t % 4, :]
                        if t < 4:
                            dve.tensor_scalar(dst, psum[:, t % 4, :], col("bq", t), SCALE, ALU.add, ALU.mult)\
                               .then_inc(qk_ready.sem, 1)
                        else:
                            dve.tensor_scalar(dst, psum[:, t % 4, :], col("bk", t - 4), None, ALU.add)\
                               .then_inc(qk_ready.sem, 1)
                    dve.wait_ge(v_raw.sem, v_raw.at(r))
                    for c in range(CH):
                        dve.tensor_tensor(v[:, c, :, 0:DH],
                                          psum[:, MISC, c * P:(c + 1) * P].rearrange("p (h d) -> p h d", d=DH),
                                          L3A.of(w, "bv").rearrange("p (h d) -> p h d", d=DH), ALU.add)\
                           .then_inc(v_ready.sem, 1)

                    def keep(n):
                        dve.wait_ge(turned.sem, turned.at(r, n))
                        if n >= 3:
                            dve.wait_ge(drawn.sem, drawn.at(r, n - 3))
                        dve.tensor_copy(prob_t[:, n % 3, :], psum[:, TURN + n % 2, :]).then_inc(even_kept.sem, 1)

                    def divide(c):
                        dve.wait_ge(drawn.sem, drawn.at(r, c * H + H - 1))
                        num = psum[:, NUM + c % 2, 0:H * DV].rearrange("p (h d) -> p h d", d=DV)
                        dve.reciprocal(rden[:, c, :], num[:, :, DH]).then_inc(rden_ready.sem, 1)
                        dve.wait_ge(rden_ready.sem, rden_ready.at(r, c))
                        dve.tensor_tensor(att[:, c, :].rearrange("p (h d) -> p h d", d=DH), num[:, :, 0:DH],
                                          rden[:, c, :].unsqueeze(2).to_broadcast([P, H, DH]), ALU.mult)\
                           .then_inc(att_ready.sem, 1)

                    for n in range(STEPS):
                        dve.wait_ge(sim_ready.sem, sim_ready.at(r, n))
                        dve.tensor_reduce(nmax[:, n:n + 1], psum[:, SIM + n % 3, :], AX.X, ALU.max, negate=True)\
                           .then_inc(nmax_ready.sem, 1)
                        if n >= 2 and n % 2 == 0:
                            keep(n - 2)
                        if n % H == 8 and n > H:
                            divide(n // H - 1)
                    keep(STEPS - 2)
                    divide(CH - 1)
                    dve.wait_ge(out_ready.sem, out_ready.at(r))
                    dve.scalar_tensor_tensor(out=res[:, :], in0=psum[:, 2, :], scalar=col("bo"), in1=x[:, :],
                                             op0=ALU.add, op1=ALU.add).then_inc(res_ready.sem, 1)
                    dve.wait_ge(res_ready.sem, res_ready.at(r))
                    norm.vector(dve, r, res[:, :])
                    dve.wait_ge(norm.rstd_ready.sem, norm.rstd_ready.at(r))
                    dve.scalar_tensor_tensor(out=scaled[:, :], in0=norm.centred[:, :], scalar=col("gamma"),
                                             in1=norm.rstd[:, :], op0=ALU.mult, op1=ALU.mult)\
                       .then_inc(scaled_ready.sem, 1)
                    dve.wait_ge(scaled_ready.sem, scaled_ready.at(r))
                    dve.tensor_scalar(core.s[:, cols(r)], scaled[:, :], col("beta"), None, ALU.add)\
                       .then_inc(round_done.sem, 1)


L3_EXPERTS, L3_RANK = 8, 16
L3F = Fields(("weight", P), ("gate", L3_EXPERTS), ("u", P), ("v", P))


def l3_ffn_layout(np, i):
    g = lambda k: i["L3_ffn_" + k]
    return {"l3f": pack(np, [g("weight").T, g("gate_w").T, g("lora_U").reshape(P, P).T,
                             g("lora_V").transpose(0, 2, 1).reshape(P, P)])}


LAYOUTS.append(l3_ffn_layout)


def l3_ffn_phase(core):
    nc, psum = core.nc, core.psum
    E, R, NT = L3_EXPERTS, L3_RANK, T // P
    with Phase(core, "l3f") as ph:
        w = ph.buf("w", L3F.width)
        top, gate = ph.buf("top", NT), ph.buf("gate", NT, E)
        total, rtotal = ph.buf("total", NT), ph.buf("rtotal", NT)
        gate_n = ph.buf("gate_n", NT, E)
        gate_wide = ph.buf("gate_wide", NT, P)
        low, mixed = ph.buf("low", 2, N), ph.buf("mixed", 2, N)
        w_in, logit_ready = ph.semaphore("w_in"), ph.semaphore("logit_ready")
        top_ready, shifted_ready, exp_ready = ph.semaphore("top_ready"), ph.semaphore("shifted_ready"), ph.semaphore("exp_ready")
        total_ready, rtotal_ready = ph.semaphore("total_ready"), ph.semaphore("rtotal_ready")
        gate_ready, wide_ready = ph.semaphore("gate_ready"), ph.semaphore("wide_ready")
        turned, low_raw, low_ready = ph.semaphore("turned"), ph.semaphore("low_raw"), ph.semaphore("low_ready")
        mixed_ready, out_ready, out_kept = ph.semaphore("mixed_ready"), ph.semaphore("out_ready"), ph.semaphore("out_kept")
        with nc.Block() as block:
            @block.sync
            def _(sp):
                sp.dma_start(w[:, :], core.dram["l3f"]).then_inc(w_in.sem, 16)

            @block.tensor
            def _(pe):
                pe.wait_ge(w_in.sem, 16)
                for t in range(NT):
                    mm = pe.matmul(psum[:, 0, t * E:(t + 1) * E], core.xn[:, t * P:(t + 1) * P], L3F.of(w, "gate"),
                                   start=(t == 0), stop=(t == NT - 1), skip_group_check=True)
                mm.then_inc(logit_ready.sem, 1)
                for b in range(B):
                    if b >= 2:
                        pe.wait_ge(low_ready.sem, low_ready.at(b - 2))
                    pe.matmul(psum[:, 1 + b % 2, :], L3F.of(w, "u"), core.xn[:, b * N:(b + 1) * N],
                              start=True, stop=True).then_inc(low_raw.sem, 1)
                    pe.wait_ge(wide_ready.sem, 1)
                    if b >= 2:
                        pe.wait_ge(mixed_ready.sem, mixed_ready.at(b - 2))
                    for c in range(CH):
                        mm = pe.transpose(psum[:, 3 + b % 2, c * P:(c + 1) * P], gate_wide[:, b * CH + c, :],
                                          core.c("ident"))
                    mm.then_inc(turned.sem, 1)
                    if b >= 2:
                        pe.wait_ge(out_kept.sem, out_kept.at(b - 2))
                    pe.matmul(psum[:, 5 + b % 2, :], L3F.of(w, "weight"), core.xn[:, b * N:(b + 1) * N],
                              start=True, stop=False)
                    pe.wait_ge(mixed_ready.sem, mixed_ready.at(b))
                    pe.matmul(psum[:, 5 + b % 2, :], L3F.of(w, "v"), mixed[:, b % 2, :], start=False, stop=True)\
                      .then_inc(out_ready.sem, 1)

            @block.scalar
            def _(act):
                act.wait_ge(shifted_ready.sem, 1)
                act.activation(gate[:, :, :], gate[:, :, :], ACT.Exp).then_inc(exp_ready.sem, 1)
                for b in range(B):
                    act.wait_ge(low_raw.sem, low_raw.at(b))
                    if b >= 2:
                        act.wait_ge(mixed_ready.sem, mixed_ready.at(b - 2))
                    act.mul(low[:, b % 2, :], psum[:, 1 + b % 2, :], 1.0 / R).then_inc(low_ready.sem, 1)

            @block.vector
            def _(dve):
                dve.wait_ge(logit_ready.sem, 1)
                logit = psum[:, 0, 0:NT * E].rearrange("p (t e) -> p t e", e=E)
                dve.tensor_reduce(top[:, :], logit, AX.X, ALU.max).then_inc(top_ready.sem, 1)
                dve.wait_ge(top_ready.sem, 1)
                dve.tensor_tensor(gate[:, :, :], logit, top[:, :].unsqueeze(2).to_broadcast([P, NT, E]), ALU.subtract)\
                   .then_inc(shifted_ready.sem, 1)
                dve.wait_ge(exp_ready.sem, 1)
                dve.tensor_reduce(total[:, :], gate[:, :, :], AX.X, ALU.add).then_inc(total_ready.sem, 1)
                dve.wait_ge(total_ready.sem, 1)
                dve.reciprocal(rtotal[:, :], total[:, :]).then_inc(rtotal_ready.sem, 1)
                dve.wait_ge(rtotal_ready.sem, 1)
                dve.tensor_tensor(gate_n[:, :, :], gate[:, :, :], rtotal[:, :].unsqueeze(2).to_broadcast([P, NT, E]),
                                  ALU.mult).then_inc(gate_ready.sem, 1)
                dve.wait_ge(gate_ready.sem, 1)
                dve.tensor_copy(gate_wide[:, :, :].rearrange("p t (e r) -> p (t e) r", r=R),
                                gate_n[:, :, :].rearrange("p t e -> p (t e)").unsqueeze(2).to_broadcast([P, NT * E, R]))\
                   .then_inc(wide_ready.sem, 1)
                for b in range(B):
                    dve.wait_ge(turned.sem, turned.at(b))
                    dve.wait_ge(low_ready.sem, low_ready.at(b))
                    if b >= 2:
                        dve.wait_ge(out_ready.sem, out_ready.at(b - 2))
                    dve.tensor_tensor(mixed[:, b % 2, :], psum[:, 3 + b % 2, :], low[:, b % 2, :], ALU.mult)\
                       .then_inc(mixed_ready.sem, 1)
                    dve.wait_ge(out_ready.sem, out_ready.at(b))
                    dve.tensor_copy(core.g[:, b * N:(b + 1) * N], psum[:, 5 + b % 2, :]).then_inc(out_kept.sem, 1)


def build(nc, dram):
    with ExitStack() as ctx:
        core = Core(nc, ctx, dram)
        load_phase(core)
        mix_phase(core, "norm0", mix=False)
        l0_attn_phase(core)
        l0_ffn_phase(core)
        mix_phase(core, "norm1")
        l1_attn_phase(core)
        l1_ffn_phase(core)
        mix_phase(core, "norm2")
        l2_attn_phase(core)
        l2_ffn_phase(core)
        mix_phase(core, "norm3")
        l3_attn_phase(core)
        l3_ffn_phase(core)
        mix_phase(core, "mix4", norm=False)
        store_phase(core)


def constants():
    import numpy as np
    sets = {"const": CONST, "const_l0a": CONST_L0A, "const_l0f": CONST_L0F, "const_l2f": CONST_L2F}
    out = {name: np.zeros((P, fields.width), np.float32) for name, fields in sets.items()}

    def put(name, value):
        for key, fields in sets.items():
            if name in fields.at:
                start, width = fields.at[name]
                out[key][:len(value), start:start + width] = value

    i = np.arange(P)
    put("ident", np.eye(P))
    put("mean", np.full((P, P), 1.0 / P))
    put("causal", np.arange(N)[None, :] >= i[:, None])
    put("ones64", i[:, None] // 64 == i[None, :] // 64)
    swap = np.zeros((P, P))
    for h in (0, 64):
        for d in range(32):
            swap[h + d + 32, h + d] = -1.0
            swap[h + d, h + d + 32] = 1.0
    put("swap64", swap)
    kv = np.zeros((P, 4, 9))
    for h in range(4):
        kv[32 * h:32 * h + 16, h, :] = 1.0
    put("kvmask", np.tile(kv.reshape(P, 36), (1, 4)))
    put("causal4", np.tile(i[None, :] >= i[:, None], (1, 4)))
    sign, nhalf = np.zeros((P, 4, 32)), np.zeros((P, 4, 32))
    for top in (0, 64):
        for h in range(4):
            sign[top + 8 * h:top + 8 * h + 8, h, 0:8] = 1.0
            sign[top + 8 * h:top + 8 * h + 8, h, 8:16] = -1.0
            nhalf[top + 32 + 8 * h:top + 32 + 8 * h + 8, h, 0:16] = -0.5
    put("sign", sign.reshape(P, P))
    put("nhalf", nhalf.reshape(P, P))
    key = np.arange(2 * P)[None, :] - P
    seen = (key <= i[:, None]) & (key >= i[:, None] - 64)
    put("window", np.where(seen, 0.0, -1e30))
    put("window_first", np.where(seen & (key >= 0), 0.0, -1e30))
    sel = np.zeros((8, 8, P))
    for e in range(8):
        sel[e, e, :] = 1.0
    put("sel8", sel.reshape(8, 8 * P))
    put("index8", np.tile(np.arange(8), (P, 1)))
    f = np.float32
    half = np.arange(0, 64, 2, dtype=f)
    inv = (f(1.0) / f(10000.0) ** (half / f(64))).astype(f)
    t = np.arange(N, dtype=f)
    angle = (t[:, None] * inv[None, :]).astype(f).astype(np.float64)
    base = ((half + f(0.4 * 64)) / f(1.4 * 64)).astype(np.float64)
    scale = base[None, :] ** ((t - N // 2) / 32.0)[:, None].astype(np.float64)
    four = lambda a: np.tile(a, (1, 4)).T
    cos, sin, scale = four(np.cos(angle)), four(np.sin(angle)), four(scale)
    put("rope_qc", 8.0 * cos * scale)
    put("rope_qs", 8.0 * sin * scale)
    put("rope_kc", cos / scale)
    put("rope_ks", sin / scale)
    put("eps5", np.full((P, 1), LN_EPS))
    put("eps_l2", np.full((P, 1), 2.0 ** -64))
    put("l2_back", np.full((P, 1), 15 * np.log(2.0)))
    return out


def kernel(**inputs):
    import numpy as np
    import concourse.bacc as bacc
    from concourse.bass_utils import run_bass_kernel_spmd as run

    inputs = {k: np.asarray(v) for k, v in inputs.items()}
    arrays = {"x": inputs["L0_attn_x"], **constants()}
    for phase_layout in LAYOUTS:
        arrays.update(phase_layout(np, inputs))
    arrays = {f"in_{k}": np.ascontiguousarray(v) for k, v in arrays.items()}
    nc = bacc.Bacc("TRN2", target_bir_lowering=False, num_devices=1)
    dram = {k[3:]: nc.dram_tensor(k, v.shape, F32, kind="ExternalInput").ap() for k, v in arrays.items()}
    dram["out"] = nc.dram_tensor("out", (B, N, P), F32, kind="ExternalOutput").ap()
    build(nc, dram)
    result = run(nc, [arrays], core_ids=[0])
    return result.results[0]["out"]
```

```python
from contextlib import ExitStack

import concourse.bass as bass
from concourse import mybir

P = 128
B = 4
N = 512
T = B * N
CH = N // P

F32 = mybir.dt.float32
U32 = mybir.dt.uint32
ALU = mybir.AluOpType
ACT = mybir.ActivationFunctionType
AX = mybir.AxisListType
EXP_LN_SET = "natural_log_exp_and_others"
LN_EPS = 1e-5


class Fields:

    def __init__(self, *fields):
        self.at, self.width = {}, 0
        for name, width in fields:
            self.at[name] = (self.width, width)
            self.width += width

    def of(self, buf, name, part=0, width=None):
        start, whole = self.at[name]
        width = width or whole
        return buf[:, start + part * width:start + (part + 1) * width]


CONST = Fields(("ident", P), ("mean", P), ("causal", N), ("eps5", 1))
CONST_L0A = Fields(("kvmask", 16 * 9), ("causal4", N), ("sign", P), ("nhalf", P))
CONST_L0F = Fields(("ones64", P), ("swap64", P), ("window_first", 2 * P), ("window", 2 * P),
                   ("rope_qc", N), ("rope_qs", N), ("rope_kc", N), ("rope_ks", N), ("eps_l2", 1), ("l2_back", 1))
CONST_L2F = Fields(("sel8", 8 * P), ("index8", 8))


class Signal:

    def __init__(self, sem, per_round=1):
        self.sem = sem
        self.per_round = per_round

    def at(self, r, k=0):
        return r * self.per_round + k + 1


def apart(eng, passed):
    eng.sem_inc(passed.sem, 1)


class Core:

    def __init__(self, nc, ctx, dram):
        self.nc, self.dram = nc, dram
        sb = lambda name, cols: ctx.enter_context(nc.sbuf_tensor(name, [P, cols], F32))
        self.x = sb("x_res", T)
        self.xn = sb("x_norm", T)
        self.s = sb("s_branch", T)
        self.g = sb("g_branch", T)
        self.const = sb("const", CONST.width)
        self.psum = ctx.enter_context(nc.psum_tensor("psum", [P, 8, N], F32))

    def c(self, name):
        return CONST.of(self.const, name)


class Phase:

    def __init__(self, core, name):
        self.core, self.nc, self.name = core, core.nc, name

    def __enter__(self):
        self.ctx = ExitStack()
        self.sems = []
        return self

    def buf(self, name, *shape, dtype=F32):
        return self.ctx.enter_context(self.nc.sbuf_tensor(f"{self.name}_{name}", [P, *shape], dtype))

    def semaphore(self, name, per_round=1):
        sem = self.ctx.enter_context(self.nc.semaphore(f"{self.name}_{name}"))
        self.sems.append(sem)
        return Signal(sem, per_round)

    def __exit__(self, *failure):
        if failure[0] is None:
            with self.nc.Block() as block:
                @block.sync
                def _(sp):
                    for sem in self.sems:
                        sp.sem_clear(sem)
        self.ctx.close()


def cols(r, width=N):
    return bass.ds(r * width, width)


class ColumnNorm:

    def __init__(self, ph, name, *banks, centre=True, eps="eps5"):
        self.core, self.centre, self.eps, self.banks = ph.core, centre, eps, banks
        self.centred = ph.buf(name + "_centred", N)
        self.squared = ph.buf(name + "_squared", N)
        self.logvar = ph.buf(name + "_logvar", N)
        self.rstd = ph.buf(name + "_rstd", N)
        self.mean_ready = ph.semaphore(name + "_mean_ready", len(banks))
        self.centred_ready = ph.semaphore(name + "_centred_ready", len(banks))
        self.squared_ready = ph.semaphore(name + "_squared_ready", len(banks))
        self.var_ready = ph.semaphore(name + "_var_ready", len(banks))
        self.logvar_ready = ph.semaphore(name + "_logvar_ready", len(banks))
        self.rstd_ready = ph.semaphore(name + "_rstd_ready", len(banks))

    def tensor_mean(self, pe, x, k=0):
        pe.matmul(self.core.psum[:, self.banks[k][0], :], self.core.c("mean"), x, start=True, stop=True)\
          .then_inc(self.mean_ready.sem, 1)

    def tensor_var(self, pe, r, k=0):
        pe.wait_ge(self.squared_ready.sem, self.squared_ready.at(r, k))
        pe.matmul(self.core.psum[:, self.banks[k][1], :], self.core.c("mean"), self.squared[:, :],
                  start=True, stop=True).then_inc(self.var_ready.sem, 1)

    def tensor(self, pe, r, x, k=0):
        if self.centre:
            self.tensor_mean(pe, x, k)
        self.tensor_var(pe, r, k)

    def vector(self, dve, r, x, k=0):
        dve.wait_ge(self.mean_ready.sem, self.mean_ready.at(r, k))
        dve.tensor_tensor(self.centred[:, :], x, self.core.psum[:, self.banks[k][0], :], ALU.subtract)\
           .then_inc(self.centred_ready.sem, 1)

    def scalar_square(self, act, r, x=None, k=0):
        if self.centre:
            act.wait_ge(self.centred_ready.sem, self.centred_ready.at(r, k))
            x = self.centred[:, :]
        act.activation(self.squared[:, :], x, ACT.Square).then_inc(self.squared_ready.sem, 1)

    def scalar_rstd(self, act, r, k=0):
        act.wait_ge(self.var_ready.sem, self.var_ready.at(r, k))
        act.activation(self.logvar[:, :], self.core.psum[:, self.banks[k][1], :], ACT.Ln,
                       bias=self.core.c(self.eps)).then_inc(self.logvar_ready.sem, 1)
        act.wait_ge(self.logvar_ready.sem, self.logvar_ready.at(r, k))
        act.activation(self.rstd[:, :], self.logvar[:, :], ACT.Exp, scale=-0.5)\
           .then_inc(self.rstd_ready.sem, 1)

    def scalar(self, act, r, x=None, k=0):
        self.scalar_square(act, r, x, k)
        self.scalar_rstd(act, r, k)


LAYOUTS = []


def pack(np, pieces):
    out = np.zeros((P, sum(a.shape[1] for a in pieces)), np.float32)
    at = 0
    for a in pieces:
        out[:a.shape[0], at:at + a.shape[1]] = a
        at += a.shape[1]
    return out


def blocks(np, w, size=P):
    k, n = w.shape[0] // size, w.shape[1]
    return w.reshape(k, size, n).transpose(1, 0, 2).reshape(size, k * n)


def column(v):
    return v.reshape(-1, 1)




def load_phase(core):
    nc = core.nc
    with Phase(core, "load") as ph:
        rows = ph.buf("rows", T // P, P)
        const_in = ph.semaphore("const_in")
        rows_in = ph.semaphore("rows_in")
        turned = ph.semaphore("turned")
        x_ready = ph.semaphore("x_ready")
        with nc.Block() as block:
            @block.sync
            def _(sp):
                sp.dma_start(core.const[:, :], core.dram["const"]).then_inc(const_in.sem, 16)
                sp.dma_start(rows[:, :, :], core.dram["x"].rearrange("b (c p) d -> p (b c) d", p=P))\
                  .then_inc(rows_in.sem, 16)

            @block.tensor
            def _(pe):
                pe.wait_ge(const_in.sem, 16)
                pe.wait_ge(rows_in.sem, 16)
                for b in range(B):
                    for c in range(CH):
                        turn = pe.transpose(core.psum[:, b, c * P:(c + 1) * P], rows[:, b * CH + c, :],
                                            core.c("ident"))
                    turn.then_inc(turned.sem, 1)

            @block.vector
            def _(dve):
                for b in range(B):
                    dve.wait_ge(turned.sem, b + 1)
                    dve.tensor_copy(core.x[:, b * N:(b + 1) * N], core.psum[:, b, :]).then_inc(x_ready.sem, 1)


def mix_phase(core, name, mix=True, norm=True):
    nc = core.nc
    with Phase(core, name) as ph:
        gate = ph.buf("gate", T)
        gated = ph.buf("gated", T)
        centred = ph.buf("centred", T)
        squared = ph.buf("squared", T)
        logvar = ph.buf("logvar", T)
        rstd = ph.buf("rstd", T)
        gate_ready = ph.semaphore("gate_ready")
        gated_ready = ph.semaphore("gated_ready")
        x_ready = ph.semaphore("x_ready")
        mean_ready = ph.semaphore("mean_ready")
        centred_ready = ph.semaphore("centred_ready")
        squared_ready = ph.semaphore("squared_ready")
        var_ready = ph.semaphore("var_ready")
        logvar_ready = ph.semaphore("logvar_ready")
        rstd_ready = ph.semaphore("rstd_ready")
        xn_ready = ph.semaphore("xn_ready")
        batch = [slice(b * N, (b + 1) * N) for b in range(B)]
        mean_bank = [core.psum[:, b, :] for b in range(B)]
        var_bank = [core.psum[:, B + b, :] for b in range(B)]
        with nc.Block() as block:
            @block.tensor
            def _(pe):
                if not norm:
                    return
                for b in range(B):
                    if mix:
                        pe.wait_ge(x_ready.sem, x_ready.at(b))
                    pe.matmul(mean_bank[b], core.c("mean"), core.x[:, batch[b]], start=True, stop=True)\
                      .then_inc(mean_ready.sem, 1)
                for b in range(B):
                    pe.wait_ge(squared_ready.sem, squared_ready.at(b))
                    pe.matmul(var_bank[b], core.c("mean"), squared[:, batch[b]], start=True, stop=True)\
                      .then_inc(var_ready.sem, 1)

            @block.vector
            def _(dve):
                if mix:
                    for b in range(B):
                        dve.wait_ge(gate_ready.sem, gate_ready.at(b))
                        dve.tensor_tensor(gated[:, batch[b]], core.s[:, batch[b]], gate[:, batch[b]], ALU.mult)\
                           .then_inc(gated_ready.sem, 1)
                        dve.wait_ge(gated_ready.sem, gated_ready.at(b))
                        dve.tensor_tensor(core.x[:, batch[b]], core.x[:, batch[b]], gated[:, batch[b]], ALU.add)\
                           .then_inc(x_ready.sem, 1)
                if norm:
                    for b in range(B):
                        dve.wait_ge(mean_ready.sem, mean_ready.at(b))
                        dve.tensor_tensor(centred[:, batch[b]], core.x[:, batch[b]], mean_bank[b], ALU.subtract)\
                           .then_inc(centred_ready.sem, 1)
                    for b in range(B):
                        dve.wait_ge(rstd_ready.sem, rstd_ready.at(b))
                        dve.tensor_tensor(core.xn[:, batch[b]], centred[:, batch[b]], rstd[:, batch[b]], ALU.mult)\
                           .then_inc(xn_ready.sem, 1)

            @block.scalar
            def _(act):
                if mix:
                    for b in range(B):
                        act.activation(gate[:, batch[b]], core.g[:, batch[b]], ACT.Silu).then_inc(gate_ready.sem, 1)
                if norm:
                    act.preload_act_table_set(EXP_LN_SET)
                    for b in range(B):
                        act.wait_ge(centred_ready.sem, centred_ready.at(b))
                        act.activation(squared[:, batch[b]], centred[:, batch[b]], ACT.Square)\
                           .then_inc(squared_ready.sem, 1)
                    for b in range(B):
                        act.wait_ge(var_ready.sem, var_ready.at(b))
                        act.activation(logvar[:, batch[b]], var_bank[b], ACT.Ln, bias=core.c("eps5"))\
                           .then_inc(logvar_ready.sem, 1)
                        act.wait_ge(logvar_ready.sem, logvar_ready.at(b))
                        act.activation(rstd[:, batch[b]], logvar[:, batch[b]], ACT.Exp, scale=-0.5)\
                           .then_inc(rstd_ready.sem, 1)


def store_phase(core):
    nc = core.nc
    with Phase(core, "store") as ph:
        rows = ph.buf("rows", T // P, P)
        turned = ph.semaphore("turned")
        rows_ready = ph.semaphore("rows_ready")
        stored = ph.semaphore("stored")
        out = core.dram["out"].rearrange("b (c p) d -> p (b c) d", p=P)
        with nc.Block() as block:
            @block.tensor
            def _(pe):
                for b in range(B):
                    for c in range(CH):
                        t = b * CH + c
                        turn = pe.transpose(core.psum[:, b, c * P:(c + 1) * P], core.x[:, t * P:(t + 1) * P],
                                            core.c("ident"))
                    turn.then_inc(turned.sem, 1)

            @block.vector
            def _(dve):
                for b in range(B):
                    dve.wait_ge(turned.sem, turned.at(b))
                    dve.tensor_copy(rows[:, b * CH:(b + 1) * CH, :],
                                    core.psum[:, b, :].rearrange("p (c d) -> p c d", c=CH))\
                       .then_inc(rows_ready.sem, 1)

            @block.sync
            def _(sp):
                for b in range(B):
                    sp.wait_ge(rows_ready.sem, rows_ready.at(b))
                    sp.dma_start(out[:, b * CH:(b + 1) * CH, :], rows[:, b * CH:(b + 1) * CH, :])\
                      .then_inc(stored.sem, 16)
                sp.wait_ge(stored.sem, 16 * B)


L0_LAYERS, L0_HEADS, L0_FF = 6, 16, 512
L0_DH = P // L0_HEADS
L0A = Fields(("wq", 2 * P), ("wk", 2 * P), ("wv", P), ("omega", P), ("bv", P), ("bq", 2), ("bk", 2))
L0M = Fields(("wo", P), ("w1", L0_FF), ("w2", L0_FF), ("bo", 1), ("g1", 1), ("be1", 1),
             ("bf1", L0_FF // P), ("bf2", 1), ("g2", 1), ("be2", 1))


def l0_attn_layout(np, i):
    g = lambda k: i["L0_attn_" + k]
    order = [np.concatenate([np.arange(32 * x, 32 * x + 32) for x in (2 * t, 2 * t, 2 * t + 1, 2 * t + 1)])
             for t in range(2)]
    att, mlp = [], []
    for n in range(L0_LAYERS):
        omega = np.zeros((P, 4, 32), np.float32)
        for top in (0, 64):
            for h in range(4):
                rows = slice(top + 8 * h, top + 8 * h + 8)
                omega[rows, h, 0:8] = g("omega")[n]
                omega[rows, h, 8:16] = g("omega")[n]
        att.append(pack(np, [
            g("Wq")[n][:, order[0]], g("Wq")[n][:, order[1]], g("Wk")[n][:, order[0]], g("Wk")[n][:, order[1]],
            g("Wv")[n], omega.reshape(P, P), np.tile(g("bv")[n], (P, 1)),
            g("bq")[n][order[0]][:, None], g("bq")[n][order[1]][:, None],
            g("bk")[n][order[0]][:, None], g("bk")[n][order[1]][:, None]]))
        mlp.append(pack(np, [
            g("Wo")[n], g("W1")[n], blocks(np, g("W2")[n]),
            column(g("bo")[n]), column(g("g1")[n]), column(g("be1")[n]), g("bf1")[n].reshape(-1, P).T,
            column(g("bf2")[n]), column(g("g2")[n]), column(g("be2")[n])]))
    return {"l0a": np.stack(att), "l0m": np.stack(mlp)}


LAYOUTS.append(l0_attn_layout)


def l0_attn_phase(core):
    nc, psum = core.nc, core.psum
    F, G, DH, DV = L0_FF // P, L0_HEADS // 4, L0_DH, L0_DH + 1
    SCALE = float(DH) ** -0.25
    ATT_EPS = 16 * 1e-6
    V_BANK, KV_BANK, TURN_BANK, NUM_BANK = 4, 5, 5, 4
    ARG_BANKS = (2, 3, 0, 1)
    K_TOK_BANKS = (4, 2, 3)
    OUT_BANK, DOWN_BANK, UP_BANKS = 6, 7, (7, 6)
    TILES = (2, 3, 0, 1)
    FEATS = (4, 5, 6, 7, 0, 1, 2, 3)
    with Phase(core, "l0a") as ph:
        wa, wm = ph.buf("wa", L0A.width), ph.buf("wm", L0M.width)
        acol = lambda name, k=0: L0A.of(wa, name, k, 1)
        mcol = lambda name, k=0: L0M.of(wm, name, k, 1)
        h_in = ph.buf("h_in", N)
        qk = ph.buf("qk", 4, N)
        omega = ph.buf("omega", P)
        omega_signed = ph.buf("omega_signed", P)
        feat = ph.buf("feat", 8, N)
        v = ph.buf("v", CH, L0_HEADS, DV)
        k_tok = ph.buf("k_tok", CH - 1, G * P)
        kv = ph.buf("kv", CH - 1, L0_HEADS * DV)
        state = ph.buf("state", CH - 1, L0_HEADS * DV)
        scores = ph.buf("scores", 2, 4, N)
        den = ph.buf("den", CH, L0_HEADS)
        rden = ph.buf("rden", CH, L0_HEADS)
        att = ph.buf("att", CH, P)
        att_t = ph.buf("att_t", N)
        res1, res2 = ph.buf("res1", N), ph.buf("res2", N)
        scaled1, scaled2 = ph.buf("scaled1", N), ph.buf("scaled2", N)
        h1 = ph.buf("h1", N)
        y = ph.buf("y", F, N)

        table = ph.buf("table", CONST_L0A.width)
        const = lambda name: CONST_L0A.of(table, name)
        table_in = ph.semaphore("table_in")
        passed = ph.semaphore("passed")
        wa_in, wm_in = ph.semaphore("wa_in", 16), ph.semaphore("wm_in", 16)
        s_ready = ph.semaphore("s_ready")
        ones_ready = ph.semaphore("ones_ready")
        omega_signed_ready, omega_ready = ph.semaphore("omega_signed_ready"), ph.semaphore("omega_ready")
        h_ready = ph.semaphore("h_ready")
        proj_ready = ph.semaphore("proj_ready", 4)
        qk_ready, qk_sq_ready = ph.semaphore("qk_ready", 4), ph.semaphore("qk_sq_ready", 4)
        v_ready, v_kept = ph.semaphore("v_ready"), ph.semaphore("v_kept")
        arg_ready, feat_ready = ph.semaphore("arg_ready", 8), ph.semaphore("feat_ready", 8)
        k_tok_ready, k_tok_kept = ph.semaphore("k_tok_ready", CH - 1), ph.semaphore("k_tok_kept", CH - 1)
        kv_ready, kv_kept = ph.semaphore("kv_ready", CH - 1), ph.semaphore("kv_kept", CH - 1)
        state_ready = ph.semaphore("state_ready", CH - 1)
        scores_ready, scores_kept = ph.semaphore("scores_ready", CH * G), ph.semaphore("scores_kept", CH * G)
        num_ready = ph.semaphore("num_ready", CH)
        den_ready, rden_ready = ph.semaphore("den_ready", CH), ph.semaphore("rden_ready", CH)
        att_ready = ph.semaphore("att_ready", CH)
        att_t_ready, att_t_kept = ph.semaphore("att_t_ready"), ph.semaphore("att_t_kept")
        out_ready, res_ready = ph.semaphore("out_ready", 2), ph.semaphore("res_ready", 2)
        norm = ColumnNorm(ph, "norm", (7, 6), (6, 7))
        scaled_ready = ph.semaphore("scaled_ready", 2)
        h1_ready = ph.semaphore("h1_ready")
        up_ready, y_ready = ph.semaphore("up_ready", F), ph.semaphore("y_ready", F)

        def steps(eng, step):
            step(0, 0, None, None, None)
            with eng.Fori(0, L0_LAYERS - 1) as layer:
                with eng.Fori(0, B - 1) as b:
                    r = layer * B + b
                    step(r + 1, layer, r, layer, b)
                step(layer * B + B, layer + 1, layer * B + B - 1, layer, B - 1)
            last = L0_LAYERS - 1
            with eng.Fori(0, B - 1) as b:
                step(b + (last * B + 1), last, b + last * B, last, b)
            step(None, None, L0_LAYERS * B - 1, last, B - 1)

        with nc.Block() as block:
            @block.sync
            def _(sp):
                sp.dma_start(table[:, :], core.dram["const_l0a"]).then_inc(table_in.sem, 16)
                sp.dma_start(wa[:, :], core.dram["l0a"][0, :, :]).then_inc(wa_in.sem, 16)
                sp.dma_start(wm[:, :], core.dram["l0m"][0, :, :]).then_inc(wm_in.sem, 16)
                with sp.Fori(0, L0_LAYERS - 1) as layer:
                    nxt = bass.ds(layer + 1, 1)
                    sp.wait_ge(k_tok_ready.sem, k_tok_ready.at(layer * B + B - 1, 0))
                    apart(sp, passed)
                    sp.dma_start(wa[:, :], core.dram["l0a"][nxt, :, :].rearrange("a p c -> (a p) c"))\
                      .then_inc(wa_in.sem, 16)
                    sp.wait_ge(s_ready.sem, s_ready.at(layer * B + B - 1) + B)
                    apart(sp, passed)
                    sp.dma_start(wm[:, :], core.dram["l0m"][nxt, :, :].rearrange("a p c -> (a p) c"))\
                      .then_inc(wm_in.sem, 16)

            @block.gpsimd
            def _(pool):
                for b in range(B):
                    pool.tensor_copy(core.s[:, b * N:(b + 1) * N], core.xn[:, b * N:(b + 1) * N])\
                        .then_inc(s_ready.sem, 1)
                pool.memset(v[:, :, :, DH:DV], 1.0).then_inc(ones_ready.sem, 1)
                pool.wait_ge(table_in.sem, 16)

                def make_omega(layer):
                    pool.wait_ge(wa_in.sem, (layer + 1) * 16)
                    pool.tensor_tensor(omega_signed[:, :], L0A.of(wa, "omega"), const("sign"), ALU.mult)\
                        .then_inc(omega_signed_ready.sem, 1)
                    pool.wait_ge(omega_signed_ready.sem, omega_signed_ready.at(layer))
                    pool.tensor_tensor(omega[:, :], omega_signed[:, :], const("nhalf"), ALU.add)\
                        .then_inc(omega_ready.sem, 1)

                def fetch(r, b):
                    pool.wait_ge(s_ready.sem, s_ready.at(r))
                    apart(pool, passed)
                    pool.tensor_copy(h_in[:, :], core.s[:, cols(b)]).then_inc(h_ready.sem, 1)

                make_omega(0)
                fetch(0, 0)
                with pool.Fori(0, L0_LAYERS - 1) as layer:
                    with pool.Fori(0, B - 1) as b:
                        r = layer * B + b
                        pool.wait_ge(v_ready.sem, v_ready.at(r))
                        fetch(r + 1, b + 1)
                    pool.wait_ge(v_ready.sem, v_ready.at(layer * B + B - 1))
                    fetch(layer * B + B, 0)
                    pool.wait_ge(arg_ready.sem, arg_ready.at(layer * B + B - 1, 7))
                    make_omega(layer + 1)
                with pool.Fori(0, B - 1) as b:
                    r = b + (L0_LAYERS - 1) * B
                    pool.wait_ge(v_ready.sem, v_ready.at(r))
                    fetch(r + 1, b + 1)

            @block.tensor
            def _(pe):
                pe.wait_ge(table_in.sem, 16)
                pe.wait_ge(ones_ready.sem, 1)

                def project(r, layer):
                    pe.wait_ge(wa_in.sem, (layer + 1) * 16)
                    pe.wait_ge(h_ready.sem, h_ready.at(r))
                    for t in TILES:
                        pe.matmul(psum[:, t, :], L0A.of(wa, "wq" if t < 2 else "wk", t % 2, P), h_in[:, :],
                                  start=True, stop=True).then_inc(proj_ready.sem, 1)

                def project_v(r):
                    for c in range(CH):
                        mm = pe.matmul(psum[:, V_BANK, c * P:(c + 1) * P], h_in[:, c * P:(c + 1) * P],
                                       L0A.of(wa, "wv"), start=(c == 0), stop=(c == CH - 1),
                                       skip_group_check=True)
                    mm.then_inc(v_ready.sem, 1)

                def exponents(r, layer, ks):
                    pe.wait_ge(omega_ready.sem, omega_ready.at(layer))
                    for k in ks:
                        t, half = FEATS[k] // 2, 64 * (FEATS[k] % 2)
                        pe.wait_ge(qk_sq_ready.sem, qk_sq_ready.at(r, k // 2))
                        if k < 4:
                            pe.wait_ge(qk_ready.sem, qk_ready.at(r, k))
                        else:
                            pe.wait_ge(feat_ready.sem, feat_ready.at(r, k - 4))
                        pe.matmul(psum[:, ARG_BANKS[k % 4], :], omega[half:half + 64, :],
                                  qk[half:half + 64, t, :], start=True, stop=True).then_inc(arg_ready.sem, 1)

                def turn_keys(r):
                    pe.wait_ge(v_kept.sem, v_kept.at(r))
                    for c in range(CH - 1):
                        pe.wait_ge(feat_ready.sem, feat_ready.at(r, 3 + c))
                        for g in range(G):
                            mm = pe.transpose(psum[:, K_TOK_BANKS[c], g * P:(g + 1) * P],
                                              feat[:, 4 + g, c * P:(c + 1) * P], core.c("ident"))
                        mm.then_inc(k_tok_ready.sem, 1)

                def key_value(r, c):
                    pe.wait_ge(k_tok_kept.sem, k_tok_kept.at(r, c))
                    if c >= 1:
                        pe.wait_ge(kv_kept.sem, kv_kept.at(r, c - 1))
                    for g in range(G):
                        mm = pe.matmul(psum[:, KV_BANK, g * 4 * DV:(g + 1) * 4 * DV], k_tok[:, c, g * P:(g + 1) * P],
                                       v[:, c, 4 * g:4 * g + 4, :],
                                       start=(g == 0), stop=(g == G - 1), skip_group_check=True)
                    mm.then_inc(kv_ready.sem, 1)

                def score(r, c):
                    if c == 0:
                        pe.wait_ge(feat_ready.sem, feat_ready.at(r, 7))
                        pe.wait_ge(k_tok_kept.sem, k_tok_kept.at(r, CH - 2))
                    else:
                        pe.wait_ge(scores_kept.sem, scores_kept.at(r, c * 4 - 1))
                    for g in range(G):
                        for h in range(4):
                            rows = slice(32 * h, 32 * h + 16)
                            mm = pe.matmul(psum[:, h, g * P:(g + 1) * P],
                                           feat[rows, 4 + g, c * P:(c + 1) * P],
                                           feat[rows, g, c * P:(c + 1) * P],
                                           start=(g == 0), stop=(g == G - 1), skip_group_check=True)
                            if g == G - 1:
                                mm.then_inc(scores_ready.sem, 1)

                def gather(r, c):
                    if c >= 1:
                        pe.wait_ge(att_ready.sem, att_ready.at(r, c - 1))
                        pe.wait_ge(state_ready.sem, state_ready.at(r, c - 1))
                    pe.wait_ge(scores_kept.sem, scores_kept.at(r, c * 4 + 3))
                    for g in range(G):
                        if c >= 1:
                            pe.matmul(psum[:, NUM_BANK, g * 4 * DV:(g + 1) * 4 * DV],
                                      feat[:, g, c * P:(c + 1) * P],
                                      state[:, c - 1, g * 4 * DV:(g + 1) * 4 * DV],
                                      start=(g == 0), stop=False, skip_group_check=True)
                        for h in range(4):
                            mm = pe.matmul(psum[:, NUM_BANK, (4 * g + h) * DV:(4 * g + h + 1) * DV],
                                           scores[:, c % 2, h, g * P:(g + 1) * P], v[:, c, 4 * g + h, :],
                                           start=(c == 0 and g == 0 and h == 0),
                                           stop=(g == G - 1 and h == 3), skip_group_check=True)
                    mm.then_inc(num_ready.sem, 1)

                def turn(r, c):
                    if c == 0:
                        pe.wait_ge(kv_kept.sem, kv_kept.at(r, CH - 2))
                    pe.wait_ge(att_ready.sem, att_ready.at(r, c))
                    mm = pe.transpose(psum[:, TURN_BANK, c * P:(c + 1) * P], att[:, c, :], core.c("ident"))
                    if c == CH - 1:
                        mm.then_inc(att_t_ready.sem, 1)

                def output(m, layer):
                    pe.wait_ge(wm_in.sem, (layer + 1) * 16)
                    pe.wait_ge(att_t_kept.sem, att_t_kept.at(m))
                    pe.matmul(psum[:, OUT_BANK, :], L0M.of(wm, "wo"), att_t[:, :], start=True, stop=True)\
                      .then_inc(out_ready.sem, 1)

                def mean(m, k):
                    pe.wait_ge(res_ready.sem, res_ready.at(m, k))
                    norm.tensor_mean(pe, (res1, res2)[k][:, :], k)

                def up(m):
                    pe.wait_ge(h1_ready.sem, h1_ready.at(m))
                    for f in range(F):
                        if f >= 2:
                            pe.wait_ge(y_ready.sem, y_ready.at(m, f - 2))
                        pe.matmul(psum[:, UP_BANKS[f % 2], :], L0M.of(wm, "w1", f, P), h1[:, :],
                                  start=True, stop=True).then_inc(up_ready.sem, 1)

                def down(m):
                    pe.wait_ge(y_ready.sem, y_ready.at(m, F - 1))
                    for f in range(F):
                        mm = pe.matmul(psum[:, DOWN_BANK, :], L0M.of(wm, "w2", f, P), y[:, f, :],
                                       start=(f == 0), stop=(f == F - 1))
                    mm.then_inc(out_ready.sem, 1)

                def step(a, a_layer, m, m_layer, m_batch):
                    if a is not None:
                        project(a, a_layer)
                    if m is not None:
                        turn(m, CH - 1)
                    if a is not None:
                        project_v(a)
                        exponents(a, a_layer, range(0, 4))
                    if m is not None:
                        output(m, m_layer)
                    if a is not None:
                        exponents(a, a_layer, range(4, 8))
                    if m is not None:
                        mean(m, 0)
                    if a is not None:
                        turn_keys(a)
                    if m is not None:
                        norm.tensor_var(pe, m, 0)
                    if a is not None:
                        key_value(a, 0)
                        score(a, 0)
                        key_value(a, 1)
                    if m is not None:
                        up(m)
                    if a is not None:
                        score(a, 1)
                        key_value(a, 2)
                        gather(a, 0)
                    if m is not None:
                        down(m)
                    if a is not None:
                        score(a, 2)
                        turn(a, 0)
                        gather(a, 1)
                    if m is not None:
                        mean(m, 1)
                    if a is not None:
                        score(a, 3)
                        turn(a, 1)
                        gather(a, 2)
                    if m is not None:
                        norm.tensor_var(pe, m, 1)
                    if a is not None:
                        turn(a, 2)
                        gather(a, 3)

                steps(pe, step)

            @block.scalar
            def _(act):
                act.wait_ge(table_in.sem, 16)
                act.preload_act_table_set(EXP_LN_SET)

                def square(r, ks):
                    for k in ks:
                        act.wait_ge(qk_ready.sem, qk_ready.at(r, k))
                        for rows in (slice(32, 64), slice(96, 128)):
                            sq = act.activation(qk[rows, TILES[k], :], qk[rows, TILES[k], :], ACT.Square)
                        sq.then_inc(qk_sq_ready.sem, 1)

                def features(r, ks):
                    for k in ks:
                        act.wait_ge(arg_ready.sem, arg_ready.at(r, k))
                        act.activation(feat[:, FEATS[k], :], psum[:, ARG_BANKS[k % 4], :], ACT.Exp)\
                           .then_inc(feat_ready.sem, 1)

                def keep_keys(r, c):
                    act.wait_ge(k_tok_ready.sem, k_tok_ready.at(r, c))
                    act.copy(k_tok[:, c, :], psum[:, K_TOK_BANKS[c], :]).then_inc(k_tok_kept.sem, 1)

                def step(a, a_layer, m, m_layer, m_batch):
                    if a is not None:
                        square(a, (0, 1, 2))
                    if m is not None:
                        act.wait_ge(att_t_ready.sem, att_t_ready.at(m))
                        act.copy(att_t[:, :], psum[:, TURN_BANK, :]).then_inc(att_t_kept.sem, 1)
                    if a is not None:
                        square(a, (3,))
                        features(a, range(8))
                        keep_keys(a, 0)
                    if m is not None:
                        norm.scalar_square(act, m, k=0)
                    if a is not None:
                        keep_keys(a, 1)
                        keep_keys(a, 2)
                    if m is not None:
                        norm.scalar_rstd(act, m, 0)
                        act.wait_ge(wm_in.sem, (m_layer + 1) * 16)
                        for f in range(F):
                            act.wait_ge(up_ready.sem, up_ready.at(m, f))
                            act.activation(y[:, f, :], psum[:, UP_BANKS[f % 2], :], ACT.Relu, bias=mcol("bf1", f))\
                               .then_inc(y_ready.sem, 1)
                        norm.scalar(act, m, k=1)

                steps(act, step)

            @block.vector
            def _(dve):
                dve.wait_ge(table_in.sem, 16)
                dve.wait_ge(ones_ready.sem, 1)

                def keep_qk(r, layer):
                    dve.wait_ge(wa_in.sem, (layer + 1) * 16)
                    for k in range(4):
                        t = TILES[k]
                        dve.wait_ge(proj_ready.sem, proj_ready.at(r, k))
                        dve.tensor_scalar(qk[:, t, :], psum[:, t, :], acol("bq" if t < 2 else "bk", t % 2), SCALE,
                                          ALU.add, ALU.mult).then_inc(qk_ready.sem, 1)

                def keep_v(r):
                    dve.wait_ge(v_ready.sem, v_ready.at(r))
                    dve.tensor_tensor(v[:, :, :, 0:DH],
                                      psum[:, V_BANK, :].rearrange("p (c h d) -> p c h d", c=CH, d=DH),
                                      L0A.of(wa, "bv").rearrange("p (h d) -> p h d", d=DH).unsqueeze(1)
                                      .to_broadcast([P, CH, L0_HEADS, DH]), ALU.add).then_inc(v_kept.sem, 1)

                def keep_state(r, c):
                    dve.wait_ge(kv_ready.sem, kv_ready.at(r, c))
                    dst = state if c == 0 else kv
                    dve.tensor_tensor(dst[:, c, :], psum[:, KV_BANK, 0:L0_HEADS * DV], const("kvmask"),
                                      ALU.mult).then_inc(kv_kept.sem, 1)
                    dve.wait_ge(kv_kept.sem, kv_kept.at(r, c))
                    if c == 0:
                        dve.sem_inc(state_ready.sem, 1)
                    else:
                        dve.wait_ge(state_ready.sem, state_ready.at(r, c - 1))
                        dve.tensor_tensor(state[:, c, :], state[:, c - 1, :], kv[:, c, :], ALU.add)\
                           .then_inc(state_ready.sem, 1)

                def mask(r, c):
                    for h in range(4):
                        dve.wait_ge(scores_ready.sem, scores_ready.at(r, c * 4 + h))
                        dve.tensor_tensor(scores[:, c % 2, h, :], psum[:, h, :], const("causal4"),
                                          ALU.mult).then_inc(scores_kept.sem, 1)

                def divide(r, c):
                    dve.wait_ge(num_ready.sem, num_ready.at(r, c))
                    num = psum[:, NUM_BANK, 0:L0_HEADS * DV].rearrange("p (h d) -> p h d", d=DV)
                    dve.tensor_scalar(den[:, c, :], num[:, :, DH], ATT_EPS, None, ALU.add)\
                       .then_inc(den_ready.sem, 1)
                    dve.wait_ge(den_ready.sem, den_ready.at(r, c))
                    dve.reciprocal(rden[:, c, :], den[:, c, :]).then_inc(rden_ready.sem, 1)
                    dve.wait_ge(rden_ready.sem, rden_ready.at(r, c))
                    dve.tensor_tensor(att[:, c, :].rearrange("p (h d) -> p h d", d=DH), num[:, :, 0:DH],
                                      rden[:, c, :].unsqueeze(2).to_broadcast([P, L0_HEADS, DH]), ALU.mult)\
                       .then_inc(att_ready.sem, 1)

                def scale(m, k, scaled, gain):
                    dve.wait_ge(norm.rstd_ready.sem, norm.rstd_ready.at(m, k))
                    dve.scalar_tensor_tensor(out=scaled[:, :], in0=norm.centred[:, :], scalar=gain,
                                             in1=norm.rstd[:, :], op0=ALU.mult, op1=ALU.mult)\
                       .then_inc(scaled_ready.sem, 1)
                    dve.wait_ge(scaled_ready.sem, scaled_ready.at(m, k))

                def step(a, a_layer, m, m_layer, m_batch):
                    if a is not None:
                        keep_qk(a, a_layer)
                        keep_v(a)
                    if m is not None:
                        dve.wait_ge(wm_in.sem, (m_layer + 1) * 16)
                        dve.wait_ge(out_ready.sem, out_ready.at(m, 0))
                        dve.scalar_tensor_tensor(out=res1[:, :], in0=psum[:, OUT_BANK, :], scalar=mcol("bo"),
                                                 in1=core.s[:, cols(m_batch)], op0=ALU.add, op1=ALU.add)\
                           .then_inc(res_ready.sem, 1)
                        dve.wait_ge(res_ready.sem, res_ready.at(m, 0))
                        norm.vector(dve, m, res1[:, :], 0)
                    if a is not None:
                        keep_state(a, 0)
                    if m is not None:
                        scale(m, 0, scaled1, mcol("g1"))
                        dve.tensor_scalar(h1[:, :], scaled1[:, :], mcol("be1"), None, ALU.add)\
                           .then_inc(h1_ready.sem, 1)
                    if a is not None:
                        mask(a, 0)
                        keep_state(a, 1)
                        mask(a, 1)
                        keep_state(a, 2)
                        divide(a, 0)
                    if m is not None:
                        dve.wait_ge(h1_ready.sem, h1_ready.at(m))
                        dve.wait_ge(out_ready.sem, out_ready.at(m, 1))
                        dve.scalar_tensor_tensor(out=res2[:, :], in0=psum[:, DOWN_BANK, :], scalar=mcol("bf2"),
                                                 in1=h1[:, :], op0=ALU.add, op1=ALU.add).then_inc(res_ready.sem, 1)
                    if a is not None:
                        mask(a, 2)
                        divide(a, 1)
                    if m is not None:
                        dve.wait_ge(res_ready.sem, res_ready.at(m, 1))
                        norm.vector(dve, m, res2[:, :], 1)
                    if a is not None:
                        mask(a, 3)
                        divide(a, 2)
                    if m is not None:
                        scale(m, 1, scaled2, mcol("g2"))
                        dve.tensor_scalar(core.s[:, cols(m_batch)], scaled2[:, :], mcol("be2"), None, ALU.add)\
                           .then_inc(s_ready.sem, 1)
                    if a is not None:
                        divide(a, 3)

                steps(dve, step)


L0F_LAYERS, L0F_HEADS, L0F_INNER, L0F_HID = 2, 8, 512, 341
L0F_TILES = L0F_INNER // P
L0F_HT = -(-L0F_HID // P)
L0F = Fields(("wq", L0F_INNER), ("wk", L0F_INNER), ("wv", L0F_INNER), ("wo", L0F_INNER),
             ("w1", 2 * L0F_HT * P), ("w2", L0F_HT * P), ("q_scale", 1), ("k_scale", 1), ("ln_g", 1), ("ln_b", 1),
             ("b1", 2 * L0F_HT), ("b2", 1))


def l0_ffn_layout(np, i):
    g = lambda k: i["L0_ffn_" + k]
    hid = L0F_HID

    def halves(a):
        out = np.zeros((a.shape[0], 2, L0F_HT * P), np.float32)
        for x in range(2):
            out[:, x, :hid] = a[:, x * hid:(x + 1) * hid]
        return out.reshape(a.shape[0], 2 * L0F_HT, P)

    out = []
    for n in range(L0F_LAYERS):
        w2 = np.zeros((L0F_HT * P, P), np.float32)
        w2[:hid] = g("w2")[n]
        out.append(pack(np, [
            g("wqkv")[n], blocks(np, g("wo")[n]), halves(g("w1")[n]).reshape(P, 2 * L0F_HT * P), blocks(np, w2),
            np.tile(g("q_scale")[n], 2)[:, None], np.tile(g("k_scale")[n], 2)[:, None],
            column(g("ln_g")[n]), column(g("ln_b")[n]), halves(g("b1")[n][None])[0].T, column(g("b2")[n])]))
    return {"l0f": np.stack(out)}


LAYOUTS.append(l0_ffn_layout)


def l0_ffn_phase(core):
    nc, psum = core.nc, core.psum
    H, TL, HT, W = L0F_HEADS, L0F_TILES, L0F_HT, 64
    with Phase(core, "l0f") as ph:
        w = ph.buf("w", L0F.width)
        col = lambda name, k=0: L0F.of(w, name, k, 1)
        swap = ph.buf("swap", 2, P)
        h_in = ph.buf("h_in", N)
        sq = ph.buf("sq", 2, N)
        log, rinv = ph.buf("log", 2, N), ph.buf("rinv", 2, N)
        unit = ph.buf("unit", 2, N)
        unit_s = ph.buf("unit_s", 2, N)
        by_cos, by_sin = ph.buf("by_cos", 2, N), ph.buf("by_sin", 2, N)
        qk = ph.buf("qk", 2 * TL, N)
        v = ph.buf("v", CH, L0F_INNER)
        sim = ph.buf("sim", H, 2 * P)
        nmax, total, rtotal = ph.buf("nmax", CH, H), ph.buf("total", CH, H), ph.buf("rtotal", CH, H)
        prob = ph.buf("prob", H, 2 * P)
        prob_n = ph.buf("prob_n", H, 2 * P)
        prob_t = ph.buf("prob_t", 2 * H, P)
        o = ph.buf("o", TL, N)
        x1, shifted = ph.buf("x1", N), ph.buf("shifted", N)
        scaled, hn = ph.buf("scaled", N), ph.buf("hn", N)
        gelu, hidden = ph.buf("gelu", HT, N), ph.buf("hidden", HT, N)
        head = [(s // 2) % 2 + 2 * (2 * (s // 4) + s % 2) for s in range(H)]

        table = ph.buf("table", CONST_L0F.width)
        const = lambda name: CONST_L0F.of(table, name)
        table_in = ph.semaphore("table_in")
        passed = ph.semaphore("passed")
        w_in, zeroed = ph.semaphore("w_in"), ph.semaphore("zeroed", 3)
        copied = ph.semaphore("copied", B)
        round_done = ph.semaphore("round_done")
        swap_ready = ph.semaphore("swap_ready", 2)
        h_ready = ph.semaphore("h_ready", 2)
        qk_raw, sq_ready = ph.semaphore("qk_raw", 8), ph.semaphore("sq_ready", 8)
        sum_ready = ph.semaphore("sum_ready", 8)
        log_ready, rinv_ready = ph.semaphore("log_ready", 8), ph.semaphore("rinv_ready", 8)
        scaled_unit = ph.semaphore("scaled_unit", 8)
        unit_ready, rot_ready = ph.semaphore("unit_ready", 8), ph.semaphore("rot_ready", 8)
        cos_ready, sin_ready = ph.semaphore("cos_ready", 8), ph.semaphore("sin_ready", 8)
        qk_ready = ph.semaphore("qk_ready", 8)
        v_ready, v_kept = ph.semaphore("v_ready", CH), ph.semaphore("v_kept", CH)
        sim_ready, sim_kept = ph.semaphore("sim_ready", CH), ph.semaphore("sim_kept", CH)
        nmax_ready, prob_ready = ph.semaphore("nmax_ready", CH), ph.semaphore("prob_ready", CH)
        rtotal_ready, prob_n_ready = ph.semaphore("rtotal_ready", CH), ph.semaphore("prob_n_ready", CH)
        turned, turned_kept = ph.semaphore("turned", 4 * CH), ph.semaphore("turned_kept", 4 * CH)
        o_ready, o_kept = ph.semaphore("o_ready", CH), ph.semaphore("o_kept", CH)
        y_ready = ph.semaphore("y_ready", 2)
        x1_ready, shifted_ready = ph.semaphore("x1_ready"), ph.semaphore("shifted_ready", 2)
        norm = ColumnNorm(ph, "norm", (1, 2))
        scaled_ready, hn_ready = ph.semaphore("scaled_ready"), ph.semaphore("hn_ready")
        up_ready, gelu_ready, hidden_ready = ph.semaphore("up_ready", 2 * HT), ph.semaphore("gelu_ready", HT), ph.semaphore("hidden_ready", HT)

        def keys(c):
            return slice(W if c else P, 2 * P)

        with nc.Block() as block:
            @block.sync
            def _(sp):
                sp.dma_start(table[:, :], core.dram["const_l0f"]).then_inc(table_in.sem, 16)
                with sp.Fori(0, L0F_LAYERS) as layer:
                    sp.wait_ge(round_done.sem, layer * B + 1)
                    sp.dma_start(w[:, :], core.dram["l0f"][bass.ds(layer, 1), :, :].rearrange("a p c -> (a p) c"))\
                      .then_inc(w_in.sem, 16)

            @block.gpsimd
            def _(pool):
                pool.wait_ge(table_in.sem, 16)
                for b in range(B):
                    pool.tensor_copy(core.g[:, b * N:(b + 1) * N], core.xn[:, b * N:(b + 1) * N])\
                        .then_inc(copied.sem, 1)
                with pool.Fori(0, L0F_LAYERS) as layer:
                    pool.wait_ge(w_in.sem, layer * 16 + 16)
                    apart(pool, passed)
                    with pool.Fori(0, B) as b:
                        r = layer * B + b
                        pool.wait_ge(round_done.sem, r + 1)
                        for t in range(8):
                            pool.wait_ge(unit_ready.sem, unit_ready.at(r, t))
                            if t >= 2:
                                pool.wait_ge(qk_ready.sem, qk_ready.at(r, t - 2))
                            apart(pool, passed)
                            pool.tensor_scalar(unit_s[:, t % 2, :], unit[:, t % 2, :],
                                               col("q_scale" if t < 4 else "k_scale"), None, ALU.mult)\
                                .then_inc(scaled_unit.sem, 1)
                            pool.wait_ge(scaled_unit.sem, scaled_unit.at(r, t))
                            pool.tensor_tensor(by_cos[:, t % 2, :], unit_s[:, t % 2, :],
                                               const("rope_qc" if t < 4 else "rope_kc"), ALU.mult)\
                                .then_inc(cos_ready.sem, 1)
                        for c in range(CH):
                            pool.wait_ge(rtotal_ready.sem, rtotal_ready.at(r, c))
                            pool.wait_ge(prob_ready.sem, prob_ready.at(r, c))
                            if c >= 1:
                                pool.wait_ge(turned.sem, turned.at(r, 4 * c - 1))
                            k = keys(c)
                            pool.tensor_tensor(prob_n[:, :, k], prob[:, :, k],
                                               rtotal[:, c, :].unsqueeze(2).to_broadcast([P, H, 2 * P - k.start]),
                                               ALU.mult).then_inc(prob_n_ready.sem, 1)

            @block.tensor
            def _(pe):
                pe.wait_ge(table_in.sem, 16)
                pe.wait_ge(zeroed.sem, 3)
                with pe.Fori(0, L0F_LAYERS) as layer:
                    pe.wait_ge(w_in.sem, layer * 16 + 16)
                    apart(pe, passed)
                    with pe.Fori(0, B) as b:
                        r = layer * B + b
                        pe.wait_ge(h_ready.sem, h_ready.at(r, 1))

                        def project(t):
                            if t >= 2:
                                pe.wait_ge(unit_ready.sem, unit_ready.at(r, t - 2))
                            pe.matmul(psum[:, t % 2, :], L0F.of(w, "wq" if t < 4 else "wk", t % 4, P), h_in[:, :],
                                      start=True, stop=True).then_inc(qk_raw.sem, 1)

                        def sum_squares(t):
                            pe.wait_ge(sq_ready.sem, sq_ready.at(r, t))
                            pe.matmul(psum[:, 2 + t % 2, :], const("ones64"), sq[:, t % 2, :],
                                      start=True, stop=True).then_inc(sum_ready.sem, 1)

                        def rotate(t):
                            pe.wait_ge(unit_ready.sem, unit_ready.at(r, t))
                            if t == 0:
                                pe.wait_ge(swap_ready.sem, swap_ready.at(layer, 1))
                            if t >= 2:
                                pe.wait_ge(sin_ready.sem, sin_ready.at(r, t - 2))
                            pe.matmul(psum[:, 4 + t % 2, :], swap[:, 0 if t < 4 else 1, :], unit[:, t % 2, :],
                                      start=True, stop=True).then_inc(rot_ready.sem, 1)

                        def value(c):
                            if c >= 2:
                                pe.wait_ge(v_kept.sem, v_kept.at(r, c - 2))
                            pe.matmul(psum[:, 6 + c % 2, :], h_in[:, c * P:(c + 1) * P], L0F.of(w, "wv"),
                                      start=True, stop=True).then_inc(v_ready.sem, 1)

                        project(0)
                        project(1)
                        value(0)
                        value(1)
                        for t in range(8):
                            sum_squares(t)
                            if t == 2 or t == 4:
                                value(t // 2 + 1)
                            rotate(t)
                            if t + 2 < 8:
                                project(t + 2)

                        def score(c):
                            if c == 0:
                                pe.wait_ge(qk_ready.sem, qk_ready.at(r, 7))
                                pe.wait_ge(v_kept.sem, v_kept.at(r, CH - 1))
                            else:
                                pe.wait_ge(sim_kept.sem, sim_kept.at(r, c - 1))
                            k = keys(c)
                            first = (c - 1) * P + k.start
                            for u in range(2):
                                for bank in range(4):
                                    h = head[2 * bank + u]
                                    rows = slice(64 * (h % 2), 64 * (h % 2) + 64)
                                    mm = pe.matmul(psum[:, bank, u * 2 * P + k.start:u * 2 * P + 2 * P],
                                                   qk[rows, h // 2, c * P:(c + 1) * P],
                                                   qk[rows, TL + h // 2, first:(c + 1) * P],
                                                   start=(u == 0), stop=(u == 1), skip_group_check=True)
                            mm.then_inc(sim_ready.sem, 1)

                        def turn(c):
                            pe.wait_ge(prob_n_ready.sem, prob_n_ready.at(r, c))
                            for j in range(4):
                                n = 4 * c + j
                                if n >= 3:
                                    pe.wait_ge(turned_kept.sem, turned_kept.at(r, n - 3))
                                for i in range(4):
                                    slot, own = 2 * j + i // 2, i % 2
                                    if c == 0 and not own:
                                        continue
                                    mm = pe.transpose(psum[:, 4 + n % 3, i * P:(i + 1) * P],
                                                      prob_n[:, slot, own * P:(own + 1) * P], core.c("ident"))
                                mm.then_inc(turned.sem, 1)

                        def draw(c):
                            if c >= 1:
                                pe.wait_ge(o_kept.sem, o_kept.at(r, c - 1))
                            pe.wait_ge(turned_kept.sem, turned_kept.at(r, 4 * c + 3))
                            for s in range(H):
                                h = head[s]
                                rows = slice(64 * (h % 2), 64 * (h % 2) + 64)
                                dst = psum[rows, 7, (h // 2) * P:(h // 2 + 1) * P]
                                for own in ((0, 1) if c else (1,)):
                                    mm = pe.matmul(dst, v[:, c - 1 + own, h * W:(h + 1) * W],
                                                   prob_t[:, 2 * s + own, :],
                                                   start=(own == 0 or c == 0) , stop=(own == 1),
                                                   skip_group_check=True)
                            mm.then_inc(o_ready.sem, 1)

                        score(0)
                        for c in range(CH):
                            if c + 1 < CH:
                                score(c + 1)
                            turn(c)
                            draw(c)
                        pe.wait_ge(o_kept.sem, o_kept.at(r, CH - 1))
                        for t in range(TL):
                            mm = pe.matmul(psum[:, 0, :], L0F.of(w, "wo", t, P), o[:, t, :],
                                           start=(t == 0), stop=(t == TL - 1))
                        mm.then_inc(y_ready.sem, 1)
                        pe.wait_ge(shifted_ready.sem, shifted_ready.at(r, 1))
                        norm.tensor(pe, r, shifted[:, :])
                        pe.wait_ge(hn_ready.sem, hn_ready.at(r))
                        for t in [HT + x for x in range(HT)] + list(range(HT)):
                            pe.matmul(psum[:, 2 + t, :], L0F.of(w, "w1", t, P), hn[:, :], start=True, stop=True)\
                              .then_inc(up_ready.sem, 1)
                        for t in range(HT):
                            pe.wait_ge(hidden_ready.sem, hidden_ready.at(r, t))
                            mm = pe.matmul(psum[:, 0, :], L0F.of(w, "w2", t, P), hidden[:, t, :],
                                           start=(t == 0), stop=(t == HT - 1))
                        mm.then_inc(y_ready.sem, 1)

            @block.scalar
            def _(act):
                act.wait_ge(table_in.sem, 16)
                with act.Fori(0, L0F_LAYERS) as layer:
                    act.wait_ge(w_in.sem, layer * 16 + 16)
                    apart(act, passed)
                    with act.Fori(0, B) as b:
                        r = layer * B + b
                        act.wait_ge(round_done.sem, r + 1)
                        apart(act, passed)
                        act.preload_act_table_set(EXP_LN_SET)

                        def square(t):
                            act.wait_ge(qk_raw.sem, qk_raw.at(r, t))
                            if t >= 2:
                                act.wait_ge(sum_ready.sem, sum_ready.at(r, t - 2))
                            act.activation(sq[:, t % 2, :], psum[:, t % 2, :], ACT.Square).then_inc(sq_ready.sem, 1)

                        def inverse(t):
                            act.wait_ge(sum_ready.sem, sum_ready.at(r, t))
                            act.activation(log[:, t % 2, :], psum[:, 2 + t % 2, :], ACT.Ln, scale=2.0 ** 30,
                                           bias=const("eps_l2")).then_inc(log_ready.sem, 1)
                            act.wait_ge(log_ready.sem, log_ready.at(r, t))
                            if t >= 2:
                                act.wait_ge(unit_ready.sem, unit_ready.at(r, t - 2))
                            act.activation(rinv[:, t % 2, :], log[:, t % 2, :], ACT.Exp, scale=-0.5,
                                           bias=const("l2_back")).then_inc(rinv_ready.sem, 1)

                        def keep_value(c):
                            act.wait_ge(v_ready.sem, v_ready.at(r, c))
                            act.copy(v[:, c, :], psum[:, 6 + c % 2, :]).then_inc(v_kept.sem, 1)

                        square(0)
                        square(1)
                        keep_value(0)
                        keep_value(1)
                        for t in range(8):
                            inverse(t)
                            if t == 2 or t == 4:
                                keep_value(t // 2 + 1)
                            if t + 2 < 8:
                                square(t + 2)
                        for c in range(CH):
                            act.wait_ge(nmax_ready.sem, nmax_ready.at(r, c))
                            if c >= 1:
                                act.wait_ge(prob_n_ready.sem, prob_n_ready.at(r, c - 1))
                            k = keys(c)
                            for s in range(H):
                                e = act.activation(prob[:, s, k], sim[:, s, k], ACT.Exp, bias=nmax[:, c, s:s + 1],
                                                   accum_out=total[:, c, s:s + 1])
                            e.then_inc(prob_ready.sem, 1)
                            for j in range(4):
                                n = 4 * c + j
                                act.wait_ge(turned.sem, turned.at(r, n))
                                if c >= 1:
                                    act.wait_ge(o_ready.sem, o_ready.at(r, c - 1))
                                dst = prob_t[:, 4 * j:4 * j + 4, :]
                                src = psum[:, 4 + n % 3, :].rearrange("p (i q) -> p i q", i=4)
                                if c == 0:
                                    dst, src = prob_t[:, 4 * j + 1:4 * j + 4:2, :], src[:, 1:4:2, :]
                                act.copy(dst, src).then_inc(turned_kept.sem, 1)
                            act.wait_ge(o_ready.sem, o_ready.at(r, c))
                            act.copy(o[:, :, c * P:(c + 1) * P], psum[:, 7, :].rearrange("p (t q) -> p t q", t=TL))\
                               .then_inc(o_kept.sem, 1)
                        norm.scalar(act, r)
                        for t in range(HT):
                            act.wait_ge(up_ready.sem, up_ready.at(r, t))
                            act.activation(gelu[:, t, :], psum[:, 2 + HT + t, :], ACT.Gelu, bias=col("b1", HT + t))\
                               .then_inc(gelu_ready.sem, 1)

            @block.vector
            def _(dve):
                dve.wait_ge(table_in.sem, 16)
                dve.sem_inc(round_done.sem, 1)
                dve.memset(h_in[64:P, 0:1], 0.0).then_inc(zeroed.sem, 1)
                dve.memset(shifted[64:P, 0:1], 0.0).then_inc(zeroed.sem, 1)
                dve.memset(prob_n[:, :, 0:W], 0.0).then_inc(zeroed.sem, 1)
                dve.wait_ge(copied.sem, B)
                with dve.Fori(0, L0F_LAYERS) as layer:
                    dve.wait_ge(w_in.sem, layer * 16 + 16)
                    dve.tensor_scalar(swap[:, 0, :], const("swap64"), col("q_scale"), None, ALU.mult)\
                       .then_inc(swap_ready.sem, 1)
                    dve.tensor_scalar(swap[:, 1, :], const("swap64"), col("k_scale"), None, ALU.mult)\
                       .then_inc(swap_ready.sem, 1)
                    apart(dve, passed)
                    with dve.Fori(0, B) as b:
                        r = layer * B + b
                        dve.wait_ge(round_done.sem, r + 1)
                        dve.tensor_copy(h_in[0:64, :], core.g[0:64, cols(b)]).then_inc(h_ready.sem, 1)
                        dve.tensor_copy(h_in[64:P, 1:N], core.g[64:P, bass.ds(b * N, N - 1)]).then_inc(h_ready.sem, 1)

                        def divide(t):
                            dve.wait_ge(rinv_ready.sem, rinv_ready.at(r, t))
                            if t >= 2:
                                dve.wait_ge(rot_ready.sem, rot_ready.at(r, t - 2))
                                dve.wait_ge(cos_ready.sem, cos_ready.at(r, t - 2))
                            dve.scalar_tensor_tensor(out=unit[:, t % 2, :], in0=rinv[:, t % 2, :], scalar=1e12,
                                                     in1=psum[:, t % 2, :], op0=ALU.min, op1=ALU.mult)\
                               .then_inc(unit_ready.sem, 1)

                        def rotate(t):
                            dve.wait_ge(rot_ready.sem, rot_ready.at(r, t))
                            dve.tensor_tensor(by_sin[:, t % 2, :], psum[:, 4 + t % 2, :],
                                              const("rope_qs" if t < 4 else "rope_ks"), ALU.mult)\
                               .then_inc(sin_ready.sem, 1)
                            dve.wait_ge(sin_ready.sem, sin_ready.at(r, t))
                            dve.wait_ge(cos_ready.sem, cos_ready.at(r, t))
                            dve.tensor_tensor(qk[:, t, :], by_cos[:, t % 2, :], by_sin[:, t % 2, :], ALU.add)\
                               .then_inc(qk_ready.sem, 1)

                        for t in range(9):
                            if t < 8:
                                divide(t)
                            if t >= 1:
                                rotate(t - 1)

                        def mask(c):
                            dve.wait_ge(sim_ready.sem, sim_ready.at(r, c))
                            if c >= 1:
                                dve.wait_ge(prob_ready.sem, prob_ready.at(r, c - 1))
                            k = keys(c)
                            bias = const("window" if c else "window_first")[:, k]
                            dve.tensor_tensor(sim[:, :, k],
                                              psum[:, 0:4, :].rearrange("p b (u k) -> p (b u) k", u=2)[:, :, k],
                                              bias.unsqueeze(1).to_broadcast([P, H, 2 * P - k.start]), ALU.add)\
                               .then_inc(sim_kept.sem, 1)
                            dve.wait_ge(sim_kept.sem, sim_kept.at(r, c))
                            dve.tensor_reduce(nmax[:, c, :], sim[:, :, k], AX.X, ALU.max, negate=True)\
                               .then_inc(nmax_ready.sem, 1)

                        for c in range(CH + 1):
                            if c < CH:
                                mask(c)
                            if c >= 1:
                                dve.wait_ge(prob_ready.sem, prob_ready.at(r, c - 1))
                                dve.reciprocal(rtotal[:, c - 1, :], total[:, c - 1, :]).then_inc(rtotal_ready.sem, 1)
                        dve.wait_ge(y_ready.sem, y_ready.at(r, 0))
                        dve.tensor_tensor(x1[:, :], core.g[:, cols(b)], psum[:, 0, :], ALU.add)\
                           .then_inc(x1_ready.sem, 1)
                        dve.wait_ge(x1_ready.sem, x1_ready.at(r))
                        dve.tensor_copy(shifted[0:64, :], x1[0:64, :]).then_inc(shifted_ready.sem, 1)
                        dve.tensor_copy(shifted[64:P, 1:N], x1[64:P, 0:N - 1]).then_inc(shifted_ready.sem, 1)
                        dve.wait_ge(shifted_ready.sem, shifted_ready.at(r, 1))
                        norm.vector(dve, r, shifted[:, :])
                        dve.wait_ge(norm.rstd_ready.sem, norm.rstd_ready.at(r))
                        dve.scalar_tensor_tensor(out=scaled[:, :], in0=norm.centred[:, :], scalar=col("ln_g"),
                                                 in1=norm.rstd[:, :], op0=ALU.mult, op1=ALU.mult)\
                           .then_inc(scaled_ready.sem, 1)
                        dve.wait_ge(scaled_ready.sem, scaled_ready.at(r))
                        dve.tensor_scalar(hn[:, :], scaled[:, :], col("ln_b"), None, ALU.add).then_inc(hn_ready.sem, 1)
                        for t in range(HT):
                            dve.wait_ge(up_ready.sem, up_ready.at(r, HT + t))
                            dve.wait_ge(gelu_ready.sem, gelu_ready.at(r, t))
                            dve.scalar_tensor_tensor(out=hidden[:, t, :], in0=psum[:, 2 + t, :], scalar=col("b1", t),
                                                     in1=gelu[:, t, :], op0=ALU.add, op1=ALU.mult)\
                               .then_inc(hidden_ready.sem, 1)
                        dve.wait_ge(y_ready.sem, y_ready.at(r, 1))
                        dve.scalar_tensor_tensor(out=core.g[:, cols(b)], in0=psum[:, 0, :], scalar=col("b2"),
                                                 in1=x1[:, :], op0=ALU.add, op1=ALU.add).then_inc(round_done.sem, 1)


L1_HEADS, L1_INTER = 8, 512
L1A = Fields(("wq", L1_HEADS * P), ("wk", L1_HEADS * P), ("wv", L1_HEADS * P), ("wo", L1_HEADS * P),
             ("gate", L1_INTER), ("up", L1_INTER), ("down", L1_INTER),
             ("attn_norm", 1), ("out_norm", 1), ("mlp_norm", 1))


def l1_attn_layout(np, i):
    g = lambda k: i["L1_attn_" + k]
    return {"l1a": pack(np, [
        g("Wq"), g("Wk"), g("Wv"), blocks(np, g("Wo")), g("Wgate"), g("Wup"), blocks(np, g("Wdown")),
        column(g("attn_norm_w")), column(g("attn_out_norm_w")), column(g("mlp_norm_w"))])}


LAYOUTS.append(l1_attn_layout)


def l1_attn_phase(core):
    nc, psum = core.nc, core.psum
    H, F = L1_HEADS, L1_INTER // P
    Q, K, S, O, Y, V = 0, 1, 2, 4, 6, 7
    with Phase(core, "l1a") as ph:
        w = ph.buf("w", L1A.width)
        col = lambda name: L1A.of(w, name)
        h_t = ph.buf("h", N)
        v = ph.buf("v", CH, H * P)
        q = ph.buf("q", 2, N)
        k = ph.buf("k", 2, N)
        scores = ph.buf("scores", 2, CH, N)
        normed = ph.buf("normed", 2, N)
        out_sq, out_log, out_rstd = ph.buf("out_sq", N), ph.buf("out_log", N), ph.buf("out_rstd", N)
        x1 = ph.buf("x1", N)
        silu = ph.buf("silu", F, N)
        hidden = ph.buf("hidden", F, N)

        passed = ph.semaphore("passed")
        w_in = ph.semaphore("w_in")
        round_done = ph.semaphore("round_done")
        norm = ColumnNorm(ph, "norm", (V, V), (V, V), centre=False)
        h_ready = ph.semaphore("h_ready", 2)
        v_ready = ph.semaphore("v_ready", 2 * CH)
        v_kept = ph.semaphore("v_kept", 2 * CH)
        q_ready, q_kept = ph.semaphore("q_ready", H), ph.semaphore("q_kept", H)
        k_ready, k_kept = ph.semaphore("k_ready", H), ph.semaphore("k_kept", H)
        scores_ready = ph.semaphore("scores_ready", H * CH)
        scores_kept = ph.semaphore("scores_kept", H * CH)
        out_ready = ph.semaphore("out_ready", H)
        out_sq_ready = ph.semaphore("out_sq_ready", H)
        out_var_ready = ph.semaphore("out_var_ready", H)
        out_log_ready = ph.semaphore("out_log_ready", H)
        out_rstd_ready = ph.semaphore("out_rstd_ready", H)
        normed_ready = ph.semaphore("normed_ready", H)
        y_ready = ph.semaphore("y_ready", 2)
        x1_ready = ph.semaphore("x1_ready")
        gate_ready, silu_ready = ph.semaphore("gate_ready", F), ph.semaphore("silu_ready", F)
        up_ready, hidden_ready = ph.semaphore("up_ready", F), ph.semaphore("hidden_ready", F)

        with nc.Block() as block:
            @block.sync
            def _(sp):
                sp.dma_start(w[:, :], core.dram["l1a"]).then_inc(w_in.sem, 16)

            @block.tensor
            def _(pe):
                pe.wait_ge(w_in.sem, 16)
                with pe.Fori(0, B) as b:
                    pe.wait_ge(round_done.sem, round_done.at(b))
                    norm.tensor(pe, b, None, 0)
                    pe.wait_ge(h_ready.sem, h_ready.at(b, 0))
                    for c in range(CH):
                        for half in range(2):
                            n = 2 * c + half
                            if n >= 4:
                                pe.wait_ge(v_kept.sem, v_kept.at(b, n - 4))
                            pe.matmul(psum[:, n % 4, :], h_t[:, c * P:(c + 1) * P],
                                      L1A.of(w, "wv", half, N), start=True, stop=True)\
                              .then_inc(v_ready.sem, 1)
                    pe.wait_ge(v_kept.sem, v_kept.at(b, 2 * CH - 1))

                    def query_key(h):
                        if h >= 1:
                            pe.wait_ge(q_kept.sem, q_kept.at(b, h - 1))
                            pe.wait_ge(k_kept.sem, k_kept.at(b, h - 1))
                        pe.matmul(psum[:, Q, :], L1A.of(w, "wq", h, P), h_t[:, :], start=True, stop=True)\
                          .then_inc(q_ready.sem, 1)
                        pe.matmul(psum[:, K, :], L1A.of(w, "wk", h, P), h_t[:, :], start=True, stop=True)\
                          .then_inc(k_ready.sem, 1)

                    def score(h, c):
                        n = h * CH + c
                        if n >= 2:
                            pe.wait_ge(scores_kept.sem, scores_kept.at(b, n - 2))
                        pe.matmul(psum[:, S + c % 2, 0:N - c * P], k[:, h % 2, c * P:(c + 1) * P],
                                  q[:, h % 2, c * P:N], start=True, stop=True).then_inc(scores_ready.sem, 1)

                    def output(h):
                        for c in range(CH):
                            pe.wait_ge(scores_kept.sem, scores_kept.at(b, h * CH + c))
                            mm = pe.matmul(psum[:, O + h % 2, c * P:N], v[:, c, h * P:(h + 1) * P],
                                           scores[:, h % 2, c, 0:N - c * P], start=(c == 0), stop=(c == CH - 1))
                        mm.then_inc(out_ready.sem, 1)

                    def out_var(h):
                        pe.wait_ge(out_sq_ready.sem, out_sq_ready.at(b, h))
                        pe.matmul(psum[:, V, :], core.c("mean"), out_sq[:, :], start=True, stop=True)\
                          .then_inc(out_var_ready.sem, 1)

                    def project(h):
                        pe.wait_ge(normed_ready.sem, normed_ready.at(b, h))
                        mm = pe.matmul(psum[:, Y, :], L1A.of(w, "wo", h, P), normed[:, h % 2, :],
                                       start=(h == 0), stop=(h == H - 1))
                        if h == H - 1:
                            mm.then_inc(y_ready.sem, 1)

                    query_key(0)
                    for h in range(H):
                        pe.wait_ge(q_kept.sem, q_kept.at(b, h))
                        pe.wait_ge(k_kept.sem, k_kept.at(b, h))
                        score(h, 0)
                        score(h, 1)
                        if h + 1 < H:
                            query_key(h + 1)
                        score(h, 2)
                        score(h, 3)
                        if h >= 1:
                            out_var(h - 1)
                        output(h)
                        if h >= 1:
                            project(h - 1)
                    out_var(H - 1)
                    project(H - 1)

                    norm.tensor(pe, b, None, 1)
                    pe.wait_ge(h_ready.sem, h_ready.at(b, 1))
                    for f in range(F):
                        if f >= 1:
                            pe.wait_ge(silu_ready.sem, silu_ready.at(b, f - 1))
                            pe.wait_ge(hidden_ready.sem, hidden_ready.at(b, f - 1))
                        pe.matmul(psum[:, Q, :], L1A.of(w, "gate", f, P), h_t[:, :], start=True, stop=True)\
                          .then_inc(gate_ready.sem, 1)
                        pe.matmul(psum[:, K, :], L1A.of(w, "up", f, P), h_t[:, :], start=True, stop=True)\
                          .then_inc(up_ready.sem, 1)
                    for f in range(F):
                        pe.wait_ge(hidden_ready.sem, hidden_ready.at(b, f))
                        mm = pe.matmul(psum[:, Y, :], L1A.of(w, "down", f, P), hidden[:, f, :],
                                       start=(f == 0), stop=(f == F - 1))
                    mm.then_inc(y_ready.sem, 1)

            @block.scalar
            def _(act):
                with act.Fori(0, B) as b:
                    act.wait_ge(round_done.sem, round_done.at(b))
                    apart(act, passed)
                    act.preload_act_table_set(EXP_LN_SET)
                    norm.scalar(act, b, core.xn[:, cols(b)], 0)
                    for n in range(2 * CH):
                        act.wait_ge(v_ready.sem, v_ready.at(b, n))
                        act.copy(v[:, n // 2, (n % 2) * N:(n % 2 + 1) * N], psum[:, n % 4, :])\
                           .then_inc(v_kept.sem, 1)

                    def keep(h):
                        act.wait_ge(q_ready.sem, q_ready.at(b, h))
                        act.copy(q[:, h % 2, :], psum[:, Q, :]).then_inc(q_kept.sem, 1)
                        act.wait_ge(k_ready.sem, k_ready.at(b, h))
                        act.copy(k[:, h % 2, :], psum[:, K, :]).then_inc(k_kept.sem, 1)

                    def out_norm(h):
                        act.wait_ge(out_ready.sem, out_ready.at(b, h))
                        if h >= 1:
                            act.wait_ge(normed_ready.sem, normed_ready.at(b, h - 1))
                        act.activation(out_sq[:, :], psum[:, O + h % 2, :], ACT.Square)\
                           .then_inc(out_sq_ready.sem, 1)
                        act.wait_ge(out_var_ready.sem, out_var_ready.at(b, h))
                        act.activation(out_log[:, :], psum[:, V, :], ACT.Ln, bias=core.c("eps5"))\
                           .then_inc(out_log_ready.sem, 1)
                        act.wait_ge(out_log_ready.sem, out_log_ready.at(b, h))
                        act.activation(out_rstd[:, :], out_log[:, :], ACT.Exp, scale=-0.5)\
                           .then_inc(out_rstd_ready.sem, 1)

                    keep(0)
                    for h in range(H):
                        if h + 1 < H:
                            keep(h + 1)
                        out_norm(h)
                    act.wait_ge(x1_ready.sem, x1_ready.at(b))
                    norm.scalar(act, b, x1[:, :], 1)
                    for f in range(F):
                        act.wait_ge(gate_ready.sem, gate_ready.at(b, f))
                        act.activation(silu[:, f, :], psum[:, Q, :], ACT.Silu).then_inc(silu_ready.sem, 1)

            @block.vector
            def _(dve):
                dve.sem_inc(round_done.sem, 1)
                dve.wait_ge(w_in.sem, 16)
                with dve.Fori(0, B) as b:
                    dve.wait_ge(norm.rstd_ready.sem, norm.rstd_ready.at(b, 0))
                    dve.scalar_tensor_tensor(out=h_t[:, :], in0=core.xn[:, cols(b)], scalar=col("attn_norm"),
                                             in1=norm.rstd[:, :], op0=ALU.mult, op1=ALU.mult)\
                       .then_inc(h_ready.sem, 1)

                    def mask(h):
                        for c in range(CH):
                            dve.wait_ge(scores_ready.sem, scores_ready.at(b, h * CH + c))
                            dve.tensor_tensor(scores[:, h % 2, c, 0:N - c * P], psum[:, S + c % 2, 0:N - c * P],
                                              core.c("causal")[:, 0:N - c * P], ALU.mult)\
                               .then_inc(scores_kept.sem, 1)

                    def apply_norm(h):
                        dve.wait_ge(out_rstd_ready.sem, out_rstd_ready.at(b, h))
                        dve.scalar_tensor_tensor(out=normed[:, h % 2, :], in0=psum[:, O + h % 2, :],
                                                 scalar=col("out_norm"), in1=out_rstd[:, :],
                                                 op0=ALU.mult, op1=ALU.mult).then_inc(normed_ready.sem, 1)

                    for h in range(H):
                        mask(h)
                        if h >= 1:
                            apply_norm(h - 1)
                    apply_norm(H - 1)
                    dve.wait_ge(y_ready.sem, y_ready.at(b, 0))
                    dve.tensor_tensor(x1[:, :], core.xn[:, cols(b)], psum[:, Y, :], ALU.add)\
                       .then_inc(x1_ready.sem, 1)
                    dve.wait_ge(norm.rstd_ready.sem, norm.rstd_ready.at(b, 1))
                    dve.scalar_tensor_tensor(out=h_t[:, :], in0=x1[:, :], scalar=col("mlp_norm"),
                                             in1=norm.rstd[:, :], op0=ALU.mult, op1=ALU.mult)\
                       .then_inc(h_ready.sem, 1)
                    for f in range(F):
                        dve.wait_ge(silu_ready.sem, silu_ready.at(b, f))
                        dve.wait_ge(up_ready.sem, up_ready.at(b, f))
                        dve.tensor_tensor(hidden[:, f, :], silu[:, f, :], psum[:, K, :], ALU.mult)\
                           .then_inc(hidden_ready.sem, 1)
                    dve.wait_ge(y_ready.sem, y_ready.at(b, 1))
                    dve.tensor_tensor(core.s[:, cols(b)], x1[:, :], psum[:, Y, :], ALU.add)\
                       .then_inc(round_done.sem, 1)


L1_EXPERTS, L1_SLOTS = 64, 32
L1_E = L1_EXPERTS * L1_SLOTS
ET = L1_E // P
PIECE = Fields(("w", 16 * P), ("bias", 4 * P))


def l1_ffn_layout(np, i):
    g = lambda k: i["L1_ffn_" + k]
    pieces = []
    for n in range(4):
        w = g("expert_w")[16 * n:16 * n + 16].transpose(1, 0, 2).reshape(P, 16 * P)
        bias = np.repeat(g("expert_b")[16 * n:16 * n + 16], L1_SLOTS, axis=0)
        pieces.append(pack(np, [w, blocks(np, bias)]))
    return {"l1f_phi": g("phi_w").T, "l1f_phi_b": np.tile(g("phi_b"), (P, 1)), "l1f_experts": np.stack(pieces)}


LAYOUTS.append(l1_ffn_layout)


def l1_ffn_phase(core):
    with ExitStack() as ctx:
        combine = ctx.enter_context(core.nc.sbuf_tensor("l1f_combine", [P, ET, T], F32))
        l1_route_phase(core, combine)
        l1_expert_phase(core, combine)


def l1_route_phase(core, combine):
    nc, psum = core.nc, core.psum
    NT = T // P
    LOGIT, TURN = 4, 6
    with Phase(core, "l1r") as ph:
        phi = ph.buf("phi", L1_E)
        phi_b = ph.buf("phi_b", L1_E)
        logit = ph.buf("logit", L1_E)
        dispatch = ph.buf("dispatch", L1_E)
        combine_tok = core.g
        x_t, x_tok = ph.buf("x_t", P), ph.buf("x_tok", P)
        nmax_e = ph.buf("max_e", L1_EXPERTS)
        nmax_s = ph.buf("max_s", L1_SLOTS)
        sum_e, rsum_e = ph.buf("sum_e", L1_EXPERTS), ph.buf("rsum_e", L1_EXPERTS)
        sum_s, rsum_s = ph.buf("sum_s", L1_SLOTS), ph.buf("rsum_s", P)
        rsum_t = ph.buf("rsum_t", P)

        w_in, zeroed = ph.semaphore("w_in"), ph.semaphore("zeroed")
        round_done = ph.semaphore("round_done")
        x_t_ready, x_turned, x_tok_ready = ph.semaphore("x_t_ready"), ph.semaphore("x_turned"), ph.semaphore("x_tok_ready")
        logit_ready, logit_kept = ph.semaphore("logit_ready", 4), ph.semaphore("logit_kept", 4)
        max_ready = ph.semaphore("max_ready", 2)
        shifted_ready, exp_ready = ph.semaphore("shifted_ready", 2), ph.semaphore("exp_ready", 2)
        sum_ready, rsum_ready = ph.semaphore("sum_ready", 2), ph.semaphore("rsum_ready", 2)
        dispatch_ready, summed = ph.semaphore("dispatch_ready"), ph.semaphore("summed")
        rsum_turned, rsum_t_ready = ph.semaphore("rsum_turned"), ph.semaphore("rsum_t_ready")
        turned, turned_kept = ph.semaphore("turned", 4), ph.semaphore("turned_kept", 4)

        by_expert = lambda a: a.rearrange("p (n s) -> p n s", s=L1_SLOTS)
        by_slot = lambda a: a.rearrange("p (n s) -> p s n", s=L1_SLOTS)

        with nc.Block() as block:
            @block.sync
            def _(sp):
                sp.dma_start(phi[:, :], core.dram["l1f_phi"]).then_inc(w_in.sem, 16)
                sp.dma_start(phi_b[:, :], core.dram["l1f_phi_b"]).then_inc(w_in.sem, 16)

            @block.tensor
            def _(pe):
                pe.wait_ge(w_in.sem, 32)
                pe.wait_ge(zeroed.sem, 1)
                for n in range(4):
                    pe.matmul(psum[:, n, :], x_tok[:, :], phi[:, n * N:(n + 1) * N],
                              start=True, stop=False, skip_group_check=True)
                with pe.Fori(0, NT) as t:
                    pe.wait_ge(round_done.sem, round_done.at(t))
                    pe.wait_ge(x_t_ready.sem, x_t_ready.at(t))
                    for n in range(4):
                        if n >= 2:
                            pe.wait_ge(logit_kept.sem, logit_kept.at(t, n - 2))
                        pe.matmul(psum[:, LOGIT + n % 2, :], x_t[:, :], phi[:, n * N:(n + 1) * N],
                                  start=True, stop=True).then_inc(logit_ready.sem, 1)
                    pe.transpose(psum[:, TURN, 0:P], x_t[:, :], core.c("ident")).then_inc(x_turned.sem, 1)
                    pe.wait_ge(x_tok_ready.sem, x_tok_ready.at(t))
                    pe.wait_ge(dispatch_ready.sem, dispatch_ready.at(t))
                    for n in range(4):
                        mm = pe.matmul(psum[:, n, :], x_tok[:, :], dispatch[:, n * N:(n + 1) * N],
                                       start=False, stop=False, skip_group_check=True)
                    mm.then_inc(summed.sem, 1)
                    pe.wait_ge(rsum_ready.sem, rsum_ready.at(t, 1))
                    pe.transpose(psum[:, TURN, 0:P], rsum_s[:, :], core.c("ident")).then_inc(rsum_turned.sem, 1)
                    pe.wait_ge(exp_ready.sem, exp_ready.at(t, 1))
                    for n in range(4):
                        if n == 1:
                            pe.wait_ge(rsum_t_ready.sem, rsum_t_ready.at(t))
                        if n >= 2:
                            pe.wait_ge(turned_kept.sem, turned_kept.at(t, n - 2))
                        for i in range(4):
                            e = 4 * n + i
                            mm = pe.transpose(psum[:, TURN + (n + 1) % 2, i * P:(i + 1) * P],
                                              combine_tok[:, e * P:(e + 1) * P], core.c("ident"))
                        mm.then_inc(turned.sem, 1)

            @block.gpsimd
            def _(pool):
                with pool.Fori(0, NT) as t:
                    pool.wait_ge(round_done.sem, round_done.at(t))
                    pool.wait_ge(max_ready.sem, max_ready.at(t, 0))
                    pool.tensor_tensor(by_expert(dispatch[:, :]), by_expert(logit[:, :]),
                                       nmax_e[:, :].unsqueeze(2).to_broadcast([P, L1_EXPERTS, L1_SLOTS]),
                                       ALU.subtract).then_inc(shifted_ready.sem, 1)
                    pool.wait_ge(max_ready.sem, max_ready.at(t, 1))
                    pool.tensor_tensor(by_expert(combine_tok[:, :]), by_expert(logit[:, :]),
                                       nmax_s[:, :].unsqueeze(1).to_broadcast([P, L1_EXPERTS, L1_SLOTS]),
                                       ALU.subtract).then_inc(shifted_ready.sem, 1)

            @block.scalar
            def _(act):
                with act.Fori(0, NT) as t:
                    act.wait_ge(round_done.sem, round_done.at(t))
                    act.copy(x_t[:, :], core.xn[:, cols(t, P)]).then_inc(x_t_ready.sem, 1)
                    act.wait_ge(x_turned.sem, x_turned.at(t))
                    act.copy(x_tok[:, :], psum[:, TURN, 0:P]).then_inc(x_tok_ready.sem, 1)
                    for k, buf in enumerate((dispatch, combine_tok)):
                        act.wait_ge(shifted_ready.sem, shifted_ready.at(t, k))
                        act.activation(buf[:, :], buf[:, :], ACT.Exp).then_inc(exp_ready.sem, 1)

            @block.vector
            def _(dve):
                dve.sem_inc(round_done.sem, 1)
                dve.memset(x_tok[:, :], 0.0).then_inc(zeroed.sem, 1)
                dve.wait_ge(w_in.sem, 32)
                with dve.Fori(0, NT) as t:
                    for n in range(4):
                        dve.wait_ge(logit_ready.sem, logit_ready.at(t, n))
                        dve.tensor_tensor(logit[:, n * N:(n + 1) * N], psum[:, LOGIT + n % 2, :],
                                          phi_b[:, n * N:(n + 1) * N], ALU.add).then_inc(logit_kept.sem, 1)
                    dve.wait_ge(logit_kept.sem, logit_kept.at(t, 3))
                    dve.tensor_reduce(nmax_e[:, :], by_expert(logit[:, :]), AX.X, ALU.max).then_inc(max_ready.sem, 1)
                    dve.tensor_reduce(nmax_s[:, :], by_slot(logit[:, :]), AX.X, ALU.max).then_inc(max_ready.sem, 1)
                    dve.wait_ge(exp_ready.sem, exp_ready.at(t, 0))
                    dve.tensor_reduce(sum_e[:, :], by_expert(dispatch[:, :]), AX.X, ALU.add).then_inc(sum_ready.sem, 1)
                    dve.wait_ge(sum_ready.sem, sum_ready.at(t, 0))
                    dve.reciprocal(rsum_e[:, :], sum_e[:, :]).then_inc(rsum_ready.sem, 1)
                    dve.wait_ge(rsum_ready.sem, rsum_ready.at(t, 0))
                    dve.tensor_tensor(by_expert(dispatch[:, :]), by_expert(dispatch[:, :]),
                                      rsum_e[:, :].unsqueeze(2).to_broadcast([P, L1_EXPERTS, L1_SLOTS]), ALU.mult)\
                       .then_inc(dispatch_ready.sem, 1)
                    dve.wait_ge(exp_ready.sem, exp_ready.at(t, 1))
                    dve.tensor_reduce(sum_s[:, :], by_slot(combine_tok[:, :]), AX.X, ALU.add)\
                       .then_inc(sum_ready.sem, 1)
                    dve.wait_ge(sum_ready.sem, sum_ready.at(t, 1))
                    dve.reciprocal(rsum_s[:, :].rearrange("p (j s) -> p j s", j=4),
                                   sum_s[:, :].unsqueeze(1).to_broadcast([P, 4, L1_SLOTS]))\
                       .then_inc(rsum_ready.sem, 1)
                    dve.wait_ge(rsum_turned.sem, rsum_turned.at(t))
                    dve.tensor_copy(rsum_t[:, :], psum[:, TURN, 0:P]).then_inc(rsum_t_ready.sem, 1)
                    dve.wait_ge(rsum_t_ready.sem, rsum_t_ready.at(t))
                    for n in range(4):
                        dve.wait_ge(turned.sem, turned.at(t, n))
                        keep = dve.tensor_tensor(combine[:, 4 * n:4 * n + 4, cols(t, P)],
                                                 psum[:, TURN + (n + 1) % 2, :].rearrange("p (i q) -> p i q", i=4),
                                                 rsum_t[:, :].unsqueeze(1).to_broadcast([P, 4, P]), ALU.mult)
                        keep.then_inc(turned_kept.sem, 1)
                    dve.wait_ge(turned_kept.sem, turned_kept.at(t, 3))
                    dve.wait_ge(summed.sem, summed.at(t))
                    dve.sem_inc(round_done.sem, 1)


def l1_expert_phase(core, combine):
    nc, psum = core.nc, core.psum
    with Phase(core, "l1e") as ph:
        piece = ph.buf("piece", 2, PIECE.width)
        slots = core.g
        out = ph.buf("slots_out", ET, P)
        pieces_in = [ph.semaphore("pieces_in_even"), ph.semaphore("pieces_in_odd")]
        clipped, normed, slots_ready = ph.semaphore("clipped"), ph.semaphore("normed"), ph.semaphore("slots_ready")
        out_ready, out_kept = ph.semaphore("out_ready"), ph.semaphore("out_kept")
        y_ready, y_kept = ph.semaphore("y_ready"), ph.semaphore("y_kept")
        norm = ColumnNorm(ph, "norm", (4, 5))
        quarter = [slice(n * N, (n + 1) * N) for n in range(4)]

        with nc.Block() as block:
            @block.sync
            def _(sp):
                for n in range(4):
                    if n >= 2:
                        sp.wait_ge(out_ready.sem, out_ready.at(n - 2))
                        sp.wait_ge(out_kept.sem, out_kept.at(n - 2))
                    sp.dma_start(piece[:, n % 2, :], core.dram["l1f_experts"][n]).then_inc(pieces_in[n % 2].sem, 16)

            @block.tensor
            def _(pe):
                for n in range(4):
                    pe.wait_ge(clipped.sem, clipped.at(n))
                    if n:
                        pe.wait_ge(norm.rstd_ready.sem, norm.rstd_ready.at(n - 1))
                    norm.tensor(pe, n, slots[:, quarter[n]])
                pe.wait_ge(slots_ready.sem, slots_ready.at(3))
                for n in range(4):
                    pe.wait_ge(pieces_in[n % 2].sem, 16 * (n // 2) + 16)
                    w = piece[:, n % 2, :]
                    for i in range(4):
                        for j in range(4):
                            expert = 4 * i + j
                            first = (16 * n + expert) * L1_SLOTS
                            mm = pe.matmul(psum[32 * j:32 * j + 32, n, i * P:(i + 1) * P],
                                           slots[:, first:first + L1_SLOTS], PIECE.of(w, "w", expert, P),
                                           start=(i == 0), stop=(i == 3), skip_group_check=True)
                    mm.then_inc(out_ready.sem, 1)
                for b in range(B):
                    pe.wait_ge(out_kept.sem, out_kept.at(3))
                    for e in range(ET):
                        mm = pe.matmul(psum[:, 4 + b, :], out[:, e, :], combine[:, e, b * N:(b + 1) * N],
                                       start=(e == 0), stop=(e == ET - 1))
                    mm.then_inc(y_ready.sem, 1)

            @block.scalar
            def _(act):
                act.preload_act_table_set(EXP_LN_SET)
                for n in range(4):
                    if n:
                        act.wait_ge(normed.sem, normed.at(n - 1))
                    norm.scalar(act, n)
                for n in range(4):
                    act.wait_ge(normed.sem, normed.at(n))
                    act.activation(slots[:, quarter[n]], slots[:, quarter[n]], ACT.Tanh).then_inc(slots_ready.sem, 1)

            @block.vector
            def _(dve):
                for n in range(4):
                    dve.tensor_scalar(slots[:, quarter[n]], psum[:, n, :], -33000.0, 65000.0, ALU.max, ALU.min)\
                       .then_inc(clipped.sem, 1)
                    dve.wait_ge(clipped.sem, clipped.at(n))
                    norm.vector(dve, n, slots[:, quarter[n]])
                    dve.wait_ge(norm.rstd_ready.sem, norm.rstd_ready.at(n))
                    dve.tensor_tensor(slots[:, quarter[n]], norm.centred[:, :], norm.rstd[:, :], ALU.mult)\
                       .then_inc(normed.sem, 1)
                for n in range(4):
                    dve.wait_ge(out_ready.sem, out_ready.at(n))
                    dve.tensor_tensor(out[:, 4 * n:4 * n + 4, :],
                                      psum[:, n, :].rearrange("p (i h) -> p i h", i=4),
                                      PIECE.of(piece[:, n % 2, :], "bias").rearrange("p (i h) -> p i h", i=4),
                                      ALU.add).then_inc(out_kept.sem, 1)
                for b in range(B):
                    dve.wait_ge(y_ready.sem, y_ready.at(b))
                    dve.tensor_copy(core.g[:, b * N:(b + 1) * N], psum[:, 4 + b, :]).then_inc(y_kept.sem, 1)


L2_SSM = 64
L2_GATES = 3
L2A = Fields(("wb", P), ("wih", 3 * P), ("wd", P), ("wa", P), ("wc", P), ("whh", 3 * P), ("proj", P),
             ("gate", 2 * P), ("bb", 1), ("cb", 1), ("db", 1), ("bih", 3), ("bhh", 3), ("pb", 1), ("gb", 2))


def l2_attn_layout(np, i):
    g = lambda k: i["L2_attn_" + k]
    bw = np.zeros((P, P), np.float32)
    bw[:, :L2_SSM] = g("Bw").T
    a = np.zeros((L2_SSM, P), np.float32)
    a[:, :L2_SSM] = g("A").T
    gate = np.repeat(g("gate_w")[:, :, None], P, axis=2)
    return {"l2a": pack(np, [
        bw, g("W_ih").T, g("Dw").T, a, g("Cw").T, g("W_hh").T, g("proj_w").T, gate[0], gate[1],
        column(g("Bb")), column(g("Cb")), column(g("Db")), g("b_ih").reshape(3, P).T, g("b_hh").reshape(3, P).T,
        column(g("proj_b")), np.tile(g("gate_b"), (P, 1))])}


LAYOUTS.append(l2_attn_layout)


def l2_attn_phase(core):
    with ExitStack() as ctx:
        sb = lambda name, *shape: ctx.enter_context(core.nc.sbuf_tensor("l2a_" + name, [P, *shape], F32))
        w = sb("w", L2A.width)
        drive = sb("drive", N + 32, 4, B)
        trail_h = sb("trail_h", N, B)
        trail_s = sb("trail_s", N, B)
        l2_drive_phase(core, w, drive)
        l2_scan_phase(core, w, drive, trail_h, trail_s)
        l2_output_phase(core, w, trail_h, trail_s)


def l2_drive_phase(core, w, drive):
    nc, psum = core.nc, core.psum
    with Phase(core, "l2d") as ph:
        w_in, made, kept = ph.semaphore("w_in"), ph.semaphore("made"), ph.semaphore("kept")
        col = lambda name, k=0: L2A.of(w, name, k, 1)
        with nc.Block() as block:
            @block.sync
            def _(sp):
                sp.dma_start(w[:, :], core.dram["l2a"]).then_inc(w_in.sem, 16)

            @block.tensor
            def _(pe):
                pe.wait_ge(w_in.sem, 16)
                for n in range(4 * B):
                    part, b = n // B, n % B
                    if n >= 8:
                        pe.wait_ge(kept.sem, kept.at(n - 8))
                    lhs = L2A.of(w, "wih", part, P) if part < 3 else L2A.of(w, "wb")
                    pe.matmul(psum[:, n % 8, :], lhs, core.xn[:, b * N:(b + 1) * N], start=True, stop=True)\
                      .then_inc(made.sem, 1)

            @block.vector
            def _(dve):
                dve.memset(drive[:, N:, :, :], 0.0)
                dve.wait_ge(w_in.sem, 16)
                for n in range(4 * B):
                    part, b = n // B, n % B
                    dve.wait_ge(made.sem, made.at(n))
                    if part < 2:
                        biases = (col("bih", part), col("bhh", part), ALU.add, ALU.add)
                    else:
                        biases = (col("bih", 2) if part == 2 else col("bb"), None, ALU.add)
                    dve.tensor_scalar(drive[:, 0:N, part, b], psum[:, n % 8, :], *biases).then_inc(kept.sem, 1)


def l2_scan_phase(core, w, drive, trail_h, trail_s):
    nc, psum = core.nc, core.psum
    U, S = 16, L2_SSM
    R, NB, Z, SB = 0, 1, 2, 3
    with Phase(core, "l2s") as ph:
        now = ph.buf("now", 2, U, 4, B)
        h = ph.buf("h", 2, U, B)
        s = ph.buf("s", 2, U, B)
        r_in, r = ph.buf("r_in", B), ph.buf("r", B)
        z_in, z, not_z = ph.buf("z_in", B), ph.buf("z", B), ph.buf("not_z", B)
        rn, n_in, n = ph.buf("rn", B), ph.buf("n_in", B), ph.buf("n", B)
        zh, zn = ph.buf("zh", B), ph.buf("zn", B)
        s_in, s_sig = ph.buf("s_in", B), ph.buf("s_sig", B)
        col = lambda name, k=0: L2A.of(w, name, k, 1)

        K = 2 * U
        zeroed = ph.semaphore("zeroed", 2)
        now_ready, moved = ph.semaphore("now_ready", 2), ph.semaphore("moved", 4)
        r_raw, n_raw, z_raw, s_raw = (ph.semaphore(x, K) for x in ("r_raw", "n_raw", "z_raw", "s_raw"))
        r_in_ready, r_ready = ph.semaphore("r_in_ready", K), ph.semaphore("r_ready", K)
        z_in_ready, z_ready, not_z_ready = ph.semaphore("z_in_ready", K), ph.semaphore("z_ready", K), ph.semaphore("not_z_ready", K)
        rn_ready, n_in_ready, n_ready = ph.semaphore("rn_ready", K), ph.semaphore("n_in_ready", K), ph.semaphore("n_ready", K)
        zh_ready, zn_ready = ph.semaphore("zh_ready", K), ph.semaphore("zn_ready", K)
        h_ready = ph.semaphore("h_ready", K)
        s_in_ready, s_sig_ready, s_ready = ph.semaphore("s_in_ready", K), ph.semaphore("s_sig_ready", K), ph.semaphore("s_ready", K)
        ROUNDS = N // K

        def before(buf, i):
            j = (i - 1) % K
            return buf[:, j // U, j % U, :]

        def at(buf, i):
            return buf[:, i // U, i % U, :]

        with nc.Block() as block:
            @block.gpsimd
            def _(pool):
                pool.sem_inc(moved.sem, 4)
                pool.memset(h[:, 1, U - 1, :], 0.0).then_inc(zeroed.sem, 1)
                pool.memset(s[:, 1, U - 1, :], 0.0).then_inc(zeroed.sem, 1)
                for half in range(2):
                    pool.tensor_copy(now[:, half, :, :, :], drive[:, half * U:(half + 1) * U, :, :])\
                        .then_inc(now_ready.sem, 1)
                with pool.Fori(0, ROUNDS) as k:
                    for half in range(2):
                        pool.wait_ge(h_ready.sem, h_ready.at(k, half * U + U))
                        pool.wait_ge(s_ready.sem, s_ready.at(k, half * U + U))
                        pool.tensor_copy(trail_h[:, bass.ds(k * K + half * U, U), :], h[:, half, :, :])\
                            .then_inc(moved.sem, 1)
                        pool.tensor_copy(trail_s[0:S, bass.ds(k * K + half * U, U), :], s[0:S, half, :, :])\
                            .then_inc(moved.sem, 1)
                        pool.tensor_copy(now[:, half, :, :, :], drive[:, bass.ds(k * K + K + half * U, U), :, :])\
                            .then_inc(now_ready.sem, 1)

            @block.tensor
            def _(pe):
                pe.wait_ge(zeroed.sem, 2)
                with pe.Fori(0, ROUNDS) as k:
                    for i in range(K):
                        pe.wait_ge(h_ready.sem, h_ready.at(k, i))
                        for bank, gate, raw in ((R, 0, r_raw), (NB, 2, n_raw), (Z, 1, z_raw)):
                            pe.matmul(psum[:, bank, 0:B], L2A.of(w, "whh", gate, P), before(h, i),
                                      start=True, stop=True).then_inc(raw.sem, 1)
                        pe.wait_ge(s_ready.sem, s_ready.at(k, i))
                        pe.matmul(psum[:, SB, 0:B], L2A.of(w, "wa")[0:S, :], before(s, i)[0:S, :],
                                  start=True, stop=True).then_inc(s_raw.sem, 1)

            @block.scalar
            def _(act):
                act.preload_act_table_set("sigmoid_and_others")
                with act.Fori(0, ROUNDS) as k:
                    for i in range(K):
                        act.wait_ge(r_in_ready.sem, r_in_ready.at(k, i))
                        act.activation(r[:, :], r_in[:, :], ACT.Sigmoid).then_inc(r_ready.sem, 1)
                        act.wait_ge(z_in_ready.sem, z_in_ready.at(k, i))
                        act.activation(z[:, :], z_in[:, :], ACT.Sigmoid).then_inc(z_ready.sem, 1)
                        act.wait_ge(n_in_ready.sem, n_in_ready.at(k, i))
                        act.activation(n[:, :], n_in[:, :], ACT.Tanh).then_inc(n_ready.sem, 1)
                        act.wait_ge(s_in_ready.sem, s_in_ready.at(k, i))
                        act.activation(s_sig[0:S, :], s_in[0:S, :], ACT.Sigmoid).then_inc(s_sig_ready.sem, 1)

            @block.vector
            def _(dve):
                dve.wait_ge(zeroed.sem, 2)
                dve.sem_inc(h_ready.sem, 1)
                dve.sem_inc(s_ready.sem, 1)
                with dve.Fori(0, ROUNDS) as k:
                    for i in range(K):
                        if i % U == 0:
                            dve.wait_ge(now_ready.sem, now_ready.at(k, i // U))
                            dve.wait_ge(moved.sem, k * 4 + (4 if i else 2))
                        drv = lambda part: now[:, i // U, i % U, part, :]
                        dve.wait_ge(r_raw.sem, r_raw.at(k, i))
                        dve.tensor_tensor(r_in[:, :], psum[:, R, 0:B], drv(0), ALU.add).then_inc(r_in_ready.sem, 1)
                        dve.wait_ge(r_ready.sem, r_ready.at(k, i))
                        dve.wait_ge(n_raw.sem, n_raw.at(k, i))
                        dve.scalar_tensor_tensor(out=rn[:, :], in0=psum[:, NB, 0:B], scalar=col("bhh", 2),
                                                 in1=r[:, :], op0=ALU.add, op1=ALU.mult).then_inc(rn_ready.sem, 1)
                        dve.wait_ge(rn_ready.sem, rn_ready.at(k, i))
                        dve.tensor_tensor(n_in[:, :], rn[:, :], drv(2), ALU.add).then_inc(n_in_ready.sem, 1)
                        dve.wait_ge(z_raw.sem, z_raw.at(k, i))
                        dve.tensor_tensor(z_in[:, :], psum[:, Z, 0:B], drv(1), ALU.add).then_inc(z_in_ready.sem, 1)
                        dve.wait_ge(s_raw.sem, s_raw.at(k, i))
                        dve.tensor_tensor(s_in[0:S, :], psum[0:S, SB, 0:B], drv(3)[0:S, :], ALU.add)\
                           .then_inc(s_in_ready.sem, 1)
                        dve.wait_ge(z_ready.sem, z_ready.at(k, i))
                        dve.tensor_scalar(not_z[:, :], z[:, :], -1.0, 1.0, ALU.mult, ALU.add)\
                           .then_inc(not_z_ready.sem, 1)
                        dve.tensor_tensor(zh[:, :], z[:, :], before(h, i), ALU.mult).then_inc(zh_ready.sem, 1)
                        dve.wait_ge(n_ready.sem, n_ready.at(k, i))
                        dve.wait_ge(not_z_ready.sem, not_z_ready.at(k, i))
                        dve.tensor_tensor(zn[:, :], not_z[:, :], n[:, :], ALU.mult).then_inc(zn_ready.sem, 1)
                        dve.wait_ge(zn_ready.sem, zn_ready.at(k, i))
                        dve.wait_ge(zh_ready.sem, zh_ready.at(k, i))
                        dve.tensor_tensor(at(h, i), zn[:, :], zh[:, :], ALU.add).then_inc(h_ready.sem, 1)
                        dve.wait_ge(s_sig_ready.sem, s_sig_ready.at(k, i))
                        dve.wait_ge(s_in_ready.sem, s_in_ready.at(k, i))
                        dve.tensor_tensor(at(s, i)[0:S, :], s_in[0:S, :], s_sig[0:S, :], ALU.mult)\
                           .then_inc(s_ready.sem, 1)


def l2_output_phase(core, w, trail_h, trail_s):
    nc, psum = core.nc, core.psum
    S = L2_SSM
    with Phase(core, "l2o") as ph:
        bias = ph.buf("bias", 1)
        gate, part = ph.buf("gate", 2, 2, N), ph.buf("part", 2, 2, N)
        bias_ready = ph.semaphore("bias_ready")
        gate_raw, gate_ready = ph.semaphore("gate_raw", 2), ph.semaphore("gate_ready", 2)
        y_ready, part_ready, out_ready = ph.semaphore("y_ready", 2), ph.semaphore("part_ready", 2), ph.semaphore("out_ready")
        col = lambda name, k=0: L2A.of(w, name, k, 1)
        with nc.Block() as block:
            @block.tensor
            def _(pe):
                for b in range(B):
                    x = core.xn[:, b * N:(b + 1) * N]
                    bank = 4 * (b % 2)
                    if b >= 2:
                        pe.wait_ge(part_ready.sem, part_ready.at(b - 2, 1))
                    for g in range(2):
                        pe.matmul(psum[:, bank + g, :], L2A.of(w, "gate", g, P), x, start=True, stop=True)\
                          .then_inc(gate_raw.sem, 1)
                    pe.matmul(psum[:, bank + 2, :], L2A.of(w, "wd"), x, start=True, stop=False)
                    pe.matmul(psum[:, bank + 2, :], L2A.of(w, "wc")[0:S, :], trail_s[0:S, :, b],
                              start=False, stop=True).then_inc(y_ready.sem, 1)
                    pe.matmul(psum[:, bank + 3, :], L2A.of(w, "proj"), trail_h[:, :, b], start=True, stop=True)\
                      .then_inc(y_ready.sem, 1)

            @block.scalar
            def _(act):
                for b in range(B):
                    if b >= 2:
                        act.wait_ge(part_ready.sem, part_ready.at(b - 2, 1))
                    for g in range(2):
                        act.wait_ge(gate_raw.sem, gate_raw.at(b, g))
                        act.activation(gate[:, b % 2, g, :], psum[:, 4 * (b % 2) + g, :], ACT.Sigmoid,
                                       bias=col("gb", g)).then_inc(gate_ready.sem, 1)

            @block.vector
            def _(dve):
                dve.tensor_tensor(bias[:, :], col("cb"), col("db"), ALU.add).then_inc(bias_ready.sem, 1)
                dve.wait_ge(bias_ready.sem, 1)
                for b in range(B):
                    if b >= 2:
                        dve.wait_ge(out_ready.sem, out_ready.at(b - 2))
                    for g in range(2):
                        dve.wait_ge(gate_ready.sem, gate_ready.at(b, g))
                        dve.wait_ge(y_ready.sem, y_ready.at(b, g))
                        dve.scalar_tensor_tensor(out=part[:, b % 2, g, :], in0=psum[:, 4 * (b % 2) + 2 + g, :],
                                                 scalar=col("pb") if g else bias[:, :], in1=gate[:, b % 2, g, :],
                                                 op0=ALU.add, op1=ALU.mult).then_inc(part_ready.sem, 1)
                    dve.wait_ge(part_ready.sem, part_ready.at(b, 1))
                    dve.tensor_tensor(core.s[:, b * N:(b + 1) * N], part[:, b % 2, 0, :], part[:, b % 2, 1, :],
                                      ALU.add).then_inc(out_ready.sem, 1)


L2_EXPERTS = 8
L2F = Fields(("gate", L2_EXPERTS), ("w1", L2_EXPERTS * P), ("w2", L2_EXPERTS * P), ("w3", L2_EXPERTS * P),
             ("b1", L2_EXPERTS), ("b2", L2_EXPERTS), ("b3", L2_EXPERTS), ("gb", 1))


def l2_ffn_layout(np, i):
    g = lambda k: i["L2_ffn_" + k]
    side = lambda w: w.transpose(1, 0, 2).reshape(P, L2_EXPERTS * P)
    return {"l2f": pack(np, [g("gate_w"), side(g("w1")), side(g("w2")), side(g("w3")),
                             g("b1").T, g("b2").T, g("b3").T, column(g("gate_b"))])}


LAYOUTS.append(l2_ffn_layout)


def l2_ffn_phase(core):
    with ExitStack() as ctx:
        sb = lambda name, *shape: ctx.enter_context(core.nc.sbuf_tensor("l2f_" + name, [P, *shape], F32))
        w = sb("w", L2F.width)
        table = sb("table", CONST_L2F.width)
        picked = sb("picked", T)
        weight = sb("weight", T)
        l2_pick_phase(core, w, table, picked, weight)
        l2_expert_phase(core, w, table, picked, weight)


def l2_pick_phase(core, w, table, picked, weight):
    nc, psum = core.nc, core.psum
    E, NT = L2_EXPERTS, T // P
    with Phase(core, "l2p") as ph:
        logit, prob = ph.buf("logit", T), ph.buf("prob", T)
        nmax, total, rtotal = ph.buf("nmax", B), ph.buf("total", B), ph.buf("rtotal", B)
        prob_tok, top = ph.buf("prob_tok", NT, E), ph.buf("top", NT, E)
        index = ph.buf("index", NT, E, dtype=U32)
        index_f = ph.buf("index_f", NT, 2)
        is_pick = ph.buf("is_pick", 2, NT, E)
        picked_tok = ph.buf("picked_tok", NT, E)
        w_in = ph.semaphore("w_in")
        logit_raw, logit_ready, nmax_ready = ph.semaphore("logit_raw"), ph.semaphore("logit_ready"), ph.semaphore("nmax_ready")
        exp_ready, rtotal_ready, prob_ready = ph.semaphore("exp_ready"), ph.semaphore("rtotal_ready"), ph.semaphore("prob_ready")
        turned, prob_tok_ready = ph.semaphore("turned"), ph.semaphore("prob_tok_ready")
        top_ready, index_ready, index_f_ready = ph.semaphore("top_ready"), ph.semaphore("index_ready"), ph.semaphore("index_f_ready")
        is_pick_ready, picked_tok_ready = ph.semaphore("is_pick_ready"), ph.semaphore("picked_tok_ready")
        back, picked_ready, weight_ready = ph.semaphore("back"), ph.semaphore("picked_ready"), ph.semaphore("weight_ready")
        batch = [slice(b * N, (b + 1) * N) for b in range(B)]
        with nc.Block() as block:
            @block.sync
            def _(sp):
                sp.dma_start(w[:, :], core.dram["l2f"]).then_inc(w_in.sem, 16)
                sp.dma_start(table[:, :], core.dram["const_l2f"]).then_inc(w_in.sem, 16)

            @block.tensor
            def _(pe):
                pe.wait_ge(w_in.sem, 32)
                for b in range(B):
                    pe.matmul(psum[0:E, b, :], L2F.of(w, "gate"), core.xn[:, batch[b]], start=True, stop=True)\
                      .then_inc(logit_raw.sem, 1)
                pe.wait_ge(prob_ready.sem, prob_ready.at(B - 1))
                for t in range(NT):
                    mm = pe.transpose(psum[:, 4, t * E:(t + 1) * E], prob[0:E, t * P:(t + 1) * P],
                                      core.c("ident")[0:E, 0:E])
                mm.then_inc(turned.sem, 1)
                pe.wait_ge(picked_tok_ready.sem, 1)
                for b in range(B):
                    for c in range(CH):
                        mm = pe.transpose(psum[0:E, b, c * P:(c + 1) * P], picked_tok[:, b * CH + c, :],
                                          core.c("ident"))
                    mm.then_inc(back.sem, 1)

            @block.scalar
            def _(act):
                for b in range(B):
                    act.wait_ge(nmax_ready.sem, nmax_ready.at(b))
                    act.activation(prob[0:E, batch[b]], logit[0:E, batch[b]], ACT.Exp, bias=nmax[0:E, b:b + 1],
                                   accum_out=total[0:E, b:b + 1]).then_inc(exp_ready.sem, 1)

            @block.vector
            def _(dve):
                dve.wait_ge(w_in.sem, 32)
                for b in range(B):
                    dve.wait_ge(logit_raw.sem, logit_raw.at(b))
                    dve.tensor_scalar(logit[0:E, batch[b]], psum[0:E, b, :], L2F.of(w, "gb")[0:E, :], None, ALU.add)\
                       .then_inc(logit_ready.sem, 1)
                    dve.wait_ge(logit_ready.sem, logit_ready.at(b))
                    dve.tensor_reduce(nmax[0:E, b:b + 1], logit[0:E, batch[b]], AX.X, ALU.max, negate=True)\
                       .then_inc(nmax_ready.sem, 1)
                for b in range(B):
                    dve.wait_ge(exp_ready.sem, exp_ready.at(b))
                    dve.reciprocal(rtotal[0:E, b:b + 1], total[0:E, b:b + 1]).then_inc(rtotal_ready.sem, 1)
                    dve.wait_ge(rtotal_ready.sem, rtotal_ready.at(b))
                    dve.tensor_scalar(prob[0:E, batch[b]], prob[0:E, batch[b]], rtotal[0:E, b:b + 1], None, ALU.mult)\
                       .then_inc(prob_ready.sem, 1)
                dve.wait_ge(turned.sem, 1)
                dve.tensor_copy(prob_tok[:, :, :], psum[:, 4, 0:NT * E].rearrange("p (t e) -> p t e", e=E))\
                   .then_inc(prob_tok_ready.sem, 1)
                dve.wait_ge(prob_tok_ready.sem, 1)
                for t in range(NT):
                    dve.max(top[:, t, :], prob_tok[:, t, :]).then_inc(top_ready.sem, 1)
                dve.wait_ge(top_ready.sem, top_ready.at(NT - 1))
                for t in range(NT):
                    dve.max_index(index[:, t, :], top[:, t, :], prob_tok[:, t, :]).then_inc(index_ready.sem, 1)
                dve.wait_ge(index_ready.sem, index_ready.at(NT - 1))
                dve.tensor_copy(index_f[:, :, :], index[:, :, 0:2]).then_inc(index_f_ready.sem, 1)
                dve.wait_ge(index_f_ready.sem, 1)
                for k in range(2):
                    dve.tensor_tensor(is_pick[:, k, :, :],
                                      CONST_L2F.of(table, "index8").unsqueeze(1).to_broadcast([P, NT, E]),
                                      index_f[:, :, k:k + 1].to_broadcast([P, NT, E]), ALU.is_equal)\
                       .then_inc(is_pick_ready.sem, 1)
                dve.wait_ge(is_pick_ready.sem, is_pick_ready.at(1))
                dve.tensor_tensor(picked_tok[:, :, :], is_pick[:, 0, :, :], is_pick[:, 1, :, :], ALU.add)\
                   .then_inc(picked_tok_ready.sem, 1)
                for b in range(B):
                    dve.wait_ge(back.sem, back.at(b))
                    dve.tensor_copy(picked[0:E, batch[b]], psum[0:E, b, :]).then_inc(picked_ready.sem, 1)
                    dve.wait_ge(picked_ready.sem, picked_ready.at(b))
                    dve.tensor_tensor(weight[0:E, batch[b]], prob[0:E, batch[b]], picked[0:E, batch[b]], ALU.mult)\
                       .then_inc(weight_ready.sem, 1)


def l2_expert_phase(core, w, table, picked, weight):
    nc, psum = core.nc, core.psum
    E = L2_EXPERTS
    with Phase(core, "l2e") as ph:
        h1, h2, y = ph.buf("h1", 2, N), ph.buf("h2", 2, N), ph.buf("y", 2, N)
        weighted = ph.buf("weighted", 2, N)
        part = ph.buf("part", E)
        total = ph.buf("total", E)
        total_t = ph.buf("total_t", P)
        passed = ph.semaphore("passed")
        round_done = ph.semaphore("round_done")
        up1, up2, up3 = ph.semaphore("up1", E), ph.semaphore("up2", E), ph.semaphore("up3", E)
        h1_ready, h2_ready, y_ready = ph.semaphore("h1_ready", E), ph.semaphore("h2_ready", E), ph.semaphore("y_ready", E)
        spread, part_ready = ph.semaphore("spread", E), ph.semaphore("part_ready", E)
        started, turned, total_ready = ph.semaphore("started"), ph.semaphore("turned"), ph.semaphore("total_ready")
        out_ready, out_kept = ph.semaphore("out_ready"), ph.semaphore("out_kept")
        col = lambda name, k: L2F.of(w, name, k, 1)
        with nc.Block() as block:
            @block.tensor
            def _(pe):
                with pe.Fori(0, B) as b:
                    pe.wait_ge(round_done.sem, round_done.at(b))
                    x, wt = core.xn[:, cols(b)], weight[0:E, cols(b)]
                    for i in range(E + 3):
                        if i < E:
                            if i >= 2:
                                pe.wait_ge(h1_ready.sem, h1_ready.at(b, i - 2))
                            pe.matmul(psum[:, i % 2, :], L2F.of(w, "w1", i, P), x, start=True, stop=True)\
                              .then_inc(up1.sem, 1)
                        if 0 <= i - 1 < E:
                            e = i - 1
                            pe.wait_ge(h1_ready.sem, h1_ready.at(b, e))
                            if e >= 2:
                                pe.wait_ge(h2_ready.sem, h2_ready.at(b, e - 2))
                            pe.matmul(psum[:, 2 + e % 2, :], L2F.of(w, "w2", e, P), h1[:, e % 2, :],
                                      start=True, stop=True).then_inc(up2.sem, 1)
                        if 0 <= i - 2 < E:
                            e = i - 2
                            pe.wait_ge(h2_ready.sem, h2_ready.at(b, e))
                            if e >= 2:
                                pe.wait_ge(y_ready.sem, y_ready.at(b, e - 2))
                            pe.matmul(psum[:, 4 + e % 2, :], L2F.of(w, "w3", e, P), h2[:, e % 2, :],
                                      start=True, stop=True).then_inc(up3.sem, 1)
                        if 0 <= i - 3 < E:
                            e = i - 3
                            if e >= 2:
                                pe.wait_ge(part_ready.sem, part_ready.at(b, e - 2))
                            apart(pe, passed)
                            pe.matmul(psum[:, 6 + e % 2, :], CONST_L2F.of(table, "sel8", e, P)[0:E, :], wt,
                                      start=True, stop=True).then_inc(spread.sem, 1)
                pe.wait_ge(round_done.sem, round_done.at(B))
                pe.transpose(psum[0:E, 0, 0:P], total[:, :], core.c("ident")).then_inc(turned.sem, 1)
                pe.wait_ge(total_ready.sem, 1)
                for b in range(B):
                    pe.matmul(psum[:, 1 + b, :], total_t[0:E, :], picked[0:E, b * N:(b + 1) * N],
                              start=True, stop=True).then_inc(out_ready.sem, 1)

            @block.scalar
            def _(act):
                with act.Fori(0, B) as b:
                    act.wait_ge(round_done.sem, round_done.at(b))
                    for i in range(E + 2):
                        if i < E:
                            act.wait_ge(up1.sem, up1.at(b, i))
                            if i >= 2:
                                act.wait_ge(up2.sem, up2.at(b, i - 2))
                            act.activation(h1[:, i % 2, :], psum[:, i % 2, :], ACT.Relu, bias=col("b1", i))\
                               .then_inc(h1_ready.sem, 1)
                        if i >= 2:
                            e = i - 2
                            act.wait_ge(up3.sem, up3.at(b, e))
                            if e >= 2:
                                act.wait_ge(part_ready.sem, part_ready.at(b, e - 2))
                            act.activation(y[:, e % 2, :], psum[:, 4 + e % 2, :], ACT.Relu, bias=col("b3", e))\
                               .then_inc(y_ready.sem, 1)

            @block.vector
            def _(dve):
                dve.sem_inc(round_done.sem, 1)
                dve.memset(total[:, :], 0.0).then_inc(started.sem, 1)
                dve.wait_ge(started.sem, 1)
                with dve.Fori(0, B) as b:
                    for i in range(E + 2):
                        if i < E:
                            dve.wait_ge(up2.sem, up2.at(b, i))
                            if i >= 2:
                                dve.wait_ge(up3.sem, up3.at(b, i - 2))
                            dve.tensor_scalar(h2[:, i % 2, :], psum[:, 2 + i % 2, :], col("b2", i), 0.0,
                                              ALU.add, ALU.max).then_inc(h2_ready.sem, 1)
                        if i >= 2:
                            e = i - 2
                            dve.wait_ge(y_ready.sem, y_ready.at(b, e))
                            dve.wait_ge(spread.sem, spread.at(b, e))
                            if e >= 2:
                                dve.wait_ge(part_ready.sem, part_ready.at(b, e - 2))
                            dve.tensor_tensor_reduce(out=weighted[:, e % 2, :], in0=y[:, e % 2, :],
                                                     in1=psum[:, 6 + e % 2, :], scale=1.0, scalar=0.0,
                                                     op0=ALU.mult, op1=ALU.add, accum_out=part[:, e:e + 1])\
                               .then_inc(part_ready.sem, 1)
                    dve.wait_ge(part_ready.sem, part_ready.at(b, E - 1))
                    dve.wait_ge(round_done.sem, b + 1)
                    dve.tensor_tensor(total[:, :], total[:, :], part[:, :], ALU.add).then_inc(round_done.sem, 1)
                dve.wait_ge(turned.sem, 1)
                dve.tensor_copy(total_t[0:E, :], psum[0:E, 0, 0:P]).then_inc(total_ready.sem, 1)
                for b in range(B):
                    dve.wait_ge(out_ready.sem, out_ready.at(b))
                    dve.tensor_copy(core.g[:, b * N:(b + 1) * N], psum[:, 1 + b, :]).then_inc(out_kept.sem, 1)


L3_HEADS = 16
L3A = Fields(("wq", 4 * P), ("wk", 4 * P), ("wv", P), ("wo", P), ("bv", P), ("bq", 4), ("bk", 4), ("bo", 1),
             ("gamma", 1), ("beta", 1))


def l3_attn_layout(np, i):
    g = lambda k: i["L3_attn_" + k]

    def spread(a):
        out = np.zeros((a.shape[0], L3_HEADS, 32), np.float32)
        out[:, :, :8] = a.reshape(-1, L3_HEADS, 8)
        return out.reshape(-1, 4 * P)

    return {"l3a": pack(np, [
        spread(g("Wq")), spread(g("Wk")), g("Wv"), g("Wo"), np.tile(g("bv"), (P, 1)),
        spread(g("bq")[None]).reshape(4, P).T, spread(g("bk")[None]).reshape(4, P).T,
        column(g("bo")), column(g("gamma")), column(g("beta"))])}


LAYOUTS.append(l3_attn_layout)


def l3_attn_phase(core):
    nc, psum = core.nc, core.psum
    H, DH, DV = L3_HEADS, 8, 9
    SCALE = float(DH) ** -0.5
    SIM, TURN, NUM, MISC = 0, 3, 5, 7
    STEPS = CH * H
    with Phase(core, "l3a") as ph:
        w = ph.buf("w", L3A.width)
        col = lambda name, k=0: L3A.of(w, name, k, 1)
        x = ph.buf("x", N)
        q, k = ph.buf("q", 4, N), ph.buf("k", 4, N)
        v = ph.buf("v", CH, H, DV)
        nmax = ph.buf("nmax", STEPS)
        prob = ph.buf("prob", 3, N)
        prob_t = ph.buf("prob_t", 3, N)
        rden = ph.buf("rden", CH, H)
        att, att_t = ph.buf("att", CH, P), ph.buf("att_t", N)
        res, scaled = ph.buf("res", N), ph.buf("scaled", N)

        w_in, ones_ready = ph.semaphore("w_in"), ph.semaphore("ones_ready")
        round_done = ph.semaphore("round_done")
        x_ready = ph.semaphore("x_ready")
        qk_raw, qk_ready = ph.semaphore("qk_raw", 8), ph.semaphore("qk_ready", 8)
        v_raw, v_ready = ph.semaphore("v_raw"), ph.semaphore("v_ready", CH)
        sim_ready, nmax_ready, prob_ready = (ph.semaphore(s, STEPS) for s in ("sim_ready", "nmax_ready", "prob_ready"))
        turned = ph.semaphore("turned", STEPS)
        even_kept, odd_kept = ph.semaphore("even_kept", STEPS // 2), ph.semaphore("odd_kept", STEPS // 2)
        drawn = ph.semaphore("drawn", STEPS)
        rden_ready, att_ready = ph.semaphore("rden_ready", CH), ph.semaphore("att_ready", CH)
        att_turned, att_t_ready = ph.semaphore("att_turned"), ph.semaphore("att_t_ready")
        out_ready, res_ready, scaled_ready = ph.semaphore("out_ready"), ph.semaphore("res_ready"), ph.semaphore("scaled_ready")
        norm = ColumnNorm(ph, "norm", (0, 1))

        def wait_turned_kept(eng, r, n):
            kept = odd_kept if n % 2 else even_kept
            eng.wait_ge(kept.sem, kept.at(r, n // 2))

        with nc.Block() as block:
            @block.sync
            def _(sp):
                sp.dma_start(w[:, :], core.dram["l3a"]).then_inc(w_in.sem, 16)

            @block.gpsimd
            def _(pool):
                pool.memset(v[:, :, :, DH:DV], 1.0).then_inc(ones_ready.sem, 1)
                with pool.Fori(0, B) as r:
                    pool.wait_ge(round_done.sem, round_done.at(r))
                    pool.tensor_copy(x[:, :], core.xn[:, cols(r)]).then_inc(x_ready.sem, 1)

            @block.tensor
            def _(pe):
                pe.wait_ge(w_in.sem, 16)
                pe.wait_ge(ones_ready.sem, 1)
                with pe.Fori(0, B) as r:
                    pe.wait_ge(x_ready.sem, x_ready.at(r))
                    for t in range(8):
                        if t >= 4:
                            pe.wait_ge(qk_ready.sem, qk_ready.at(r, t - 4))
                        pe.matmul(psum[:, t % 4, :], L3A.of(w, "wq" if t < 4 else "wk", t % 4, P), x[:, :],
                                  start=True, stop=True).then_inc(qk_raw.sem, 1)
                    for c in range(CH):
                        mm = pe.matmul(psum[:, MISC, c * P:(c + 1) * P], x[:, c * P:(c + 1) * P], L3A.of(w, "wv"),
                                       start=(c == 0), stop=(c == CH - 1), skip_group_check=True)
                    mm.then_inc(v_raw.sem, 1)
                    pe.wait_ge(qk_ready.sem, qk_ready.at(r, 7))
                    pe.wait_ge(v_ready.sem, v_ready.at(r, CH - 1))

                    def score(n):
                        c, h = n // H, n % H
                        if n >= 3:
                            pe.wait_ge(prob_ready.sem, prob_ready.at(r, n - 3))
                        rows = slice(32 * (h % 4), 32 * (h % 4) + DH)
                        pe.matmul(psum[:, SIM + n % 3, :], q[rows, h // 4, c * P:(c + 1) * P], k[rows, h // 4, :],
                                  start=True, stop=True).then_inc(sim_ready.sem, 1)

                    def turn(n):
                        pe.wait_ge(prob_ready.sem, prob_ready.at(r, n))
                        if n >= 2:
                            wait_turned_kept(pe, r, n - 2)
                        for j in range(CH):
                            mm = pe.transpose(psum[:, TURN + n % 2, j * P:(j + 1) * P],
                                              prob[:, n % 3, j * P:(j + 1) * P], core.c("ident"))
                        mm.then_inc(turned.sem, 1)

                    def draw(n):
                        c, h = n // H, n % H
                        if h == 0 and c >= 2:
                            pe.wait_ge(att_ready.sem, att_ready.at(r, c - 2))
                        wait_turned_kept(pe, r, n)
                        for j in range(CH):
                            mm = pe.matmul(psum[:, NUM + c % 2, h * DV:(h + 1) * DV],
                                           prob_t[:, n % 3, j * P:(j + 1) * P], v[:, j, h, :],
                                           start=(h == 0 and j == 0), stop=(h == H - 1 and j == CH - 1),
                                           skip_group_check=True)
                        mm.then_inc(drawn.sem, 1)

                    for i in range(STEPS + 4):
                        if i < STEPS:
                            score(i)
                        if 0 <= i - 2 < STEPS:
                            turn(i - 2)
                        if 0 <= i - 4 < STEPS:
                            draw(i - 4)
                    for c in range(CH):
                        pe.wait_ge(att_ready.sem, att_ready.at(r, c))
                        mm = pe.transpose(psum[:, MISC, c * P:(c + 1) * P], att[:, c, :], core.c("ident"))
                    mm.then_inc(att_turned.sem, 1)
                    pe.wait_ge(att_t_ready.sem, att_t_ready.at(r))
                    pe.matmul(psum[:, 2, :], L3A.of(w, "wo"), att_t[:, :], start=True, stop=True)\
                      .then_inc(out_ready.sem, 1)
                    pe.wait_ge(res_ready.sem, res_ready.at(r))
                    norm.tensor(pe, r, res[:, :])

            @block.scalar
            def _(act):
                act.preload_act_table_set(EXP_LN_SET)
                with act.Fori(0, B) as r:
                    def keep(n):
                        act.wait_ge(turned.sem, turned.at(r, n))
                        if n >= 3:
                            act.wait_ge(drawn.sem, drawn.at(r, n - 3))
                        act.copy(prob_t[:, n % 3, :], psum[:, TURN + n % 2, :]).then_inc(odd_kept.sem, 1)

                    for n in range(STEPS):
                        act.wait_ge(nmax_ready.sem, nmax_ready.at(r, n))
                        if n >= 3:
                            act.wait_ge(turned.sem, turned.at(r, n - 3))
                        act.activation(prob[:, n % 3, :], psum[:, SIM + n % 3, :], ACT.Exp, bias=nmax[:, n:n + 1])\
                           .then_inc(prob_ready.sem, 1)
                        if n >= 3 and n % 2:
                            keep(n - 2)
                    keep(STEPS - 1)
                    act.wait_ge(att_turned.sem, att_turned.at(r))
                    act.copy(att_t[:, :], psum[:, MISC, :]).then_inc(att_t_ready.sem, 1)
                    norm.scalar(act, r)

            @block.vector
            def _(dve):
                dve.sem_inc(round_done.sem, 1)
                dve.wait_ge(w_in.sem, 16)
                dve.wait_ge(ones_ready.sem, 1)
                with dve.Fori(0, B) as r:
                    for t in range(8):
                        dve.wait_ge(qk_raw.sem, qk_raw.at(r, t))
                        dst = (q if t < 4 else k)[:, t % 4, :]
                        if t < 4:
                            dve.tensor_scalar(dst, psum[:, t % 4, :], col("bq", t), SCALE, ALU.add, ALU.mult)\
                               .then_inc(qk_ready.sem, 1)
                        else:
                            dve.tensor_scalar(dst, psum[:, t % 4, :], col("bk", t - 4), None, ALU.add)\
                               .then_inc(qk_ready.sem, 1)
                    dve.wait_ge(v_raw.sem, v_raw.at(r))
                    for c in range(CH):
                        dve.tensor_tensor(v[:, c, :, 0:DH],
                                          psum[:, MISC, c * P:(c + 1) * P].rearrange("p (h d) -> p h d", d=DH),
                                          L3A.of(w, "bv").rearrange("p (h d) -> p h d", d=DH), ALU.add)\
                           .then_inc(v_ready.sem, 1)

                    def keep(n):
                        dve.wait_ge(turned.sem, turned.at(r, n))
                        if n >= 3:
                            dve.wait_ge(drawn.sem, drawn.at(r, n - 3))
                        dve.tensor_copy(prob_t[:, n % 3, :], psum[:, TURN + n % 2, :]).then_inc(even_kept.sem, 1)

                    def divide(c):
                        dve.wait_ge(drawn.sem, drawn.at(r, c * H + H - 1))
                        num = psum[:, NUM + c % 2, 0:H * DV].rearrange("p (h d) -> p h d", d=DV)
                        dve.reciprocal(rden[:, c, :], num[:, :, DH]).then_inc(rden_ready.sem, 1)
                        dve.wait_ge(rden_ready.sem, rden_ready.at(r, c))
                        dve.tensor_tensor(att[:, c, :].rearrange("p (h d) -> p h d", d=DH), num[:, :, 0:DH],
                                          rden[:, c, :].unsqueeze(2).to_broadcast([P, H, DH]), ALU.mult)\
                           .then_inc(att_ready.sem, 1)

                    for n in range(STEPS):
                        dve.wait_ge(sim_ready.sem, sim_ready.at(r, n))
                        dve.tensor_reduce(nmax[:, n:n + 1], psum[:, SIM + n % 3, :], AX.X, ALU.max, negate=True)\
                           .then_inc(nmax_ready.sem, 1)
                        if n >= 2 and n % 2 == 0:
                            keep(n - 2)
                        if n % H == 8 and n > H:
                            divide(n // H - 1)
                    keep(STEPS - 2)
                    divide(CH - 1)
                    dve.wait_ge(out_ready.sem, out_ready.at(r))
                    dve.scalar_tensor_tensor(out=res[:, :], in0=psum[:, 2, :], scalar=col("bo"), in1=x[:, :],
                                             op0=ALU.add, op1=ALU.add).then_inc(res_ready.sem, 1)
                    dve.wait_ge(res_ready.sem, res_ready.at(r))
                    norm.vector(dve, r, res[:, :])
                    dve.wait_ge(norm.rstd_ready.sem, norm.rstd_ready.at(r))
                    dve.scalar_tensor_tensor(out=scaled[:, :], in0=norm.centred[:, :], scalar=col("gamma"),
                                             in1=norm.rstd[:, :], op0=ALU.mult, op1=ALU.mult)\
                       .then_inc(scaled_ready.sem, 1)
                    dve.wait_ge(scaled_ready.sem, scaled_ready.at(r))
                    dve.tensor_scalar(core.s[:, cols(r)], scaled[:, :], col("beta"), None, ALU.add)\
                       .then_inc(round_done.sem, 1)


L3_EXPERTS, L3_RANK = 8, 16
L3F = Fields(("weight", P), ("gate", L3_EXPERTS), ("u", P), ("v", P))


def l3_ffn_layout(np, i):
    g = lambda k: i["L3_ffn_" + k]
    return {"l3f": pack(np, [g("weight").T, g("gate_w").T, g("lora_U").reshape(P, P).T,
                             g("lora_V").transpose(0, 2, 1).reshape(P, P)])}


LAYOUTS.append(l3_ffn_layout)


def l3_ffn_phase(core):
    nc, psum = core.nc, core.psum
    E, R, NT = L3_EXPERTS, L3_RANK, T // P
    with Phase(core, "l3f") as ph:
        w = ph.buf("w", L3F.width)
        top, gate = ph.buf("top", NT), ph.buf("gate", NT, E)
        total, rtotal = ph.buf("total", NT), ph.buf("rtotal", NT)
        gate_n = ph.buf("gate_n", NT, E)
        gate_wide = ph.buf("gate_wide", NT, P)
        low, mixed = ph.buf("low", 2, N), ph.buf("mixed", 2, N)
        w_in, logit_ready = ph.semaphore("w_in"), ph.semaphore("logit_ready")
        top_ready, shifted_ready, exp_ready = ph.semaphore("top_ready"), ph.semaphore("shifted_ready"), ph.semaphore("exp_ready")
        total_ready, rtotal_ready = ph.semaphore("total_ready"), ph.semaphore("rtotal_ready")
        gate_ready, wide_ready = ph.semaphore("gate_ready"), ph.semaphore("wide_ready")
        turned, low_raw, low_ready = ph.semaphore("turned"), ph.semaphore("low_raw"), ph.semaphore("low_ready")
        mixed_ready, out_ready, out_kept = ph.semaphore("mixed_ready"), ph.semaphore("out_ready"), ph.semaphore("out_kept")
        with nc.Block() as block:
            @block.sync
            def _(sp):
                sp.dma_start(w[:, :], core.dram["l3f"]).then_inc(w_in.sem, 16)

            @block.tensor
            def _(pe):
                pe.wait_ge(w_in.sem, 16)
                for t in range(NT):
                    mm = pe.matmul(psum[:, 0, t * E:(t + 1) * E], core.xn[:, t * P:(t + 1) * P], L3F.of(w, "gate"),
                                   start=(t == 0), stop=(t == NT - 1), skip_group_check=True)
                mm.then_inc(logit_ready.sem, 1)
                for b in range(B):
                    if b >= 2:
                        pe.wait_ge(low_ready.sem, low_ready.at(b - 2))
                    pe.matmul(psum[:, 1 + b % 2, :], L3F.of(w, "u"), core.xn[:, b * N:(b + 1) * N],
                              start=True, stop=True).then_inc(low_raw.sem, 1)
                    pe.wait_ge(wide_ready.sem, 1)
                    if b >= 2:
                        pe.wait_ge(mixed_ready.sem, mixed_ready.at(b - 2))
                    for c in range(CH):
                        mm = pe.transpose(psum[:, 3 + b % 2, c * P:(c + 1) * P], gate_wide[:, b * CH + c, :],
                                          core.c("ident"))
                    mm.then_inc(turned.sem, 1)
                    if b >= 2:
                        pe.wait_ge(out_kept.sem, out_kept.at(b - 2))
                    pe.matmul(psum[:, 5 + b % 2, :], L3F.of(w, "weight"), core.xn[:, b * N:(b + 1) * N],
                              start=True, stop=False)
                    pe.wait_ge(mixed_ready.sem, mixed_ready.at(b))
                    pe.matmul(psum[:, 5 + b % 2, :], L3F.of(w, "v"), mixed[:, b % 2, :], start=False, stop=True)\
                      .then_inc(out_ready.sem, 1)

            @block.scalar
            def _(act):
                act.wait_ge(shifted_ready.sem, 1)
                act.activation(gate[:, :, :], gate[:, :, :], ACT.Exp).then_inc(exp_ready.sem, 1)
                for b in range(B):
                    act.wait_ge(low_raw.sem, low_raw.at(b))
                    if b >= 2:
                        act.wait_ge(mixed_ready.sem, mixed_ready.at(b - 2))
                    act.mul(low[:, b % 2, :], psum[:, 1 + b % 2, :], 1.0 / R).then_inc(low_ready.sem, 1)

            @block.vector
            def _(dve):
                dve.wait_ge(logit_ready.sem, 1)
                logit = psum[:, 0, 0:NT * E].rearrange("p (t e) -> p t e", e=E)
                dve.tensor_reduce(top[:, :], logit, AX.X, ALU.max).then_inc(top_ready.sem, 1)
                dve.wait_ge(top_ready.sem, 1)
                dve.tensor_tensor(gate[:, :, :], logit, top[:, :].unsqueeze(2).to_broadcast([P, NT, E]), ALU.subtract)\
                   .then_inc(shifted_ready.sem, 1)
                dve.wait_ge(exp_ready.sem, 1)
                dve.tensor_reduce(total[:, :], gate[:, :, :], AX.X, ALU.add).then_inc(total_ready.sem, 1)
                dve.wait_ge(total_ready.sem, 1)
                dve.reciprocal(rtotal[:, :], total[:, :]).then_inc(rtotal_ready.sem, 1)
                dve.wait_ge(rtotal_ready.sem, 1)
                dve.tensor_tensor(gate_n[:, :, :], gate[:, :, :], rtotal[:, :].unsqueeze(2).to_broadcast([P, NT, E]),
                                  ALU.mult).then_inc(gate_ready.sem, 1)
                dve.wait_ge(gate_ready.sem, 1)
                dve.tensor_copy(gate_wide[:, :, :].rearrange("p t (e r) -> p (t e) r", r=R),
                                gate_n[:, :, :].rearrange("p t e -> p (t e)").unsqueeze(2).to_broadcast([P, NT * E, R]))\
                   .then_inc(wide_ready.sem, 1)
                for b in range(B):
                    dve.wait_ge(turned.sem, turned.at(b))
                    dve.wait_ge(low_ready.sem, low_ready.at(b))
                    if b >= 2:
                        dve.wait_ge(out_ready.sem, out_ready.at(b - 2))
                    dve.tensor_tensor(mixed[:, b % 2, :], psum[:, 3 + b % 2, :], low[:, b % 2, :], ALU.mult)\
                       .then_inc(mixed_ready.sem, 1)
                    dve.wait_ge(out_ready.sem, out_ready.at(b))
                    dve.tensor_copy(core.g[:, b * N:(b + 1) * N], psum[:, 5 + b % 2, :]).then_inc(out_kept.sem, 1)


def build(nc, dram):
    with ExitStack() as ctx:
        core = Core(nc, ctx, dram)
        load_phase(core)
        mix_phase(core, "norm0", mix=False)
        l0_attn_phase(core)
        l0_ffn_phase(core)
        mix_phase(core, "norm1")
        l1_attn_phase(core)
        l1_ffn_phase(core)
        mix_phase(core, "norm2")
        l2_attn_phase(core)
        l2_ffn_phase(core)
        mix_phase(core, "norm3")
        l3_attn_phase(core)
        l3_ffn_phase(core)
        mix_phase(core, "mix4", norm=False)
        store_phase(core)


def constants():
    import numpy as np
    sets = {"const": CONST, "const_l0a": CONST_L0A, "const_l0f": CONST_L0F, "const_l2f": CONST_L2F}
    out = {name: np.zeros((P, fields.width), np.float32) for name, fields in sets.items()}

    def put(name, value):
        for key, fields in sets.items():
            if name in fields.at:
                start, width = fields.at[name]
                out[key][:len(value), start:start + width] = value

    i = np.arange(P)
    put("ident", np.eye(P))
    put("mean", np.full((P, P), 1.0 / P))
    put("causal", np.arange(N)[None, :] >= i[:, None])
    put("ones64", i[:, None] // 64 == i[None, :] // 64)
    swap = np.zeros((P, P))
    for h in (0, 64):
        for d in range(32):
            swap[h + d + 32, h + d] = -1.0
            swap[h + d, h + d + 32] = 1.0
    put("swap64", swap)
    kv = np.zeros((P, 4, 9))
    for h in range(4):
        kv[32 * h:32 * h + 16, h, :] = 1.0
    put("kvmask", np.tile(kv.reshape(P, 36), (1, 4)))
    put("causal4", np.tile(i[None, :] >= i[:, None], (1, 4)))
    sign, nhalf = np.zeros((P, 4, 32)), np.zeros((P, 4, 32))
    for top in (0, 64):
        for h in range(4):
            sign[top + 8 * h:top + 8 * h + 8, h, 0:8] = 1.0
            sign[top + 8 * h:top + 8 * h + 8, h, 8:16] = -1.0
            nhalf[top + 32 + 8 * h:top + 32 + 8 * h + 8, h, 0:16] = -0.5
    put("sign", sign.reshape(P, P))
    put("nhalf", nhalf.reshape(P, P))
    key = np.arange(2 * P)[None, :] - P
    seen = (key <= i[:, None]) & (key >= i[:, None] - 64)
    put("window", np.where(seen, 0.0, -1e30))
    put("window_first", np.where(seen & (key >= 0), 0.0, -1e30))
    sel = np.zeros((8, 8, P))
    for e in range(8):
        sel[e, e, :] = 1.0
    put("sel8", sel.reshape(8, 8 * P))
    put("index8", np.tile(np.arange(8), (P, 1)))
    f = np.float32
    half = np.arange(0, 64, 2, dtype=f)
    inv = (f(1.0) / f(10000.0) ** (half / f(64))).astype(f)
    t = np.arange(N, dtype=f)
    angle = (t[:, None] * inv[None, :]).astype(f).astype(np.float64)
    base = ((half + f(0.4 * 64)) / f(1.4 * 64)).astype(np.float64)
    scale = base[None, :] ** ((t - N // 2) / 32.0)[:, None].astype(np.float64)
    four = lambda a: np.tile(a, (1, 4)).T
    cos, sin, scale = four(np.cos(angle)), four(np.sin(angle)), four(scale)
    put("rope_qc", 8.0 * cos * scale)
    put("rope_qs", 8.0 * sin * scale)
    put("rope_kc", cos / scale)
    put("rope_ks", sin / scale)
    put("eps5", np.full((P, 1), LN_EPS))
    put("eps_l2", np.full((P, 1), 2.0 ** -64))
    put("l2_back", np.full((P, 1), 15 * np.log(2.0)))
    return out


def kernel(**inputs):
    import numpy as np
    import concourse.bacc as bacc
    from concourse.bass_utils import run_bass_kernel_spmd as run

    inputs = {k: np.asarray(v) for k, v in inputs.items()}
    arrays = {"x": inputs["L0_attn_x"], **constants()}
    for phase_layout in LAYOUTS:
        arrays.update(phase_layout(np, inputs))
    arrays = {f"in_{k}": np.ascontiguousarray(v) for k, v in arrays.items()}
    nc = bacc.Bacc("TRN2", target_bir_lowering=False, num_devices=1)
    dram = {k[3:]: nc.dram_tensor(k, v.shape, F32, kind="ExternalInput").ap() for k, v in arrays.items()}
    dram["out"] = nc.dram_tensor("out", (B, N, P), F32, kind="ExternalOutput").ap()
    build(nc, dram)
    result = run(nc, [arrays], core_ids=[0])
    return result.results[0]["out"]
```

```python
from contextlib import ExitStack

import concourse.bass as bass
from concourse import mybir

P = 128
B = 4
N = 512
T = B * N
CH = N // P

F32 = mybir.dt.float32
U32 = mybir.dt.uint32
ALU = mybir.AluOpType
ACT = mybir.ActivationFunctionType
AX = mybir.AxisListType
EXP_LN_SET = "natural_log_exp_and_others"
LN_EPS = 1e-5


class Fields:

    def __init__(self, *fields):
        self.at, self.width = {}, 0
        for name, width in fields:
            self.at[name] = (self.width, width)
            self.width += width

    def of(self, buf, name, part=0, width=None):
        start, whole = self.at[name]
        width = width or whole
        return buf[:, start + part * width:start + (part + 1) * width]


CONST = Fields(("ident", P), ("mean", P), ("causal", N), ("eps5", 1))
CONST_L0A = Fields(("kvmask", 16 * 9), ("causal4", N), ("sign", P), ("nhalf", P), ("head_rows", 8))
CONST_L0F = Fields(("ones64", P), ("swap64", P), ("window_first", 2 * P), ("window", 2 * P),
                   ("rope_qc", N), ("rope_qs", N), ("rope_kc", N), ("rope_ks", N), ("eps_l2", 1), ("l2_back", 1))
CONST_L3A = Fields(("less1", 2), ("less2", 2))
CONST_L2F = Fields(("sel8", 8 * P), ("index8", 8))


class Signal:

    def __init__(self, sem, per_round=1):
        self.sem = sem
        self.per_round = per_round

    def at(self, r, k=0):
        return r * self.per_round + k + 1


def apart(eng, passed):
    eng.sem_inc(passed.sem, 1)


class Core:

    def __init__(self, nc, ctx, dram):
        self.nc, self.dram = nc, dram
        sb = lambda name, cols: ctx.enter_context(nc.sbuf_tensor(name, [P, cols], F32))
        self.x = sb("x_res", T)
        self.xn = sb("x_norm", T)
        self.s = sb("s_branch", T)
        self.g = sb("g_branch", T)
        self.const = sb("const", CONST.width)
        self.psum = ctx.enter_context(nc.psum_tensor("psum", [P, 8, N], F32))

    def c(self, name):
        return CONST.of(self.const, name)


class Phase:

    def __init__(self, core, name):
        self.core, self.nc, self.name = core, core.nc, name

    def __enter__(self):
        self.ctx = ExitStack()
        self.sems = []
        return self

    def buf(self, name, *shape, dtype=F32):
        return self.ctx.enter_context(self.nc.sbuf_tensor(f"{self.name}_{name}", [P, *shape], dtype))

    def semaphore(self, name, per_round=1):
        sem = self.ctx.enter_context(self.nc.semaphore(f"{self.name}_{name}"))
        self.sems.append(sem)
        return Signal(sem, per_round)

    def __exit__(self, *failure):
        if failure[0] is None:
            with self.nc.Block() as block:
                @block.sync
                def _(sp):
                    for sem in self.sems:
                        sp.sem_clear(sem)
        self.ctx.close()


def cols(r, width=N):
    return bass.ds(r * width, width)


class ColumnNorm:

    def __init__(self, ph, name, *banks, centre=True, eps="eps5"):
        self.core, self.centre, self.eps, self.banks = ph.core, centre, eps, banks
        self.centred = ph.buf(name + "_centred", N)
        self.squared = ph.buf(name + "_squared", N)
        self.logvar = ph.buf(name + "_logvar", N)
        self.rstd = ph.buf(name + "_rstd", N)
        self.mean_ready = ph.semaphore(name + "_mean_ready", len(banks))
        self.centred_ready = ph.semaphore(name + "_centred_ready", len(banks))
        self.squared_ready = ph.semaphore(name + "_squared_ready", len(banks))
        self.var_ready = ph.semaphore(name + "_var_ready", len(banks))
        self.logvar_ready = ph.semaphore(name + "_logvar_ready", len(banks))
        self.rstd_ready = ph.semaphore(name + "_rstd_ready", len(banks))

    def tensor_mean(self, pe, x, k=0):
        pe.matmul(self.core.psum[:, self.banks[k][0], :], self.core.c("mean"), x, start=True, stop=True)\
          .then_inc(self.mean_ready.sem, 1)

    def tensor_var(self, pe, r, k=0):
        pe.wait_ge(self.squared_ready.sem, self.squared_ready.at(r, k))
        pe.matmul(self.core.psum[:, self.banks[k][1], :], self.core.c("mean"), self.squared[:, :],
                  start=True, stop=True).then_inc(self.var_ready.sem, 1)

    def tensor(self, pe, r, x, k=0):
        if self.centre:
            self.tensor_mean(pe, x, k)
        self.tensor_var(pe, r, k)

    def vector(self, dve, r, x, k=0):
        dve.wait_ge(self.mean_ready.sem, self.mean_ready.at(r, k))
        dve.tensor_tensor(self.centred[:, :], x, self.core.psum[:, self.banks[k][0], :], ALU.subtract)\
           .then_inc(self.centred_ready.sem, 1)

    def scalar_square(self, act, r, x=None, k=0):
        if self.centre:
            act.wait_ge(self.centred_ready.sem, self.centred_ready.at(r, k))
            x = self.centred[:, :]
        act.activation(self.squared[:, :], x, ACT.Square).then_inc(self.squared_ready.sem, 1)

    def scalar_rstd(self, act, r, k=0):
        act.wait_ge(self.var_ready.sem, self.var_ready.at(r, k))
        act.activation(self.logvar[:, :], self.core.psum[:, self.banks[k][1], :], ACT.Ln,
                       bias=self.core.c(self.eps)).then_inc(self.logvar_ready.sem, 1)
        act.wait_ge(self.logvar_ready.sem, self.logvar_ready.at(r, k))
        act.activation(self.rstd[:, :], self.logvar[:, :], ACT.Exp, scale=-0.5)\
           .then_inc(self.rstd_ready.sem, 1)

    def scalar(self, act, r, x=None, k=0):
        self.scalar_square(act, r, x, k)
        self.scalar_rstd(act, r, k)


LAYOUTS = []


def pack(np, pieces):
    out = np.zeros((P, sum(a.shape[1] for a in pieces)), np.float32)
    at = 0
    for a in pieces:
        out[:a.shape[0], at:at + a.shape[1]] = a
        at += a.shape[1]
    return out


def blocks(np, w, size=P):
    k, n = w.shape[0] // size, w.shape[1]
    return w.reshape(k, size, n).transpose(1, 0, 2).reshape(size, k * n)


def column(v):
    return v.reshape(-1, 1)




def load_phase(core):
    nc = core.nc
    with Phase(core, "load") as ph:
        rows = ph.buf("rows", T // P, P)
        const_in = ph.semaphore("const_in")
        rows_in = ph.semaphore("rows_in")
        turned = ph.semaphore("turned")
        x_ready = ph.semaphore("x_ready")
        with nc.Block() as block:
            @block.sync
            def _(sp):
                sp.dma_start(core.const[:, :], core.dram["const"]).then_inc(const_in.sem, 16)
                sp.dma_start(rows[:, :, :], core.dram["x"].rearrange("b (c p) d -> p (b c) d", p=P))\
                  .then_inc(rows_in.sem, 16)

            @block.tensor
            def _(pe):
                pe.wait_ge(const_in.sem, 16)
                pe.wait_ge(rows_in.sem, 16)
                for b in range(B):
                    for c in range(CH):
                        turn = pe.transpose(core.psum[:, b, c * P:(c + 1) * P], rows[:, b * CH + c, :],
                                            core.c("ident"))
                    turn.then_inc(turned.sem, 1)

            @block.vector
            def _(dve):
                for b in range(B):
                    dve.wait_ge(turned.sem, b + 1)
                    dve.tensor_copy(core.x[:, b * N:(b + 1) * N], core.psum[:, b, :]).then_inc(x_ready.sem, 1)


def mix_phase(core, name, mix=True, norm=True):
    nc = core.nc
    with Phase(core, name) as ph:
        gate = ph.buf("gate", T)
        gated = ph.buf("gated", T)
        centred = ph.buf("centred", T)
        squared = ph.buf("squared", T)
        logvar = ph.buf("logvar", T)
        rstd = ph.buf("rstd", T)
        gate_ready = ph.semaphore("gate_ready")
        gated_ready = ph.semaphore("gated_ready")
        x_ready = ph.semaphore("x_ready")
        mean_ready = ph.semaphore("mean_ready")
        centred_ready = ph.semaphore("centred_ready")
        squared_ready = ph.semaphore("squared_ready")
        var_ready = ph.semaphore("var_ready")
        logvar_ready = ph.semaphore("logvar_ready")
        rstd_ready = ph.semaphore("rstd_ready")
        xn_ready = ph.semaphore("xn_ready")
        batch = [slice(b * N, (b + 1) * N) for b in range(B)]
        mean_bank = [core.psum[:, b, :] for b in range(B)]
        var_bank = [core.psum[:, B + b, :] for b in range(B)]
        with nc.Block() as block:
            @block.tensor
            def _(pe):
                if not norm:
                    return
                for b in range(B):
                    if mix:
                        pe.wait_ge(x_ready.sem, x_ready.at(b))
                    pe.matmul(mean_bank[b], core.c("mean"), core.x[:, batch[b]], start=True, stop=True)\
                      .then_inc(mean_ready.sem, 1)
                for b in range(B):
                    pe.wait_ge(squared_ready.sem, squared_ready.at(b))
                    pe.matmul(var_bank[b], core.c("mean"), squared[:, batch[b]], start=True, stop=True)\
                      .then_inc(var_ready.sem, 1)

            @block.vector
            def _(dve):
                if mix:
                    for b in range(B):
                        dve.wait_ge(gate_ready.sem, gate_ready.at(b))
                        dve.tensor_tensor(gated[:, batch[b]], core.s[:, batch[b]], gate[:, batch[b]], ALU.mult)\
                           .then_inc(gated_ready.sem, 1)
                        dve.wait_ge(gated_ready.sem, gated_ready.at(b))
                        dve.tensor_tensor(core.x[:, batch[b]], core.x[:, batch[b]], gated[:, batch[b]], ALU.add)\
                           .then_inc(x_ready.sem, 1)
                if norm:
                    for b in range(B):
                        dve.wait_ge(mean_ready.sem, mean_ready.at(b))
                        dve.tensor_tensor(centred[:, batch[b]], core.x[:, batch[b]], mean_bank[b], ALU.subtract)\
                           .then_inc(centred_ready.sem, 1)
                    for b in range(B):
                        dve.wait_ge(rstd_ready.sem, rstd_ready.at(b))
                        dve.tensor_tensor(core.xn[:, batch[b]], centred[:, batch[b]], rstd[:, batch[b]], ALU.mult)\
                           .then_inc(xn_ready.sem, 1)

            @block.scalar
            def _(act):
                if mix:
                    for b in range(B):
                        act.activation(gate[:, batch[b]], core.g[:, batch[b]], ACT.Silu).then_inc(gate_ready.sem, 1)
                if norm:
                    act.preload_act_table_set(EXP_LN_SET)
                    for b in range(B):
                        act.wait_ge(centred_ready.sem, centred_ready.at(b))
                        act.activation(squared[:, batch[b]], centred[:, batch[b]], ACT.Square)\
                           .then_inc(squared_ready.sem, 1)
                    for b in range(B):
                        act.wait_ge(var_ready.sem, var_ready.at(b))
                        act.activation(logvar[:, batch[b]], var_bank[b], ACT.Ln, bias=core.c("eps5"))\
                           .then_inc(logvar_ready.sem, 1)
                        act.wait_ge(logvar_ready.sem, logvar_ready.at(b))
                        act.activation(rstd[:, batch[b]], logvar[:, batch[b]], ACT.Exp, scale=-0.5)\
                           .then_inc(rstd_ready.sem, 1)


def store_phase(core):
    nc = core.nc
    with Phase(core, "store") as ph:
        rows = ph.buf("rows", T // P, P)
        turned = ph.semaphore("turned")
        rows_ready = ph.semaphore("rows_ready")
        stored = ph.semaphore("stored")
        out = core.dram["out"].rearrange("b (c p) d -> p (b c) d", p=P)
        with nc.Block() as block:
            @block.tensor
            def _(pe):
                for b in range(B):
                    for c in range(CH):
                        t = b * CH + c
                        turn = pe.transpose(core.psum[:, b, c * P:(c + 1) * P], core.x[:, t * P:(t + 1) * P],
                                            core.c("ident"))
                    turn.then_inc(turned.sem, 1)

            @block.vector
            def _(dve):
                for b in range(B):
                    dve.wait_ge(turned.sem, turned.at(b))
                    dve.tensor_copy(rows[:, b * CH:(b + 1) * CH, :],
                                    core.psum[:, b, :].rearrange("p (c d) -> p c d", c=CH))\
                       .then_inc(rows_ready.sem, 1)

            @block.sync
            def _(sp):
                for b in range(B):
                    sp.wait_ge(rows_ready.sem, rows_ready.at(b))
                    sp.dma_start(out[:, b * CH:(b + 1) * CH, :], rows[:, b * CH:(b + 1) * CH, :])\
                      .then_inc(stored.sem, 16)
                sp.wait_ge(stored.sem, 16 * B)


L0_LAYERS, L0_HEADS, L0_FF = 6, 16, 512
L0_DH = P // L0_HEADS
L0A = Fields(("wq", 2 * P), ("wk", 2 * P), ("wv", P), ("omega", P), ("bv", P), ("bq", 2), ("bk", 2))
L0M = Fields(("wo", P), ("w1", L0_FF), ("w2", L0_FF), ("bo", 1), ("g1", 1), ("be1", 1),
             ("bf1", L0_FF // P), ("bf2", 1), ("g2", 1), ("be2", 1))


def l0_attn_layout(np, i):
    g = lambda k: i["L0_attn_" + k]
    order = [np.concatenate([np.arange(32 * x, 32 * x + 32) for x in (2 * t, 2 * t, 2 * t + 1, 2 * t + 1)])
             for t in range(2)]
    att, mlp = [], []
    for n in range(L0_LAYERS):
        omega = np.zeros((P, 8, 16), np.float32)
        for j in range(8):
            rows = slice(64 * (j // 4) + 8 * (j % 4), 64 * (j // 4) + 8 * (j % 4) + 8)
            omega[rows, j, 0:8] = g("omega")[n]
            omega[rows, j, 8:16] = g("omega")[n]
        att.append(pack(np, [
            g("Wq")[n][:, order[0]], g("Wq")[n][:, order[1]], g("Wk")[n][:, order[0]], g("Wk")[n][:, order[1]],
            g("Wv")[n], omega.reshape(P, P), np.tile(g("bv")[n], (P, 1)),
            g("bq")[n][order[0]][:, None], g("bq")[n][order[1]][:, None],
            g("bk")[n][order[0]][:, None], g("bk")[n][order[1]][:, None]]))
        mlp.append(pack(np, [
            g("Wo")[n], g("W1")[n], blocks(np, g("W2")[n]),
            column(g("bo")[n]), column(g("g1")[n]), column(g("be1")[n]), g("bf1")[n].reshape(-1, P).T,
            column(g("bf2")[n]), column(g("g2")[n]), column(g("be2")[n])]))
    return {"l0a": np.stack(att), "l0m": np.stack(mlp)}


LAYOUTS.append(l0_attn_layout)


def l0_attn_phase(core):
    nc, psum = core.nc, core.psum
    F, G, DH, DV = L0_FF // P, L0_HEADS // 4, L0_DH, L0_DH + 1
    SCALE = float(DH) ** -0.25
    ATT_EPS = 16 * 1e-6
    TL, W8 = 2, 8 * DV
    V_BANK, KV_BANK, TURN_BANK, NUM_BANK = 6, 5, 5, 4
    K_TOK_BANKS = (4, 5)
    OUT_BANK, DOWN_BANK, UP_BANKS = 6, 7, (7, 6)
    TILES = (2, 3, 0, 1)
    with Phase(core, "l0a") as ph:
        wa, wm = ph.buf("wa", L0A.width), ph.buf("wm", L0M.width)
        acol = lambda name, k=0: L0A.of(wa, name, k, 1)
        mcol = lambda name, k=0: L0M.of(wm, name, k, 1)
        h_in = ph.buf("h_in", N)
        qk = ph.buf("qk", 4, N)
        omega = ph.buf("omega", P)
        omega_signed = ph.buf("omega_signed", P)
        feat = ph.buf("feat", 2 * TL, N)
        apart_q = ph.buf("apart_q", G, CH, 4, P)
        v = ph.buf("v", CH, L0_HEADS, DV)
        k_tok = ph.buf("k_tok", CH - 1, TL * P)
        kv = ph.buf("kv", CH - 1, L0_HEADS * DV)
        state = ph.buf("state", CH - 1, L0_HEADS * DV)
        scores = ph.buf("scores", 2, 4, N)
        den = ph.buf("den", CH, L0_HEADS)
        rden = ph.buf("rden", CH, L0_HEADS)
        att = ph.buf("att", CH, P)
        att_t = ph.buf("att_t", N)
        res1, res2 = ph.buf("res1", N), ph.buf("res2", N)
        scaled1, scaled2 = ph.buf("scaled1", N), ph.buf("scaled2", N)
        h1 = ph.buf("h1", N)
        y = ph.buf("y", F, N)

        table = ph.buf("table", CONST_L0A.width)
        const = lambda name: CONST_L0A.of(table, name)
        table_in = ph.semaphore("table_in")
        passed = ph.semaphore("passed")
        wa_in, wm_in = ph.semaphore("wa_in", 16), ph.semaphore("wm_in", 16)
        s_ready = ph.semaphore("s_ready")
        ones_ready = ph.semaphore("ones_ready")
        omega_signed_ready, omega_ready = ph.semaphore("omega_signed_ready"), ph.semaphore("omega_ready")
        h_ready = ph.semaphore("h_ready")
        proj_ready = ph.semaphore("proj_ready", 4)
        qk_ready, qk_sq_ready = ph.semaphore("qk_ready", 4), ph.semaphore("qk_sq_ready", 4)
        v_ready, v_kept = ph.semaphore("v_ready"), ph.semaphore("v_kept")
        placed01, placed23 = ph.semaphore("placed01", G), ph.semaphore("placed23", G)
        arg_ready, feat_ready = ph.semaphore("arg_ready", 4), ph.semaphore("feat_ready", 4)
        k_tok_ready, k_tok_kept = ph.semaphore("k_tok_ready", 2), ph.semaphore("k_tok_kept", 2)
        kv_ready, kv_kept = ph.semaphore("kv_ready", CH - 1), ph.semaphore("kv_kept", CH - 1)
        state_ready = ph.semaphore("state_ready", CH - 1)
        scores_ready, scores_kept = ph.semaphore("scores_ready", CH * G), ph.semaphore("scores_kept", CH * G)
        num_ready = ph.semaphore("num_ready", CH)
        den_ready, rden_ready = ph.semaphore("den_ready", CH), ph.semaphore("rden_ready", CH)
        att_ready = ph.semaphore("att_ready", CH)
        att_t_ready, att_t_kept = ph.semaphore("att_t_ready"), ph.semaphore("att_t_kept")
        out_ready, res_ready = ph.semaphore("out_ready", 2), ph.semaphore("res_ready", 2)
        norm = ColumnNorm(ph, "norm", (7, 6), (6, 7))
        scaled_ready = ph.semaphore("scaled_ready", 2)
        h1_ready = ph.semaphore("h1_ready")
        up_ready, y_ready = ph.semaphore("up_ready", F), ph.semaphore("y_ready", F)

        def steps(eng, step):
            step(0, 0, None, None, None)
            with eng.Fori(0, L0_LAYERS - 1) as layer:
                with eng.Fori(0, B - 1) as b:
                    r = layer * B + b
                    step(r + 1, layer, r, layer, b)
                step(layer * B + B, layer + 1, layer * B + B - 1, layer, B - 1)
            last = L0_LAYERS - 1
            with eng.Fori(0, B - 1) as b:
                step(b + (last * B + 1), last, b + last * B, last, b)
            step(None, None, L0_LAYERS * B - 1, last, B - 1)

        with nc.Block() as block:
            @block.sync
            def _(sp):
                sp.dma_start(table[:, :], core.dram["const_l0a"]).then_inc(table_in.sem, 16)
                sp.dma_start(wa[:, :], core.dram["l0a"][0, :, :]).then_inc(wa_in.sem, 16)
                sp.dma_start(wm[:, :], core.dram["l0m"][0, :, :]).then_inc(wm_in.sem, 16)
                with sp.Fori(0, L0_LAYERS - 1) as layer:
                    nxt = bass.ds(layer + 1, 1)
                    sp.wait_ge(k_tok_ready.sem, k_tok_ready.at(layer * B + B - 1, 0))
                    apart(sp, passed)
                    sp.dma_start(wa[:, :], core.dram["l0a"][nxt, :, :].rearrange("a p c -> (a p) c"))\
                      .then_inc(wa_in.sem, 16)
                    sp.wait_ge(s_ready.sem, s_ready.at(layer * B + B - 1) + B)
                    apart(sp, passed)
                    sp.dma_start(wm[:, :], core.dram["l0m"][nxt, :, :].rearrange("a p c -> (a p) c"))\
                      .then_inc(wm_in.sem, 16)

            @block.gpsimd
            def _(pool):
                for b in range(B):
                    pool.tensor_copy(core.s[:, b * N:(b + 1) * N], core.xn[:, b * N:(b + 1) * N])\
                        .then_inc(s_ready.sem, 1)
                pool.memset(v[:, :, :, DH:DV], 1.0).then_inc(ones_ready.sem, 1)
                pool.wait_ge(table_in.sem, 16)

                def make_omega(layer):
                    pool.wait_ge(wa_in.sem, (layer + 1) * 16)
                    pool.tensor_tensor(omega_signed[:, :], L0A.of(wa, "omega"), const("sign"), ALU.mult)\
                        .then_inc(omega_signed_ready.sem, 1)
                    pool.wait_ge(omega_signed_ready.sem, omega_signed_ready.at(layer))
                    pool.tensor_tensor(omega[:, :], omega_signed[:, :], const("nhalf"), ALU.add)\
                        .then_inc(omega_ready.sem, 1)

                def fetch(r, b):
                    pool.wait_ge(s_ready.sem, s_ready.at(r))
                    apart(pool, passed)
                    pool.tensor_copy(h_in[:, :], core.s[:, cols(b)]).then_inc(h_ready.sem, 1)

                make_omega(0)
                fetch(0, 0)
                with pool.Fori(0, L0_LAYERS - 1) as layer:
                    with pool.Fori(0, B - 1) as b:
                        r = layer * B + b
                        pool.wait_ge(v_ready.sem, v_ready.at(r))
                        fetch(r + 1, b + 1)
                    pool.wait_ge(v_ready.sem, v_ready.at(layer * B + B - 1))
                    fetch(layer * B + B, 0)
                    pool.wait_ge(arg_ready.sem, arg_ready.at(layer * B + B - 1, 3))
                    make_omega(layer + 1)
                with pool.Fori(0, B - 1) as b:
                    r = b + (L0_LAYERS - 1) * B
                    pool.wait_ge(v_ready.sem, v_ready.at(r))
                    fetch(r + 1, b + 1)

            @block.tensor
            def _(pe):
                pe.wait_ge(table_in.sem, 16)
                pe.wait_ge(ones_ready.sem, 1)

                def project(r, layer, n):
                    if n == 0:
                        pe.wait_ge(wa_in.sem, (layer + 1) * 16)
                        pe.wait_ge(h_ready.sem, h_ready.at(r))
                    t = TILES[n]
                    pe.matmul(psum[:, t, :], L0A.of(wa, "wq" if t < 2 else "wk", t % 2, P), h_in[:, :],
                              start=True, stop=True).then_inc(proj_ready.sem, 1)

                def project_v(r):
                    for c in range(CH):
                        mm = pe.matmul(psum[:, V_BANK, c * P:(c + 1) * P], h_in[:, c * P:(c + 1) * P],
                                       L0A.of(wa, "wv"), start=(c == 0), stop=(c == CH - 1),
                                       skip_group_check=True)
                    mm.then_inc(v_ready.sem, 1)

                def exponents(r, layer, ks):
                    pe.wait_ge(omega_ready.sem, omega_ready.at(layer))
                    for k in ks:
                        pe.wait_ge(qk_ready.sem, qk_ready.at(r, k))
                        pe.wait_ge(qk_sq_ready.sem, qk_sq_ready.at(r, k))
                        pe.matmul(psum[:, TILES[k], :], omega[:, :], qk[:, TILES[k], :], start=True, stop=True)\
                          .then_inc(arg_ready.sem, 1)

                def turn_keys(r, part):
                    pe.wait_ge(feat_ready.sem, feat_ready.at(r, 1))
                    for c in ((0, 1), (2,))[part]:
                        for t in range(TL):
                            at = (c % 2) * TL * P + t * P
                            mm = pe.transpose(psum[:, K_TOK_BANKS[part], at:at + P],
                                              feat[:, TL + t, c * P:(c + 1) * P], core.c("ident"))
                    mm.then_inc(k_tok_ready.sem, 1)

                def key_value(r, c):
                    if c == 0:
                        pe.wait_ge(v_kept.sem, v_kept.at(r))
                        pe.wait_ge(k_tok_kept.sem, k_tok_kept.at(r, 1))
                    else:
                        pe.wait_ge(kv_kept.sem, kv_kept.at(r, c - 1))
                    for t in range(TL):
                        mm = pe.matmul(psum[:, KV_BANK, t * W8:(t + 1) * W8], k_tok[:, c, t * P:(t + 1) * P],
                                       v[:, c, 8 * t:8 * t + 8, :],
                                       start=(t == 0), stop=(t == TL - 1), skip_group_check=True)
                    mm.then_inc(kv_ready.sem, 1)

                def score(r, c, g):
                    if c == 0:
                        pe.wait_ge(feat_ready.sem, feat_ready.at(r, 3))
                        pe.wait_ge(placed01.sem, placed01.at(r, g))
                        pe.wait_ge(placed23.sem, placed23.at(r, g))
                    else:
                        pe.wait_ge(scores_kept.sem, scores_kept.at(r, (c - 1) * G + g))
                    pe.matmul(psum[:, g, :], feat[:, TL + g // 2, c * P:(c + 1) * P], apart_q[:, g, c, :, :],
                              start=True, stop=True).then_inc(scores_ready.sem, 1)

                def gather(r, c, g):
                    if g == 0:
                        if c >= 1:
                            pe.wait_ge(att_ready.sem, att_ready.at(r, c - 1))
                            pe.wait_ge(state_ready.sem, state_ready.at(r, c - 1))
                        else:
                            pe.wait_ge(k_tok_kept.sem, k_tok_kept.at(r, 0))
                    if c >= 1 and g % 2 == 0:
                        t = g // 2
                        pe.matmul(psum[:, NUM_BANK, t * W8:(t + 1) * W8],
                                  feat[:, t, c * P:(c + 1) * P], state[:, c - 1, t * W8:(t + 1) * W8],
                                  start=(t == 0), stop=False, skip_group_check=True)
                    pe.wait_ge(scores_kept.sem, scores_kept.at(r, c * G + g))
                    for h in range(4):
                        mm = pe.matmul(psum[:, NUM_BANK, (4 * g + h) * DV:(4 * g + h + 1) * DV],
                                       scores[:, c % 2, g, h * P:(h + 1) * P], v[:, c, 4 * g + h, :],
                                       start=(c == 0 and g == 0 and h == 0),
                                       stop=(g == G - 1 and h == 3), skip_group_check=True)
                    if g == G - 1:
                        mm.then_inc(num_ready.sem, 1)

                def turn(r, c):
                    if c == 0:
                        pe.wait_ge(kv_kept.sem, kv_kept.at(r, CH - 2))
                    pe.wait_ge(att_ready.sem, att_ready.at(r, c))
                    mm = pe.transpose(psum[:, TURN_BANK, c * P:(c + 1) * P], att[:, c, :], core.c("ident"))
                    if c == CH - 1:
                        mm.then_inc(att_t_ready.sem, 1)

                def output(m, layer, a):
                    pe.wait_ge(wm_in.sem, (layer + 1) * 16)
                    if a is not None:
                        pe.wait_ge(v_kept.sem, v_kept.at(a))
                    pe.wait_ge(att_t_kept.sem, att_t_kept.at(m))
                    pe.matmul(psum[:, OUT_BANK, :], L0M.of(wm, "wo"), att_t[:, :], start=True, stop=True)\
                      .then_inc(out_ready.sem, 1)

                def mean(m, k):
                    pe.wait_ge(res_ready.sem, res_ready.at(m, k))
                    norm.tensor_mean(pe, (res1, res2)[k][:, :], k)

                def up(m):
                    pe.wait_ge(h1_ready.sem, h1_ready.at(m))
                    for f in range(F):
                        if f >= 2:
                            pe.wait_ge(y_ready.sem, y_ready.at(m, f - 2))
                        pe.matmul(psum[:, UP_BANKS[f % 2], :], L0M.of(wm, "w1", f, P), h1[:, :],
                                  start=True, stop=True).then_inc(up_ready.sem, 1)

                def down(m):
                    pe.wait_ge(y_ready.sem, y_ready.at(m, F - 1))
                    for f in range(F):
                        mm = pe.matmul(psum[:, DOWN_BANK, :], L0M.of(wm, "w2", f, P), y[:, f, :],
                                       start=(f == 0), stop=(f == F - 1))
                    mm.then_inc(out_ready.sem, 1)

                def step(a, a_layer, m, m_layer, m_batch):
                    for n in range(4):
                        if a is not None:
                            project(a, a_layer, n)
                        if m is not None:
                            gather(m, 3, n)
                    if a is not None:
                        project_v(a)
                        exponents(a, a_layer, range(0, 2))
                    if m is not None:
                        turn(m, CH - 1)
                    if a is not None:
                        exponents(a, a_layer, range(2, 4))
                    if m is not None:
                        output(m, m_layer, a)
                    if a is not None:
                        if m is not None:
                            pe.wait_ge(att_ready.sem, att_ready.at(m, CH - 1))
                        turn_keys(a, 0)
                        turn_keys(a, 1)
                    if m is not None:
                        mean(m, 0)
                    if a is not None:
                        key_value(a, 0)
                    if m is not None:
                        norm.tensor_var(pe, m, 0)
                    if a is not None:
                        for g in range(G):
                            score(a, 0, g)
                        key_value(a, 1)
                    if m is not None:
                        up(m)
                    if a is not None:
                        for g in range(G):
                            score(a, 1, g)
                            gather(a, 0, g)
                        key_value(a, 2)
                    if m is not None:
                        down(m)
                    if a is not None:
                        turn(a, 0)
                        for g in range(G):
                            score(a, 2, g)
                            gather(a, 1, g)
                    if m is not None:
                        mean(m, 1)
                    if a is not None:
                        turn(a, 1)
                        for g in range(G):
                            score(a, 3, g)
                            gather(a, 2, g)
                    if m is not None:
                        norm.tensor_var(pe, m, 1)
                    if a is not None:
                        turn(a, 2)

                steps(pe, step)

            @block.scalar
            def _(act):
                act.wait_ge(table_in.sem, 16)
                act.preload_act_table_set(EXP_LN_SET)

                def square(r, ks):
                    for k in ks:
                        act.wait_ge(qk_ready.sem, qk_ready.at(r, k))
                        for rows in (slice(32, 64), slice(96, 128)):
                            sq = act.activation(qk[rows, TILES[k], :], qk[rows, TILES[k], :], ACT.Square)
                        sq.then_inc(qk_sq_ready.sem, 1)

                def features(r):
                    for k in range(4):
                        act.wait_ge(arg_ready.sem, arg_ready.at(r, k))
                        act.activation(feat[:, TILES[k], :], psum[:, TILES[k], :], ACT.Exp)\
                           .then_inc(feat_ready.sem, 1)

                def place01(r, g):
                    act.wait_ge(feat_ready.sem, feat_ready.at(r, 2 + g // 2))
                    for h in (0, 1):
                        last = act.activation(apart_q[:, g, :, h, :],
                                              feat[:, g // 2, :].rearrange("p (c q) -> p c q", c=CH), ACT.Relu,
                                              scale=CONST_L0A.of(table, "head_rows", 4 * (g % 2) + h, 1))
                    last.then_inc(placed01.sem, 1)

                def keep_keys(r, part):
                    act.wait_ge(k_tok_ready.sem, k_tok_ready.at(r, part))
                    cs = (slice(0, 2), slice(2, 3))[part]
                    width = (cs.stop - cs.start) * TL * P
                    act.copy(k_tok[:, cs, :].rearrange("p c k -> p (c k)"), psum[:, K_TOK_BANKS[part], 0:width])\
                       .then_inc(k_tok_kept.sem, 1)

                def step(a, a_layer, m, m_layer, m_batch):
                    if a is not None:
                        square(a, range(4))
                    if m is not None:
                        act.wait_ge(att_t_ready.sem, att_t_ready.at(m))
                        act.copy(att_t[:, :], psum[:, TURN_BANK, :]).then_inc(att_t_kept.sem, 1)
                    if a is not None:
                        features(a)
                        keep_keys(a, 0)
                        keep_keys(a, 1)
                        place01(a, 0)
                    if m is not None:
                        norm.scalar_square(act, m, k=0)
                    if a is not None:
                        place01(a, 1)
                        place01(a, 2)
                    if m is not None:
                        norm.scalar_rstd(act, m, 0)
                    if a is not None:
                        place01(a, 3)
                    if m is not None:
                        act.wait_ge(wm_in.sem, (m_layer + 1) * 16)
                        for f in range(F):
                            act.wait_ge(up_ready.sem, up_ready.at(m, f))
                            act.activation(y[:, f, :], psum[:, UP_BANKS[f % 2], :], ACT.Relu, bias=mcol("bf1", f))\
                               .then_inc(y_ready.sem, 1)
                        norm.scalar(act, m, k=1)

                steps(act, step)

            @block.vector
            def _(dve):
                dve.wait_ge(table_in.sem, 16)
                dve.wait_ge(ones_ready.sem, 1)

                def keep_qk(r, layer):
                    dve.wait_ge(wa_in.sem, (layer + 1) * 16)
                    for k in range(4):
                        t = TILES[k]
                        dve.wait_ge(proj_ready.sem, proj_ready.at(r, k))
                        dve.tensor_scalar(qk[:, t, :], psum[:, t, :], acol("bq" if t < 2 else "bk", t % 2), SCALE,
                                          ALU.add, ALU.mult).then_inc(qk_ready.sem, 1)

                def keep_v(r):
                    dve.wait_ge(v_ready.sem, v_ready.at(r))
                    dve.tensor_tensor(v[:, :, :, 0:DH],
                                      psum[:, V_BANK, :].rearrange("p (c h d) -> p c h d", c=CH, d=DH),
                                      L0A.of(wa, "bv").rearrange("p (h d) -> p h d", d=DH).unsqueeze(1)
                                      .to_broadcast([P, CH, L0_HEADS, DH]), ALU.add).then_inc(v_kept.sem, 1)

                def place23(r, g):
                    dve.wait_ge(feat_ready.sem, feat_ready.at(r, 2 + g // 2))
                    for h in (2, 3):
                        last = dve.tensor_scalar(apart_q[:, g, :, h, :],
                                                 feat[:, g // 2, :].rearrange("p (c q) -> p c q", c=CH),
                                                 CONST_L0A.of(table, "head_rows", 4 * (g % 2) + h, 1), None, ALU.mult)
                    last.then_inc(placed23.sem, 1)

                def keep_state(r, c):
                    dve.wait_ge(kv_ready.sem, kv_ready.at(r, c))
                    dst = state if c == 0 else kv
                    dve.tensor_tensor(dst[:, c, :], psum[:, KV_BANK, 0:L0_HEADS * DV], const("kvmask"),
                                      ALU.mult).then_inc(kv_kept.sem, 1)
                    dve.wait_ge(kv_kept.sem, kv_kept.at(r, c))
                    if c == 0:
                        dve.sem_inc(state_ready.sem, 1)
                    else:
                        dve.wait_ge(state_ready.sem, state_ready.at(r, c - 1))
                        dve.tensor_tensor(state[:, c, :], state[:, c - 1, :], kv[:, c, :], ALU.add)\
                           .then_inc(state_ready.sem, 1)

                def mask(r, c):
                    for g in range(G):
                        dve.wait_ge(scores_ready.sem, scores_ready.at(r, c * G + g))
                        dve.tensor_tensor(scores[:, c % 2, g, :], psum[:, g, :], const("causal4"),
                                          ALU.mult).then_inc(scores_kept.sem, 1)

                def divide(r, c):
                    dve.wait_ge(num_ready.sem, num_ready.at(r, c))
                    num = psum[:, NUM_BANK, 0:L0_HEADS * DV].rearrange("p (h d) -> p h d", d=DV)
                    dve.tensor_scalar(den[:, c, :], num[:, :, DH], ATT_EPS, None, ALU.add)\
                       .then_inc(den_ready.sem, 1)
                    dve.wait_ge(den_ready.sem, den_ready.at(r, c))
                    dve.reciprocal(rden[:, c, :], den[:, c, :]).then_inc(rden_ready.sem, 1)
                    dve.wait_ge(rden_ready.sem, rden_ready.at(r, c))
                    dve.tensor_tensor(att[:, c, :].rearrange("p (h d) -> p h d", d=DH), num[:, :, 0:DH],
                                      rden[:, c, :].unsqueeze(2).to_broadcast([P, L0_HEADS, DH]), ALU.mult)\
                       .then_inc(att_ready.sem, 1)

                def scale(m, k, scaled, gain):
                    dve.wait_ge(norm.rstd_ready.sem, norm.rstd_ready.at(m, k))
                    dve.scalar_tensor_tensor(out=scaled[:, :], in0=norm.centred[:, :], scalar=gain,
                                             in1=norm.rstd[:, :], op0=ALU.mult, op1=ALU.mult)\
                       .then_inc(scaled_ready.sem, 1)
                    dve.wait_ge(scaled_ready.sem, scaled_ready.at(m, k))

                def step(a, a_layer, m, m_layer, m_batch):
                    if a is not None:
                        keep_qk(a, a_layer)
                    if m is not None:
                        divide(m, 3)
                    if a is not None:
                        keep_v(a)
                    if m is not None:
                        dve.wait_ge(wm_in.sem, (m_layer + 1) * 16)
                        dve.wait_ge(out_ready.sem, out_ready.at(m, 0))
                        dve.scalar_tensor_tensor(out=res1[:, :], in0=psum[:, OUT_BANK, :], scalar=mcol("bo"),
                                                 in1=core.s[:, cols(m_batch)], op0=ALU.add, op1=ALU.add)\
                           .then_inc(res_ready.sem, 1)
                        dve.wait_ge(res_ready.sem, res_ready.at(m, 0))
                        norm.vector(dve, m, res1[:, :], 0)
                    if a is not None:
                        place23(a, 0)
                        place23(a, 1)
                        keep_state(a, 0)
                        place23(a, 2)
                        place23(a, 3)
                    if m is not None:
                        scale(m, 0, scaled1, mcol("g1"))
                        dve.tensor_scalar(h1[:, :], scaled1[:, :], mcol("be1"), None, ALU.add)\
                           .then_inc(h1_ready.sem, 1)
                    if a is not None:
                        mask(a, 0)
                        keep_state(a, 1)
                        mask(a, 1)
                        divide(a, 0)
                        keep_state(a, 2)
                    if m is not None:
                        dve.wait_ge(h1_ready.sem, h1_ready.at(m))
                        dve.wait_ge(out_ready.sem, out_ready.at(m, 1))
                        dve.scalar_tensor_tensor(out=res2[:, :], in0=psum[:, DOWN_BANK, :], scalar=mcol("bf2"),
                                                 in1=h1[:, :], op0=ALU.add, op1=ALU.add).then_inc(res_ready.sem, 1)
                    if a is not None:
                        mask(a, 2)
                        divide(a, 1)
                    if m is not None:
                        dve.wait_ge(res_ready.sem, res_ready.at(m, 1))
                        norm.vector(dve, m, res2[:, :], 1)
                    if a is not None:
                        mask(a, 3)
                        divide(a, 2)
                    if m is not None:
                        scale(m, 1, scaled2, mcol("g2"))
                        dve.tensor_scalar(core.s[:, cols(m_batch)], scaled2[:, :], mcol("be2"), None, ALU.add)\
                           .then_inc(s_ready.sem, 1)

                steps(dve, step)


L0F_LAYERS, L0F_HEADS, L0F_INNER, L0F_HID = 2, 8, 512, 341
L0F_TILES = L0F_INNER // P
L0F_HT = -(-L0F_HID // P)
L0FE = Fields(("wq", L0F_INNER), ("wk", L0F_INNER), ("wv", L0F_INNER), ("q_scale", 1), ("k_scale", 1))
L0FL = Fields(("wo", L0F_INNER), ("w1", 2 * L0F_HT * P), ("w2", L0F_HT * P), ("ln_g", 1), ("ln_b", 1),
              ("b1", 2 * L0F_HT), ("b2", 1))


def l0_ffn_layout(np, i):
    g = lambda k: i["L0_ffn_" + k]
    hid = L0F_HID

    def halves(a):
        out = np.zeros((a.shape[0], 2, L0F_HT * P), np.float32)
        for x in range(2):
            out[:, x, :hid] = a[:, x * hid:(x + 1) * hid]
        return out.reshape(a.shape[0], 2 * L0F_HT, P)

    early, late = [], []
    for n in range(L0F_LAYERS):
        w2 = np.zeros((L0F_HT * P, P), np.float32)
        w2[:hid] = g("w2")[n]
        early.append(pack(np, [g("wqkv")[n], np.tile(g("q_scale")[n], 2)[:, None],
                               np.tile(g("k_scale")[n], 2)[:, None]]))
        late.append(pack(np, [
            blocks(np, g("wo")[n]), halves(g("w1")[n]).reshape(P, 2 * L0F_HT * P), blocks(np, w2),
            column(g("ln_g")[n]), column(g("ln_b")[n]), halves(g("b1")[n][None])[0].T, column(g("b2")[n])]))
    return {"l0fe": np.stack(early), "l0fl": np.stack(late)}


LAYOUTS.append(l0_ffn_layout)


def l0_ffn_phase(core):
    nc, psum = core.nc, core.psum
    H, TL, HT, W = L0F_HEADS, L0F_TILES, L0F_HT, 64
    T8 = 2 * TL
    TURN_BANKS, O_BANK, RAW_BANK, SUM_BANK, V_BANK, ROT_BANK = (2, 3), 4, 5, 6, 6, 7
    GATE_BANKS, UP_BANKS, WO_BANK, DOWN_BANK = (0, 1, 2), (3, 4, 0), 0, 1
    with Phase(core, "l0f") as ph:
        we, wl = ph.buf("we", L0FE.width), ph.buf("wl", L0FL.width)
        ecol = lambda name, k=0: L0FE.of(we, name, k, 1)
        lcol = lambda name, k=0: L0FL.of(wl, name, k, 1)
        swap = ph.buf("swap", 2, P)
        rope = ph.buf("rope", 2, N)
        h_in = ph.buf("h_in", N)
        sq = ph.buf("sq", 2, N)
        log, rinv = ph.buf("log", 2, N), ph.buf("rinv", 2, N)
        unit = ph.buf("unit", 2, N)
        by_cos, by_sin = ph.buf("by_cos", 2, N), ph.buf("by_sin", 2, N)
        qk = ph.buf("qk", 2, T8, N)
        v = ph.buf("v", 2, CH, L0F_INNER)
        sim = ph.buf("sim", H, 2 * P)
        nmax, total, rtotal = ph.buf("nmax", CH, H), ph.buf("total", CH, H), ph.buf("rtotal", CH, H)
        prob = ph.buf("prob", H, 2 * P)
        prob_n = ph.buf("prob_n", H, 2 * P)
        prob_t = ph.buf("prob_t", 2 * H, P)
        o = ph.buf("o", TL, N)
        x1, shifted = ph.buf("x1", N), ph.buf("shifted", N)
        scaled, hn = ph.buf("scaled", N), ph.buf("hn", N)
        gelu, hidden = ph.buf("gelu", HT, N), ph.buf("hidden", HT, N)
        head = [(s // 2) % 2 + 2 * (2 * (s // 4) + s % 2) for s in range(H)]

        table = ph.buf("table", CONST_L0F.width)
        const = lambda name: CONST_L0F.of(table, name)
        table_in = ph.semaphore("table_in")
        passed = ph.semaphore("passed")
        we_in, wl_in, zeroed = ph.semaphore("we_in"), ph.semaphore("wl_in"), ph.semaphore("zeroed", 3)
        g_ready = ph.semaphore("g_ready")
        swap_ready, rope_ready = ph.semaphore("swap_ready", 2), ph.semaphore("rope_ready", 2)
        h_ready = ph.semaphore("h_ready", 2)
        qk_raw, sq_ready, sum_ready = (ph.semaphore(x, T8) for x in ("qk_raw", "sq_ready", "sum_ready"))
        log_ready, rinv_ready = ph.semaphore("log_ready", T8), ph.semaphore("rinv_ready", T8)
        unit_ready, rot_ready = ph.semaphore("unit_ready", T8), ph.semaphore("rot_ready", T8)
        cos_ready, sin_ready = ph.semaphore("cos_ready", T8), ph.semaphore("sin_ready", T8)
        qk_ready = ph.semaphore("qk_ready", T8)
        v_ready, v_kept = ph.semaphore("v_ready", CH), ph.semaphore("v_kept", CH)
        sim_ready, sim_kept = ph.semaphore("sim_ready", 2 * CH), ph.semaphore("sim_kept", 2 * CH)
        nmax_ready, prob_ready = ph.semaphore("nmax_ready", 2 * CH), ph.semaphore("prob_ready", 2 * CH)
        rtotal_ready, prob_n_ready = ph.semaphore("rtotal_ready", 2 * CH), ph.semaphore("prob_n_ready", 2 * CH)
        turned, turned_kept = ph.semaphore("turned", 4 * CH), ph.semaphore("turned_kept", 4 * CH)
        o_ready, o_kept = ph.semaphore("o_ready", CH), ph.semaphore("o_kept", CH)
        wo_ready, down_ready = ph.semaphore("wo_ready"), ph.semaphore("down_ready")
        x1_ready, shifted_ready = ph.semaphore("x1_ready"), ph.semaphore("shifted_ready", 2)
        norm = ColumnNorm(ph, "norm", (1, 2))
        scaled_ready, hn_ready = ph.semaphore("scaled_ready"), ph.semaphore("hn_ready")
        gate_raw, up_raw = ph.semaphore("gate_raw", HT), ph.semaphore("up_raw", HT)
        gelu_ready, hidden_ready = ph.semaphore("gelu_ready", HT), ph.semaphore("hidden_ready", HT)

        def keys(c):
            return slice(W if c else P, 2 * P)

        def steps(layer, step):
            step(layer * B + 0, None, None)
            for b in range(B - 1):
                step(layer * B + (b + 1), layer * B + b, b)
            step(None, layer * B + (B - 1), B - 1)

        with nc.Block() as block:
            @block.sync
            def _(sp):
                sp.dma_start(table[:, :], core.dram["const_l0f"]).then_inc(table_in.sem, 16)
                sp.dma_start(we[:, :], core.dram["l0fe"][0, :, :]).then_inc(we_in.sem, 16)
                sp.dma_start(wl[:, :], core.dram["l0fl"][0, :, :]).then_inc(wl_in.sem, 16)
                with sp.Fori(1, L0F_LAYERS) as layer:
                    this = bass.ds(layer, 1)
                    sp.wait_ge(qk_ready.sem, qk_ready.at(layer * B - 1, T8 - 1))
                    sp.dma_start(we[:, :], core.dram["l0fe"][this, :, :].rearrange("a p c -> (a p) c"))\
                      .then_inc(we_in.sem, 16)
                    sp.wait_ge(g_ready.sem, g_ready.at(layer * B - 1) + B)
                    sp.dma_start(wl[:, :], core.dram["l0fl"][this, :, :].rearrange("a p c -> (a p) c"))\
                      .then_inc(wl_in.sem, 16)

            @block.gpsimd
            def _(pool):
                for b in range(B):
                    pool.tensor_copy(core.g[:, b * N:(b + 1) * N], core.xn[:, b * N:(b + 1) * N])\
                        .then_inc(g_ready.sem, 1)
                pool.wait_ge(table_in.sem, 16)
                with pool.Fori(0, L0F_LAYERS) as layer:
                    pool.wait_ge(we_in.sem, layer * 16 + 16)
                    apart(pool, passed)
                    for x, (cosines, gain) in enumerate((("rope_qc", "q_scale"), ("rope_kc", "k_scale"))):
                        pool.tensor_scalar(rope[:, x, :], const(cosines), ecol(gain), None, ALU.mult)\
                            .then_inc(rope_ready.sem, 1)
                    pool.wait_ge(rope_ready.sem, rope_ready.at(layer, 1))

                    def cosine(e, t):
                        if e is not None:
                            pool.wait_ge(unit_ready.sem, unit_ready.at(e, t))
                            if t >= 2:
                                pool.wait_ge(qk_ready.sem, qk_ready.at(e, t - 2))
                            pool.tensor_tensor(by_cos[:, t % 2, :], unit[:, t % 2, :], rope[:, t // TL, :], ALU.mult)\
                                .then_inc(cos_ready.sem, 1)

                    def normalise(m, n):
                        if m is not None:
                            c, half = n // 2, slice(4 * (n % 2), 4 * (n % 2) + 4)
                            pool.wait_ge(rtotal_ready.sem, rtotal_ready.at(m, n))
                            pool.wait_ge(prob_ready.sem, prob_ready.at(m, n))
                            if c >= 1:
                                pool.wait_ge(turned.sem, turned.at(m, 4 * c - 1))
                            k = keys(c)
                            pool.tensor_tensor(prob_n[:, half, k], prob[:, half, k],
                                               rtotal[:, c, half].unsqueeze(2).to_broadcast([P, 4, 2 * P - k.start]),
                                               ALU.mult).then_inc(prob_n_ready.sem, 1)

                    def step(e, m, batch):
                        cosine(e, 0)
                        normalise(m, 0)
                        cosine(e, 1)
                        normalise(m, 1)
                        cosine(e, 2)
                        normalise(m, 2)
                        normalise(m, 3)
                        cosine(e, 3)
                        normalise(m, 4)
                        normalise(m, 5)
                        cosine(e, 4)
                        normalise(m, 6)
                        normalise(m, 7)
                        cosine(e, 5)
                        cosine(e, 6)
                        cosine(e, 7)

                    steps(layer, step)

            @block.tensor
            def _(pe):
                pe.wait_ge(table_in.sem, 16)
                pe.wait_ge(zeroed.sem, 3)
                with pe.Fori(0, L0F_LAYERS) as layer:
                    pe.wait_ge(we_in.sem, layer * 16 + 16)
                    pe.wait_ge(swap_ready.sem, swap_ready.at(layer, 1))
                    apart(pe, passed)

                    def project(e, t):
                        if e is not None:
                            if t == 0:
                                pe.wait_ge(h_ready.sem, h_ready.at(e, 1))
                            else:
                                pe.wait_ge(unit_ready.sem, unit_ready.at(e, t - 1))
                            pe.matmul(psum[:, RAW_BANK, :], L0FE.of(we, "wq" if t < TL else "wk", t % TL, P),
                                      h_in[:, :], start=True, stop=True).then_inc(qk_raw.sem, 1)

                    def sum_squares(e, t):
                        if e is not None:
                            pe.wait_ge(sq_ready.sem, sq_ready.at(e, t))
                            if 1 <= t <= CH:
                                pe.wait_ge(v_kept.sem, v_kept.at(e, t - 1))
                            pe.matmul(psum[:, SUM_BANK, :], const("ones64"), sq[:, t % 2, :],
                                      start=True, stop=True).then_inc(sum_ready.sem, 1)

                    def rotate(e, t):
                        if e is not None:
                            pe.wait_ge(unit_ready.sem, unit_ready.at(e, t))
                            if t >= 1:
                                pe.wait_ge(sin_ready.sem, sin_ready.at(e, t - 1))
                            pe.matmul(psum[:, ROT_BANK, :], swap[:, t // TL, :], unit[:, t % 2, :],
                                      start=True, stop=True).then_inc(rot_ready.sem, 1)
                            if t + 1 < T8:
                                project(e, t + 1)
                            if t < CH:
                                pe.matmul(psum[:, V_BANK, :], h_in[:, t * P:(t + 1) * P], L0FE.of(we, "wv"),
                                          start=True, stop=True).then_inc(v_ready.sem, 1)

                    def score(m, n, parity):
                        if m is None:
                            return
                        c, half = n // 2, n % 2
                        if n == 0:
                            pe.wait_ge(qk_ready.sem, qk_ready.at(m, T8 - 1))
                            pe.wait_ge(v_kept.sem, v_kept.at(m, CH - 1))
                            pe.wait_ge(g_ready.sem, m + B)
                        else:
                            pe.wait_ge(sim_kept.sem, sim_kept.at(m, n - 1))
                        k = keys(c)
                        first = (c - 1) * P + k.start
                        for u in range(2):
                            for bank in range(2):
                                h = head[4 * half + 2 * bank + u]
                                rows = slice(64 * (h % 2), 64 * (h % 2) + 64)
                                mm = pe.matmul(psum[:, bank, u * 2 * P + k.start:u * 2 * P + 2 * P],
                                               qk[rows, parity, h // 2, c * P:(c + 1) * P],
                                               qk[rows, parity, TL + h // 2, first:(c + 1) * P],
                                               start=(u == 0), stop=(u == 1), skip_group_check=True)
                        mm.then_inc(sim_ready.sem, 1)

                    def turn(m, c):
                        if m is None:
                            return
                        for j in range(4):
                            n = 4 * c + j
                            pe.wait_ge(prob_n_ready.sem, prob_n_ready.at(m, 2 * c + j // 2))
                            if n >= 2:
                                pe.wait_ge(turned_kept.sem, turned_kept.at(m, n - 2))
                            for i in range(4):
                                slot, own = 2 * j + i // 2, i % 2
                                if c == 0 and not own:
                                    continue
                                mm = pe.transpose(psum[:, TURN_BANKS[n % 2], i * P:(i + 1) * P],
                                                  prob_n[:, slot, own * P:(own + 1) * P], core.c("ident"))
                            mm.then_inc(turned.sem, 1)

                    def draw(m, n, parity):
                        if m is None:
                            return
                        c, half = n // 2, n % 2
                        if half == 0 and c >= 1:
                            pe.wait_ge(o_kept.sem, o_kept.at(m, c - 1))
                        pe.wait_ge(turned_kept.sem, turned_kept.at(m, 4 * c + 2 * half + 1))
                        for s in range(4 * half, 4 * half + 4):
                            h = head[s]
                            rows = slice(64 * (h % 2), 64 * (h % 2) + 64)
                            dst = psum[rows, O_BANK, (h // 2) * P:(h // 2 + 1) * P]
                            for own in ((0, 1) if c else (1,)):
                                mm = pe.matmul(dst, v[:, parity, c - 1 + own, h * W:(h + 1) * W],
                                               prob_t[:, 2 * s + own, :],
                                               start=(own == 0 or c == 0), stop=(own == 1), skip_group_check=True)
                        if half == 1:
                            mm.then_inc(o_ready.sem, 1)

                    def output(m):
                        if m is not None:
                            pe.wait_ge(wl_in.sem, layer * 16 + 16)
                            pe.wait_ge(o_kept.sem, o_kept.at(m, CH - 1))
                            for t in range(TL):
                                mm = pe.matmul(psum[:, WO_BANK, :], L0FL.of(wl, "wo", t, P), o[:, t, :],
                                               start=(t == 0), stop=(t == TL - 1))
                            mm.then_inc(wo_ready.sem, 1)

                    def mean(m):
                        if m is not None:
                            pe.wait_ge(shifted_ready.sem, shifted_ready.at(m, 1))
                            norm.tensor_mean(pe, shifted[:, :])

                    def variance(m):
                        if m is not None:
                            norm.tensor_var(pe, m)

                    def geglu(m):
                        if m is None:
                            return
                        pe.wait_ge(hn_ready.sem, hn_ready.at(m))
                        for t in range(HT):
                            pe.matmul(psum[:, GATE_BANKS[t], :], L0FL.of(wl, "w1", HT + t, P), hn[:, :],
                                      start=True, stop=True).then_inc(gate_raw.sem, 1)
                        for t in range(HT):
                            if t == 2:
                                pe.wait_ge(gelu_ready.sem, gelu_ready.at(m, 0))
                            pe.matmul(psum[:, UP_BANKS[t], :], L0FL.of(wl, "w1", t, P), hn[:, :],
                                      start=True, stop=True).then_inc(up_raw.sem, 1)
                        pe.wait_ge(gelu_ready.sem, gelu_ready.at(m, 1))
                        for t in range(HT):
                            pe.wait_ge(hidden_ready.sem, hidden_ready.at(m, t))
                            mm = pe.matmul(psum[:, DOWN_BANK, :], L0FL.of(wl, "w2", t, P), hidden[:, t, :],
                                           start=(t == 0), stop=(t == HT - 1))
                        mm.then_inc(down_ready.sem, 1)

                    def step(e, m, batch):
                        parity = batch % 2 if batch is not None else None
                        project(e, 0)
                        score(m, 0, parity)
                        sum_squares(e, 0)
                        score(m, 1, parity)
                        rotate(e, 0)
                        score(m, 2, parity)
                        sum_squares(e, 1)
                        score(m, 3, parity)
                        turn(m, 0)
                        rotate(e, 1)
                        draw(m, 0, parity)
                        sum_squares(e, 2)
                        draw(m, 1, parity)
                        score(m, 4, parity)
                        rotate(e, 2)
                        score(m, 5, parity)
                        turn(m, 1)
                        sum_squares(e, 3)
                        draw(m, 2, parity)
                        rotate(e, 3)
                        draw(m, 3, parity)
                        score(m, 6, parity)
                        sum_squares(e, 4)
                        score(m, 7, parity)
                        turn(m, 2)
                        rotate(e, 4)
                        draw(m, 4, parity)
                        sum_squares(e, 5)
                        draw(m, 5, parity)
                        rotate(e, 5)
                        turn(m, 3)
                        draw(m, 6, parity)
                        draw(m, 7, parity)
                        sum_squares(e, 6)
                        output(m)
                        rotate(e, 6)
                        mean(m)
                        sum_squares(e, 7)
                        variance(m)
                        rotate(e, 7)
                        geglu(m)

                    steps(layer, step)

            @block.scalar
            def _(act):
                act.wait_ge(table_in.sem, 16)
                with act.Fori(0, L0F_LAYERS) as layer:
                    def square(e, t):
                        if e is not None:
                            act.wait_ge(qk_raw.sem, qk_raw.at(e, t))
                            if t >= 2:
                                act.wait_ge(sum_ready.sem, sum_ready.at(e, t - 2))
                            act.activation(sq[:, t % 2, :], psum[:, RAW_BANK, :], ACT.Square)\
                               .then_inc(sq_ready.sem, 1)

                    def inverse(e, t):
                        if e is not None:
                            act.wait_ge(sum_ready.sem, sum_ready.at(e, t))
                            act.activation(log[:, t % 2, :], psum[:, SUM_BANK, :], ACT.Ln, scale=2.0 ** 30,
                                           bias=const("eps_l2")).then_inc(log_ready.sem, 1)
                            act.wait_ge(log_ready.sem, log_ready.at(e, t))
                            if t >= 2:
                                act.wait_ge(unit_ready.sem, unit_ready.at(e, t - 2))
                            act.activation(rinv[:, t % 2, :], log[:, t % 2, :], ACT.Exp, scale=-0.5,
                                           bias=const("l2_back")).then_inc(rinv_ready.sem, 1)

                    def keep_value(e, c, batch):
                        if e is not None:
                            parity = (batch + 1) % 2 if batch is not None else 0
                            act.wait_ge(v_ready.sem, v_ready.at(e, c))
                            act.copy(v[:, parity, c, :], psum[:, V_BANK, :]).then_inc(v_kept.sem, 1)

                    def exponentials(m, n):
                        if m is not None:
                            c = n // 2
                            act.wait_ge(nmax_ready.sem, nmax_ready.at(m, n))
                            if c >= 1:
                                act.wait_ge(prob_n_ready.sem, prob_n_ready.at(m, n - 2))
                            k = keys(c)
                            for s in range(4 * (n % 2), 4 * (n % 2) + 4):
                                e = act.activation(prob[:, s, k], sim[:, s, k], ACT.Exp, bias=nmax[:, c, s:s + 1],
                                                   accum_out=total[:, c, s:s + 1])
                            e.then_inc(prob_ready.sem, 1)

                    def keep_turned(m, c):
                        if m is not None:
                            for j in range(4):
                                n = 4 * c + j
                                act.wait_ge(turned.sem, turned.at(m, n))
                                if c >= 1:
                                    act.wait_ge(o_ready.sem, o_ready.at(m, c - 1))
                                dst = prob_t[:, 4 * j:4 * j + 4, :]
                                src = psum[:, TURN_BANKS[n % 2], :].rearrange("p (i q) -> p i q", i=4)
                                if c == 0:
                                    dst, src = prob_t[:, 4 * j + 1:4 * j + 4:2, :], src[:, 1:4:2, :]
                                act.copy(dst, src).then_inc(turned_kept.sem, 1)

                    def keep_o(m, c):
                        if m is not None:
                            act.wait_ge(o_ready.sem, o_ready.at(m, c))
                            act.copy(o[:, :, c * P:(c + 1) * P], psum[:, O_BANK, :].rearrange("p (t q) -> p t q", t=TL))\
                               .then_inc(o_kept.sem, 1)

                    def step(e, m, batch):
                        act.preload_act_table_set(EXP_LN_SET)
                        square(e, 0)
                        inverse(e, 0)
                        exponentials(m, 0)
                        exponentials(m, 1)
                        square(e, 1)
                        keep_value(e, 0, batch)
                        inverse(e, 1)
                        exponentials(m, 2)
                        keep_turned(m, 0)
                        exponentials(m, 3)
                        square(e, 2)
                        keep_value(e, 1, batch)
                        inverse(e, 2)
                        keep_o(m, 0)
                        square(e, 3)
                        exponentials(m, 4)
                        keep_value(e, 2, batch)
                        keep_turned(m, 1)
                        inverse(e, 3)
                        exponentials(m, 5)
                        square(e, 4)
                        keep_value(e, 3, batch)
                        keep_o(m, 1)
                        inverse(e, 4)
                        exponentials(m, 6)
                        keep_turned(m, 2)
                        exponentials(m, 7)
                        square(e, 5)
                        inverse(e, 5)
                        keep_o(m, 2)
                        square(e, 6)
                        keep_turned(m, 3)
                        keep_o(m, 3)
                        inverse(e, 6)
                        square(e, 7)
                        if m is not None:
                            norm.scalar_square(act, m)
                        inverse(e, 7)
                        if m is not None:
                            norm.scalar_rstd(act, m)
                            for t in range(HT):
                                act.wait_ge(gate_raw.sem, gate_raw.at(m, t))
                                act.activation(gelu[:, t, :], psum[:, GATE_BANKS[t], :], ACT.Gelu,
                                               bias=lcol("b1", HT + t)).then_inc(gelu_ready.sem, 1)

                    steps(layer, step)

            @block.vector
            def _(dve):
                dve.wait_ge(table_in.sem, 16)
                dve.memset(h_in[64:P, 0:1], 0.0).then_inc(zeroed.sem, 1)
                dve.memset(shifted[64:P, 0:1], 0.0).then_inc(zeroed.sem, 1)
                dve.memset(prob_n[:, :, 0:W], 0.0).then_inc(zeroed.sem, 1)

                def fetch(r, b):
                    dve.wait_ge(g_ready.sem, g_ready.at(r))
                    dve.tensor_copy(h_in[0:64, :], core.g[0:64, b * N:(b + 1) * N]).then_inc(h_ready.sem, 1)
                    dve.tensor_copy(h_in[64:P, 1:N], core.g[64:P, b * N:(b + 1) * N - 1]).then_inc(h_ready.sem, 1)

                fetch(0, 0)
                with dve.Fori(0, L0F_LAYERS) as layer:
                    dve.wait_ge(we_in.sem, layer * 16 + 16)
                    dve.tensor_scalar(swap[:, 0, :], const("swap64"), ecol("q_scale"), None, ALU.mult)\
                       .then_inc(swap_ready.sem, 1)
                    dve.tensor_scalar(swap[:, 1, :], const("swap64"), ecol("k_scale"), None, ALU.mult)\
                       .then_inc(swap_ready.sem, 1)

                    def divide(e, t):
                        if e is not None:
                            dve.wait_ge(rinv_ready.sem, rinv_ready.at(e, t))
                            if t >= 2:
                                dve.wait_ge(rot_ready.sem, rot_ready.at(e, t - 2))
                                dve.wait_ge(cos_ready.sem, cos_ready.at(e, t - 2))
                            dve.scalar_tensor_tensor(out=unit[:, t % 2, :], in0=rinv[:, t % 2, :], scalar=1e12,
                                                     in1=psum[:, RAW_BANK, :], op0=ALU.min, op1=ALU.mult)\
                               .then_inc(unit_ready.sem, 1)

                    def add_rotated(e, t, batch):
                        if e is not None:
                            parity = (batch + 1) % 2 if batch is not None else 0
                            dve.wait_ge(rot_ready.sem, rot_ready.at(e, t))
                            dve.tensor_tensor(by_sin[:, t % 2, :], psum[:, ROT_BANK, :],
                                              const("rope_qs" if t < TL else "rope_ks"), ALU.mult)\
                               .then_inc(sin_ready.sem, 1)
                            dve.wait_ge(sin_ready.sem, sin_ready.at(e, t))
                            dve.wait_ge(cos_ready.sem, cos_ready.at(e, t))
                            dve.tensor_tensor(qk[:, parity, t, :], by_cos[:, t % 2, :], by_sin[:, t % 2, :], ALU.add)\
                               .then_inc(qk_ready.sem, 1)

                    def mask(m, n):
                        if m is not None:
                            c, half = n // 2, slice(4 * (n % 2), 4 * (n % 2) + 4)
                            dve.wait_ge(sim_ready.sem, sim_ready.at(m, n))
                            if c >= 1:
                                dve.wait_ge(prob_ready.sem, prob_ready.at(m, n - 2))
                            k = keys(c)
                            bias = const("window" if c else "window_first")[:, k]
                            dve.tensor_tensor(sim[:, half, k],
                                              psum[:, 0:2, :].rearrange("p b (u k) -> p (b u) k", u=2)[:, :, k],
                                              bias.unsqueeze(1).to_broadcast([P, 4, 2 * P - k.start]), ALU.add)\
                               .then_inc(sim_kept.sem, 1)
                            dve.wait_ge(sim_kept.sem, sim_kept.at(m, n))
                            dve.tensor_reduce(nmax[:, c, half], sim[:, half, k], AX.X, ALU.max, negate=True)\
                               .then_inc(nmax_ready.sem, 1)

                    def invert_total(m, n):
                        if m is not None:
                            c, half = n // 2, slice(4 * (n % 2), 4 * (n % 2) + 4)
                            dve.wait_ge(prob_ready.sem, prob_ready.at(m, n))
                            dve.reciprocal(rtotal[:, c, half], total[:, c, half]).then_inc(rtotal_ready.sem, 1)

                    def step(e, m, batch):
                        mask(m, 0)
                        divide(e, 0)
                        mask(m, 1)
                        add_rotated(e, 0, batch)
                        invert_total(m, 0)
                        invert_total(m, 1)
                        mask(m, 2)
                        divide(e, 1)
                        mask(m, 3)
                        add_rotated(e, 1, batch)
                        divide(e, 2)
                        invert_total(m, 2)
                        invert_total(m, 3)
                        mask(m, 4)
                        add_rotated(e, 2, batch)
                        mask(m, 5)
                        divide(e, 3)
                        add_rotated(e, 3, batch)
                        invert_total(m, 4)
                        invert_total(m, 5)
                        mask(m, 6)
                        divide(e, 4)
                        mask(m, 7)
                        add_rotated(e, 4, batch)
                        invert_total(m, 6)
                        invert_total(m, 7)
                        divide(e, 5)
                        add_rotated(e, 5, batch)
                        divide(e, 6)
                        if m is not None:
                            dve.wait_ge(wl_in.sem, layer * 16 + 16)
                            dve.wait_ge(wo_ready.sem, wo_ready.at(m))
                            dve.tensor_tensor(x1[:, :], core.g[:, batch * N:(batch + 1) * N], psum[:, WO_BANK, :],
                                              ALU.add).then_inc(x1_ready.sem, 1)
                            dve.wait_ge(x1_ready.sem, x1_ready.at(m))
                            dve.tensor_copy(shifted[0:64, :], x1[0:64, :]).then_inc(shifted_ready.sem, 1)
                            dve.tensor_copy(shifted[64:P, 1:N], x1[64:P, 0:N - 1]).then_inc(shifted_ready.sem, 1)
                        add_rotated(e, 6, batch)
                        if m is not None:
                            dve.wait_ge(shifted_ready.sem, shifted_ready.at(m, 1))
                            norm.vector(dve, m, shifted[:, :])
                        divide(e, 7)
                        if m is not None:
                            dve.wait_ge(norm.rstd_ready.sem, norm.rstd_ready.at(m))
                            dve.scalar_tensor_tensor(out=scaled[:, :], in0=norm.centred[:, :], scalar=lcol("ln_g"),
                                                     in1=norm.rstd[:, :], op0=ALU.mult, op1=ALU.mult)\
                               .then_inc(scaled_ready.sem, 1)
                            dve.wait_ge(scaled_ready.sem, scaled_ready.at(m))
                            dve.tensor_scalar(hn[:, :], scaled[:, :], lcol("ln_b"), None, ALU.add)\
                               .then_inc(hn_ready.sem, 1)
                        add_rotated(e, 7, batch)
                        if m is not None:
                            for t in range(HT):
                                dve.wait_ge(up_raw.sem, up_raw.at(m, t))
                                dve.wait_ge(gelu_ready.sem, gelu_ready.at(m, t))
                                dve.scalar_tensor_tensor(out=hidden[:, t, :], in0=psum[:, UP_BANKS[t], :],
                                                         scalar=lcol("b1", t), in1=gelu[:, t, :],
                                                         op0=ALU.add, op1=ALU.mult).then_inc(hidden_ready.sem, 1)
                        if e is not None:
                            dve.wait_ge(qk_raw.sem, qk_raw.at(e, T8 - 1))
                            dve.wait_ge(v_ready.sem, v_ready.at(e, CH - 1))
                            after = 1 if batch is None else batch + 2
                            fetch(e + 1, after % B)
                        if m is not None:
                            dve.wait_ge(down_ready.sem, down_ready.at(m))
                            dve.scalar_tensor_tensor(out=core.g[:, batch * N:(batch + 1) * N],
                                                     in0=psum[:, DOWN_BANK, :], scalar=lcol("b2"), in1=x1[:, :],
                                                     op0=ALU.add, op1=ALU.add).then_inc(g_ready.sem, 1)

                    steps(layer, step)


L1_HEADS, L1_INTER = 8, 512
L1A = Fields(("wq", L1_HEADS * P), ("wk", L1_HEADS * P), ("wv", L1_HEADS * P), ("wo", L1_HEADS * P),
             ("gate", L1_INTER), ("up", L1_INTER), ("down", L1_INTER),
             ("attn_norm", 1), ("out_norm", 1), ("mlp_norm", 1))


def l1_attn_layout(np, i):
    g = lambda k: i["L1_attn_" + k]
    return {"l1a": pack(np, [
        g("Wq"), g("Wk"), g("Wv"), blocks(np, g("Wo")), g("Wgate"), g("Wup"), blocks(np, g("Wdown")),
        column(g("attn_norm_w")), column(g("attn_out_norm_w")), column(g("mlp_norm_w"))])}


LAYOUTS.append(l1_attn_layout)


def l1_attn_phase(core):
    nc, psum = core.nc, core.psum
    H, F = L1_HEADS, L1_INTER // P
    Q, K, S, O, Y, V = 0, 1, 2, 4, 6, 7
    with Phase(core, "l1a") as ph:
        w = ph.buf("w", L1A.width)
        col = lambda name: L1A.of(w, name)
        h_t = ph.buf("h", N)
        v = ph.buf("v", CH, H * P)
        q = ph.buf("q", 2, N)
        k = ph.buf("k", 2, N)
        scores = ph.buf("scores", 2, CH, N)
        normed = ph.buf("normed", 2, N)
        out_sq, out_log, out_rstd = ph.buf("out_sq", N), ph.buf("out_log", N), ph.buf("out_rstd", N)
        x1 = ph.buf("x1", N)
        silu = ph.buf("silu", F, N)
        hidden = ph.buf("hidden", F, N)

        passed = ph.semaphore("passed")
        w_in = ph.semaphore("w_in")
        round_done = ph.semaphore("round_done")
        norm = ColumnNorm(ph, "norm", (V, V), (V, V), centre=False)
        h_ready = ph.semaphore("h_ready", 2)
        v_ready = ph.semaphore("v_ready", 2 * CH)
        v_kept = ph.semaphore("v_kept", 2 * CH)
        q_ready, q_kept = ph.semaphore("q_ready", H), ph.semaphore("q_kept", H)
        k_ready, k_kept = ph.semaphore("k_ready", H), ph.semaphore("k_kept", H)
        scores_ready = ph.semaphore("scores_ready", H * CH)
        scores_kept = ph.semaphore("scores_kept", H * CH)
        out_ready = ph.semaphore("out_ready", H)
        out_sq_ready = ph.semaphore("out_sq_ready", H)
        out_var_ready = ph.semaphore("out_var_ready", H)
        out_log_ready = ph.semaphore("out_log_ready", H)
        out_rstd_ready = ph.semaphore("out_rstd_ready", H)
        normed_ready = ph.semaphore("normed_ready", H)
        y_ready = ph.semaphore("y_ready", 2)
        x1_ready = ph.semaphore("x1_ready")
        gate_ready, silu_ready = ph.semaphore("gate_ready", F), ph.semaphore("silu_ready", F)
        up_ready, hidden_ready = ph.semaphore("up_ready", F), ph.semaphore("hidden_ready", F)

        with nc.Block() as block:
            @block.sync
            def _(sp):
                sp.dma_start(w[:, :], core.dram["l1a"]).then_inc(w_in.sem, 16)

            @block.tensor
            def _(pe):
                pe.wait_ge(w_in.sem, 16)
                with pe.Fori(0, B) as b:
                    pe.wait_ge(round_done.sem, round_done.at(b))
                    norm.tensor(pe, b, None, 0)
                    pe.wait_ge(h_ready.sem, h_ready.at(b, 0))
                    for c in range(CH):
                        for half in range(2):
                            n = 2 * c + half
                            pe.matmul(psum[:, n, :], h_t[:, c * P:(c + 1) * P],
                                      L1A.of(w, "wv", half, N), start=True, stop=True)\
                              .then_inc(v_ready.sem, 1)
                    pe.wait_ge(v_kept.sem, v_kept.at(b, 2 * CH - 1))

                    def query_key(h):
                        if h >= 1:
                            pe.wait_ge(q_kept.sem, q_kept.at(b, h - 1))
                            pe.wait_ge(k_kept.sem, k_kept.at(b, h - 1))
                        pe.matmul(psum[:, Q, :], L1A.of(w, "wq", h, P), h_t[:, :], start=True, stop=True)\
                          .then_inc(q_ready.sem, 1)
                        pe.matmul(psum[:, K, :], L1A.of(w, "wk", h, P), h_t[:, :], start=True, stop=True)\
                          .then_inc(k_ready.sem, 1)

                    def score(h, c):
                        n = h * CH + c
                        if n >= 2:
                            pe.wait_ge(scores_kept.sem, scores_kept.at(b, n - 2))
                        pe.matmul(psum[:, S + c % 2, 0:N - c * P], k[:, h % 2, c * P:(c + 1) * P],
                                  q[:, h % 2, c * P:N], start=True, stop=True).then_inc(scores_ready.sem, 1)

                    def output(h):
                        for c in range(CH):
                            pe.wait_ge(scores_kept.sem, scores_kept.at(b, h * CH + c))
                            mm = pe.matmul(psum[:, O + h % 2, c * P:N], v[:, c, h * P:(h + 1) * P],
                                           scores[:, h % 2, c, 0:N - c * P], start=(c == 0), stop=(c == CH - 1))
                        mm.then_inc(out_ready.sem, 1)

                    def out_var(h):
                        pe.wait_ge(out_sq_ready.sem, out_sq_ready.at(b, h))
                        pe.matmul(psum[:, V, :], core.c("mean"), out_sq[:, :], start=True, stop=True)\
                          .then_inc(out_var_ready.sem, 1)

                    def project(h):
                        pe.wait_ge(normed_ready.sem, normed_ready.at(b, h))
                        mm = pe.matmul(psum[:, Y, :], L1A.of(w, "wo", h, P), normed[:, h % 2, :],
                                       start=(h == 0), stop=(h == H - 1))
                        if h == H - 1:
                            mm.then_inc(y_ready.sem, 1)

                    query_key(0)
                    for h in range(H):
                        pe.wait_ge(q_kept.sem, q_kept.at(b, h))
                        pe.wait_ge(k_kept.sem, k_kept.at(b, h))
                        score(h, 0)
                        score(h, 1)
                        if h + 1 < H:
                            query_key(h + 1)
                        score(h, 2)
                        score(h, 3)
                        if h >= 1:
                            out_var(h - 1)
                        output(h)
                        if h >= 1:
                            project(h - 1)
                    out_var(H - 1)
                    project(H - 1)

                    norm.tensor(pe, b, None, 1)
                    pe.wait_ge(h_ready.sem, h_ready.at(b, 1))
                    for f in range(F):
                        pe.matmul(psum[:, f, :], L1A.of(w, "gate", f, P), h_t[:, :], start=True, stop=True)\
                          .then_inc(gate_ready.sem, 1)
                        pe.matmul(psum[:, F + f, :], L1A.of(w, "up", f, P), h_t[:, :], start=True, stop=True)\
                          .then_inc(up_ready.sem, 1)
                    pe.wait_ge(hidden_ready.sem, hidden_ready.at(b, Y - F))
                    for f in range(F):
                        pe.wait_ge(hidden_ready.sem, hidden_ready.at(b, f))
                        mm = pe.matmul(psum[:, Y, :], L1A.of(w, "down", f, P), hidden[:, f, :],
                                       start=(f == 0), stop=(f == F - 1))
                    mm.then_inc(y_ready.sem, 1)

            @block.scalar
            def _(act):
                with act.Fori(0, B) as b:
                    act.wait_ge(round_done.sem, round_done.at(b))
                    apart(act, passed)
                    act.preload_act_table_set(EXP_LN_SET)
                    norm.scalar(act, b, core.xn[:, cols(b)], 0)
                    for n in range(2 * CH):
                        act.wait_ge(v_ready.sem, v_ready.at(b, n))
                        act.copy(v[:, n // 2, (n % 2) * N:(n % 2 + 1) * N], psum[:, n, :])\
                           .then_inc(v_kept.sem, 1)

                    def keep(h):
                        act.wait_ge(q_ready.sem, q_ready.at(b, h))
                        act.copy(q[:, h % 2, :], psum[:, Q, :]).then_inc(q_kept.sem, 1)
                        act.wait_ge(k_ready.sem, k_ready.at(b, h))
                        act.copy(k[:, h % 2, :], psum[:, K, :]).then_inc(k_kept.sem, 1)

                    def out_norm(h):
                        act.wait_ge(out_ready.sem, out_ready.at(b, h))
                        if h >= 1:
                            act.wait_ge(normed_ready.sem, normed_ready.at(b, h - 1))
                        act.activation(out_sq[:, :], psum[:, O + h % 2, :], ACT.Square)\
                           .then_inc(out_sq_ready.sem, 1)
                        act.wait_ge(out_var_ready.sem, out_var_ready.at(b, h))
                        act.activation(out_log[:, :], psum[:, V, :], ACT.Ln, bias=core.c("eps5"))\
                           .then_inc(out_log_ready.sem, 1)
                        act.wait_ge(out_log_ready.sem, out_log_ready.at(b, h))
                        act.activation(out_rstd[:, :], out_log[:, :], ACT.Exp, scale=-0.5)\
                           .then_inc(out_rstd_ready.sem, 1)

                    keep(0)
                    for h in range(H):
                        if h + 1 < H:
                            keep(h + 1)
                        out_norm(h)
                    act.wait_ge(x1_ready.sem, x1_ready.at(b))
                    norm.scalar(act, b, x1[:, :], 1)
                    for f in range(F):
                        act.wait_ge(gate_ready.sem, gate_ready.at(b, f))
                        act.activation(silu[:, f, :], psum[:, f, :], ACT.Silu).then_inc(silu_ready.sem, 1)

            @block.vector
            def _(dve):
                dve.sem_inc(round_done.sem, 1)
                dve.wait_ge(w_in.sem, 16)
                with dve.Fori(0, B) as b:
                    dve.wait_ge(norm.rstd_ready.sem, norm.rstd_ready.at(b, 0))
                    dve.scalar_tensor_tensor(out=h_t[:, :], in0=core.xn[:, cols(b)], scalar=col("attn_norm"),
                                             in1=norm.rstd[:, :], op0=ALU.mult, op1=ALU.mult)\
                       .then_inc(h_ready.sem, 1)

                    def mask(h):
                        for c in range(CH):
                            dve.wait_ge(scores_ready.sem, scores_ready.at(b, h * CH + c))
                            dve.tensor_tensor(scores[:, h % 2, c, 0:N - c * P], psum[:, S + c % 2, 0:N - c * P],
                                              core.c("causal")[:, 0:N - c * P], ALU.mult)\
                               .then_inc(scores_kept.sem, 1)

                    def apply_norm(h):
                        dve.wait_ge(out_rstd_ready.sem, out_rstd_ready.at(b, h))
                        dve.scalar_tensor_tensor(out=normed[:, h % 2, :], in0=psum[:, O + h % 2, :],
                                                 scalar=col("out_norm"), in1=out_rstd[:, :],
                                                 op0=ALU.mult, op1=ALU.mult).then_inc(normed_ready.sem, 1)

                    for h in range(H):
                        mask(h)
                        if h >= 1:
                            apply_norm(h - 1)
                    apply_norm(H - 1)
                    dve.wait_ge(y_ready.sem, y_ready.at(b, 0))
                    dve.tensor_tensor(x1[:, :], core.xn[:, cols(b)], psum[:, Y, :], ALU.add)\
                       .then_inc(x1_ready.sem, 1)
                    dve.wait_ge(norm.rstd_ready.sem, norm.rstd_ready.at(b, 1))
                    dve.scalar_tensor_tensor(out=h_t[:, :], in0=x1[:, :], scalar=col("mlp_norm"),
                                             in1=norm.rstd[:, :], op0=ALU.mult, op1=ALU.mult)\
                       .then_inc(h_ready.sem, 1)
                    for f in range(F):
                        dve.wait_ge(silu_ready.sem, silu_ready.at(b, f))
                        dve.wait_ge(up_ready.sem, up_ready.at(b, f))
                        dve.tensor_tensor(hidden[:, f, :], silu[:, f, :], psum[:, F + f, :], ALU.mult)\
                           .then_inc(hidden_ready.sem, 1)
                    dve.wait_ge(y_ready.sem, y_ready.at(b, 1))
                    dve.tensor_tensor(core.s[:, cols(b)], x1[:, :], psum[:, Y, :], ALU.add)\
                       .then_inc(round_done.sem, 1)


L1_EXPERTS, L1_SLOTS = 64, 32
L1_E = L1_EXPERTS * L1_SLOTS
ET = L1_E // P
PIECE = Fields(("w", 16 * P), ("bias", 4 * P))


def l1_ffn_layout(np, i):
    g = lambda k: i["L1_ffn_" + k]
    pieces = []
    for n in range(4):
        w = g("expert_w")[16 * n:16 * n + 16].transpose(1, 0, 2).reshape(P, 16 * P)
        bias = np.repeat(g("expert_b")[16 * n:16 * n + 16], L1_SLOTS, axis=0)
        pieces.append(pack(np, [w, blocks(np, bias)]))
    return {"l1f_phi": g("phi_w").T, "l1f_phi_b": np.tile(g("phi_b"), (P, 1)), "l1f_experts": np.stack(pieces)}


LAYOUTS.append(l1_ffn_layout)


def l1_ffn_phase(core):
    with ExitStack() as ctx:
        combine = ctx.enter_context(core.nc.sbuf_tensor("l1f_combine", [P, ET, T], F32))
        l1_route_phase(core, combine)
        l1_expert_phase(core, combine)


def l1_route_phase(core, combine):
    nc, psum = core.nc, core.psum
    NT = T // P
    LOGIT, TURN = 4, 6
    with Phase(core, "l1r") as ph:
        phi = ph.buf("phi", L1_E)
        phi_b = ph.buf("phi_b", L1_E)
        logit = ph.buf("logit", L1_E)
        dispatch = ph.buf("dispatch", L1_E)
        combine_tok = core.g
        x_t, x_tok = ph.buf("x_t", P), ph.buf("x_tok", P)
        nmax_e = ph.buf("max_e", L1_EXPERTS)
        nmax_s = ph.buf("max_s", L1_SLOTS)
        sum_e, rsum_e = ph.buf("sum_e", L1_EXPERTS), ph.buf("rsum_e", L1_EXPERTS)
        sum_s, rsum_s = ph.buf("sum_s", L1_SLOTS), ph.buf("rsum_s", P)
        rsum_t = ph.buf("rsum_t", P)

        w_in, zeroed = ph.semaphore("w_in"), ph.semaphore("zeroed")
        passed = ph.semaphore("passed")
        x_t_ready, x_turned, x_tok_ready = ph.semaphore("x_t_ready"), ph.semaphore("x_turned"), ph.semaphore("x_tok_ready")
        logit_ready, logit_kept = ph.semaphore("logit_ready", 4), ph.semaphore("logit_kept", 4)
        max_ready = ph.semaphore("max_ready", 2)
        shifted_ready, exp_ready = ph.semaphore("shifted_ready", 2), ph.semaphore("exp_ready", 2)
        sum_ready, rsum_ready = ph.semaphore("sum_ready", 2), ph.semaphore("rsum_ready", 2)
        dispatch_ready, summed = ph.semaphore("dispatch_ready"), ph.semaphore("summed")
        rsum_turned, rsum_t_ready = ph.semaphore("rsum_turned"), ph.semaphore("rsum_t_ready")
        turned, turned_kept = ph.semaphore("turned", 4), ph.semaphore("turned_kept", 4)

        by_expert = lambda a: a.rearrange("p (n s) -> p n s", s=L1_SLOTS)
        by_slot = lambda a: a.rearrange("p (n s) -> p s n", s=L1_SLOTS)

        def steps(eng, step):
            with eng.Fori(0, NT - 1) as t:
                step(t, True)
            step(NT - 1, False)

        with nc.Block() as block:
            @block.sync
            def _(sp):
                sp.dma_start(phi[:, :], core.dram["l1f_phi"]).then_inc(w_in.sem, 16)
                sp.dma_start(phi_b[:, :], core.dram["l1f_phi_b"]).then_inc(w_in.sem, 16)

            @block.tensor
            def _(pe):
                pe.wait_ge(w_in.sem, 32)
                pe.wait_ge(zeroed.sem, 1)
                for n in range(4):
                    pe.matmul(psum[:, n, :], x_tok[:, :], phi[:, n * N:(n + 1) * N],
                              start=True, stop=False, skip_group_check=True)

                def logits(t, before):
                    pe.wait_ge(x_t_ready.sem, x_t_ready.at(t))
                    for n in range(4):
                        if n == 2 and before:
                            pe.wait_ge(sum_ready.sem, sum_ready.at(t - 1, 0))
                        pe.matmul(psum[:, LOGIT + n, :], x_t[:, :], phi[:, n * N:(n + 1) * N],
                                  start=True, stop=True).then_inc(logit_ready.sem, 1)

                def turn_x(t):
                    pe.wait_ge(logit_kept.sem, logit_kept.at(t, TURN - LOGIT))
                    pe.transpose(psum[:, TURN, 0:P], x_t[:, :], core.c("ident")).then_inc(x_turned.sem, 1)

                def step(t, after):
                    if after:
                        logits(t + 1, True)
                    pe.wait_ge(x_tok_ready.sem, x_tok_ready.at(t))
                    pe.wait_ge(dispatch_ready.sem, dispatch_ready.at(t))
                    for n in range(4):
                        mm = pe.matmul(psum[:, n, :], x_tok[:, :], dispatch[:, n * N:(n + 1) * N],
                                       start=False, stop=False, skip_group_check=True)
                    mm.then_inc(summed.sem, 1)
                    if after:
                        turn_x(t + 1)
                        pe.wait_ge(x_tok_ready.sem, x_tok_ready.at(t + 1))
                    pe.wait_ge(rsum_ready.sem, rsum_ready.at(t, 1))
                    pe.transpose(psum[:, TURN, 0:P], rsum_s[:, :], core.c("ident")).then_inc(rsum_turned.sem, 1)
                    pe.wait_ge(exp_ready.sem, exp_ready.at(t, 1))
                    if after:
                        pe.wait_ge(logit_kept.sem, logit_kept.at(t + 1, 3))
                    for n in range(4):
                        if n == 1:
                            pe.wait_ge(rsum_t_ready.sem, rsum_t_ready.at(t))
                        if n >= 2:
                            pe.wait_ge(turned_kept.sem, turned_kept.at(t, n - 2))
                        for i in range(4):
                            e = 4 * n + i
                            mm = pe.transpose(psum[:, TURN + (n + 1) % 2, i * P:(i + 1) * P],
                                              combine_tok[:, e * P:(e + 1) * P], core.c("ident"))
                        mm.then_inc(turned.sem, 1)

                logits(0, False)
                turn_x(0)
                steps(pe, step)

            @block.gpsimd
            def _(pool):
                def shift(t, before):
                    pool.wait_ge(max_ready.sem, max_ready.at(t, 0))
                    if before:
                        pool.wait_ge(summed.sem, summed.at(t - 1))
                    pool.tensor_tensor(by_expert(dispatch[:, :]), by_expert(logit[:, :]),
                                       nmax_e[:, :].unsqueeze(2).to_broadcast([P, L1_EXPERTS, L1_SLOTS]),
                                       ALU.subtract).then_inc(shifted_ready.sem, 1)
                    pool.wait_ge(max_ready.sem, max_ready.at(t, 1))
                    if before:
                        pool.wait_ge(turned.sem, turned.at(t - 1, 3))
                    pool.tensor_tensor(by_expert(combine_tok[:, :]), by_expert(logit[:, :]),
                                       nmax_s[:, :].unsqueeze(1).to_broadcast([P, L1_EXPERTS, L1_SLOTS]),
                                       ALU.subtract).then_inc(shifted_ready.sem, 1)

                shift(0, False)
                with pool.Fori(1, NT) as t:
                    shift(t, True)

            @block.scalar
            def _(act):
                def fetch(t):
                    act.copy(x_t[:, :], core.xn[:, cols(t, P)]).then_inc(x_t_ready.sem, 1)

                def keep_x(t):
                    act.wait_ge(x_turned.sem, x_turned.at(t))
                    act.copy(x_tok[:, :], psum[:, TURN, 0:P]).then_inc(x_tok_ready.sem, 1)

                def exponential(t, k):
                    buf = (dispatch, combine_tok)[k]
                    act.wait_ge(shifted_ready.sem, shifted_ready.at(t, k))
                    act.activation(buf[:, :], buf[:, :], ACT.Exp).then_inc(exp_ready.sem, 1)

                def step(t, after):
                    if after:
                        apart(act, passed)
                        fetch(t + 1)
                    exponential(t, 1)
                    if after:
                        keep_x(t + 1)
                        exponential(t + 1, 0)

                fetch(0)
                act.wait_ge(zeroed.sem, 1)
                act.wait_ge(logit_ready.sem, 1)
                keep_x(0)
                exponential(0, 0)
                steps(act, step)

            @block.vector
            def _(dve):
                dve.memset(x_tok[:, :], 0.0).then_inc(zeroed.sem, 1)
                dve.wait_ge(w_in.sem, 32)

                def front(t, before):
                    if before:
                        dve.wait_ge(shifted_ready.sem, shifted_ready.at(t - 1, 1))
                    for n in range(4):
                        dve.wait_ge(logit_ready.sem, logit_ready.at(t, n))
                        dve.tensor_tensor(logit[:, n * N:(n + 1) * N], psum[:, LOGIT + n, :],
                                          phi_b[:, n * N:(n + 1) * N], ALU.add).then_inc(logit_kept.sem, 1)
                    dve.wait_ge(logit_kept.sem, logit_kept.at(t, 3))
                    dve.tensor_reduce(nmax_e[:, :], by_expert(logit[:, :]), AX.X, ALU.max).then_inc(max_ready.sem, 1)
                    dve.tensor_reduce(nmax_s[:, :], by_slot(logit[:, :]), AX.X, ALU.max).then_inc(max_ready.sem, 1)

                def step(t, after):
                    dve.wait_ge(exp_ready.sem, exp_ready.at(t, 0))
                    dve.tensor_reduce(sum_e[:, :], by_expert(dispatch[:, :]), AX.X, ALU.add).then_inc(sum_ready.sem, 1)
                    dve.wait_ge(sum_ready.sem, sum_ready.at(t, 0))
                    dve.reciprocal(rsum_e[:, :], sum_e[:, :]).then_inc(rsum_ready.sem, 1)
                    dve.wait_ge(rsum_ready.sem, rsum_ready.at(t, 0))
                    dve.tensor_tensor(by_expert(dispatch[:, :]), by_expert(dispatch[:, :]),
                                      rsum_e[:, :].unsqueeze(2).to_broadcast([P, L1_EXPERTS, L1_SLOTS]), ALU.mult)\
                       .then_inc(dispatch_ready.sem, 1)
                    if after:
                        front(t + 1, True)
                    dve.wait_ge(exp_ready.sem, exp_ready.at(t, 1))
                    dve.tensor_reduce(sum_s[:, :], by_slot(combine_tok[:, :]), AX.X, ALU.add)\
                       .then_inc(sum_ready.sem, 1)
                    dve.wait_ge(sum_ready.sem, sum_ready.at(t, 1))
                    dve.reciprocal(rsum_s[:, :].rearrange("p (j s) -> p j s", j=4),
                                   sum_s[:, :].unsqueeze(1).to_broadcast([P, 4, L1_SLOTS]))\
                       .then_inc(rsum_ready.sem, 1)
                    dve.wait_ge(rsum_turned.sem, rsum_turned.at(t))
                    dve.tensor_copy(rsum_t[:, :], psum[:, TURN, 0:P]).then_inc(rsum_t_ready.sem, 1)
                    dve.wait_ge(rsum_t_ready.sem, rsum_t_ready.at(t))
                    for n in range(4):
                        dve.wait_ge(turned.sem, turned.at(t, n))
                        keep = dve.tensor_tensor(combine[:, 4 * n:4 * n + 4, cols(t, P)],
                                                 psum[:, TURN + (n + 1) % 2, :].rearrange("p (i q) -> p i q", i=4),
                                                 rsum_t[:, :].unsqueeze(1).to_broadcast([P, 4, P]), ALU.mult)
                        keep.then_inc(turned_kept.sem, 1)
                    dve.wait_ge(turned_kept.sem, turned_kept.at(t, 3))

                front(0, False)
                steps(dve, step)


def l1_expert_phase(core, combine):
    nc, psum = core.nc, core.psum
    with Phase(core, "l1e") as ph:
        piece = ph.buf("piece", 2, PIECE.width)
        slots = core.g
        out = ph.buf("slots_out", ET, P)
        pieces_in = [ph.semaphore("pieces_in_even"), ph.semaphore("pieces_in_odd")]
        clipped, normed, slots_ready = ph.semaphore("clipped"), ph.semaphore("normed"), ph.semaphore("slots_ready")
        out_ready, out_kept = ph.semaphore("out_ready"), ph.semaphore("out_kept")
        y_ready, y_kept = ph.semaphore("y_ready"), ph.semaphore("y_kept")
        norm = ColumnNorm(ph, "norm", (4, 5))
        quarter = [slice(n * N, (n + 1) * N) for n in range(4)]

        with nc.Block() as block:
            @block.sync
            def _(sp):
                for n in range(4):
                    if n >= 2:
                        sp.wait_ge(out_ready.sem, out_ready.at(n - 2))
                        sp.wait_ge(out_kept.sem, out_kept.at(n - 2))
                    sp.dma_start(piece[:, n % 2, :], core.dram["l1f_experts"][n]).then_inc(pieces_in[n % 2].sem, 16)

            @block.tensor
            def _(pe):
                for n in range(4):
                    pe.wait_ge(clipped.sem, clipped.at(n))
                    if n:
                        pe.wait_ge(norm.rstd_ready.sem, norm.rstd_ready.at(n - 1))
                    norm.tensor(pe, n, slots[:, quarter[n]])
                pe.wait_ge(slots_ready.sem, slots_ready.at(3))
                for n in range(4):
                    pe.wait_ge(pieces_in[n % 2].sem, 16 * (n // 2) + 16)
                    w = piece[:, n % 2, :]
                    for i in range(4):
                        for j in range(4):
                            expert = 4 * i + j
                            first = (16 * n + expert) * L1_SLOTS
                            mm = pe.matmul(psum[32 * j:32 * j + 32, n, i * P:(i + 1) * P],
                                           slots[:, first:first + L1_SLOTS], PIECE.of(w, "w", expert, P),
                                           start=(i == 0), stop=(i == 3), skip_group_check=True)
                    mm.then_inc(out_ready.sem, 1)
                for b in range(B):
                    pe.wait_ge(out_kept.sem, out_kept.at(3))
                    for e in range(ET):
                        mm = pe.matmul(psum[:, 4 + b, :], out[:, e, :], combine[:, e, b * N:(b + 1) * N],
                                       start=(e == 0), stop=(e == ET - 1))
                    mm.then_inc(y_ready.sem, 1)

            @block.scalar
            def _(act):
                act.preload_act_table_set(EXP_LN_SET)
                for n in range(4):
                    if n:
                        act.wait_ge(normed.sem, normed.at(n - 1))
                    norm.scalar(act, n)
                for n in range(4):
                    act.wait_ge(normed.sem, normed.at(n))
                    act.activation(slots[:, quarter[n]], slots[:, quarter[n]], ACT.Tanh).then_inc(slots_ready.sem, 1)

            @block.vector
            def _(dve):
                for n in range(4):
                    dve.tensor_scalar(slots[:, quarter[n]], psum[:, n, :], -33000.0, 65000.0, ALU.max, ALU.min)\
                       .then_inc(clipped.sem, 1)
                    dve.wait_ge(clipped.sem, clipped.at(n))
                    norm.vector(dve, n, slots[:, quarter[n]])
                    dve.wait_ge(norm.rstd_ready.sem, norm.rstd_ready.at(n))
                    dve.tensor_tensor(slots[:, quarter[n]], norm.centred[:, :], norm.rstd[:, :], ALU.mult)\
                       .then_inc(normed.sem, 1)
                for n in range(4):
                    dve.wait_ge(out_ready.sem, out_ready.at(n))
                    dve.tensor_tensor(out[:, 4 * n:4 * n + 4, :],
                                      psum[:, n, :].rearrange("p (i h) -> p i h", i=4),
                                      PIECE.of(piece[:, n % 2, :], "bias").rearrange("p (i h) -> p i h", i=4),
                                      ALU.add).then_inc(out_kept.sem, 1)
                for b in range(B):
                    dve.wait_ge(y_ready.sem, y_ready.at(b))
                    dve.tensor_copy(core.g[:, b * N:(b + 1) * N], psum[:, 4 + b, :]).then_inc(y_kept.sem, 1)


L2_SSM = 64
L2_GATES = 3
L2A = Fields(("wb", P), ("wih", 3 * P), ("wd", P), ("wa", P), ("wc", P), ("whh", 3 * P), ("proj", P),
             ("gate", 2 * P), ("bb", 1), ("cb", 1), ("db", 1), ("bih", 3), ("bhh", 3), ("pb", 1), ("gb", 2))


def l2_attn_layout(np, i):
    g = lambda k: i["L2_attn_" + k]
    bw = np.zeros((P, P), np.float32)
    bw[:, :L2_SSM] = g("Bw").T
    a = np.zeros((L2_SSM, P), np.float32)
    a[:, :L2_SSM] = g("A").T
    gate = np.repeat(g("gate_w")[:, :, None], P, axis=2)
    return {"l2a": pack(np, [
        bw, g("W_ih").T, g("Dw").T, a, g("Cw").T, g("W_hh").T, g("proj_w").T, gate[0], gate[1],
        column(g("Bb")), column(g("Cb")), column(g("Db")), g("b_ih").reshape(3, P).T, g("b_hh").reshape(3, P).T,
        column(g("proj_b")), np.tile(g("gate_b"), (P, 1))])}


LAYOUTS.append(l2_attn_layout)


def l2_attn_phase(core):
    with ExitStack() as ctx:
        sb = lambda name, *shape: ctx.enter_context(core.nc.sbuf_tensor("l2a_" + name, [P, *shape], F32))
        w = sb("w", L2A.width)
        drive = sb("drive", N + 32, 4, B)
        trail_h = sb("trail_h", N, B)
        trail_s = sb("trail_s", N, B)
        l2_drive_phase(core, w, drive)
        l2_scan_phase(core, w, drive, trail_h, trail_s)
        l2_output_phase(core, w, trail_h, trail_s)


def l2_drive_phase(core, w, drive):
    nc, psum = core.nc, core.psum
    with Phase(core, "l2d") as ph:
        w_in, made, kept = ph.semaphore("w_in"), ph.semaphore("made"), ph.semaphore("kept")
        col = lambda name, k=0: L2A.of(w, name, k, 1)
        with nc.Block() as block:
            @block.sync
            def _(sp):
                sp.dma_start(w[:, :], core.dram["l2a"]).then_inc(w_in.sem, 16)

            @block.tensor
            def _(pe):
                pe.wait_ge(w_in.sem, 16)
                for n in range(4 * B):
                    part, b = n // B, n % B
                    if n >= 8:
                        pe.wait_ge(kept.sem, kept.at(n - 8))
                    lhs = L2A.of(w, "wih", part, P) if part < 3 else L2A.of(w, "wb")
                    pe.matmul(psum[:, n % 8, :], lhs, core.xn[:, b * N:(b + 1) * N], start=True, stop=True)\
                      .then_inc(made.sem, 1)

            @block.vector
            def _(dve):
                dve.memset(drive[:, N:, :, :], 0.0)
                dve.wait_ge(w_in.sem, 16)
                for n in range(4 * B):
                    part, b = n // B, n % B
                    dve.wait_ge(made.sem, made.at(n))
                    if part < 2:
                        biases = (col("bih", part), col("bhh", part), ALU.add, ALU.add)
                    else:
                        biases = (col("bih", 2) if part == 2 else col("bb"), None, ALU.add)
                    dve.tensor_scalar(drive[:, 0:N, part, b], psum[:, n % 8, :], *biases).then_inc(kept.sem, 1)


def l2_scan_phase(core, w, drive, trail_h, trail_s):
    nc, psum = core.nc, core.psum
    U, S = 16, L2_SSM
    R, NB, Z, SB = 0, 1, 2, 3
    with Phase(core, "l2s") as ph:
        now = ph.buf("now", 2, U, 4, B)
        h = ph.buf("h", 2, U, B)
        s = ph.buf("s", 2, U, B)
        r_in, r = ph.buf("r_in", B), ph.buf("r", B)
        z, not_z = ph.buf("z", B), ph.buf("not_z", B)
        rn, n_in, n = ph.buf("rn", B), ph.buf("n_in", B), ph.buf("n", B)
        zh, zn = ph.buf("zh", B), ph.buf("zn", B)
        s_in, s_sig = ph.buf("s_in", B), ph.buf("s_sig", B)
        col = lambda name, k=0: L2A.of(w, name, k, 1)

        K = 2 * U
        passed = ph.semaphore("passed")
        zeroed = ph.semaphore("zeroed", 2)
        now_ready, moved = ph.semaphore("now_ready", 2), ph.semaphore("moved", 4)
        r_raw, n_raw, z_raw, s_raw = (ph.semaphore(x, K) for x in ("r_raw", "n_raw", "z_raw", "s_raw"))
        r_in_ready, r_ready = ph.semaphore("r_in_ready", K), ph.semaphore("r_ready", K)
        z_ready, not_z_ready = ph.semaphore("z_ready", K), ph.semaphore("not_z_ready", K)
        rn_ready, n_in_ready, n_ready = ph.semaphore("rn_ready", K), ph.semaphore("n_in_ready", K), ph.semaphore("n_ready", K)
        zh_ready, zn_ready = ph.semaphore("zh_ready", K), ph.semaphore("zn_ready", K)
        h_ready = ph.semaphore("h_ready", K)
        s_in_ready, s_sig_ready, s_ready = ph.semaphore("s_in_ready", K), ph.semaphore("s_sig_ready", K), ph.semaphore("s_ready", K)
        ROUNDS = N // K

        def before(buf, i):
            j = (i - 1) % K
            return buf[:, j // U, j % U, :]

        def at(buf, i):
            return buf[:, i // U, i % U, :]

        with nc.Block() as block:
            @block.gpsimd
            def _(pool):
                pool.sem_inc(moved.sem, 4)
                pool.memset(h[:, 1, U - 1, :], 0.0).then_inc(zeroed.sem, 1)
                pool.memset(s[:, 1, U - 1, :], 0.0).then_inc(zeroed.sem, 1)
                for half in range(2):
                    pool.tensor_copy(now[:, half, :, :, :], drive[:, half * U:(half + 1) * U, :, :])\
                        .then_inc(now_ready.sem, 1)
                with pool.Fori(0, ROUNDS) as k:
                    for half in range(2):
                        pool.wait_ge(h_ready.sem, h_ready.at(k, half * U + U))
                        pool.wait_ge(s_ready.sem, s_ready.at(k, half * U + U))
                        pool.tensor_copy(trail_h[:, bass.ds(k * K + half * U, U), :], h[:, half, :, :])\
                            .then_inc(moved.sem, 1)
                        pool.tensor_copy(trail_s[0:S, bass.ds(k * K + half * U, U), :], s[0:S, half, :, :])\
                            .then_inc(moved.sem, 1)
                        pool.tensor_copy(now[:, half, :, :, :], drive[:, bass.ds(k * K + K + half * U, U), :, :])\
                            .then_inc(now_ready.sem, 1)

            @block.tensor
            def _(pe):
                pe.wait_ge(zeroed.sem, 2)
                with pe.Fori(0, ROUNDS) as k:
                    for i in range(K):
                        if i % U == 0:
                            pe.wait_ge(now_ready.sem, now_ready.at(k, i // U))
                        pe.wait_ge(not_z_ready.sem, not_z_ready.at(k, i))
                        pe.matmul(psum[:, Z, 0:B], core.c("ident"), now[:, i // U, i % U, 1, :],
                                  start=True, stop=False)
                        pe.wait_ge(h_ready.sem, h_ready.at(k, i))
                        for bank, gate, raw in ((R, 0, r_raw), (NB, 2, n_raw), (Z, 1, z_raw)):
                            pe.matmul(psum[:, bank, 0:B], L2A.of(w, "whh", gate, P), before(h, i),
                                      start=(bank != Z), stop=True).then_inc(raw.sem, 1)
                        pe.wait_ge(s_ready.sem, s_ready.at(k, i))
                        apart(pe, passed)
                        pe.matmul(psum[0:S, SB, 0:B], L2A.of(w, "wa")[0:S, 0:S], before(s, i)[0:S, :],
                                  start=True, stop=True).then_inc(s_raw.sem, 1)

            @block.scalar
            def _(act):
                act.preload_act_table_set("sigmoid_and_others")
                act.sem_inc(not_z_ready.sem, 1)
                with act.Fori(0, ROUNDS) as k:
                    for i in range(K):
                        act.wait_ge(r_in_ready.sem, r_in_ready.at(k, i))
                        act.activation(r[:, :], r_in[:, :], ACT.Sigmoid).then_inc(r_ready.sem, 1)
                        act.wait_ge(n_in_ready.sem, n_in_ready.at(k, i))
                        act.activation(n[:, :], n_in[:, :], ACT.Tanh).then_inc(n_ready.sem, 1)
                        act.wait_ge(z_raw.sem, z_raw.at(k, i))
                        act.activation(z[:, :], psum[:, Z, 0:B], ACT.Sigmoid).then_inc(z_ready.sem, 1)
                        act.activation(not_z[:, :], psum[:, Z, 0:B], ACT.Sigmoid, scale=-1.0)\
                           .then_inc(not_z_ready.sem, 1)
                        act.wait_ge(s_in_ready.sem, s_in_ready.at(k, i))
                        act.activation(s_sig[0:S, :], s_in[0:S, :], ACT.Sigmoid).then_inc(s_sig_ready.sem, 1)

            @block.vector
            def _(dve):
                dve.wait_ge(zeroed.sem, 2)
                dve.sem_inc(h_ready.sem, 1)
                dve.sem_inc(s_ready.sem, 1)
                with dve.Fori(0, ROUNDS) as k:
                    for i in range(K):
                        if i % U == 0:
                            dve.wait_ge(now_ready.sem, now_ready.at(k, i // U))
                            dve.wait_ge(moved.sem, k * 4 + (4 if i else 2))
                        drv = lambda part: now[:, i // U, i % U, part, :]
                        dve.wait_ge(r_raw.sem, r_raw.at(k, i))
                        dve.tensor_tensor(r_in[:, :], psum[:, R, 0:B], drv(0), ALU.add).then_inc(r_in_ready.sem, 1)
                        dve.wait_ge(r_ready.sem, r_ready.at(k, i))
                        dve.wait_ge(n_raw.sem, n_raw.at(k, i))
                        dve.scalar_tensor_tensor(out=rn[:, :], in0=psum[:, NB, 0:B], scalar=col("bhh", 2),
                                                 in1=r[:, :], op0=ALU.add, op1=ALU.mult).then_inc(rn_ready.sem, 1)
                        dve.wait_ge(rn_ready.sem, rn_ready.at(k, i))
                        dve.tensor_tensor(n_in[:, :], rn[:, :], drv(2), ALU.add).then_inc(n_in_ready.sem, 1)
                        dve.wait_ge(z_ready.sem, z_ready.at(k, i))
                        dve.tensor_tensor(zh[:, :], z[:, :], before(h, i), ALU.mult).then_inc(zh_ready.sem, 1)
                        dve.wait_ge(n_ready.sem, n_ready.at(k, i))
                        dve.wait_ge(not_z_ready.sem, not_z_ready.at(k, i) + 1)
                        dve.tensor_tensor(zn[:, :], not_z[:, :], n[:, :], ALU.mult).then_inc(zn_ready.sem, 1)
                        dve.wait_ge(zn_ready.sem, zn_ready.at(k, i))
                        dve.wait_ge(zh_ready.sem, zh_ready.at(k, i))
                        dve.tensor_tensor(at(h, i), zn[:, :], zh[:, :], ALU.add).then_inc(h_ready.sem, 1)
                        dve.wait_ge(s_raw.sem, s_raw.at(k, i))
                        dve.tensor_tensor(s_in[0:S, :], psum[0:S, SB, 0:B], drv(3)[0:S, :], ALU.add)\
                           .then_inc(s_in_ready.sem, 1)
                        dve.wait_ge(s_sig_ready.sem, s_sig_ready.at(k, i))
                        dve.wait_ge(s_in_ready.sem, s_in_ready.at(k, i))
                        dve.tensor_tensor(at(s, i)[0:S, :], s_in[0:S, :], s_sig[0:S, :], ALU.mult)\
                           .then_inc(s_ready.sem, 1)


def l2_output_phase(core, w, trail_h, trail_s):
    nc, psum = core.nc, core.psum
    S = L2_SSM
    with Phase(core, "l2o") as ph:
        bias = ph.buf("bias", 1)
        gate, part = ph.buf("gate", 2, 2, N), ph.buf("part", 2, 2, N)
        bias_ready = ph.semaphore("bias_ready")
        gate_raw, gate_ready = ph.semaphore("gate_raw", 2), ph.semaphore("gate_ready", 2)
        y_ready, part_ready, out_ready = ph.semaphore("y_ready", 2), ph.semaphore("part_ready", 2), ph.semaphore("out_ready")
        col = lambda name, k=0: L2A.of(w, name, k, 1)
        with nc.Block() as block:
            @block.tensor
            def _(pe):
                for b in range(B):
                    x = core.xn[:, b * N:(b + 1) * N]
                    bank = 4 * (b % 2)
                    if b >= 2:
                        pe.wait_ge(part_ready.sem, part_ready.at(b - 2, 1))
                    for g in range(2):
                        pe.matmul(psum[:, bank + g, :], L2A.of(w, "gate", g, P), x, start=True, stop=True)\
                          .then_inc(gate_raw.sem, 1)
                    pe.matmul(psum[:, bank + 2, :], L2A.of(w, "wd"), x, start=True, stop=False)
                    pe.matmul(psum[:, bank + 2, :], L2A.of(w, "wc")[0:S, :], trail_s[0:S, :, b],
                              start=False, stop=True).then_inc(y_ready.sem, 1)
                    pe.matmul(psum[:, bank + 3, :], L2A.of(w, "proj"), trail_h[:, :, b], start=True, stop=True)\
                      .then_inc(y_ready.sem, 1)

            @block.scalar
            def _(act):
                for b in range(B):
                    if b >= 2:
                        act.wait_ge(part_ready.sem, part_ready.at(b - 2, 1))
                    for g in range(2):
                        act.wait_ge(gate_raw.sem, gate_raw.at(b, g))
                        act.activation(gate[:, b % 2, g, :], psum[:, 4 * (b % 2) + g, :], ACT.Sigmoid,
                                       bias=col("gb", g)).then_inc(gate_ready.sem, 1)

            @block.vector
            def _(dve):
                dve.tensor_tensor(bias[:, :], col("cb"), col("db"), ALU.add).then_inc(bias_ready.sem, 1)
                dve.wait_ge(bias_ready.sem, 1)
                for b in range(B):
                    if b >= 2:
                        dve.wait_ge(out_ready.sem, out_ready.at(b - 2))
                    for g in range(2):
                        dve.wait_ge(gate_ready.sem, gate_ready.at(b, g))
                        dve.wait_ge(y_ready.sem, y_ready.at(b, g))
                        dve.scalar_tensor_tensor(out=part[:, b % 2, g, :], in0=psum[:, 4 * (b % 2) + 2 + g, :],
                                                 scalar=col("pb") if g else bias[:, :], in1=gate[:, b % 2, g, :],
                                                 op0=ALU.add, op1=ALU.mult).then_inc(part_ready.sem, 1)
                    dve.wait_ge(part_ready.sem, part_ready.at(b, 1))
                    dve.tensor_tensor(core.s[:, b * N:(b + 1) * N], part[:, b % 2, 0, :], part[:, b % 2, 1, :],
                                      ALU.add).then_inc(out_ready.sem, 1)


L2_EXPERTS = 8
L2F = Fields(("gate", L2_EXPERTS), ("w1", L2_EXPERTS * P), ("w2", L2_EXPERTS * P), ("w3", L2_EXPERTS * P),
             ("b1", L2_EXPERTS), ("b2", L2_EXPERTS), ("b3", L2_EXPERTS), ("gb", 1))


def l2_ffn_layout(np, i):
    g = lambda k: i["L2_ffn_" + k]
    side = lambda w: w.transpose(1, 0, 2).reshape(P, L2_EXPERTS * P)
    return {"l2f": pack(np, [g("gate_w"), side(g("w1")), side(g("w2")), side(g("w3")),
                             g("b1").T, g("b2").T, g("b3").T, column(g("gate_b"))])}


LAYOUTS.append(l2_ffn_layout)


def l2_ffn_phase(core):
    with ExitStack() as ctx:
        sb = lambda name, *shape: ctx.enter_context(core.nc.sbuf_tensor("l2f_" + name, [P, *shape], F32))
        w = sb("w", L2F.width)
        table = sb("table", CONST_L2F.width)
        picked = sb("picked", T)
        weight = sb("weight", T)
        l2_pick_phase(core, w, table, picked, weight)
        l2_expert_phase(core, w, table, picked, weight)


def l2_pick_phase(core, w, table, picked, weight):
    nc, psum = core.nc, core.psum
    E, NT = L2_EXPERTS, T // P
    with Phase(core, "l2p") as ph:
        logit, prob = ph.buf("logit", T), ph.buf("prob", T)
        nmax, total, rtotal = ph.buf("nmax", B), ph.buf("total", B), ph.buf("rtotal", B)
        prob_tok, top = ph.buf("prob_tok", NT, E), ph.buf("top", NT, E)
        index = ph.buf("index", NT, E, dtype=U32)
        index_f = ph.buf("index_f", NT, 2)
        is_pick = ph.buf("is_pick", 2, NT, E)
        picked_tok = ph.buf("picked_tok", NT, E)
        w_in = ph.semaphore("w_in")
        logit_raw, logit_ready, nmax_ready = ph.semaphore("logit_raw"), ph.semaphore("logit_ready"), ph.semaphore("nmax_ready")
        exp_ready, rtotal_ready, prob_ready = ph.semaphore("exp_ready"), ph.semaphore("rtotal_ready"), ph.semaphore("prob_ready")
        turned, prob_tok_ready = ph.semaphore("turned"), ph.semaphore("prob_tok_ready")
        top_ready, index_ready, index_f_ready = ph.semaphore("top_ready"), ph.semaphore("index_ready"), ph.semaphore("index_f_ready")
        is_pick_ready, picked_tok_ready = ph.semaphore("is_pick_ready"), ph.semaphore("picked_tok_ready")
        back, picked_ready, weight_ready = ph.semaphore("back"), ph.semaphore("picked_ready"), ph.semaphore("weight_ready")
        batch = [slice(b * N, (b + 1) * N) for b in range(B)]
        with nc.Block() as block:
            @block.sync
            def _(sp):
                sp.dma_start(w[:, :], core.dram["l2f"]).then_inc(w_in.sem, 16)
                sp.dma_start(table[:, :], core.dram["const_l2f"]).then_inc(w_in.sem, 16)

            @block.tensor
            def _(pe):
                pe.wait_ge(w_in.sem, 32)
                for b in range(B):
                    pe.matmul(psum[0:E, b, :], L2F.of(w, "gate"), core.xn[:, batch[b]], start=True, stop=True)\
                      .then_inc(logit_raw.sem, 1)
                pe.wait_ge(prob_ready.sem, prob_ready.at(B - 1))
                for t in range(NT):
                    mm = pe.transpose(psum[:, 4, t * E:(t + 1) * E], prob[0:E, t * P:(t + 1) * P],
                                      core.c("ident")[0:E, 0:E])
                mm.then_inc(turned.sem, 1)
                pe.wait_ge(picked_tok_ready.sem, 1)
                for b in range(B):
                    for c in range(CH):
                        mm = pe.transpose(psum[0:E, b, c * P:(c + 1) * P], picked_tok[:, b * CH + c, :],
                                          core.c("ident"))
                    mm.then_inc(back.sem, 1)

            @block.scalar
            def _(act):
                for b in range(B):
                    act.wait_ge(nmax_ready.sem, nmax_ready.at(b))
                    act.activation(prob[0:E, batch[b]], logit[0:E, batch[b]], ACT.Exp, bias=nmax[0:E, b:b + 1],
                                   accum_out=total[0:E, b:b + 1]).then_inc(exp_ready.sem, 1)

            @block.vector
            def _(dve):
                dve.wait_ge(w_in.sem, 32)
                for b in range(B):
                    dve.wait_ge(logit_raw.sem, logit_raw.at(b))
                    dve.tensor_scalar(logit[0:E, batch[b]], psum[0:E, b, :], L2F.of(w, "gb")[0:E, :], None, ALU.add)\
                       .then_inc(logit_ready.sem, 1)
                    dve.wait_ge(logit_ready.sem, logit_ready.at(b))
                    dve.tensor_reduce(nmax[0:E, b:b + 1], logit[0:E, batch[b]], AX.X, ALU.max, negate=True)\
                       .then_inc(nmax_ready.sem, 1)
                for b in range(B):
                    dve.wait_ge(exp_ready.sem, exp_ready.at(b))
                    dve.reciprocal(rtotal[0:E, b:b + 1], total[0:E, b:b + 1]).then_inc(rtotal_ready.sem, 1)
                    dve.wait_ge(rtotal_ready.sem, rtotal_ready.at(b))
                    dve.tensor_scalar(prob[0:E, batch[b]], prob[0:E, batch[b]], rtotal[0:E, b:b + 1], None, ALU.mult)\
                       .then_inc(prob_ready.sem, 1)
                dve.wait_ge(turned.sem, 1)
                dve.tensor_copy(prob_tok[:, :, :], psum[:, 4, 0:NT * E].rearrange("p (t e) -> p t e", e=E))\
                   .then_inc(prob_tok_ready.sem, 1)
                dve.wait_ge(prob_tok_ready.sem, 1)
                for t in range(NT):
                    dve.max(top[:, t, :], prob_tok[:, t, :]).then_inc(top_ready.sem, 1)
                dve.wait_ge(top_ready.sem, top_ready.at(NT - 1))
                for t in range(NT):
                    dve.max_index(index[:, t, :], top[:, t, :], prob_tok[:, t, :]).then_inc(index_ready.sem, 1)
                dve.wait_ge(index_ready.sem, index_ready.at(NT - 1))
                dve.tensor_copy(index_f[:, :, :], index[:, :, 0:2]).then_inc(index_f_ready.sem, 1)
                dve.wait_ge(index_f_ready.sem, 1)
                for k in range(2):
                    dve.tensor_tensor(is_pick[:, k, :, :],
                                      CONST_L2F.of(table, "index8").unsqueeze(1).to_broadcast([P, NT, E]),
                                      index_f[:, :, k:k + 1].to_broadcast([P, NT, E]), ALU.is_equal)\
                       .then_inc(is_pick_ready.sem, 1)
                dve.wait_ge(is_pick_ready.sem, is_pick_ready.at(1))
                dve.tensor_tensor(picked_tok[:, :, :], is_pick[:, 0, :, :], is_pick[:, 1, :, :], ALU.add)\
                   .then_inc(picked_tok_ready.sem, 1)
                for b in range(B):
                    dve.wait_ge(back.sem, back.at(b))
                    dve.tensor_copy(picked[0:E, batch[b]], psum[0:E, b, :]).then_inc(picked_ready.sem, 1)
                    dve.wait_ge(picked_ready.sem, picked_ready.at(b))
                    dve.tensor_tensor(weight[0:E, batch[b]], prob[0:E, batch[b]], picked[0:E, batch[b]], ALU.mult)\
                       .then_inc(weight_ready.sem, 1)


def l2_expert_phase(core, w, table, picked, weight):
    nc, psum = core.nc, core.psum
    E = L2_EXPERTS
    with Phase(core, "l2e") as ph:
        h1, h2, y = ph.buf("h1", 2, N), ph.buf("h2", 2, N), ph.buf("y", 2, N)
        weighted = ph.buf("weighted", 2, N)
        part = ph.buf("part", E)
        total = ph.buf("total", E)
        total_t = ph.buf("total_t", P)
        passed = ph.semaphore("passed")
        round_done = ph.semaphore("round_done")
        up1, up2, up3 = ph.semaphore("up1", E), ph.semaphore("up2", E), ph.semaphore("up3", E)
        h1_ready, h2_ready, y_ready = ph.semaphore("h1_ready", E), ph.semaphore("h2_ready", E), ph.semaphore("y_ready", E)
        spread, part_ready = ph.semaphore("spread", E), ph.semaphore("part_ready", E)
        started, turned, total_ready = ph.semaphore("started"), ph.semaphore("turned"), ph.semaphore("total_ready")
        out_ready, out_kept = ph.semaphore("out_ready"), ph.semaphore("out_kept")
        col = lambda name, k: L2F.of(w, name, k, 1)
        with nc.Block() as block:
            @block.tensor
            def _(pe):
                with pe.Fori(0, B) as b:
                    pe.wait_ge(round_done.sem, round_done.at(b))
                    x, wt = core.xn[:, cols(b)], weight[0:E, cols(b)]
                    for i in range(E + 3):
                        if i < E:
                            if i >= 2:
                                pe.wait_ge(h1_ready.sem, h1_ready.at(b, i - 2))
                            pe.matmul(psum[:, i % 2, :], L2F.of(w, "w1", i, P), x, start=True, stop=True)\
                              .then_inc(up1.sem, 1)
                        if 0 <= i - 1 < E:
                            e = i - 1
                            pe.wait_ge(h1_ready.sem, h1_ready.at(b, e))
                            if e >= 2:
                                pe.wait_ge(h2_ready.sem, h2_ready.at(b, e - 2))
                            pe.matmul(psum[:, 2 + e % 2, :], L2F.of(w, "w2", e, P), h1[:, e % 2, :],
                                      start=True, stop=True).then_inc(up2.sem, 1)
                        if 0 <= i - 2 < E:
                            e = i - 2
                            pe.wait_ge(h2_ready.sem, h2_ready.at(b, e))
                            if e >= 2:
                                pe.wait_ge(y_ready.sem, y_ready.at(b, e - 2))
                            pe.matmul(psum[:, 4 + e % 2, :], L2F.of(w, "w3", e, P), h2[:, e % 2, :],
                                      start=True, stop=True).then_inc(up3.sem, 1)
                        if 0 <= i - 3 < E:
                            e = i - 3
                            if e >= 2:
                                pe.wait_ge(part_ready.sem, part_ready.at(b, e - 2))
                            apart(pe, passed)
                            pe.matmul(psum[:, 6 + e % 2, :], CONST_L2F.of(table, "sel8", e, P)[0:E, :], wt,
                                      start=True, stop=True).then_inc(spread.sem, 1)
                pe.wait_ge(round_done.sem, round_done.at(B))
                pe.transpose(psum[0:E, 0, 0:P], total[:, :], core.c("ident")).then_inc(turned.sem, 1)
                pe.wait_ge(total_ready.sem, 1)
                for b in range(B):
                    pe.matmul(psum[:, 1 + b, :], total_t[0:E, :], picked[0:E, b * N:(b + 1) * N],
                              start=True, stop=True).then_inc(out_ready.sem, 1)

            @block.scalar
            def _(act):
                with act.Fori(0, B) as b:
                    act.wait_ge(round_done.sem, round_done.at(b))
                    for i in range(E + 2):
                        if i < E:
                            act.wait_ge(up1.sem, up1.at(b, i))
                            if i >= 2:
                                act.wait_ge(up2.sem, up2.at(b, i - 2))
                            act.activation(h1[:, i % 2, :], psum[:, i % 2, :], ACT.Relu, bias=col("b1", i))\
                               .then_inc(h1_ready.sem, 1)
                        if i >= 2:
                            e = i - 2
                            act.wait_ge(up3.sem, up3.at(b, e))
                            if e >= 2:
                                act.wait_ge(part_ready.sem, part_ready.at(b, e - 2))
                            act.activation(y[:, e % 2, :], psum[:, 4 + e % 2, :], ACT.Relu, bias=col("b3", e))\
                               .then_inc(y_ready.sem, 1)

            @block.vector
            def _(dve):
                dve.sem_inc(round_done.sem, 1)
                dve.memset(total[:, :], 0.0).then_inc(started.sem, 1)
                dve.wait_ge(started.sem, 1)
                with dve.Fori(0, B) as b:
                    for i in range(E + 2):
                        if i < E:
                            dve.wait_ge(up2.sem, up2.at(b, i))
                            if i >= 2:
                                dve.wait_ge(up3.sem, up3.at(b, i - 2))
                            dve.tensor_scalar(h2[:, i % 2, :], psum[:, 2 + i % 2, :], col("b2", i), 0.0,
                                              ALU.add, ALU.max).then_inc(h2_ready.sem, 1)
                        if i >= 2:
                            e = i - 2
                            dve.wait_ge(y_ready.sem, y_ready.at(b, e))
                            dve.wait_ge(spread.sem, spread.at(b, e))
                            if e >= 2:
                                dve.wait_ge(part_ready.sem, part_ready.at(b, e - 2))
                            dve.tensor_tensor_reduce(out=weighted[:, e % 2, :], in0=y[:, e % 2, :],
                                                     in1=psum[:, 6 + e % 2, :], scale=1.0, scalar=0.0,
                                                     op0=ALU.mult, op1=ALU.add, accum_out=part[:, e:e + 1])\
                               .then_inc(part_ready.sem, 1)
                    dve.wait_ge(part_ready.sem, part_ready.at(b, E - 1))
                    dve.wait_ge(round_done.sem, b + 1)
                    dve.tensor_tensor(total[:, :], total[:, :], part[:, :], ALU.add).then_inc(round_done.sem, 1)
                dve.wait_ge(turned.sem, 1)
                dve.tensor_copy(total_t[0:E, :], psum[0:E, 0, 0:P]).then_inc(total_ready.sem, 1)
                for b in range(B):
                    dve.wait_ge(out_ready.sem, out_ready.at(b))
                    dve.tensor_copy(core.g[:, b * N:(b + 1) * N], psum[:, 1 + b, :]).then_inc(out_kept.sem, 1)


L3_HEADS, L3_DH = 16, 8
L3_TILES = L3_HEADS // 2
L3A = Fields(("wq", L3_TILES * P), ("wk", L3_TILES * P), ("wv", P), ("wo", P), ("bv", P),
             ("bq", L3_TILES), ("bk", L3_TILES), ("bo", 1), ("gamma", 1), ("beta", 1))


def l3_attn_layout(np, i):
    g = lambda k: i["L3_attn_" + k]

    def spread(a):
        out = np.zeros((a.shape[0], L3_HEADS, 8, L3_DH), np.float32)
        out[:] = a.reshape(-1, L3_HEADS, 1, L3_DH)
        return out.reshape(-1, L3_TILES * P)

    return {"l3a": pack(np, [
        spread(g("Wq")), spread(g("Wk")), g("Wv"), g("Wo"), np.tile(g("bv"), (P, 1)),
        spread(g("bq")[None]).reshape(L3_TILES, P).T, spread(g("bk")[None]).reshape(L3_TILES, P).T,
        column(g("bo")), column(g("gamma")), column(g("beta"))])}


LAYOUTS.append(l3_attn_layout)


def l3_attn_phase(core):
    nc, psum = core.nc, core.psum
    H, DH, DV, TL = L3_HEADS, L3_DH, L3_DH + 1, L3_TILES
    SCALE = float(DH) ** -0.5
    SIM, TURN, NUM, MAKE, TAIL = 0, 2, 4, 6, 7
    STEPS, ITEMS = CH * H, 2 * TL
    BF16 = mybir.dt.bfloat16
    LATE = {1: ITEMS - 2, 3: ITEMS - 1}
    EARLY = {8 * (m // 2) + 5 + 2 * (m % 2): m for m in range(ITEMS - 2)}
    with Phase(core, "l3a") as ph:
        w = ph.buf("w", L3A.width)
        col = lambda name, k=0: L3A.of(w, name, k, 1)
        table = ph.buf("table", CONST_L3A.width)
        q = ph.buf("q", TL, N, dtype=BF16)
        k = ph.buf("k", TL, 2, N, dtype=BF16)
        full, part1 = ph.buf("full", 2, N), ph.buf("part1", 2, N, dtype=BF16)
        rest, part2 = ph.buf("rest", 2, N), ph.buf("part2", 2, N, dtype=BF16)
        v = ph.buf("v", B * CH, H * DV)
        nmax = ph.buf("nmax", STEPS)
        prob = ph.buf("prob", 4, N)
        prob_t = ph.buf("prob_t", 4, N)
        rden = ph.buf("rden", CH, H)
        att, att_t = ph.buf("att", CH, P), ph.buf("att_t", N)
        res, scaled = ph.buf("res", N), ph.buf("scaled", N)

        w_in, set_ready = ph.semaphore("w_in"), ph.semaphore("set_ready")
        raw, full_ready, part1_ready, rest_ready, part2_ready, split_ready = (
            ph.semaphore(s, ITEMS) for s in ("raw", "full_ready", "part1_ready", "rest_ready", "part2_ready",
                                             "split_ready"))
        v_raw, v_ready = ph.semaphore("v_raw"), ph.semaphore("v_ready")
        sim_ready, nmax_ready, prob_ready = (ph.semaphore(s, STEPS) for s in ("sim_ready", "nmax_ready", "prob_ready"))
        turned = ph.semaphore("turned", STEPS)
        even_kept, odd_kept = ph.semaphore("even_kept", STEPS // 2), ph.semaphore("odd_kept", STEPS // 2)
        drawn = ph.semaphore("drawn", STEPS)
        rden_ready, att_ready = ph.semaphore("rden_ready", CH), ph.semaphore("att_ready", CH)
        att_turned, att_t_ready = ph.semaphore("att_turned"), ph.semaphore("att_t_ready")
        out_ready, res_ready = ph.semaphore("out_ready"), ph.semaphore("res_ready")
        scaled_ready, s_ready = ph.semaphore("scaled_ready"), ph.semaphore("s_ready")
        norm = ColumnNorm(ph, "norm", (TAIL, TAIL))

        def started(r, n, back):
            return n >= back or not (isinstance(r, int) and r == 0)

        def rounds(eng, step, end):
            step(0, False, True)
            with eng.Fori(1, B - 1) as r:
                step(r, True, True)
            step(B - 1, True, False)
            end(B - 1)

        with nc.Block() as block:
            @block.sync
            def _(sp):
                sp.dma_start(w[:, :], core.dram["l3a"]).then_inc(w_in.sem, 16)
                sp.dma_start(table[:, :], core.dram["const_l3a"]).then_inc(w_in.sem, 16)

            @block.gpsimd
            def _(pool):
                pool.memset(k[:, :, :, :], 0.0).then_inc(set_ready.sem, 1)
                pool.memset(v[:, :, :].rearrange("p c (h d) -> p c h d", d=DV)[:, :, :, DH:DV], 1.0)\
                    .then_inc(set_ready.sem, 1)

            @block.tensor
            def _(pe):
                pe.wait_ge(w_in.sem, 32)
                pe.wait_ge(set_ready.sem, 2)

                def project(r, m):
                    if started(r, m, 1):
                        pe.wait_ge(full_ready.sem, full_ready.at(r, m - 1))
                    pe.matmul(psum[:, MAKE, :], L3A.of(w, "wk" if m % 2 else "wq", m // 2, P), core.xn[:, cols(r)],
                              start=True, stop=True).then_inc(raw.sem, 1)

                def project_v(b):
                    for c in range(CH):
                        first = b * N + c * P
                        mm = pe.matmul(psum[:, b, c * P:(c + 1) * P], core.xn[:, first:first + P], L3A.of(w, "wv"),
                                       start=(c == 0), stop=(c == CH - 1), skip_group_check=True)
                    mm.then_inc(v_raw.sem, 1)

                def score(r, n):
                    h, c = n // CH, n % CH
                    if n % (2 * CH) == 0:
                        pe.wait_ge(split_ready.sem, split_ready.at(r, 2 * (h // 2) + 1))
                    if started(r, n, 2):
                        pe.wait_ge(prob_ready.sem, prob_ready.at(r, n - 2))
                    pe.matmul(psum[:, SIM + n % 2, :], q[:, h // 2, c * P:(c + 1) * P], k[:, h // 2, h % 2, :],
                              start=True, stop=True).then_inc(sim_ready.sem, 1)

                def turn(r, n):
                    pe.wait_ge(prob_ready.sem, prob_ready.at(r, n))
                    if started(r, n, 2):
                        kept = odd_kept if n % 2 else even_kept
                        pe.wait_ge(kept.sem, kept.at(r, n // 2 - 1))
                    for j in range(CH):
                        mm = pe.transpose(psum[:, TURN + n % 2, j * P:(j + 1) * P],
                                          prob[:, n % 4, j * P:(j + 1) * P], core.c("ident"))
                    mm.then_inc(turned.sem, 1)

                def draw(r, n):
                    h, c = n % STEPS // CH, n % CH
                    if n in (0, 2) and started(r, n, 3):
                        pe.wait_ge(att_ready.sem, att_ready.at(r, c + 1 - CH))
                    kept = odd_kept if n % 2 else even_kept
                    pe.wait_ge(kept.sem, kept.at(r, n // 2))
                    at = (c % 2) * H * DV + h * DV
                    for j in range(CH):
                        mm = pe.matmul(psum[:, NUM + c // 2, at:at + DV],
                                       prob_t[:, n % 4, j * P:(j + 1) * P],
                                       v[:, bass.ds((r if n >= 0 else r - 1) * CH + j, 1), h * DV:(h + 1) * DV],
                                       start=(h == 0 and c % 2 == 0 and j == 0),
                                       stop=(h == H - 1 and c % 2 == 1 and j == CH - 1), skip_group_check=True)
                    mm.then_inc(drawn.sem, 1)

                def turn_att(r):
                    for c in range(CH):
                        pe.wait_ge(att_ready.sem, att_ready.at(r, c))
                        mm = pe.transpose(psum[:, TAIL, c * P:(c + 1) * P], att[:, c, :], core.c("ident"))
                    mm.then_inc(att_turned.sem, 1)

                def output(r):
                    pe.wait_ge(att_t_ready.sem, att_t_ready.at(r))
                    pe.matmul(psum[:, TAIL, :], L3A.of(w, "wo"), att_t[:, :], start=True, stop=True)\
                      .then_inc(out_ready.sem, 1)

                def mean(r):
                    pe.wait_ge(res_ready.sem, res_ready.at(r))
                    norm.tensor_mean(pe, res[:, :])

                def step(r, before, after):
                    for i in range(STEPS):
                        score(r, i)
                        if before or i >= 2:
                            turn(r, i - 2)
                        if before or i >= 4:
                            draw(r, i - 4)
                        if i in LATE:
                            project(r, LATE[i])
                        if after and i in EARLY:
                            project(r + 1, EARLY[i])
                        if before and i == 8:
                            turn_att(r - 1)
                        if before and i == 12:
                            output(r - 1)
                        if before and i == 16:
                            mean(r - 1)
                        if before and i == 20:
                            norm.tensor_var(pe, r - 1)

                def end(r):
                    for i in range(STEPS, STEPS + 4):
                        if i < STEPS + 2:
                            turn(r, i - 2)
                        draw(r, i - 4)
                    turn_att(r)
                    output(r)
                    mean(r)
                    norm.tensor_var(pe, r)

                for b in range(B):
                    project_v(b)
                for m in range(ITEMS - 2):
                    project(0, m)
                pe.wait_ge(v_ready.sem, v_ready.at(B - 1))
                rounds(pe, step, end)

            @block.scalar
            def _(act):
                act.preload_act_table_set(EXP_LN_SET)

                def round1(r, m):
                    act.wait_ge(full_ready.sem, full_ready.at(r, m))
                    if started(r, m, 2):
                        act.wait_ge(rest_ready.sem, rest_ready.at(r, m - 2))
                    act.copy(part1[:, m % 2, :], full[:, m % 2, :]).then_inc(part1_ready.sem, 1)

                def round2(r, m):
                    act.wait_ge(rest_ready.sem, rest_ready.at(r, m))
                    if started(r, m, 2):
                        act.wait_ge(split_ready.sem, split_ready.at(r, m - 2))
                    act.copy(part2[:, m % 2, :], rest[:, m % 2, :]).then_inc(part2_ready.sem, 1)

                def exponential(r, n):
                    act.wait_ge(nmax_ready.sem, nmax_ready.at(r, n))
                    if started(r, n, 4):
                        act.wait_ge(turned.sem, turned.at(r, n - 4))
                    act.activation(prob[:, n % 4, :], psum[:, SIM + n % 2, :], ACT.Exp, bias=nmax[:, n:n + 1])\
                       .then_inc(prob_ready.sem, 1)

                def keep(r, n):
                    act.wait_ge(turned.sem, turned.at(r, n))
                    if started(r, n, 4):
                        act.wait_ge(drawn.sem, drawn.at(r, n - 4))
                    act.copy(prob_t[:, n % 4, :], psum[:, TURN + n % 2, :]).then_inc(odd_kept.sem, 1)

                def keep_att(r):
                    act.wait_ge(att_turned.sem, att_turned.at(r))
                    act.copy(att_t[:, :], psum[:, TAIL, :]).then_inc(att_t_ready.sem, 1)

                def step(r, before, after):
                    for i in range(STEPS):
                        exponential(r, i)
                        if i % 2 and (before or i >= 3):
                            keep(r, i - 2)
                        if i - 2 in LATE:
                            round1(r, LATE[i - 2])
                        if i - 5 in LATE:
                            round2(r, LATE[i - 5])
                        if after and i - 2 in EARLY:
                            round1(r + 1, EARLY[i - 2])
                        if after and i - 5 in EARLY:
                            round2(r + 1, EARLY[i - 5])
                        if before and i == 9:
                            keep_att(r - 1)
                        if before and i == 18:
                            norm.scalar_square(act, r - 1)
                        if before and i == 21:
                            norm.scalar_rstd(act, r - 1)

                def end(r):
                    keep(r, STEPS - 1)
                    keep_att(r)
                    norm.scalar(act, r)

                for m in range(ITEMS - 1):
                    if m < ITEMS - 2:
                        round1(0, m)
                    if m >= 1:
                        round2(0, m - 1)
                rounds(act, step, end)

            @block.vector
            def _(dve):
                dve.wait_ge(w_in.sem, 32)
                dve.wait_ge(set_ready.sem, 2)

                def keep_full(r, m):
                    dve.wait_ge(raw.sem, raw.at(r, m))
                    if started(r, m, 2):
                        dve.wait_ge(rest_ready.sem, rest_ready.at(r, m - 2))
                    if m % 2:
                        dve.tensor_scalar(full[:, 1, :], psum[:, MAKE, :], col("bk", m // 2), None, ALU.add)\
                           .then_inc(full_ready.sem, 1)
                    else:
                        dve.tensor_scalar(full[:, 0, :], psum[:, MAKE, :], col("bq", m // 2), SCALE,
                                          ALU.add, ALU.mult).then_inc(full_ready.sem, 1)

                def subtract1(r, m):
                    dve.wait_ge(part1_ready.sem, part1_ready.at(r, m))
                    if started(r, m, 2):
                        dve.wait_ge(split_ready.sem, split_ready.at(r, m - 2))
                    dve.scalar_tensor_tensor(out=rest[:, m % 2, :], in0=part1[:, m % 2, :],
                                             scalar=CONST_L3A.of(table, "less1", m % 2, 1),
                                             in1=full[:, m % 2, :], op0=ALU.mult, op1=ALU.add)\
                       .then_inc(rest_ready.sem, 1)

                def subtract2(r, m):
                    dve.wait_ge(part2_ready.sem, part2_ready.at(r, m))
                    if m % 2 == 0:
                        dve.scalar_tensor_tensor(out=q[:, m // 2, :], in0=part2[:, 0, :],
                                                 scalar=CONST_L3A.of(table, "less2", 0, 1), in1=rest[:, 0, :],
                                                 op0=ALU.mult, op1=ALU.add).then_inc(split_ready.sem, 1)
                    else:
                        for u in range(2):
                            rows = slice(64 * u, 64 * u + 64)
                            part = dve.scalar_tensor_tensor(
                                out=k[rows, m // 2, u, :], in0=part2[rows, 1, :],
                                scalar=CONST_L3A.of(table, "less2", 1, 1)[rows, :], in1=rest[rows, 1, :],
                                op0=ALU.mult, op1=ALU.add)
                        part.then_inc(split_ready.sem, 1)

                def keep_v(b):
                    dve.wait_ge(v_raw.sem, v_raw.at(b))
                    dve.tensor_tensor(v[:, b * CH:(b + 1) * CH, :].rearrange("p c (h d) -> p c h d", d=DV)[:, :, :, 0:DH],
                                      psum[:, b, :].rearrange("p (c h d) -> p c h d", c=CH, d=DH),
                                      L3A.of(w, "bv").rearrange("p (h d) -> p h d", d=DH).unsqueeze(1)
                                      .to_broadcast([P, CH, H, DH]), ALU.add).then_inc(v_ready.sem, 1)

                def greatest(r, n):
                    dve.wait_ge(sim_ready.sem, sim_ready.at(r, n))
                    dve.tensor_reduce(nmax[:, n:n + 1], psum[:, SIM + n % 2, :], AX.X, ALU.max, negate=True)\
                       .then_inc(nmax_ready.sem, 1)

                def keep(r, n):
                    dve.wait_ge(turned.sem, turned.at(r, n))
                    if started(r, n, 4):
                        dve.wait_ge(drawn.sem, drawn.at(r, n - 4))
                    dve.tensor_copy(prob_t[:, n % 4, :], psum[:, TURN + n % 2, :]).then_inc(even_kept.sem, 1)

                def divide(r, c):
                    dve.wait_ge(drawn.sem, drawn.at(r, STEPS - CH + c | 1))
                    num = psum[:, NUM + c // 2, (c % 2) * H * DV:(c % 2 + 1) * H * DV]
                    num = num.rearrange("p (h d) -> p h d", d=DV)
                    dve.reciprocal(rden[:, c, :], num[:, :, DH]).then_inc(rden_ready.sem, 1)
                    dve.wait_ge(rden_ready.sem, rden_ready.at(r, c))
                    dve.tensor_tensor(att[:, c, :].rearrange("p (h d) -> p h d", d=DH), num[:, :, 0:DH],
                                      rden[:, c, :].unsqueeze(2).to_broadcast([P, H, DH]), ALU.mult)\
                       .then_inc(att_ready.sem, 1)

                def add_input(r):
                    dve.wait_ge(out_ready.sem, out_ready.at(r))
                    dve.scalar_tensor_tensor(out=res[:, :], in0=psum[:, TAIL, :], scalar=col("bo"),
                                             in1=core.xn[:, cols(r)], op0=ALU.add, op1=ALU.add)\
                       .then_inc(res_ready.sem, 1)

                def centre(r):
                    dve.wait_ge(res_ready.sem, res_ready.at(r))
                    norm.vector(dve, r, res[:, :])

                def scale(r):
                    dve.wait_ge(norm.rstd_ready.sem, norm.rstd_ready.at(r))
                    dve.scalar_tensor_tensor(out=scaled[:, :], in0=norm.centred[:, :], scalar=col("gamma"),
                                             in1=norm.rstd[:, :], op0=ALU.mult, op1=ALU.mult)\
                       .then_inc(scaled_ready.sem, 1)
                    dve.wait_ge(scaled_ready.sem, scaled_ready.at(r))
                    dve.tensor_scalar(core.s[:, cols(r)], scaled[:, :], col("beta"), None, ALU.add)\
                       .then_inc(s_ready.sem, 1)

                def step(r, before, after):
                    for i in range(STEPS):
                        greatest(r, i)
                        if i % 2 == 0 and (before or i >= 2):
                            keep(r, i - 2)
                        if before and i in (2, 4):
                            divide(r - 1, i - 2)
                            divide(r - 1, i - 1)
                        if i - 1 in LATE:
                            keep_full(r, LATE[i - 1])
                        if i - 4 in LATE:
                            subtract1(r, LATE[i - 4])
                        if i - 6 in LATE:
                            subtract2(r, LATE[i - 6])
                        if after and i - 1 in EARLY:
                            keep_full(r + 1, EARLY[i - 1])
                        if after and i - 4 in EARLY:
                            subtract1(r + 1, EARLY[i - 4])
                        if after and i - 6 in EARLY:
                            subtract2(r + 1, EARLY[i - 6])
                        if before and i == 13:
                            add_input(r - 1)
                        if before and i == 17:
                            centre(r - 1)
                        if before and i == 23:
                            scale(r - 1)

                def end(r):
                    keep(r, STEPS - 2)
                    for c in range(CH):
                        divide(r, c)
                    add_input(r)
                    centre(r)
                    scale(r)

                for b in range(B):
                    keep_v(b)
                for m in range(ITEMS):
                    if m < ITEMS - 2:
                        keep_full(0, m)
                    if 1 <= m < ITEMS - 1:
                        subtract1(0, m - 1)
                    if m >= 2:
                        subtract2(0, m - 2)
                rounds(dve, step, end)


L3_EXPERTS, L3_RANK = 8, 16
L3F = Fields(("weight", P), ("gate", L3_EXPERTS), ("u", P), ("v", P))


def l3_ffn_layout(np, i):
    g = lambda k: i["L3_ffn_" + k]
    return {"l3f": pack(np, [g("weight").T, g("gate_w").T, g("lora_U").reshape(P, P).T,
                             g("lora_V").transpose(0, 2, 1).reshape(P, P)])}


LAYOUTS.append(l3_ffn_layout)


def l3_ffn_phase(core):
    nc, psum = core.nc, core.psum
    E, R, NT = L3_EXPERTS, L3_RANK, T // P
    with Phase(core, "l3f") as ph:
        w = ph.buf("w", L3F.width)
        top, gate = ph.buf("top", NT), ph.buf("gate", NT, E)
        total, rtotal = ph.buf("total", NT), ph.buf("rtotal", NT)
        gate_n = ph.buf("gate_n", NT, E)
        gate_wide = ph.buf("gate_wide", NT, P)
        low, mixed = ph.buf("low", 2, N), ph.buf("mixed", 2, N)
        w_in, logit_ready = ph.semaphore("w_in"), ph.semaphore("logit_ready")
        top_ready, shifted_ready, exp_ready = ph.semaphore("top_ready"), ph.semaphore("shifted_ready"), ph.semaphore("exp_ready")
        total_ready, rtotal_ready = ph.semaphore("total_ready"), ph.semaphore("rtotal_ready")
        gate_ready, wide_ready = ph.semaphore("gate_ready"), ph.semaphore("wide_ready")
        turned, low_raw, low_ready = ph.semaphore("turned"), ph.semaphore("low_raw"), ph.semaphore("low_ready")
        mixed_ready, out_ready, out_kept = ph.semaphore("mixed_ready"), ph.semaphore("out_ready"), ph.semaphore("out_kept")
        with nc.Block() as block:
            @block.sync
            def _(sp):
                sp.dma_start(w[:, :], core.dram["l3f"]).then_inc(w_in.sem, 16)

            @block.tensor
            def _(pe):
                pe.wait_ge(w_in.sem, 16)
                for t in range(NT):
                    mm = pe.matmul(psum[:, 0, t * E:(t + 1) * E], core.xn[:, t * P:(t + 1) * P], L3F.of(w, "gate"),
                                   start=(t == 0), stop=(t == NT - 1), skip_group_check=True)
                mm.then_inc(logit_ready.sem, 1)
                for b in range(B):
                    if b >= 2:
                        pe.wait_ge(low_ready.sem, low_ready.at(b - 2))
                    pe.matmul(psum[:, 1 + b % 2, :], L3F.of(w, "u"), core.xn[:, b * N:(b + 1) * N],
                              start=True, stop=True).then_inc(low_raw.sem, 1)
                    pe.wait_ge(wide_ready.sem, 1)
                    if b >= 2:
                        pe.wait_ge(mixed_ready.sem, mixed_ready.at(b - 2))
                    for c in range(CH):
                        mm = pe.transpose(psum[:, 3 + b % 2, c * P:(c + 1) * P], gate_wide[:, b * CH + c, :],
                                          core.c("ident"))
                    mm.then_inc(turned.sem, 1)
                    if b >= 2:
                        pe.wait_ge(out_kept.sem, out_kept.at(b - 2))
                    pe.matmul(psum[:, 5 + b % 2, :], L3F.of(w, "weight"), core.xn[:, b * N:(b + 1) * N],
                              start=True, stop=False)
                    pe.wait_ge(mixed_ready.sem, mixed_ready.at(b))
                    pe.matmul(psum[:, 5 + b % 2, :], L3F.of(w, "v"), mixed[:, b % 2, :], start=False, stop=True)\
                      .then_inc(out_ready.sem, 1)

            @block.scalar
            def _(act):
                act.wait_ge(shifted_ready.sem, 1)
                act.activation(gate[:, :, :], gate[:, :, :], ACT.Exp).then_inc(exp_ready.sem, 1)
                for b in range(B):
                    act.wait_ge(low_raw.sem, low_raw.at(b))
                    if b >= 2:
                        act.wait_ge(mixed_ready.sem, mixed_ready.at(b - 2))
                    act.mul(low[:, b % 2, :], psum[:, 1 + b % 2, :], 1.0 / R).then_inc(low_ready.sem, 1)

            @block.vector
            def _(dve):
                dve.wait_ge(logit_ready.sem, 1)
                logit = psum[:, 0, 0:NT * E].rearrange("p (t e) -> p t e", e=E)
                dve.tensor_reduce(top[:, :], logit, AX.X, ALU.max).then_inc(top_ready.sem, 1)
                dve.wait_ge(top_ready.sem, 1)
                dve.tensor_tensor(gate[:, :, :], logit, top[:, :].unsqueeze(2).to_broadcast([P, NT, E]), ALU.subtract)\
                   .then_inc(shifted_ready.sem, 1)
                dve.wait_ge(exp_ready.sem, 1)
                dve.tensor_reduce(total[:, :], gate[:, :, :], AX.X, ALU.add).then_inc(total_ready.sem, 1)
                dve.wait_ge(total_ready.sem, 1)
                dve.reciprocal(rtotal[:, :], total[:, :]).then_inc(rtotal_ready.sem, 1)
                dve.wait_ge(rtotal_ready.sem, 1)
                dve.tensor_tensor(gate_n[:, :, :], gate[:, :, :], rtotal[:, :].unsqueeze(2).to_broadcast([P, NT, E]),
                                  ALU.mult).then_inc(gate_ready.sem, 1)
                dve.wait_ge(gate_ready.sem, 1)
                dve.tensor_copy(gate_wide[:, :, :].rearrange("p t (e r) -> p (t e) r", r=R),
                                gate_n[:, :, :].rearrange("p t e -> p (t e)").unsqueeze(2).to_broadcast([P, NT * E, R]))\
                   .then_inc(wide_ready.sem, 1)
                for b in range(B):
                    dve.wait_ge(turned.sem, turned.at(b))
                    dve.wait_ge(low_ready.sem, low_ready.at(b))
                    if b >= 2:
                        dve.wait_ge(out_ready.sem, out_ready.at(b - 2))
                    dve.tensor_tensor(mixed[:, b % 2, :], psum[:, 3 + b % 2, :], low[:, b % 2, :], ALU.mult)\
                       .then_inc(mixed_ready.sem, 1)
                    dve.wait_ge(out_ready.sem, out_ready.at(b))
                    dve.tensor_copy(core.g[:, b * N:(b + 1) * N], psum[:, 5 + b % 2, :]).then_inc(out_kept.sem, 1)


def build(nc, dram):
    with ExitStack() as ctx:
        core = Core(nc, ctx, dram)
        load_phase(core)
        mix_phase(core, "norm0", mix=False)
        l0_attn_phase(core)
        l0_ffn_phase(core)
        mix_phase(core, "norm1")
        l1_attn_phase(core)
        l1_ffn_phase(core)
        mix_phase(core, "norm2")
        l2_attn_phase(core)
        l2_ffn_phase(core)
        mix_phase(core, "norm3")
        l3_attn_phase(core)
        l3_ffn_phase(core)
        mix_phase(core, "mix4", norm=False)
        store_phase(core)


def constants():
    import numpy as np
    sets = {"const": CONST, "const_l0a": CONST_L0A, "const_l0f": CONST_L0F, "const_l2f": CONST_L2F,
            "const_l3a": CONST_L3A}
    out = {name: np.zeros((P, fields.width), np.float32) for name, fields in sets.items()}

    def put(name, value):
        for key, fields in sets.items():
            if name in fields.at:
                start, width = fields.at[name]
                out[key][:len(value), start:start + width] = value

    i = np.arange(P)
    put("ident", np.eye(P))
    put("mean", np.full((P, P), 1.0 / P))
    put("causal", np.arange(N)[None, :] >= i[:, None])
    put("ones64", i[:, None] // 64 == i[None, :] // 64)
    swap = np.zeros((P, P))
    for h in (0, 64):
        for d in range(32):
            swap[h + d + 32, h + d] = -1.0
            swap[h + d, h + d + 32] = 1.0
    put("swap64", swap)
    head_rows = np.repeat(np.eye(8), 16, axis=0)
    put("head_rows", head_rows)
    put("kvmask", np.tile(np.repeat(head_rows, 9, axis=1), (1, 2)))
    put("causal4", np.tile(i[None, :] >= i[:, None], (1, 4)))
    sign, nhalf = np.zeros((P, 8, 16)), np.zeros((P, 8, 16))
    for j in range(8):
        top = 64 * (j // 4) + 8 * (j % 4)
        sign[top:top + 8, j, 0:8] = 1.0
        sign[top:top + 8, j, 8:16] = -1.0
        nhalf[top + 32:top + 40, j, :] = -0.5
    put("sign", sign.reshape(P, P))
    put("nhalf", nhalf.reshape(P, P))
    key = np.arange(2 * P)[None, :] - P
    seen = (key <= i[:, None]) & (key >= i[:, None] - 64)
    put("window", np.where(seen, 0.0, -1e30))
    put("window_first", np.where(seen & (key >= 0), 0.0, -1e30))
    parts = np.repeat([[1, 1, 1, 2, 2, 3, 2, 3], [1, 2, 3, 1, 2, 1, 3, 2]], L3_DH, axis=1)
    parts = np.tile(parts, (1, 2)).T
    put("less1", -1.0 * (parts >= 2))
    put("less2", -1.0 * (parts == 3))
    sel = np.zeros((8, 8, P))
    for e in range(8):
        sel[e, e, :] = 1.0
    put("sel8", sel.reshape(8, 8 * P))
    put("index8", np.tile(np.arange(8), (P, 1)))
    f = np.float32
    half = np.arange(0, 64, 2, dtype=f)
    inv = (f(1.0) / f(10000.0) ** (half / f(64))).astype(f)
    t = np.arange(N, dtype=f)
    angle = (t[:, None] * inv[None, :]).astype(f).astype(np.float64)
    base = ((half + f(0.4 * 64)) / f(1.4 * 64)).astype(np.float64)
    scale = base[None, :] ** ((t - N // 2) / 32.0)[:, None].astype(np.float64)
    four = lambda a: np.tile(a, (1, 4)).T
    cos, sin, scale = four(np.cos(angle)), four(np.sin(angle)), four(scale)
    put("rope_qc", 8.0 * cos * scale)
    put("rope_qs", 8.0 * sin * scale)
    put("rope_kc", cos / scale)
    put("rope_ks", sin / scale)
    put("eps5", np.full((P, 1), LN_EPS))
    put("eps_l2", np.full((P, 1), 2.0 ** -64))
    put("l2_back", np.full((P, 1), 15 * np.log(2.0)))
    return out


def kernel(**inputs):
    import numpy as np
    import concourse.bacc as bacc
    from concourse.bass_utils import run_bass_kernel_spmd as run

    inputs = {k: np.asarray(v) for k, v in inputs.items()}
    arrays = {"x": inputs["L0_attn_x"], **constants()}
    for phase_layout in LAYOUTS:
        arrays.update(phase_layout(np, inputs))
    arrays = {f"in_{k}": np.ascontiguousarray(v) for k, v in arrays.items()}
    nc = bacc.Bacc("TRN2", target_bir_lowering=False, num_devices=1)
    dram = {k[3:]: nc.dram_tensor(k, v.shape, F32, kind="ExternalInput").ap() for k, v in arrays.items()}
    dram["out"] = nc.dram_tensor("out", (B, N, P), F32, kind="ExternalOutput").ap()
    build(nc, dram)
    result = run(nc, [arrays], core_ids=[0])
    return result.results[0]["out"]
```
